# Optimizing a Trainium2 kernel written in Bass

```python
import numpy as np
import jax
import jax.numpy as jnp

def _softmax(x, axis=-1):
    return jax.nn.softmax(x, axis=axis)

def _gelu(x):
    return jax.nn.gelu(x, approximate=True)

def _silu(x):
    return jax.nn.silu(x)

def _sigmoid(x):
    return jax.nn.sigmoid(x)

def _layernorm(x, axis=-1, eps=1e-05):
    m = jnp.mean(x, axis=axis, keepdims=True)
    v = jnp.var(x, axis=axis, keepdims=True)
    return (x - m) / jnp.sqrt(v + eps)

def _scatter_add(tgt, idx, src, axis=0):
    return tgt.at[idx].add(src)

def _segment_sum(src, seg, n):
    return jax.ops.segment_sum(src, seg, n)
kernel_name = 'mk_audio_tower_d4_tok_audfeat256_r4_b3e719'

def setup_inputs(seed: int=0):
    np.random.seed(seed)
    _w = jnp.asarray

    def _rec_inputs():
        import jax
        import jax.numpy as jnp
        _rk = jax.random.key(seed)
        x = 7.22013e-05 + 1.00017 * jax.random.normal(jax.random.fold_in(_rk, 1), (16, 250, 64), jnp.float32)
        return x
    x = _rec_inputs()

    def _L0_tok_setup():
        import jax, jax.numpy as jnp
        import numpy as np
        WIN = 9
        key = jax.random.key(seed)
        ks = jax.random.split(key, 4)
        N, L, C, U = (8, 1024, 64, 64)
        x = jax.random.normal(ks[0], (N, L, C), dtype=jnp.float32)
        W_qry = jax.random.normal(ks[1], (C, U), dtype=jnp.float32) * 0.05
        W_key = jax.random.normal(ks[2], (C, U), dtype=jnp.float32) * 0.05
        v = jax.random.normal(ks[3], (U,), dtype=jnp.float32) * 0.05
        b = jnp.zeros((U,), dtype=jnp.float32)
        return {'x': x, 'W_qry': W_qry, 'W_key': W_key, 'v': v, 'b': b}
    _L0_tok_all = _L0_tok_setup()
    _L0_tok_in = {k: v for k, v in _L0_tok_all.items() if k in ('W_qry', 'W_key', 'v', 'b')}
    del _L0_tok_all

    def _L0_attn_setup():
        import jax, jax.numpy as jnp
        import numpy as np
        NUM_HEADS = 8

        def _to_heads(y, R, C, H, hd):
            y = y.reshape(R, C, H, hd).transpose(0, 2, 1, 3)
            y = jnp.transpose(y, (2, 1, 0, 3)).reshape(1, H, C, R * hd)
            return y

        def _reference_tuple_inner(x, Wq, bq, Wk, bk, Wv, bv):
            R, C, E = x.shape
            H = NUM_HEADS
            hd = E // H
            q = _to_heads(x @ Wq.T + bq, R, C, H, hd)
            k = _to_heads(x @ Wk.T + bk, R, C, H, hd)
            v = _to_heads(x @ Wv.T + bv, R, C, H, hd)
            d = q.shape[-1]
            q = jax.nn.softmax(q, axis=-1)
            k = jax.nn.softmax(k, axis=-2)
            q = q * jnp.asarray(float(d) ** 0.5, dtype=q.dtype)
            attn_weights = jnp.einsum('bhnd,bhmd->bhnm', q, k).sum(0)
            context = jnp.einsum('bhnd,bhne->bhde', k, v)
            out = jnp.einsum('bhnd,bhde->hbne', q, context)
            out = out.reshape(H, C, R, hd)
            out = jnp.transpose(out, (2, 1, 0, 3)).reshape(R, C, E)
            return (out, attn_weights)
        key = jax.random.key(seed)
        ks = jax.random.split(key, 7)
        R, C, E = (16, 512, 64)
        x = jax.random.normal(ks[0], (R, C, E), dtype=jnp.float32)
        s = 0.02
        Wq = jax.random.normal(ks[1], (E, E), dtype=jnp.float32) * s
        bq = jax.random.normal(ks[2], (E,), dtype=jnp.float32) * s
        Wk = jax.random.normal(ks[3], (E, E), dtype=jnp.float32) * s
        bk = jax.random.normal(ks[4], (E,), dtype=jnp.float32) * s
        Wv = jax.random.normal(ks[5], (E, E), dtype=jnp.float32) * s
        bv = jax.random.normal(ks[6], (E,), dtype=jnp.float32) * s
        return {'x': x, 'Wq': Wq, 'bq': bq, 'Wk': Wk, 'bk': bk, 'Wv': Wv, 'bv': bv}
    _L0_attn_all = _L0_attn_setup()
    _L0_attn_in = {k: v for k, v in _L0_attn_all.items() if k in ('Wq', 'bq', 'Wk', 'bk', 'Wv', 'bv')}
    del _L0_attn_all

    def _L0_ffn_setup():
        import jax, jax.numpy as jnp
        import numpy as np
        B, S, D = (8, 1024, 64)
        H = 4 * D
        CAPACITY = 0.5
        key = jax.random.key(seed)
        ks = jax.random.split(key, 6)
        x = jax.random.normal(ks[0], (B, S, D), dtype=jnp.float32)
        attention_mask = jnp.zeros((B, 1, 1, S), dtype=jnp.float32)
        wr = jax.random.normal(ks[1], (D, 1), dtype=jnp.float32) * 0.02
        br = jnp.zeros((1,), dtype=jnp.float32)
        w1 = jax.random.normal(ks[2], (D, H), dtype=jnp.float32) * 0.02
        b1 = jnp.zeros((H,), dtype=jnp.float32)
        w2 = jax.random.normal(ks[3], (H, D), dtype=jnp.float32) * 0.02
        b2 = jnp.zeros((D,), dtype=jnp.float32)
        return {'x': x, 'attention_mask': attention_mask, 'wr': wr, 'br': br, 'w1': w1, 'b1': b1, 'w2': w2, 'b2': b2}
    _L0_ffn_all = _L0_ffn_setup()
    _L0_ffn_in = {k: v for k, v in _L0_ffn_all.items() if k in ('attention_mask', 'wr', 'br', 'w1', 'b1', 'w2', 'b2')}
    del _L0_ffn_all

    def _L1_attn_setup():
        import jax, jax.numpy as jnp
        import numpy as np
        A, Bc, Cc = (0.5, 1.0, 1.0)
        H = 8
        EPS = 1e-12

        def _normalize(t):
            n = jnp.linalg.norm(t, axis=-1, keepdims=True)
            return t / jnp.maximum(n, EPS)
        key = jax.random.key(seed)
        ks = jax.random.split(key, 5)
        B, N, C = (8, 512, 64)
        D = C // H
        x = jax.random.normal(ks[0], (B, N, C), dtype=jnp.float32)
        Wqkv = jax.random.normal(ks[1], (3 * H * D, C), dtype=jnp.float32) * 0.02
        bqkv = jnp.zeros((3 * H * D,), dtype=jnp.float32)
        Wproj = jax.random.normal(ks[2], (C, H * D), dtype=jnp.float32) * 0.02
        bproj = jnp.zeros((C,), dtype=jnp.float32)
        temperature = jnp.ones((1, H, 1, 1), dtype=jnp.float32)
        return {'x': x, 'Wqkv': Wqkv, 'bqkv': bqkv, 'Wproj': Wproj, 'bproj': bproj, 'temperature': temperature}
    _L1_attn_all = _L1_attn_setup()
    _L1_attn_in = {k: v for k, v in _L1_attn_all.items() if k in ('Wqkv', 'bqkv', 'Wproj', 'bproj', 'temperature')}
    del _L1_attn_all

    def _L1_ffn_setup():
        import jax, jax.numpy as jnp
        import numpy as np
        D_IN, D_HID, D_OUT = (64, 128, 64)
        N_EXPERTS, TOP_K = (64, 2)
        B, S = (8, 1024)
        key = jax.random.key(seed)
        ks = jax.random.split(key, 8)
        scale_in = 1.0 / np.sqrt(D_IN)
        scale_hid = 1.0 / np.sqrt(D_HID)
        return {'x': jax.random.normal(ks[0], (B, S, D_IN), dtype=jnp.float32), 'Wr': jax.random.uniform(ks[1], (D_IN, N_EXPERTS), jnp.float32, -scale_in, scale_in), 'br': jax.random.uniform(ks[2], (N_EXPERTS,), jnp.float32, -scale_in, scale_in), 'W1': jax.random.uniform(ks[3], (N_EXPERTS, D_IN, D_HID), jnp.float32, -scale_in, scale_in), 'b1': jax.random.uniform(ks[4], (N_EXPERTS, D_HID), jnp.float32, -scale_in, scale_in), 'W2': jax.random.uniform(ks[5], (N_EXPERTS, D_HID, D_OUT), jnp.float32, -scale_hid, scale_hid), 'b2': jax.random.uniform(ks[6], (N_EXPERTS, D_OUT), jnp.float32, -scale_hid, scale_hid)}
    _L1_ffn_all = _L1_ffn_setup()
    _L1_ffn_in = {k: v for k, v in _L1_ffn_all.items() if k in ('Wr', 'br', 'W1', 'b1', 'W2', 'b2')}
    del _L1_ffn_all

    def _L2_attn_setup():
        import jax, jax.numpy as jnp
        import numpy as np
        GAMMA = 0.96875
        SCALE_BASE = 512.0

        def xpos_rope(x, downscale=False):
            B, S, D = x.shape
            half = D // 2
            inv_freq = 1.0 / 10000.0 ** (jnp.arange(0, D, 2, dtype=jnp.float32) / D)
            pos = jnp.arange(S, dtype=jnp.float32)
            ang = pos[:, None] * inv_freq[None, :]
            sin, cos = (jnp.sin(ang), jnp.cos(ang))
            base = (jnp.arange(0, D, 2, dtype=jnp.float32) + 0.4 * D) / (1.4 * D)
            scale = base[None, :] ** (pos[:, None] / SCALE_BASE)
            if downscale:
                scale = 1.0 / scale
            x1 = x[..., 0::2]
            x2 = x[..., 1::2]
            r1 = (x1 * cos - x2 * sin) * scale
            r2 = (x1 * sin + x2 * cos) * scale
            out = jnp.stack([r1, r2], axis=-1).reshape(B, S, D)
            return out

        def get_D(gamma, seq_len):
            n = jnp.arange(seq_len, dtype=jnp.float32)
            diff = n[:, None] - n[None, :]
            mask = diff >= 0
            D = jnp.where(mask, gamma ** jnp.where(mask, diff, 0.0), 0.0)
            return D

        def _reference_tuple_inner(x, W_Q, W_K, W_V):
            S = x.shape[1]
            D = get_D(GAMMA, S)
            Q = xpos_rope(x @ W_Q, downscale=False)
            K = xpos_rope(x @ W_K, downscale=True)
            V = x @ W_V
            ret = jnp.einsum('bnd,bmd->bnm', Q, K) * D[None, :, :]
            out = jnp.einsum('bnm,bmv->bnv', ret, V)
            return (out, ret)
        key = jax.random.key(seed)
        k1, k2, k3, k4 = jax.random.split(key, 4)
        B, S, d_model, d_k, d_v = (8, 1024, 64, 64, 64)
        x = jax.random.normal(k1, (B, S, d_model), dtype=jnp.float32)
        W_Q = jax.random.normal(k2, (d_model, d_k), dtype=jnp.float32) / d_model
        W_K = jax.random.normal(k3, (d_model, d_k), dtype=jnp.float32) / d_model
        W_V = jax.random.normal(k4, (d_model, d_v), dtype=jnp.float32) / d_model
        return {'x': x, 'W_Q': W_Q, 'W_K': W_K, 'W_V': W_V}
    _L2_attn_all = _L2_attn_setup()
    _L2_attn_in = {k: v for k, v in _L2_attn_all.items() if k in ('W_Q', 'W_K', 'W_V')}
    del _L2_attn_all

    def _L2_ffn_setup():
        import jax, jax.numpy as jnp
        import numpy as np
        BN_EPS = 0.001

        def _bn(h, g, b, m, v):
            return g * (h - m) * jax.lax.rsqrt(v + BN_EPS) + b
        key = jax.random.key(seed)
        ks = jax.random.split(key, 8)
        B, F, Df = (64, 64, 64)
        E, H, D = (8, 64, 64)
        s1 = 1.0 / np.sqrt(Df)
        s2 = 1.0 / np.sqrt(H)
        return {'x': jax.random.normal(ks[0], (B, F, Df), jnp.float32), 'Wr': jax.random.normal(ks[1], (Df, E), jnp.float32) * s1, 'br': jnp.zeros((E,), jnp.float32), 'W1': jax.random.normal(ks[2], (E, Df, H), jnp.float32) * s1, 'b1': jnp.zeros((E, H), jnp.float32), 'g1': jnp.ones((E, H), jnp.float32), 'be1': jnp.zeros((E, H), jnp.float32), 'm1': jnp.zeros((E, H), jnp.float32), 'v1': jnp.ones((E, H), jnp.float32), 'W2': jax.random.normal(ks[3], (E, H, H), jnp.float32) * s2, 'b2': jnp.zeros((E, H), jnp.float32), 'g2': jnp.ones((E, H), jnp.float32), 'be2': jnp.zeros((E, H), jnp.float32), 'm2': jnp.zeros((E, H), jnp.float32), 'v2': jnp.ones((E, H), jnp.float32), 'Wo': jax.random.normal(ks[4], (E, H, D), jnp.float32) * s2, 'bo': jnp.zeros((E, D), jnp.float32)}
    _L2_ffn_all = _L2_ffn_setup()
    _L2_ffn_in = {k: v for k, v in _L2_ffn_all.items() if k in ('Wr', 'br', 'W1', 'b1', 'g1', 'be1', 'm1', 'v1', 'W2', 'b2', 'g2', 'be2', 'm2', 'v2', 'Wo', 'bo')}
    del _L2_ffn_all

    def _L3_attn_setup():
        import math
        import jax, jax.numpy as jnp
        import numpy as np
        D_MODEL = 64
        N_HEADS = 4
        HEAD_DIM = D_MODEL // N_HEADS
        MAX_REL = 30

        def _rel_pos_encodings(t, d_model):
            n = 2 * MAX_REL + 1
            positions = jnp.arange(n, dtype=jnp.float32)[:, None]
            div_term = jnp.exp(jnp.arange(0, d_model, 2, dtype=jnp.float32) * (-math.log(10000.0) / d_model))
            ang = positions * div_term
            enc = jnp.stack([jnp.sin(ang), jnp.cos(ang)], axis=-1).reshape(n, d_model)
            rng = jnp.arange(t)
            final_mat = jnp.clip(rng[None, :] - rng[:, None], -MAX_REL, MAX_REL) + MAX_REL
            return enc[final_mat]
        key = jax.random.key(seed)
        ks = jax.random.split(key, 12)
        d = D_MODEL
        s = 1.0 / math.sqrt(d)
        inp = {'inputs': jax.random.normal(ks[0], (16, 128, d), dtype=jnp.float32), 'ln_gamma': jnp.ones((d,), jnp.float32), 'ln_beta': jnp.zeros((d,), jnp.float32), 'Wq': jax.random.normal(ks[1], (d, d), jnp.float32) * s, 'bq': jnp.zeros((d,), jnp.float32), 'Wk': jax.random.normal(ks[2], (d, d), jnp.float32) * s, 'bk': jnp.zeros((d,), jnp.float32), 'Wv': jax.random.normal(ks[3], (d, d), jnp.float32) * s, 'bv': jnp.zeros((d,), jnp.float32), 'Wpos': jax.random.normal(ks[4], (d, d), jnp.float32) * s, 'bpos': jnp.zeros((d,), jnp.float32), 'Wo': jax.random.normal(ks[5], (d, d), jnp.float32) * s, 'bo': jnp.zeros((d,), jnp.float32), 'u_bias': jax.random.normal(ks[6], (1, N_HEADS, 1, HEAD_DIM), jnp.float32) * 0.02, 'v_bias': jax.random.normal(ks[7], (1, N_HEADS, 1, HEAD_DIM), jnp.float32) * 0.02}
        return inp
    _L3_attn_all = _L3_attn_setup()
    _L3_attn_in = {k: v for k, v in _L3_attn_all.items() if k in ('ln_gamma', 'ln_beta', 'Wq', 'bq', 'Wk', 'bk', 'Wv', 'bv', 'Wpos', 'bpos', 'Wo', 'bo', 'u_bias', 'v_bias')}
    del _L3_attn_all

    def _L3_ffn_setup():
        import jax, jax.numpy as jnp
        import numpy as np
        C = 64
        HID = 256
        E = 8
        TEMP = 1.0
        key = jax.random.key(seed)
        ks = jax.random.split(key, 7)
        x = jax.random.normal(ks[0], (8, 4096, C), dtype=jnp.float32)
        W1 = jax.random.normal(ks[1], (C, HID), dtype=jnp.float32) * 0.02
        b1 = jnp.zeros((HID,), dtype=jnp.float32)
        Wg = jax.random.normal(ks[2], (HID, E), dtype=jnp.float32) * 0.02
        bg = jnp.zeros((E,), dtype=jnp.float32)
        Wd = jax.random.normal(ks[3], (E, HID, C), dtype=jnp.float32) * 0.02
        bd = jnp.zeros((E, C), dtype=jnp.float32)
        return {'x': x, 'W1': W1, 'b1': b1, 'Wg': Wg, 'bg': bg, 'Wd': Wd, 'bd': bd}
    _L3_ffn_all = _L3_ffn_setup()
    _L3_ffn_in = {k: v for k, v in _L3_ffn_all.items() if k in ('W1', 'b1', 'Wg', 'bg', 'Wd', 'bd')}
    del _L3_ffn_all
    return {'x': x, 'L0_tok_W_qry': _L0_tok_in['W_qry'], 'L0_tok_W_key': _L0_tok_in['W_key'], 'L0_tok_v': _L0_tok_in['v'], 'L0_tok_b': _L0_tok_in['b'], 'L0_attn_Wq': _L0_attn_in['Wq'], 'L0_attn_bq': _L0_attn_in['bq'], 'L0_attn_Wk': _L0_attn_in['Wk'], 'L0_attn_bk': _L0_attn_in['bk'], 'L0_attn_Wv': _L0_attn_in['Wv'], 'L0_attn_bv': _L0_attn_in['bv'], 'L0_ffn_attention_mask': _L0_ffn_in['attention_mask'], 'L0_ffn_wr': _L0_ffn_in['wr'], 'L0_ffn_br': _L0_ffn_in['br'], 'L0_ffn_w1': _L0_ffn_in['w1'], 'L0_ffn_b1': _L0_ffn_in['b1'], 'L0_ffn_w2': _L0_ffn_in['w2'], 'L0_ffn_b2': _L0_ffn_in['b2'], 'L1_attn_Wqkv': _L1_attn_in['Wqkv'], 'L1_attn_bqkv': _L1_attn_in['bqkv'], 'L1_attn_Wproj': _L1_attn_in['Wproj'], 'L1_attn_bproj': _L1_attn_in['bproj'], 'L1_attn_temperature': _L1_attn_in['temperature'], 'L1_ffn_Wr': _L1_ffn_in['Wr'], 'L1_ffn_br': _L1_ffn_in['br'], 'L1_ffn_W1': _L1_ffn_in['W1'], 'L1_ffn_b1': _L1_ffn_in['b1'], 'L1_ffn_W2': _L1_ffn_in['W2'], 'L1_ffn_b2': _L1_ffn_in['b2'], 'L2_attn_W_Q': _L2_attn_in['W_Q'], 'L2_attn_W_K': _L2_attn_in['W_K'], 'L2_attn_W_V': _L2_attn_in['W_V'], 'L2_ffn_Wr': _L2_ffn_in['Wr'], 'L2_ffn_br': _L2_ffn_in['br'], 'L2_ffn_W1': _L2_ffn_in['W1'], 'L2_ffn_b1': _L2_ffn_in['b1'], 'L2_ffn_g1': _L2_ffn_in['g1'], 'L2_ffn_be1': _L2_ffn_in['be1'], 'L2_ffn_m1': _L2_ffn_in['m1'], 'L2_ffn_v1': _L2_ffn_in['v1'], 'L2_ffn_W2': _L2_ffn_in['W2'], 'L2_ffn_b2': _L2_ffn_in['b2'], 'L2_ffn_g2': _L2_ffn_in['g2'], 'L2_ffn_be2': _L2_ffn_in['be2'], 'L2_ffn_m2': _L2_ffn_in['m2'], 'L2_ffn_v2': _L2_ffn_in['v2'], 'L2_ffn_Wo': _L2_ffn_in['Wo'], 'L2_ffn_bo': _L2_ffn_in['bo'], 'L3_attn_ln_gamma': _L3_attn_in['ln_gamma'], 'L3_attn_ln_beta': _L3_attn_in['ln_beta'], 'L3_attn_Wq': _L3_attn_in['Wq'], 'L3_attn_bq': _L3_attn_in['bq'], 'L3_attn_Wk': _L3_attn_in['Wk'], 'L3_attn_bk': _L3_attn_in['bk'], 'L3_attn_Wv': _L3_attn_in['Wv'], 'L3_attn_bv': _L3_attn_in['bv'], 'L3_attn_Wpos': _L3_attn_in['Wpos'], 'L3_attn_bpos': _L3_attn_in['bpos'], 'L3_attn_Wo': _L3_attn_in['Wo'], 'L3_attn_bo': _L3_attn_in['bo'], 'L3_attn_u_bias': _L3_attn_in['u_bias'], 'L3_attn_v_bias': _L3_attn_in['v_bias'], 'L3_ffn_W1': _L3_ffn_in['W1'], 'L3_ffn_b1': _L3_ffn_in['b1'], 'L3_ffn_Wg': _L3_ffn_in['Wg'], 'L3_ffn_bg': _L3_ffn_in['bg'], 'L3_ffn_Wd': _L3_ffn_in['Wd'], 'L3_ffn_bd': _L3_ffn_in['bd']}

def reference(x, L0_tok_W_qry, L0_tok_W_key, L0_tok_v, L0_tok_b, L0_attn_Wq, L0_attn_bq, L0_attn_Wk, L0_attn_bk, L0_attn_Wv, L0_attn_bv, L0_ffn_attention_mask, L0_ffn_wr, L0_ffn_br, L0_ffn_w1, L0_ffn_b1, L0_ffn_w2, L0_ffn_b2, L1_attn_Wqkv, L1_attn_bqkv, L1_attn_Wproj, L1_attn_bproj, L1_attn_temperature, L1_ffn_Wr, L1_ffn_br, L1_ffn_W1, L1_ffn_b1, L1_ffn_W2, L1_ffn_b2, L2_attn_W_Q, L2_attn_W_K, L2_attn_W_V, L2_ffn_Wr, L2_ffn_br, L2_ffn_W1, L2_ffn_b1, L2_ffn_g1, L2_ffn_be1, L2_ffn_m1, L2_ffn_v1, L2_ffn_W2, L2_ffn_b2, L2_ffn_g2, L2_ffn_be2, L2_ffn_m2, L2_ffn_v2, L2_ffn_Wo, L2_ffn_bo, L3_attn_ln_gamma, L3_attn_ln_beta, L3_attn_Wq, L3_attn_bq, L3_attn_Wk, L3_attn_bk, L3_attn_Wv, L3_attn_bv, L3_attn_Wpos, L3_attn_bpos, L3_attn_Wo, L3_attn_bo, L3_attn_u_bias, L3_attn_v_bias, L3_ffn_W1, L3_ffn_b1, L3_ffn_Wg, L3_ffn_bg, L3_ffn_Wd, L3_ffn_bd):
    import jax
    import jax.numpy as jnp

    def _L0_tok_ref(x, W_qry, W_key, v, b):
        import jax, jax.numpy as jnp
        import numpy as np
        WIN = 9
        N, L, C = x.shape
        n_w = L - WIN + 1
        idx = jnp.arange(n_w)[:, None] + jnp.arange(WIN)[None, :]
        x_win = x[:, idx]
        x_ctr = x[:, WIN // 2:WIN // 2 + n_w]
        key = jnp.einsum('nwsc,cu->nwsu', x_win, W_key)
        qry = jnp.einsum('nwc,cu->nwu', x_ctr, W_qry)
        score = jnp.einsum('nwsu,u->nws', jnp.tanh(qry[:, :, None, :] + key + b), v)
        weight = jax.nn.softmax(score, axis=2)
        out = jnp.einsum('nwsc,nws->nwc', x_win, weight)
        return out

    def _L0_attn_ref(x, Wq, bq, Wk, bk, Wv, bv):
        import jax, jax.numpy as jnp
        import numpy as np
        NUM_HEADS = 8

        def _to_heads(y, R, C, H, hd):
            y = y.reshape(R, C, H, hd).transpose(0, 2, 1, 3)
            y = jnp.transpose(y, (2, 1, 0, 3)).reshape(1, H, C, R * hd)
            return y

        def _reference_tuple_inner(x, Wq, bq, Wk, bk, Wv, bv):
            R, C, E = x.shape
            H = NUM_HEADS
            hd = E // H
            q = _to_heads(x @ Wq.T + bq, R, C, H, hd)
            k = _to_heads(x @ Wk.T + bk, R, C, H, hd)
            v = _to_heads(x @ Wv.T + bv, R, C, H, hd)
            d = q.shape[-1]
            q = jax.nn.softmax(q, axis=-1)
            k = jax.nn.softmax(k, axis=-2)
            q = q * jnp.asarray(float(d) ** 0.5, dtype=q.dtype)
            attn_weights = jnp.einsum('bhnd,bhmd->bhnm', q, k).sum(0)
            context = jnp.einsum('bhnd,bhne->bhde', k, v)
            out = jnp.einsum('bhnd,bhde->hbne', q, context)
            out = out.reshape(H, C, R, hd)
            out = jnp.transpose(out, (2, 1, 0, 3)).reshape(R, C, E)
            return (out, attn_weights)
        return _reference_tuple_inner(x, Wq, bq, Wk, bk, Wv, bv)[0]

    def _L0_ffn_ref(x, attention_mask, wr, br, w1, b1, w2, b2):
        import jax, jax.numpy as jnp
        import numpy as np
        B, S, D = (8, 1024, 64)
        H = 4 * D
        CAPACITY = 0.5
        b, s, d = x.shape
        weights = (jnp.einsum('bsd,do->bso', x, wr) + br)[..., 0]
        k = max(1, int(CAPACITY * s))
        kk = k - 1 if k > 1 else 1
        _, idx = jax.lax.top_k(weights, k)
        sel_idx = idx[:, :kk]
        sel = jnp.take_along_axis(x, sel_idx[:, :, None], axis=1)
        h = jax.nn.gelu(jnp.einsum('bkd,dh->bkh', sel, w1) + b1)
        y = jnp.einsum('bkh,hd->bkd', h, w2) + b2
        w_sel = jnp.take_along_axis(weights, sel_idx, axis=1)
        y = y * w_sel[..., None]
        batch_idx = jnp.arange(b)[:, None]
        processed = jnp.zeros_like(x).at[batch_idx, sel_idx].set(y)
        return processed + x

    def _L1_attn_ref(x, Wqkv, bqkv, Wproj, bproj, temperature):
        import jax, jax.numpy as jnp
        import numpy as np
        A, Bc, Cc = (0.5, 1.0, 1.0)
        H = 8
        EPS = 1e-12

        def _normalize(t):
            n = jnp.linalg.norm(t, axis=-1, keepdims=True)
            return t / jnp.maximum(n, EPS)
        B, N, C = x.shape
        D = C // H
        scale = float(D) ** 0.25
        qkv = (x @ Wqkv.T + bqkv).reshape(B, N, 3, H, D)
        qkv = jnp.transpose(qkv, (2, 0, 3, 1, 4))
        q, k, v = (qkv[0], qkv[1], qkv[2])
        q = q * scale
        v1 = jnp.concatenate([jnp.ones((B, H, N, 1), dtype=v.dtype), v], axis=-1)
        qn = _normalize(q) * (scale * temperature)
        kn = _normalize(k) * scale
        vN = v1 / N
        kv_mod = jnp.einsum('bhni,bhnj,bhne->bhije', kn, kn, vN)
        kv = jnp.einsum('bhnd,bhne->bhde', kn, vN)
        vsum = jnp.sum(vN, axis=-2)[:, :, None, :]
        y = A * jnp.einsum('bhni,bhnj,bhije->bhne', qn, qn, kv_mod) + scale ** 2 * Bc * jnp.einsum('bhnd,bhde->bhne', qn, kv) + scale ** 4 * Cc * vsum
        y_norm, y = (y[..., :1], y[..., 1:])
        y = y / y_norm
        out = jnp.transpose(y, (0, 2, 1, 3)).reshape(B, N, H * D)
        return out @ Wproj.T + bproj

    def _L1_ffn_ref(x, Wr, br, W1, b1, W2, b2):
        import jax, jax.numpy as jnp
        import numpy as np
        D_IN, D_HID, D_OUT = (64, 128, 64)
        N_EXPERTS, TOP_K = (64, 2)
        B, S = (8, 1024)
        Bx, Sx, D = x.shape
        xf = x.reshape(-1, D)
        T = xf.shape[0]
        E = Wr.shape[1]
        logits = xf @ Wr + br
        topk_logits, topk_idx = jax.lax.top_k(logits, TOP_K)
        gates = jax.nn.softmax(topk_logits, axis=1)
        combine = jnp.zeros((T, E), xf.dtype).at[jnp.arange(T)[:, None], topk_idx].add(gates)
        out = jnp.zeros((T, W2.shape[-1]), xf.dtype)
        for e in range(E):
            h = jax.nn.relu(xf @ W1[e] + b1[e])
            y = h @ W2[e] + b2[e]
            out = out + combine[:, e:e + 1] * y
        return out.reshape(Bx, Sx, -1)

    def _L2_attn_ref(x, W_Q, W_K, W_V):
        import jax, jax.numpy as jnp
        import numpy as np
        GAMMA = 0.96875
        SCALE_BASE = 512.0

        def xpos_rope(x, downscale=False):
            B, S, D = x.shape
            half = D // 2
            inv_freq = 1.0 / 10000.0 ** (jnp.arange(0, D, 2, dtype=jnp.float32) / D)
            pos = jnp.arange(S, dtype=jnp.float32)
            ang = pos[:, None] * inv_freq[None, :]
            sin, cos = (jnp.sin(ang), jnp.cos(ang))
            base = (jnp.arange(0, D, 2, dtype=jnp.float32) + 0.4 * D) / (1.4 * D)
            scale = base[None, :] ** (pos[:, None] / SCALE_BASE)
            if downscale:
                scale = 1.0 / scale
            x1 = x[..., 0::2]
            x2 = x[..., 1::2]
            r1 = (x1 * cos - x2 * sin) * scale
            r2 = (x1 * sin + x2 * cos) * scale
            out = jnp.stack([r1, r2], axis=-1).reshape(B, S, D)
            return out

        def get_D(gamma, seq_len):
            n = jnp.arange(seq_len, dtype=jnp.float32)
            diff = n[:, None] - n[None, :]
            mask = diff >= 0
            D = jnp.where(mask, gamma ** jnp.where(mask, diff, 0.0), 0.0)
            return D

        def _reference_tuple_inner(x, W_Q, W_K, W_V):
            S = x.shape[1]
            D = get_D(GAMMA, S)
            Q = xpos_rope(x @ W_Q, downscale=False)
            K = xpos_rope(x @ W_K, downscale=True)
            V = x @ W_V
            ret = jnp.einsum('bnd,bmd->bnm', Q, K) * D[None, :, :]
            out = jnp.einsum('bnm,bmv->bnv', ret, V)
            return (out, ret)
        return _reference_tuple_inner(x, W_Q, W_K, W_V)[0]

    def _L2_ffn_ref(x, Wr, br, W1, b1, g1, be1, m1, v1, W2, b2, g2, be2, m2, v2, Wo, bo):
        import jax, jax.numpy as jnp
        import numpy as np
        BN_EPS = 0.001

        def _bn(h, g, b, m, v):
            return g * (h - m) * jax.lax.rsqrt(v + BN_EPS) + b
        feat = jnp.mean(x, axis=0)
        w = jax.nn.softmax(feat @ Wr + br, axis=-1)
        h = jnp.einsum('bfd,edh->bfeh', x, W1) + b1
        h = jax.nn.relu(_bn(h, g1, be1, m1, v1))
        h = jnp.einsum('bfeh,ehk->bfek', h, W2) + b2
        h = jax.nn.relu(_bn(h, g2, be2, m2, v2))
        y = jnp.einsum('bfeh,ehd->bfed', h, Wo) + bo
        return jnp.einsum('bfed,fe->bfd', y, w)

    def _L3_attn_ref(inputs, ln_gamma, ln_beta, Wq, bq, Wk, bk, Wv, bv, Wpos, bpos, Wo, bo, u_bias, v_bias):
        import math
        import jax, jax.numpy as jnp
        import numpy as np
        D_MODEL = 64
        N_HEADS = 4
        HEAD_DIM = D_MODEL // N_HEADS
        MAX_REL = 30

        def _rel_pos_encodings(t, d_model):
            n = 2 * MAX_REL + 1
            positions = jnp.arange(n, dtype=jnp.float32)[:, None]
            div_term = jnp.exp(jnp.arange(0, d_model, 2, dtype=jnp.float32) * (-math.log(10000.0) / d_model))
            ang = positions * div_term
            enc = jnp.stack([jnp.sin(ang), jnp.cos(ang)], axis=-1).reshape(n, d_model)
            rng = jnp.arange(t)
            final_mat = jnp.clip(rng[None, :] - rng[:, None], -MAX_REL, MAX_REL) + MAX_REL
            return enc[final_mat]
        b, t, d = inputs.shape
        h, hd = (N_HEADS, HEAD_DIM)
        mu = jnp.mean(inputs, axis=-1, keepdims=True)
        var = jnp.mean(jnp.square(inputs - mu), axis=-1, keepdims=True)
        x = (inputs - mu) * jax.lax.rsqrt(var + 1e-05) * ln_gamma + ln_beta

        def split_heads(y):
            return y.reshape(b, t, h, hd).transpose(0, 2, 1, 3)
        q = split_heads(x @ Wq.T + bq)
        k = split_heads(x @ Wk.T + bk)
        v = split_heads(x @ Wv.T + bv)
        rel = jax.lax.stop_gradient(_rel_pos_encodings(t, d))
        pos = (rel @ Wpos.T + bpos).reshape(t, t, h, hd)
        qk_score = jnp.einsum('bhtd,bhsd->bhts', q + u_bias, k)
        pos_score = jnp.einsum('bhtd,tshd->bhts', q + v_bias, pos)
        scores = (qk_score + pos_score) / math.sqrt(hd)
        attn = jax.nn.softmax(scores, axis=-1)
        ctx = jnp.einsum('bhts,bhsd->bhtd', attn, v)
        ctx = ctx.transpose(0, 2, 1, 3).reshape(b, t, d)
        return ctx @ Wo.T + bo

    def _L3_ffn_ref(x, W1, b1, Wg, bg, Wd, bd):
        import jax, jax.numpy as jnp
        import numpy as np
        C = 64
        HID = 256
        E = 8
        TEMP = 1.0
        orig_shape = x.shape
        xf = x.reshape(-1, orig_shape[-1])
        H = jax.nn.gelu(xf @ W1 + b1, approximate=False)
        probs = jax.nn.softmax((H @ Wg + bg) / TEMP, axis=-1)
        assign = jnp.argmax(probs, axis=-1)
        out = jnp.zeros_like(xf)
        for e in range(Wd.shape[0]):
            y = H @ Wd[e] + bd[e]
            sel = (assign == e)[:, None]
            out = out + jnp.where(sel, probs[:, e:e + 1] * y, 0.0)
        return out.reshape(orig_shape)
    h = _L0_tok_ref(x, L0_tok_W_qry, L0_tok_W_key, L0_tok_v, L0_tok_b)
    h = h + _L0_attn_ref(_layernorm(h, axis=-1), L0_attn_Wq, L0_attn_bq, L0_attn_Wk, L0_attn_bk, L0_attn_Wv, L0_attn_bv)
    h = h + _L0_ffn_ref(_layernorm(h, axis=-1), L0_ffn_attention_mask, L0_ffn_wr, L0_ffn_br, L0_ffn_w1, L0_ffn_b1, L0_ffn_w2, L0_ffn_b2)
    h = h + _L1_attn_ref(_layernorm(h, axis=-1), L1_attn_Wqkv, L1_attn_bqkv, L1_attn_Wproj, L1_attn_bproj, L1_attn_temperature)
    h = h + _L1_ffn_ref(_layernorm(h, axis=-1), L1_ffn_Wr, L1_ffn_br, L1_ffn_W1, L1_ffn_b1, L1_ffn_W2, L1_ffn_b2)
    h = h + _L2_attn_ref(_layernorm(h, axis=-1), L2_attn_W_Q, L2_attn_W_K, L2_attn_W_V)
    h = h + _L2_ffn_ref(_layernorm(h, axis=-1), L2_ffn_Wr, L2_ffn_br, L2_ffn_W1, L2_ffn_b1, L2_ffn_g1, L2_ffn_be1, L2_ffn_m1, L2_ffn_v1, L2_ffn_W2, L2_ffn_b2, L2_ffn_g2, L2_ffn_be2, L2_ffn_m2, L2_ffn_v2, L2_ffn_Wo, L2_ffn_bo)
    h = h + _L3_attn_ref(_layernorm(h, axis=-1), L3_attn_ln_gamma, L3_attn_ln_beta, L3_attn_Wq, L3_attn_bq, L3_attn_Wk, L3_attn_bk, L3_attn_Wv, L3_attn_bv, L3_attn_Wpos, L3_attn_bpos, L3_attn_Wo, L3_attn_bo, L3_attn_u_bias, L3_attn_v_bias)
    h = h + _L3_ffn_ref(_layernorm(h, axis=-1), L3_ffn_W1, L3_ffn_b1, L3_ffn_Wg, L3_ffn_bg, L3_ffn_Wd, L3_ffn_bd)
    return h

_drawn_inputs = setup_inputs


def setup_inputs(seed=0):
    import zlib

    import numpy as np

    out = dict(_drawn_inputs(seed))
    spreads = {'L0_tok_b': (0.0, 0.675),
     'L0_ffn_b1': (0.0, 0.8),
     'L0_ffn_b2': (0.0, 0.655),
     'L1_attn_bqkv': (0.0, 0.412),
     'L1_attn_bproj': (0.0, 0.1),
     'L1_attn_temperature': (1.0, 0.6),
     'L2_ffn_br': (0.0, 0.717),
     'L2_ffn_b1': (0.0, 0.614),
     'L2_ffn_g1': (1.0, 0.6),
     'L2_ffn_be1': (0.0, 0.713),
     'L2_ffn_m1': (0.0, 0.705),
     'L2_ffn_v1': (1.0, 0.6),
     'L2_ffn_b2': (0.0, 0.505),
     'L2_ffn_g2': (1.0, 0.596),
     'L2_ffn_be2': (0.0, 0.467),
     'L2_ffn_m2': (0.0, 0.405),
     'L2_ffn_v2': (1.0, 0.6),
     'L2_ffn_bo': (0.0, 0.333),
     'L3_attn_ln_gamma': (1.0, 0.2),
     'L3_attn_ln_beta': (0.0, 0.1),
     'L3_attn_bq': (0.0, 0.8),
     'L3_attn_bk': (0.0, 0.8),
     'L3_attn_bv': (0.0, 0.1),
     'L3_attn_bpos': (0.0, 0.8),
     'L3_attn_bo': (0.0, 0.1),
     'L3_ffn_b1': (0.0, 0.8),
     'L3_ffn_bg': (0.0, 0.71),
     'L3_ffn_bd': (0.0, 0.8)}
    factors = {'L0_attn_Wq': 8.0,
     'L0_attn_bq': 8.0,
     'L0_attn_Wk': 4.05,
     'L0_attn_bk': 8.0,
     'L0_ffn_wr': 4.611,
     'L0_ffn_w1': 8.0,
     'L0_ffn_w2': 8.0,
     'L1_attn_Wqkv': 2.985,
     'L1_ffn_b1': 4.388,
     'L3_attn_u_bias': 8.0,
     'L3_attn_v_bias': 8.0,
     'L3_ffn_W1': 8.0,
     'L3_ffn_Wg': 8.0,
     'L3_ffn_Wd': 8.0}
    for name, (base, spread) in spreads.items():
        noise = np.random.default_rng([zlib.crc32(name.encode()), seed]).standard_normal(out[name].shape)
        drawn = base * np.exp(spread * noise) if base else spread * noise
        out[name] = jnp.asarray(drawn.astype(out[name].dtype))
    for name, factor in factors.items():
        out[name] = (out[name] * factor).astype(out[name].dtype)
    return out
```

```python
from contextlib import ExitStack

import numpy as np

import concourse.bass as bass
from concourse import mybir

F32 = mybir.dt.float32
I32 = mybir.dt.int32
U32 = mybir.dt.uint32
BF16 = mybir.dt.bfloat16
ALU = mybir.AluOpType
ACT = mybir.ActivationFunctionType
AX = mybir.AxisListType

SEQS, FRAMES, FEAT, WINDOW = 16, 250, 64, 9
POS = FRAMES - WINDOW + 1
PAIRS = SEQS // 2
COLS = PAIRS * POS
TILE = POS // 2
TILES = 2 * PAIRS
CHUNK = 4 * TILE
CHUNKS = COLS // CHUNK
LN_EPS = 1e-5
EXPERTS = 64
TABLE_TILES = 128


def chunk(c):
    return slice(c * CHUNK, (c + 1) * CHUNK)


def tile(j):
    return slice(j * TILE, (j + 1) * TILE)


class Stage:

    def __init__(self, nc, name):
        self.nc, self.name, self.ctx, self.sems = nc, name, ExitStack(), []

    def __enter__(self):
        self.ctx.__enter__()
        return self

    def __exit__(self, *e):
        if self.sems and e[0] is None:
            for sem in self.sems:
                self.nc.gpsimd.sem_clear(sem)
                self.nc.release_semaphore(sem)
        return self.ctx.__exit__(*e)

    def sb(self, name, shape, dt=F32):
        return self.ctx.enter_context(self.nc.sbuf_tensor(f"{self.name}_{name}", shape, dt))

    def sem(self, name):
        self.sems.append(self.nc.alloc_semaphore(f"{self.name}_{name}"))
        return self.sems[-1]


class Weights:

    def __init__(self, nc, ctx, dram, where, groups):
        self.nc, self.dram, self.groups, self.views = nc, dram, groups, {}
        widest = max(b - a for a, b in groups[1:])
        widths = [groups[0][1], widest, widest]
        self.buffers = [ctx.enter_context(nc.sbuf_tensor(f"weights{n}", [128, k], F32)) for n, k in enumerate(widths)]
        self.loaded = [ctx.enter_context(nc.semaphore(f"loaded{g}")) for g in range(len(groups))]
        for name, (group, r, at, k) in where.items():
            at -= groups[group][0]
            self.views[name] = self.buffer(group)[:r, at:at + k]

    def buffer(self, group):
        return self.buffers[0 if group == 0 else 1 + group % 2]

    def __getitem__(self, name):
        return self.views[name]

    def load(self, eng, group):
        a, b = self.groups[group]
        eng.dma_start(self.buffer(group)[:, 0:b - a], self.dram[:, a:b]).then_inc(self.loaded[group], 16)

    def arrive(self, group):
        loaded = self.loaded[group]
        with self.nc.Block() as block:

            @block.sync
            def _(sp):
                if group == 1:
                    self.load(sp, 1)
                if group + 1 < len(self.groups):
                    self.load(sp, group + 1)

            @block.tensor
            def _(pe):
                pe.wait_ge(loaded, 16)

            @block.scalar
            def _(act):
                if group == 1:
                    self.load(act, 0)
                    act.wait_ge(self.loaded[0], 16)
                act.wait_ge(loaded, 16)

            @block.vector
            def _(dve):
                dve.wait_ge(loaded, 16)


def layer_norm(nc, name, h, x, w, ps):
    with Stage(nc, name) as s:
        centred = s.sb("centred", [128, COLS])
        squares = s.sb("squares", [128, COLS])
        std = s.sb("std", [32, TILE])
        rstd = s.sb("rstd", [32, TILE])
        mean_ready, centred_ready, squares_ready = s.sem("mean_ready"), s.sem("centred_ready"), s.sem("squares_ready")
        var_ready, std_ready, rstd_ready = s.sem("var_ready"), s.sem("std_ready"), s.sem("rstd_ready")
        scale_ready, x_ready = s.sem("scale_ready"), s.sem("x_ready")
        with nc.Block() as block:

            @block.tensor
            def _(pe):
                for c in range(CHUNKS):
                    pe.matmul(ps[c][:, :CHUNK], w["mean"], h[:, chunk(c)], start=True, stop=True).then_inc(mean_ready, 1)
                for j in range(TILES):
                    if j % 4 == 0:
                        pe.wait_ge(squares_ready, j // 4 + 1)
                    last = pe.matmul(ps[4][0:32, 0:TILE], w["var_rows"][:, 32 * j:32 * j + 32], squares[:, tile(j)],
                                     start=(j == 0), stop=(j == TILES - 1))
                last.then_inc(var_ready, 1)
                pe.wait_ge(rstd_ready, 1)
                for j in range(TILES):
                    mm = pe.matmul(ps[j // 4][:, tile(j % 4)], w["rows_out"][0:32, 128 * j:128 * j + 128], rstd[:],
                                   start=True, stop=True)
                    if j % 4 == 3:
                        mm.then_inc(scale_ready, 1)

            @block.scalar
            def _(act):
                for c in range(CHUNKS):
                    act.wait_ge(centred_ready, c + 1)
                    act.activation(squares[:, chunk(c)], centred[:, chunk(c)], ACT.Square).then_inc(squares_ready, 1)
                act.wait_ge(var_ready, 1)
                act.activation(std[:], ps[4][0:32, 0:TILE], ACT.Sqrt, bias=w["ln_eps"][0:32, :]).then_inc(std_ready, 1)

            @block.vector
            def _(dve):
                for c in range(CHUNKS):
                    dve.wait_ge(mean_ready, c + 1)
                    dve.tensor_tensor(centred[:, chunk(c)], h[:, chunk(c)], ps[c][:, :CHUNK], ALU.subtract).then_inc(centred_ready, 1)
                dve.wait_ge(std_ready, 1)
                dve.reciprocal(rstd[:], std[:]).then_inc(rstd_ready, 1)
                for c in range(CHUNKS):
                    dve.wait_ge(scale_ready, c + 1)
                    dve.tensor_tensor(x[:, chunk(c)], centred[:, chunk(c)], ps[c][:, :CHUNK], ALU.mult).then_inc(x_ready, 1)
                dve.wait_ge(x_ready, CHUNKS)


def window_attention(nc, x_dram, h, w, ps):
    with Stage(nc, "win") as s:
        frames = s.sb("frames", [128, PAIRS, FRAMES])
        query = s.sb("query", [128, PAIRS, POS])
        key = s.sb("key", [128, PAIRS, FRAMES])
        hidden = s.sb("hidden", [128, WINDOW, PAIRS, POS])
        scores = s.sb("scores", [2 * WINDOW, COLS])
        token = s.sb("token", [TILE, TILES * 2, WINDOW])
        top = s.sb("top", [TILE, TILES * 2])
        total = s.sb("total", [TILE, TILES * 2])
        weight_rows = s.sb("weight_rows", [2 * WINDOW, COLS])
        product = s.sb("product", [128, 3, PAIRS, POS])
        frames_in = s.sem("frames_in")
        query_ready, query_kept, key_ready, key_kept = s.sem("query_ready"), s.sem("query_kept"), s.sem("key_ready"), s.sem("key_kept")
        sum_ready, hidden_ready, scores_ready, scores_kept = s.sem("sum_ready"), s.sem("hidden_ready"), s.sem("scores_ready"), s.sem("scores_kept")
        turned, top_ready, less_top, exp_ready = s.sem("turned"), s.sem("top_ready"), s.sem("less_top"), s.sem("exp_ready")
        total_ready, inverse_ready, weight_ready = s.sem("total_ready"), s.sem("inverse_ready"), s.sem("weight_ready")
        rows_turned, rows_kept = s.sem("rows_turned"), s.sem("rows_kept")
        spread_ready, product_ready, added = s.sem("spread_ready"), s.sem("product_ready"), s.sem("added")
        with nc.Block() as block:

            @block.sync
            def _(sp):
                sp.dma_start(frames[:], x_dram).then_inc(frames_in, 16)

            @block.tensor
            def _(pe):
                pe.wait_ge(frames_in, 16)
                mid = WINDOW // 2
                for c in range(CHUNKS):
                    pe.matmul(ps[c][:, :CHUNK], w["win_q"], frames[:, 2 * c:2 * c + 2, mid:mid + POS], start=True, stop=True).then_inc(query_ready, 1)
                for c in range(CHUNKS):
                    pe.matmul(ps[4 + c][:, :2 * FRAMES], w["win_k"], frames[:, 2 * c:2 * c + 2, :], start=True, stop=True).then_inc(key_ready, 1)
                for o in range(WINDOW):
                    pe.wait_ge(hidden_ready, o + 1)
                    for c in range(CHUNKS):
                        if o == 0:
                            pe.wait_ge(query_kept, c + 1)
                        mm = pe.matmul(ps[c][0:2 * WINDOW, :CHUNK], w["win_v"][:, 18 * o:18 * o + 18], hidden[:, o, 2 * c:2 * c + 2, :],
                                       start=(o == 0), stop=(o == WINDOW - 1))
                        if o == WINDOW - 1:
                            mm.then_inc(scores_ready, 1)
                pe.wait_ge(key_kept, CHUNKS)
                for j in range(TILES):
                    pe.wait_ge(scores_kept, j // 4 + 1)
                    mm = pe.transpose(ps[4][0:TILE, 18 * j:18 * j + 18], scores[:, tile(j)], w["ident"][0:18, 0:18])
                mm.then_inc(turned, 1)
                pe.wait_ge(weight_ready, 1)
                for j in range(TILES):
                    mm = pe.transpose(ps[j // 4][0:18, tile(j % 4)], token[:, 2 * j:2 * j + 2, :], w["ident"][0:TILE, 0:TILE])
                    if j % 4 == 3:
                        mm.then_inc(rows_turned, 1)
                for o in range(WINDOW):
                    for c in range(CHUNKS):
                        n = o * CHUNKS + c
                        if o == 0:
                            pe.wait_ge(rows_kept, c + 1)
                        if n >= 8:
                            pe.wait_ge(product_ready, n - 7)
                        pe.matmul(ps[n % 8][:, :CHUNK], w["win_out"][0:18, 128 * o:128 * o + 128], weight_rows[:, chunk(c)],
                                  start=True, stop=True).then_inc(spread_ready, 1)

            @block.scalar
            def _(act):
                for c in range(CHUNKS):
                    act.wait_ge(query_ready, c + 1)
                    act.activation(query[:, 2 * c:2 * c + 2, :], ps[c][:, :CHUNK].rearrange("p (b n) -> p b n", b=2), ACT.Identity,
                                   bias=w["win_b"]).then_inc(query_kept, 1)
                for o in range(WINDOW):
                    act.wait_ge(sum_ready, o + 1)
                    act.activation(hidden[:, o], hidden[:, o], ACT.Tanh).then_inc(hidden_ready, 1)
                for c in range(CHUNKS):
                    act.wait_ge(scores_ready, c + 1)
                    act.activation(scores[:, chunk(c)], ps[c][0:18, :CHUNK], ACT.Copy).then_inc(scores_kept, 1)
                act.wait_ge(less_top, 1)
                act.activation(token[:], token[:], ACT.Exp).then_inc(exp_ready, 1)
                for c in range(CHUNKS):
                    act.wait_ge(rows_turned, c + 1)
                    act.activation(weight_rows[:, chunk(c)], ps[c][0:18, :CHUNK], ACT.Copy).then_inc(rows_kept, 1)

            @block.vector
            def _(dve):
                for c in range(CHUNKS):
                    dve.wait_ge(key_ready, c + 1)
                    dve.tensor_copy(key[:, 2 * c:2 * c + 2, :], ps[4 + c][:, :2 * FRAMES].rearrange("p (b n) -> p b n", b=2)).then_inc(key_kept, 1)
                dve.wait_ge(key_kept, CHUNKS)
                dve.wait_ge(query_kept, CHUNKS)
                for o in range(WINDOW):
                    dve.tensor_tensor(hidden[:, o], query[:], key[:, :, o:o + POS], ALU.add).then_inc(sum_ready, 1)
                dve.wait_ge(turned, 1)
                got = ps[4][0:TILE, 0:18 * TILES].rearrange("p (a o) -> p a o", o=WINDOW)
                dve.tensor_reduce(top[:], got, AX.X, ALU.max).then_inc(top_ready, 1)
                dve.wait_ge(top_ready, 1)
                dve.tensor_tensor(token[:], got, top[:].unsqueeze(2).to_broadcast([TILE, 2 * TILES, WINDOW]), ALU.subtract).then_inc(less_top, 1)
                dve.wait_ge(exp_ready, 1)
                dve.tensor_reduce(total[:], token[:], AX.X, ALU.add).then_inc(total_ready, 1)
                dve.wait_ge(total_ready, 1)
                dve.reciprocal(top[:], total[:]).then_inc(inverse_ready, 1)
                dve.wait_ge(inverse_ready, 1)
                dve.tensor_tensor(token[:], token[:], top[:].unsqueeze(2).to_broadcast([TILE, 2 * TILES, WINDOW]), ALU.mult).then_inc(weight_ready, 1)
                for o in range(WINDOW):
                    for c in range(CHUNKS):
                        dve.wait_ge(spread_ready, o * CHUNKS + c + 1)
                        if o >= 4:
                            dve.wait_ge(added, (o - 3) * CHUNKS)
                        dst = h if o == 0 else product[:, o % 3]
                        dst = dst[:, chunk(c)].rearrange("p (b n) -> p b n", b=2) if o == 0 else dst[:, 2 * c:2 * c + 2, :]
                        dve.tensor_tensor(dst, frames[:, 2 * c:2 * c + 2, o:o + POS],
                                          ps[(o * CHUNKS + c) % 8][:, :CHUNK].rearrange("p (b n) -> p b n", b=2), ALU.mult).then_inc(product_ready, 1)

            @block.gpsimd
            def _(pool):
                for o in range(1, WINDOW):
                    for c in range(CHUNKS):
                        pool.wait_ge(product_ready, o * CHUNKS + c + 1)
                        if o > 1:
                            pool.wait_ge(added, (o - 2) * CHUNKS + c + 1)
                        pool.tensor_tensor(h[:, chunk(c)], h[:, chunk(c)], product[:, o % 3, 2 * c:2 * c + 2, :].rearrange("p b n -> p (b n)"), ALU.add).then_inc(added, 1)
                pool.wait_ge(added, (WINDOW - 1) * CHUNKS)


def batch_axis_attention(nc, h, x, w, ps):
    blocks, hd = 8, 8
    with Stage(nc, "mix") as s:
        pos_major = {n: s.sb(n + "_pos", [TILE, 2, blocks, SEQS, hd]) for n in ("query", "key", "value")}
        entry_major = {n: s.sb(n + "_entry", [128, COLS]) for n in ("query", "key", "value")}
        row_major = {n: s.sb(n + "_row", [TILE, TILES, 128]) for n in ("key", "value")}
        mixed = s.sb("mixed", [TILE, 2, SEQS, blocks, hd])
        top = s.sb("top", [TILE, 2 * blocks])
        total = s.sb("total", [TILE, 2 * blocks])
        inverse = s.sb("inverse", [TILE, 2 * blocks])
        key_top = s.sb("key_top", [128, blocks])
        key_total = s.sb("key_total", [128, blocks])
        key_inverse = s.sb("key_inverse", [128, blocks])
        context = s.sb("context", [128, blocks, 128])
        qkv_ready, qkv_kept = s.sem("qkv_ready"), s.sem("qkv_kept")
        q_top, q_less, q_exp, q_total, q_inverse, q_scaled = (
            s.sem(n) for n in ("q_top", "q_less", "q_exp", "q_total", "q_inverse", "q_scaled"))
        key_entry_ready, key_entry_kept, value_entry_ready, value_entry_kept = (
            s.sem(n) for n in ("key_entry_ready", "key_entry_kept", "value_entry_ready", "value_entry_kept"))
        key_top_ready, key_exp, key_inverse_ready, key_scaled = (
            s.sem(n) for n in ("key_top_ready", "key_exp", "key_inverse_ready", "key_scaled"))
        value_row_ready, value_row_kept, key_row_ready, key_row_kept = (
            s.sem(n) for n in ("value_row_ready", "value_row_kept", "key_row_ready", "key_row_kept"))
        q_entry_ready, q_entry_kept, context_ready, context_kept = (
            s.sem(n) for n in ("q_entry_ready", "q_entry_kept", "context_ready", "context_kept"))
        mixed_ready, mixed_kept, back_ready, h_ready = (s.sem(n) for n in ("mixed_ready", "mixed_kept", "back_ready", "h_ready"))

        def entries(n, b):
            t, g = b // 2, b % 2
            return entry_major[n][:].rearrange("p (c k) -> p k c", k=blocks)[:, 4 * g:4 * g + 4, TILE * t:TILE * t + TILE]

        with nc.Block() as block:

            @block.tensor
            def _(pe):
                for j in range(TILES):
                    if j >= 8:
                        pe.wait_ge(qkv_kept, 3 * (j - 7))
                    pe.matmul(ps[j % 8][0:TILE, 0:384], x[:, tile(j)], w["mix_qkv"], start=True, stop=True).then_inc(qkv_ready, 1)

                def turn(name, first, ready):
                    for b in range(4):
                        for k in range(4):
                            src = pos_major[name][:, b // 2, 4 * (b % 2) + k].rearrange("p r j -> p (r j)")
                            mm = pe.transpose(ps[first + b][:, tile(k)], src, w["ident"][0:TILE, 0:TILE])
                        mm.then_inc(ready, 1)

                def turn_rows(name, first, ready):
                    for b in range(4):
                        for k in range(4):
                            mm = pe.transpose(ps[first + b][0:TILE, 128 * k:128 * k + 128], entry_major[name][:, tile(4 * b + k)], w["ident"])
                        mm.then_inc(ready, 1)

                pe.wait_ge(qkv_kept, 3 * TILES)
                turn("key", 0, key_entry_ready)
                turn("value", 4, value_entry_ready)
                pe.wait_ge(value_entry_kept, 4)
                turn_rows("value", 4, value_row_ready)
                pe.wait_ge(key_scaled, blocks)
                turn_rows("key", 0, key_row_ready)
                pe.wait_ge(q_scaled, 1)
                pe.wait_ge(value_row_kept, 4)
                turn("query", 4, q_entry_ready)
                for n in range(2):
                    pe.wait_ge(key_row_kept, 4)
                    for k in range(4):
                        for t in range(2):
                            i = 2 * (4 * n + k) + t
                            mm = pe.matmul(ps[n][:, 128 * k:128 * k + 128], row_major["key"][:, i], row_major["value"][:, i],
                                           start=(t == 0), stop=(t == 1))
                    mm.then_inc(context_ready, 1)
                pe.wait_ge(q_entry_kept, 4)
                for t in range(2):
                    for n in range(2):
                        pe.wait_ge(context_kept, n + 1)
                        for k in range(4):
                            g = 4 * n + k
                            mm = pe.matmul(ps[4 + 2 * t + n][0:TILE, 128 * k:128 * k + 128], entry_major["query"][:, tile(2 * g + t)],
                                           context[:, g, :], start=True, stop=True)
                        mm.then_inc(mixed_ready, 1)
                pe.wait_ge(mixed_kept, 4)
                pe.wait_ge(context_kept, 2)
                for j in range(TILES):
                    src = mixed[:, j % 2, 2 * (j // 2):2 * (j // 2) + 2].rearrange("p r h j -> p (r h j)")
                    mm = pe.transpose(ps[j // 4][:, tile(j % 4)], src, w["ident"][0:TILE, 0:TILE])
                    if j % 4 == 3:
                        mm.then_inc(back_ready, 1)

            @block.scalar
            def _(act):
                for b in range(4):
                    act.wait_ge(key_entry_ready, b + 1)
                    act.activation(entries("key", b), ps[b][:, :CHUNK].rearrange("p (k c) -> p k c", k=4), ACT.Copy).then_inc(key_entry_kept, 1)
                act.wait_ge(q_less, 1)
                wide = pos_major["query"]
                act.activation(wide[:], wide[:], ACT.Exp).then_inc(q_exp, 1)
                act.wait_ge(key_top_ready, 1)
                for g in range(blocks):
                    rows_ = entry_major["key"][:, g * POS:(g + 1) * POS]
                    act.activation(rows_, rows_, ACT.Exp, bias=key_top[:, g:g + 1], accum_out=key_total[:, g:g + 1]).then_inc(key_exp, 1)
                for b in range(4):
                    act.wait_ge(key_row_ready, b + 1)
                    act.activation(row_major["key"][:, 4 * b:4 * b + 4, :], ps[b][0:TILE, :].rearrange("p (k e) -> p k e", k=4), ACT.Copy).then_inc(key_row_kept, 1)
                for b in range(4):
                    act.wait_ge(q_entry_ready, b + 1)
                    act.activation(entries("query", b), ps[4 + b][:, :CHUNK].rearrange("p (k c) -> p k c", k=4), ACT.Copy).then_inc(q_entry_kept, 1)
                for n in range(2):
                    act.wait_ge(context_ready, n + 1)
                    act.activation(context[:, 4 * n:4 * n + 4, :], ps[n][:].rearrange("p (a n) -> p a n", a=4), ACT.Copy).then_inc(context_kept, 1)

            @block.vector
            def _(dve):
                for j in range(TILES):
                    dve.wait_ge(qkv_ready, j + 1)
                    for i, n in enumerate(("query", "key", "value")):
                        got = ps[j % 8][0:TILE, 128 * i:128 * i + 128].rearrange("p (a h j) -> p h a j", a=2, h=blocks)
                        bias = w["mix_qkvb"][0:TILE, 64 * i:64 * i + 64].rearrange("p (h j) -> p h j", h=blocks).unsqueeze(2).to_broadcast([TILE, blocks, 2, hd])
                        dve.tensor_tensor(pos_major[n][:, j % 2, :, 2 * (j // 2):2 * (j // 2) + 2], got, bias, ALU.add).then_inc(qkv_kept, 1)
                dve.wait_ge(qkv_kept, 3 * TILES)
                wide = pos_major["query"][:].rearrange("p t h r j -> p (t h) (r j)")
                dve.tensor_reduce(top[:], wide, AX.X, ALU.max).then_inc(q_top, 1)
                dve.wait_ge(q_top, 1)
                dve.tensor_tensor(wide, wide, top[:].unsqueeze(2).to_broadcast([TILE, 2 * blocks, 128]), ALU.subtract).then_inc(q_less, 1)
                dve.wait_ge(key_entry_kept, 4)
                dve.tensor_reduce(key_top[:], entry_major["key"][:].rearrange("p (g n) -> p g n", n=POS), AX.X, ALU.max, negate=True).then_inc(key_top_ready, 1)
                for b in range(4):
                    dve.wait_ge(value_entry_ready, b + 1)
                    dve.tensor_copy(entries("value", b), ps[4 + b][:, :CHUNK].rearrange("p (k c) -> p k c", k=4)).then_inc(value_entry_kept, 1)
                dve.wait_ge(q_exp, 1)
                dve.tensor_reduce(total[:], wide, AX.X, ALU.add).then_inc(q_total, 1)
                dve.wait_ge(q_total, 1)
                dve.reciprocal(inverse[:], total[:]).then_inc(q_inverse, 1)
                dve.wait_ge(q_inverse, 1)
                dve.tensor_scalar(top[:], inverse[:], float(SEQS * hd) ** 0.5, None, ALU.mult).then_inc(q_inverse, 1)
                dve.wait_ge(key_exp, blocks)
                dve.reciprocal(key_inverse[:], key_total[:]).then_inc(key_inverse_ready, 1)
                dve.wait_ge(key_inverse_ready, 1)
                for g in range(blocks):
                    rows_ = entry_major["key"][:, g * POS:(g + 1) * POS]
                    dve.tensor_scalar(rows_, rows_, key_inverse[:, g:g + 1], None, ALU.mult).then_inc(key_scaled, 1)
                dve.wait_ge(q_inverse, 2)
                dve.tensor_tensor(wide, wide, top[:].unsqueeze(2).to_broadcast([TILE, 2 * blocks, 128]), ALU.mult).then_inc(q_scaled, 1)
                for b in range(4):
                    dve.wait_ge(value_row_ready, b + 1)
                    dve.tensor_copy(row_major["value"][:, 4 * b:4 * b + 4, :], ps[4 + b][0:TILE, :].rearrange("p (k e) -> p k e", k=4)).then_inc(value_row_kept, 1)
                for t in range(2):
                    for n in range(2):
                        dve.wait_ge(mixed_ready, 2 * t + n + 1)
                        dst = mixed[:, t, :, 4 * n:4 * n + 4].rearrange("p r h j -> p h r j")
                        dve.tensor_copy(dst, ps[4 + 2 * t + n][0:TILE, :].rearrange("p (h r j) -> p h r j", h=4, r=SEQS)).then_inc(mixed_kept, 1)
                for c in range(CHUNKS):
                    dve.wait_ge(back_ready, c + 1)
                    dve.tensor_tensor(h[:, chunk(c)], h[:, chunk(c)], ps[c][:, :CHUNK], ALU.add).then_inc(h_ready, 1)
                dve.wait_ge(h_ready, CHUNKS)


def top_half_ffn(nc, h, x, w, ps):
    kept_tokens = max(1, int(0.5 * POS)) - 1
    with Stage(nc, "cap") as s:
        score = s.sb("score", [TILE, TILES, 2])
        above = s.sb("above", [TILE, TILES, 2])
        equal = s.sb("equal", [TILE, TILES, 2])
        gate = s.sb("gate", [TILE, TILES, 2])
        gate_wide = s.sb("gate_wide", [TILE, TILES, 2, 64])
        gate_f = s.sb("gate_f", [128, COLS])
        scratch = s.sb("scratch", [TILE, 4, POS])
        hidden = s.sb("hidden", [128, 2, 2, COLS])
        out = s.sb("out", [128, COLS])
        score_ready, score_kept, score_spread = s.sem("score_ready"), s.sem("score_kept"), s.sem("score_spread")
        counted, rank_ready, gate_ready = s.sem("counted"), s.sem("rank_ready"), s.sem("gate_ready")
        gate_spread, gate_kept = s.sem("gate_spread"), s.sem("gate_kept")
        up_ready, up_kept, down_ready = s.sem("up_ready"), s.sem("up_kept"), s.sem("down_ready")
        gated, h_plus_x, h_ready = s.sem("gated"), s.sem("h_plus_x"), s.sem("h_ready")
        with nc.Block() as block:

            @block.tensor
            def _(pe):
                for j in range(TILES):
                    mm = pe.matmul(ps[0][0:TILE, 2 * j:2 * j + 2], x[:, tile(j)], w["cap_r"], start=True, stop=True)
                mm.then_inc(score_ready, 1)
                pe.wait_ge(score_kept, 1)
                for b in range(8):
                    for k in range(4):
                        j = 4 * (b % 4) + k
                        mm = pe.transpose(ps[b][0:TILE, tile(k)], score[:, j, b // 4].unsqueeze(1).to_broadcast([TILE, TILE]), w["ident"][0:TILE, 0:TILE])
                    mm.then_inc(score_spread, 1)
                for n in range(16):
                    c, m, a = n // 4, (n // 2) % 2, n % 2
                    pe.wait_ge(counted, 64)
                    if n >= 8:
                        pe.wait_ge(up_kept, n - 7)
                    rows_ = slice(64 * a, 64 * a + 64)
                    pe.matmul(ps[n % 8][:, :CHUNK], w["cap_1"][rows_, 128 * m:128 * m + 128], x[rows_, chunk(c)], start=True, stop=True).then_inc(up_ready, 1)
                pe.wait_ge(gate_ready, 2)
                pe.wait_ge(up_kept, 12)
                for c in range(CHUNKS):
                    for k in range(4):
                        mm = pe.transpose(ps[c][:, tile(k)], gate_wide[:, 4 * c + k].rearrange("p a f -> p (a f)"), w["ident"][0:TILE, 0:TILE])
                    mm.then_inc(gate_spread, 1)
                pe.wait_ge(up_kept, 16)
                for c in range(CHUNKS):
                    for a in range(2):
                        for m in range(2):
                            mm = pe.matmul(ps[4 + c][:, :CHUNK], w["cap_2"][:, 128 * (2 * a + m):128 * (2 * a + m) + 128], hidden[:, m, a, chunk(c)],
                                           start=(a + m == 0), stop=(a + m == 2))
                    mm.then_inc(down_ready, 1)

            @block.scalar
            def _(act):
                for n in range(16):
                    c, m, a = n // 4, (n // 2) % 2, n % 2
                    act.wait_ge(up_ready, n + 1)
                    act.activation(hidden[:, m, a, chunk(c)], ps[n % 8][:, :CHUNK], ACT.Gelu_apprx_tanh, bias=w["cap_b1"][:, m:m + 1]).then_inc(up_kept, 1)
                for c in range(CHUNKS):
                    act.wait_ge(gate_spread, c + 1)
                    act.activation(gate_f[:, chunk(c)], ps[c][:, :CHUNK], ACT.Copy).then_inc(gate_kept, 1)

            @block.vector
            def _(dve):
                dve.wait_ge(score_ready, 1)
                dve.tensor_scalar(score[:], ps[0][0:TILE, 0:2 * TILES].rearrange("p (j a) -> p j a", a=2), w["cap_br"][0:TILE, :], None, ALU.add).then_inc(score_kept, 1)
                dve.wait_ge(score_kept, 1)
                for b in range(8):
                    dve.wait_ge(score_spread, b + 1)
                    for k in range(4):
                        j, a, n = 4 * (b % 4) + k, b // 4, 8 * b + 2 * k
                        seq = ps[b][0:TILE, (k // 2) * POS:(k // 2 + 1) * POS]
                        mine = score[:, j, a:a + 1]
                        if n >= 4:
                            dve.wait_ge(counted, n - 2)
                        dve.tensor_scalar(scratch[:, n % 4], seq, mine, None, ALU.is_gt, ALU.add, accum_out=above[:, j, a:a + 1]).then_inc(counted, 1)
                        dve.scalar_tensor_tensor(scratch[:, n % 4 + 1], seq, mine, w["cap_earlier"][0:TILE, POS * (j % 2):POS * (j % 2) + POS],
                                                 ALU.is_equal, ALU.mult, accum_out=equal[:, j, a:a + 1]).then_inc(counted, 1)
                dve.wait_ge(counted, 64)
                dve.tensor_tensor(above[:], above[:], equal[:], ALU.add).then_inc(rank_ready, 1)
                dve.wait_ge(rank_ready, 1)
                dve.scalar_tensor_tensor(gate[:].rearrange("p j a -> p (j a)"), above[:].rearrange("p j a -> p (j a)"), float(kept_tokens),
                                         score[:].rearrange("p j a -> p (j a)"), ALU.is_lt, ALU.mult).then_inc(gate_ready, 1)
                dve.wait_ge(gate_ready, 1)
                dve.tensor_copy(gate_wide[:], gate[:].unsqueeze(3).to_broadcast([TILE, TILES, 2, 64])).then_inc(gate_ready, 1)
                for c in range(CHUNKS):
                    dve.wait_ge(down_ready, c + 1)
                    dve.wait_ge(gate_kept, c + 1)
                    dve.scalar_tensor_tensor(out[:, chunk(c)], ps[4 + c][:, :CHUNK], w["cap_b2"], gate_f[:, chunk(c)], ALU.add, ALU.mult).then_inc(gated, 1)
                dve.wait_ge(h_plus_x, 1)
                for c in range(CHUNKS):
                    dve.wait_ge(gated, c + 1)
                    dve.tensor_tensor(h[:, chunk(c)], h[:, chunk(c)], out[:, chunk(c)], ALU.add).then_inc(h_ready, 1)
                dve.wait_ge(h_ready, CHUNKS)

            @block.gpsimd
            def _(pool):
                pool.tensor_tensor(h[:], h[:], x[:], ALU.add).then_inc(h_plus_x, 1)


def taylor_attention(nc, h, x, w, ps):
    heads, hd, feats, group = 8, 8, 45, 8
    eps = 1e-12
    scale = float(hd) ** 0.25
    seqs = 2 * TILES
    with Stage(nc, "tay") as s:
        qkv = s.sb("qkv", [TILE, 3, TILES, 2, FEAT])
        phi_k = s.sb("phi_k", [TILE, seqs, heads, feats])
        phi_q = s.sb("phi_q", [TILE, 2, group, heads, feats])
        value = s.sb("value", [TILE, seqs, heads, hd + 1])
        norm2 = s.sb("norm2", [TILE, 2, seqs, heads])
        norm = s.sb("norm", [TILE, 2, seqs, heads])
        factor = s.sb("factor", [TILE, 2, seqs, heads])
        kv = s.sb("kv", [90, SEQS, 4, 18])
        phi_t = s.sb("phi_t", [90, 4, 4, TILE])
        inverse = s.sb("inverse", [TILE, 2, 4 * heads])
        y = s.sb("y", [TILE, TILES, 2, heads, hd])
        y_f = s.sb("y_f", [128, COLS])
        squares = phi_k[:].rearrange("p a h f -> p (a h f)")[:, 0:2 * seqs * FEAT].rearrange("p (i a f) -> p i a f", i=2, a=seqs)
        (qkv_ready, qkv_kept, squared, norm2_ready, norm_ready, norm_safe, norm_inverse, factor_ready, value_ready, ones_ready,
         key_unit, query_unit, key_products, query_products, kv_ready, kv_kept, turned, turned_kept, y_ready, y_inverse, y_kept,
         back_ready, back_kept, out_ready, h_ready) = (s.sem(n) for n in (
             "qkv_ready qkv_kept squared norm2_ready norm_ready norm_safe norm_inverse factor_ready value_ready ones_ready "
             "key_unit query_unit key_products query_products kv_ready kv_kept turned turned_kept y_ready y_inverse y_kept "
             "back_ready back_kept out_ready h_ready").split())

        def vectors(i, lo, n):
            return qkv[:, i].rearrange("p j a (h e) -> p (j a) h e", h=heads)[:, lo:lo + n]

        def products(eng, phi, n, done):
            flat = phi.rearrange("p a h f -> p (a h) f")
            at = 0
            for i in range(hd):
                k = hd - i
                last = eng.tensor_tensor(flat[:, :, at:at + k], flat[:, :, 36 + i:37 + i].to_broadcast([TILE, n * heads, k]),
                                         flat[:, :, 36 + i:44], ALU.mult)
                at += k
                last.then_inc(done, 1)

        with nc.Block() as block:

            @block.tensor
            def _(pe):
                for j in range(TILES):
                    if j >= 8:
                        pe.wait_ge(qkv_kept, j - 7)
                    pe.matmul(ps[j % 8][0:TILE, 0:384], x[:, tile(j)], w["tay_qkv"], start=True, stop=True).then_inc(qkv_ready, 1)
                pe.wait_ge(key_products, hd)
                pe.wait_ge(ones_ready, 4)
                pe.wait_ge(value_ready, 1)
                pe.wait_ge(qkv_kept, TILES)
                for n in range(4):
                    for k in range(4):
                        p, a = 2 * n + k // 2, k % 2
                        for g in range(4):
                            for t in range(2):
                                col = 2 * (2 * p + t) + a
                                mm = pe.matmul(ps[n][0:90, 72 * k + 18 * g:72 * k + 18 * g + 18],
                                               phi_k[:, col, 2 * g:2 * g + 2].rearrange("p h f -> p (h f)"),
                                               value[:, col, 2 * g:2 * g + 2].rearrange("p h f -> p (h f)"), start=(t == 0), stop=(t == 1))
                    mm.then_inc(kv_ready, 1)

                def outputs(col):
                    p, k = col // 4, col % 4
                    pe.wait_ge(turned_kept, col + 1)
                    if k == 0:
                        pe.wait_ge(kv_kept, p // 2 + 1)
                        if p == 0:
                            pe.wait_ge(kv_kept, 4)
                        if p >= 4:
                            pe.wait_ge(y_kept, p - 3)
                    for g in range(4):
                        mm = pe.matmul(ps[p % 4][0:TILE, 72 * k + 18 * g:72 * k + 18 * g + 18], phi_t[:, col % 4, g, :],
                                       kv[:, 2 * p + col % 2, g, :], start=True, stop=True)
                    mm.then_inc(y_ready, 1)

                for col in range(seqs):
                    if col % group == 0:
                        pe.wait_ge(query_products, hd * (col // group + 1))
                    if col >= 4:
                        pe.wait_ge(turned_kept, col - 3)
                    for g in range(4):
                        mm = pe.transpose(ps[4 + col % 4][0:90, tile(g)],
                                          phi_q[:, (col // group) % 2, col % group, 2 * g:2 * g + 2].rearrange("p h f -> p (h f)"),
                                          w["ident"][0:TILE, 0:TILE])
                    mm.then_inc(turned, 1)
                    if col >= 2:
                        outputs(col - 2)
                outputs(seqs - 2)
                outputs(seqs - 1)
                pe.wait_ge(y_kept, PAIRS)
                for j in range(TILES):
                    mm = pe.transpose(ps[4 + j // 4][:, tile(j % 4)], y[:, j].rearrange("p a h e -> p (a h e)"), w["ident"][0:TILE, 0:TILE])
                    if j % 4 == 3:
                        mm.then_inc(back_ready, 1)
                for c in range(CHUNKS):
                    pe.wait_ge(back_kept, c + 1)
                    pe.matmul(ps[c][:, :CHUNK], w["tay_o"], y_f[:, chunk(c)], start=True, stop=True).then_inc(out_ready, 1)

            @block.scalar
            def _(act):
                act.wait_ge(qkv_kept, TILES)
                act.activation(squares, qkv[:, 0:2].rearrange("p i j a f -> p i (j a) f"), ACT.Square).then_inc(squared, 1)
                act.wait_ge(norm2_ready, 1)
                act.activation(norm[:, 0], norm2[:, 0], ACT.Sqrt, scale=scale * scale).then_inc(norm_ready, 1)
                act.activation(norm[:, 1], norm2[:, 1], ACT.Sqrt).then_inc(norm_ready, 1)
                act.wait_ge(ones_ready, 2)
                act.activation(value[:, :, :, 1:], vectors(2, 0, seqs), ACT.Copy, scale=1.0 / POS).then_inc(value_ready, 1)
                for col in range(seqs):
                    act.wait_ge(turned, col + 1)
                    if col >= 4:
                        act.wait_ge(y_ready, col - 3)
                    act.activation(phi_t[:, col % 4], ps[4 + col % 4][0:90, :CHUNK].rearrange("p (g n) -> p g n", g=4), ACT.Copy).then_inc(turned_kept, 1)
                for c in range(CHUNKS):
                    act.wait_ge(back_ready, c + 1)
                    act.activation(y_f[:, chunk(c)], ps[4 + c][:, :CHUNK], ACT.Copy).then_inc(back_kept, 1)

            @block.vector
            def _(dve):
                for j in range(TILES):
                    dve.wait_ge(qkv_ready, j + 1)
                    dve.tensor_tensor(qkv[:, :, j].rearrange("p i a f -> p i (a f)"), ps[j % 8][0:TILE, 0:384].rearrange("p (i f) -> p i f", i=3),
                                      w["tay_qkvb"][0:TILE, :].rearrange("p (i f) -> p i f", i=3), ALU.add).then_inc(qkv_kept, 1)
                dve.wait_ge(squared, 1)
                dve.tensor_reduce(norm2[:].rearrange("p i a h -> p (i a h)"), squares.rearrange("p i a (h e) -> p (i a h) e", e=hd), AX.X, ALU.add).then_inc(norm2_ready, 1)
                dve.wait_ge(norm_ready, 2)
                dve.tensor_scalar(norm[:], norm[:], eps, None, ALU.max).then_inc(norm_safe, 1)
                dve.wait_ge(norm_safe, 1)
                dve.reciprocal(norm2[:], norm[:]).then_inc(norm_inverse, 1)
                dve.wait_ge(norm_inverse, 1)
                dve.tensor_scalar(factor[:, 1], norm2[:, 1], scale, None, ALU.mult).then_inc(factor_ready, 1)
                dve.scalar_tensor_tensor(factor[:, 0], norm2[:, 0], scale * scale, w["tay_temp"][0:TILE, :].unsqueeze(1).to_broadcast([TILE, seqs, heads]),
                                         ALU.mult, ALU.mult).then_inc(factor_ready, 1)
                dve.wait_ge(factor_ready, 2)
                dve.wait_ge(ones_ready, 1)
                dve.tensor_tensor(phi_k[:, :, :, 36:44], vectors(1, 0, seqs), factor[:, 1].unsqueeze(3).to_broadcast([TILE, seqs, heads, hd]), ALU.mult).then_inc(key_unit, 1)
                dve.wait_ge(key_unit, 1)
                products(dve, phi_k[:], seqs, key_products)
                for n in range(4):
                    dve.wait_ge(kv_ready, n + 1)
                    dve.tensor_tensor(kv[:, 4 * n:4 * n + 4].rearrange("p s g f -> p (s g) f"), ps[n][0:90, 0:288].rearrange("p (s f) -> p s f", f=18),
                                      w["tay_coef"][0:90, :].unsqueeze(1).to_broadcast([90, 16, 18]), ALU.mult).then_inc(kv_kept, 1)
                for p in range(PAIRS):
                    dve.wait_ge(y_ready, 4 * p + 4)
                    got = ps[p % 4][0:TILE, 0:288].rearrange("p (n e) -> p n e", e=hd + 1)
                    dve.reciprocal(inverse[:, p % 2].unsqueeze(2), got[:, :, 0:1]).then_inc(y_inverse, 1)
                    dve.wait_ge(y_inverse, p + 1)
                    dve.tensor_tensor(y[:, 2 * p:2 * p + 2].rearrange("p j a h e -> p (j a h) e"), got[:, :, 1:],
                                      inverse[:, p % 2].unsqueeze(2).to_broadcast([TILE, 4 * heads, hd]), ALU.mult).then_inc(y_kept, 1)
                for c in range(CHUNKS):
                    dve.wait_ge(out_ready, c + 1)
                    dve.scalar_tensor_tensor(h[:, chunk(c)], ps[c][:, :CHUNK], w["tay_ob"], h[:, chunk(c)], ALU.add, ALU.add).then_inc(h_ready, 1)
                dve.wait_ge(h_ready, CHUNKS)

            @block.gpsimd
            def _(pool):
                pool.wait_ge(norm2_ready, 1)
                pool.memset(phi_k[:, :, :, 44:45], 1.0).then_inc(ones_ready, 1)
                pool.memset(value[:, :, :, 0:1], 1.0 / POS).then_inc(ones_ready, 1)
                pool.memset(phi_q[:, 0, :, :, 44:45], 1.0).then_inc(ones_ready, 1)
                pool.memset(phi_q[:, 1, :, :, 44:45], 1.0).then_inc(ones_ready, 1)
                pool.wait_ge(factor_ready, 2)
                pool.wait_ge(ones_ready, 4)
                for n in range(seqs // group):
                    if n >= 2:
                        pool.wait_ge(turned, group * (n - 1))
                    lo = group * n
                    pool.tensor_tensor(phi_q[:, n % 2, :, :, 36:44], vectors(0, lo, group),
                                       factor[:, 0, lo:lo + group].unsqueeze(3).to_broadcast([TILE, group, heads, hd]), ALU.mult).then_inc(query_unit, 1)
                    pool.wait_ge(query_unit, n + 1)
                    products(pool, phi_q[:, n % 2], group, query_products)


def expert_routing(nc, x, w, ps, r):
    cols = 2 * TILES
    tokens = r["tokens"]
    with Stage(nc, "route") as s:
        token_major = s.sb("token_major", [TILE, cols, FEAT])
        logits = s.sb("logits", [TILE, cols, EXPERTS])
        best = s.sb("best", [TILE, cols, 8])
        best_at = s.sb("best_at", [TILE, cols, 8], U32)
        chosen = s.sb("chosen", [TILE, cols, 2])
        ratio = s.sb("ratio", [TILE, cols])
        denominator = s.sb("denominator", [TILE, cols])
        choice = [s.sb(f"choice{k}", [TILE, EXPERTS, cols], BF16) for k in range(2)]
        picked = s.sb("picked", [TILE, EXPERTS, cols], BF16)
        running = s.sb("running", [TILE, EXPERTS, cols], BF16)
        before = s.sb("before", [TILE, EXPERTS, cols], BF16)
        keep = s.sb("keep", [TILE, EXPERTS, cols], BF16)
        earlier = s.sb("earlier", [TILE, TILE], BF16)
        ones = s.sb("ones", [TILE, 128], BF16)
        rounded = s.sb("rounded", [128, EXPERTS], I32)
        shifted = s.sb("shifted", [128, EXPERTS], I32)
        tiles_of = s.sb("tiles_of", [128, EXPERTS])
        end_tile = s.sb("end_tile", [128, EXPERTS])
        first_slot = s.sb("first_slot", [128, EXPERTS])
        ended = s.sb("ended", [128, EXPERTS])
        expert_col = s.sb("expert_col", [128, 1])
        places = s.sb("places", [TILE, EXPERTS, cols])
        product = s.sb("product", [TILE, EXPERTS, cols])
        slot = s.sb("slot", [TILE, cols, 2])
        split_i = s.sb("split_i", [TILE, 2, cols * 2], I32)
        split = s.sb("split", [TILE, 2, cols * 2])
        lane_hot, tile_hot = (a[:].rearrange("p e a -> p (e a)").bitcast(BF16).rearrange("p (a l) -> p a l", a=cols) for a in (product, places))
        tile_high = s.sb("tile_high", [TILE, cols, 128], BF16)
        low_digit = s.sb("low_digit", [128, 128])
        combine = logits
        second = s.sb("second", [TILE, cols, EXPERTS])
        (logits_ready, logits_kept, token_ready, token_kept, best_ready, index_ready, chosen_ready, gap_ready, ratio_ready,
         gates_ready, hot_ready, picked_ready, consts_ready, running_ready, before_ready, counts_ready, count_steps, prefix_ready,
         places_ready, product_ready, slot_ready, split_ready, hot_tiles, source_ready, low_kept, expert_turned, expert_kept,
         combine_ready, combine_turned, combine_kept, stored) = (s.sem(n) for n in (
             "logits_ready logits_kept token_ready token_kept best_ready index_ready chosen_ready gap_ready ratio_ready "
             "gates_ready hot_ready picked_ready consts_ready running_ready before_ready counts_ready count_steps prefix_ready "
             "places_ready product_ready slot_ready split_ready hot_tiles source_ready low_kept expert_turned expert_kept "
             "combine_ready combine_turned combine_kept stored").split())
        with nc.Block() as block:

            @block.tensor
            def _(pe):
                for j in range(TILES):
                    mm = pe.matmul(ps[j // 4][0:TILE, 128 * (j % 4):128 * (j % 4) + 128], x[:, tile(j)], w["moe_r"], start=True, stop=True)
                    if j % 4 == 3:
                        mm.then_inc(logits_ready, 1)
                for j in range(TILES):
                    mm = pe.transpose(ps[4 + j // 4][0:TILE, 128 * (j % 4):128 * (j % 4) + 128], x[:, tile(j)], w["ident"])
                    if j % 4 == 3:
                        mm.then_inc(token_ready, 1)
                pe.wait_ge(consts_ready, 4)
                pe.wait_ge(running_ready, 1)
                pe.wait_ge(token_kept, 4)
                pe.matmul(ps[4][:, 0:EXPERTS], ones[:], running[:, :, cols - 1], start=True, stop=True).then_inc(counts_ready, 1)
                pe.wait_ge(before_ready, 1)
                for b in range(4):
                    pe.matmul(ps[b][0:TILE, :], earlier[:], picked[:, 16 * b:16 * b + 16, :].rearrange("p e a -> p (e a)"), start=True, stop=False)
                    pe.matmul(ps[b][0:TILE, :], ones[:, 0:TILE], before[:, 16 * b:16 * b + 16, :].rearrange("p e a -> p (e a)"), start=False, stop=True).then_inc(prefix_ready, 1)
                pe.wait_ge(count_steps, 8)
                pe.transpose(ps[4][0:1, 128:256], expert_col[:], w["ident"]).then_inc(expert_turned, 1)
                for half in range(2):
                    for d in range(2):
                        pe.wait_ge(hot_tiles, 4 * half + 3 + d)
                        for k in range(cols):
                            mm = pe.matmul(ps[5 + d][:, 0:128], lane_hot[:, k], (tile_high if d == 0 else tile_hot)[:, k],
                                           start=(half + k == 0), stop=(half == 1 and k == cols - 1))
                        mm.then_inc(source_ready, 1)
                pe.wait_ge(combine_ready, 3)
                pe.wait_ge(places_ready, 4)
                for j in range(TILES):
                    mm = pe.transpose(ps[j // 4][:, tile(j % 4)], combine[:, 2 * j:2 * j + 2].rearrange("p a e -> p (a e)"), w["ident"][0:TILE, 0:TILE])
                    if j % 4 == 3:
                        mm.then_inc(combine_turned, 1)

            @block.scalar
            def _(act):
                act.activation(earlier[:], w["moe_tri"][0:TILE, :], ACT.Copy).then_inc(consts_ready, 1)
                act.activation(ones[:], w["moe_ones"][0:TILE, :], ACT.Copy).then_inc(consts_ready, 1)
                for b in range(4):
                    act.wait_ge(token_ready, b + 1)
                    act.activation(token_major[:, 8 * b:8 * b + 8].rearrange("p a f -> p (a f)"), ps[4 + b][0:TILE, :], ACT.Copy).then_inc(token_kept, 1)
                act.wait_ge(gap_ready, 1)
                act.activation(ratio[:], ratio[:], ACT.Exp).then_inc(ratio_ready, 1)
                act.wait_ge(expert_turned, 1)
                act.activation(r["expert"][:], ps[4][0:1, 128:256], ACT.Copy).then_inc(expert_kept, 1)
                act.wait_ge(source_ready, 4)
                act.activation(low_digit[:], ps[6][:, 0:128], ACT.Copy).then_inc(low_kept, 1)
                for c in range(CHUNKS):
                    act.wait_ge(combine_turned, c + 1)
                    act.activation(r["combine_t"][:, chunk(c)], ps[c][:, :CHUNK], ACT.Copy).then_inc(combine_kept, 1)

            @block.vector
            def _(dve):
                for b in range(4):
                    dve.wait_ge(logits_ready, b + 1)
                    dve.tensor_tensor(logits[:, 8 * b:8 * b + 8], ps[b][0:TILE, :].rearrange("p (a e) -> p a e", e=EXPERTS),
                                      w["moe_br"][0:TILE, :].unsqueeze(1).to_broadcast([TILE, 8, EXPERTS]), ALU.add).then_inc(logits_kept, 1)
                dve.wait_ge(logits_kept, 4)
                for a in range(cols):
                    dve.max(best[:, a], logits[:, a]).then_inc(best_ready, 1)
                for a in range(cols):
                    dve.wait_ge(best_ready, a + 1)
                    dve.max_index(best_at[:, a], best[:, a], logits[:, a]).then_inc(index_ready, 1)
                dve.tensor_tensor(ratio[:].unsqueeze(2), best[:, :, 1:2], best[:, :, 0:1], ALU.subtract).then_inc(gap_ready, 1)
                dve.wait_ge(index_ready, cols)
                dve.tensor_copy(chosen[:], best_at[:, :, 0:2]).then_inc(chosen_ready, 1)
                dve.wait_ge(chosen_ready, 1)
                for k in range(2):
                    dve.tensor_tensor(choice[k][:], w["iota"][0:TILE, 0:EXPERTS].unsqueeze(2).to_broadcast([TILE, EXPERTS, cols]),
                                      chosen[:, :, k].unsqueeze(1).to_broadcast([TILE, EXPERTS, cols]), ALU.is_equal).then_inc(hot_ready, 1)
                dve.wait_ge(ratio_ready, 1)
                dve.tensor_scalar(denominator[:], ratio[:], 1.0, None, ALU.add).then_inc(gates_ready, 1)
                dve.wait_ge(gates_ready, 1)
                dve.reciprocal(r["gates"][:, 0], denominator[:]).then_inc(gates_ready, 1)
                dve.wait_ge(gates_ready, 2)
                dve.tensor_tensor(r["gates"][:, 1], r["gates"][:, 0], ratio[:], ALU.mult).then_inc(gates_ready, 1)
                dve.wait_ge(hot_ready, 2)
                dve.tensor_tensor(picked[:], choice[0][:], choice[1][:], ALU.add).then_inc(picked_ready, 1)
                dve.wait_ge(picked_ready, 1)
                dve.wait_ge(consts_ready, 4)
                dve.tensor_tensor_scan(running[:].rearrange("p e a -> p (e a)"), keep[:].rearrange("p e a -> p (e a)"),
                                       picked[:].rearrange("p e a -> p (e a)"), 0.0, ALU.mult, ALU.add).then_inc(running_ready, 1)
                dve.wait_ge(running_ready, 1)
                dve.tensor_tensor(before[:], running[:], picked[:], ALU.subtract).then_inc(before_ready, 1)
                dve.wait_ge(counts_ready, 1)
                dve.tensor_scalar(rounded[:], ps[4][:, 0:EXPERTS], 127.0, None, ALU.add).then_inc(count_steps, 1)
                dve.wait_ge(count_steps, 1)
                dve.tensor_scalar(shifted[:], rounded[:], 7, None, ALU.arith_shift_right).then_inc(count_steps, 1)
                dve.wait_ge(count_steps, 2)
                dve.tensor_copy(tiles_of[:], shifted[:]).then_inc(count_steps, 1)
                dve.wait_ge(count_steps, 3)
                dve.tensor_tensor_scan(end_tile[:], w["moe_ones"][:, 0:EXPERTS], tiles_of[:], 0.0, ALU.mult, ALU.add).then_inc(count_steps, 1)
                dve.wait_ge(count_steps, 4)
                dve.tensor_tensor(first_slot[:], end_tile[:], tiles_of[:], ALU.subtract).then_inc(count_steps, 1)
                dve.tensor_scalar(ended[:], end_tile[:], w["iota_p"], None, ALU.is_le, ALU.add, accum_out=expert_col[:]).then_inc(count_steps, 1)
                dve.wait_ge(count_steps, 6)
                dve.tensor_scalar(first_slot[:], first_slot[:], 128.0, None, ALU.mult).then_inc(count_steps, 1)
                dve.tensor_scalar(expert_col[:], expert_col[:], EXPERTS - 1.0, None, ALU.min).then_inc(count_steps, 1)
                dve.wait_ge(count_steps, 8)
                for b in range(4):
                    dve.wait_ge(prefix_ready, b + 1)
                    dve.tensor_tensor(places[:, 16 * b:16 * b + 16], ps[b][0:TILE, :].rearrange("p (e a) -> p e a", a=cols),
                                      first_slot[0:TILE, 16 * b:16 * b + 16].unsqueeze(2).to_broadcast([TILE, 16, cols]), ALU.add).then_inc(places_ready, 1)
                dve.wait_ge(places_ready, 4)
                for k in range(2):
                    if k:
                        dve.wait_ge(slot_ready, k)
                    dve.tensor_tensor(product[:], choice[k][:], places[:], ALU.mult).then_inc(product_ready, 1)
                    dve.wait_ge(product_ready, k + 1)
                    dve.tensor_reduce(slot[:, :, k], product[:].rearrange("p e a -> p a e"), AX.X, ALU.add).then_inc(slot_ready, 1)
                dve.wait_ge(slot_ready, 2)
                dve.tensor_copy(r["slot"][:], slot[:].rearrange("p a k -> p (a k)")).then_inc(slot_ready, 1)
                dve.wait_ge(slot_ready, 3)
                dve.tensor_scalar(split_i[:, 0], r["slot"][:], 127, None, ALU.bitwise_and).then_inc(split_ready, 1)
                dve.tensor_scalar(split_i[:, 1], r["slot"][:], 7, None, ALU.arith_shift_right).then_inc(split_ready, 1)
                dve.wait_ge(split_ready, 2)
                dve.tensor_copy(split[:], split_i[:]).then_inc(split_ready, 1)
                dve.wait_ge(split_ready, 3)
                iota = w["iota"][0:TILE, :].unsqueeze(1).to_broadcast([TILE, cols, 128])
                for half in range(2):
                    mine = slice(cols * half, cols * half + cols)
                    if half:
                        dve.wait_ge(source_ready, 2)
                    dve.tensor_tensor(lane_hot, iota, split[:, 0, mine].unsqueeze(2).to_broadcast([TILE, cols, 128]), ALU.is_equal).then_inc(hot_tiles, 1)
                    dve.tensor_tensor(tile_hot, iota, split[:, 1, mine].unsqueeze(2).to_broadcast([TILE, cols, 128]), ALU.is_equal).then_inc(hot_tiles, 1)
                    dve.wait_ge(hot_tiles, 4 * half + 2)
                    dve.tensor_scalar(tile_high[:], tile_hot, w["moe_high"][0:TILE, :], None, ALU.mult).then_inc(hot_tiles, 1)
                    dve.wait_ge(hot_tiles, 4 * half + 3)
                    dve.tensor_tensor(tile_hot, tile_hot, w["moe_low"][0:TILE, mine].unsqueeze(2).to_broadcast([TILE, cols, 128]), ALU.mult).then_inc(hot_tiles, 1)
                dve.wait_ge(low_kept, 1)
                dve.scalar_tensor_tensor(r["source"][:], ps[5][:, 0:128], 64.0, low_digit[:], ALU.mult, ALU.add).then_inc(source_ready, 1)
                dve.wait_ge(source_ready, 5)

            @block.gpsimd
            def _(pool):
                pool.memset(keep[:, :, 1:], 1.0).then_inc(consts_ready, 1)
                pool.memset(keep[:, :, 0:1], 0.0).then_inc(consts_ready, 1)
                pool.wait_ge(gates_ready, 3)
                pool.wait_ge(index_ready, cols)
                for k, dst in enumerate((combine, second)):
                    pool.tensor_tensor(dst[:], choice[k][:].rearrange("p e a -> p a e"),
                                       r["gates"][:, k].unsqueeze(2).to_broadcast([TILE, cols, EXPERTS]), ALU.mult).then_inc(combine_ready, 1)
                pool.wait_ge(combine_ready, 2)
                pool.tensor_tensor(combine[:], combine[:], second[:], ALU.add).then_inc(combine_ready, 1)

            @block.sync
            def _(sp):
                sp.wait_ge(token_kept, 4)
                sp.dma_start(tokens.rearrange("(n a) f -> n (a f)", a=cols), token_major[:].rearrange("p a f -> p (a f)")).then_inc(stored, 16)
                sp.wait_ge(stored, 16)

def expert_tables(nc, w, ps, r, experts_in):
    ring, group = 8, 4
    rounds = TABLE_TILES // ring
    with Stage(nc, "table") as s:
        rows_in = s.sb("rows_in", [128, 2, ring, FEAT])
        rows_t = s.sb("rows_t", [FEAT + 1, ring, 128])
        hidden = s.sb("hidden", [128, ring, 128])
        hidden_t = s.sb("hidden_t", [128, ring, 128])
        out = s.sb("out", [128, ring, FEAT])
        gathered = [s.sem(f"gathered{g}") for g in range(4)]
        rows_here = s.sem("rows_here")
        rows_turned, rows_kept, hidden_ready, hidden_kept, hidden_turned, hidden_t_kept, out_ready, out_kept, ones_ready = (
            s.sem(n) for n in "rows_turned rows_kept hidden_ready hidden_kept hidden_turned hidden_t_kept out_ready out_kept ones_ready".split())
        stored = [s.sem(f"stored{g}") for g in range(2)]
        w1, w2 = r["w1"], r["w2"]
        table = r["table"].rearrange("(t l) f -> l t f", l=128)
        with nc.Block() as block:

            @block.gpsimd
            def _(pool):
                for n in range(TABLE_TILES):
                    if n >= 2 * ring:
                        pool.wait_ge(rows_turned, (n - 2 * ring) // group + 1)
                    pool.indirect_dma_start(out=rows_in[:, n // ring % 2, n % ring, :], out_offset=None, in_=r["tokens"],
                                            in_offset=bass.IndirectOffsetOnAxis(ap=r["source"][:, n:n + 1], axis=0)).then_inc(gathered[n // group % 4], 16)

            @block.tensor
            def _(pe):

                def turn_rows(i, place):
                    for g in range(2):
                        pe.wait_ge(gathered[2 * place + g], (i - place) * (16 * group // 2) + 16 * group)
                        pe.sem_inc(rows_here, 1)
                        for k in range(group):
                            mm = pe.transpose(ps[g][0:FEAT, 128 * k:128 * k + 128], rows_in[:, place, group * g + k, :], w["ident"])
                        mm.then_inc(rows_turned, 1)

                def experts_of(i, step):
                    registers = [pe.alloc_register(f"{step}_expert{k}") for k in range(ring)]
                    pe.load(registers, r["expert"][0:1, bass.ds(i * ring, ring)])
                    return registers, [bass.RuntimeValue.of_register_unchecked(reg, min_val=0, max_val=EXPERTS - 1) for reg in registers]

                def first_product(i, step):
                    registers, expert = experts_of(i, step)
                    for g in range(2):
                        pe.wait_ge(rows_kept, i * 2 + (g + 1))
                        for k in range(group):
                            mm = pe.matmul(ps[2 + g][:, 128 * k:128 * k + 128], rows_t[:, group * g + k, :], w1[:, bass.ds(expert[group * g + k] * 128, 128)], start=True, stop=True)
                        mm.then_inc(hidden_ready, 1)
                    for reg in registers:
                        pe.free_register(reg)

                def turn_hidden(i):
                    for g in range(2):
                        pe.wait_ge(hidden_kept, i * 2 + (g + 1))
                        for k in range(group):
                            mm = pe.transpose(ps[4 + g][:, 128 * k:128 * k + 128], hidden[:, group * g + k, :], w["ident"])
                        mm.then_inc(hidden_turned, 1)

                def second_product(i, step):
                    registers, expert = experts_of(i, step)
                    for g in range(2):
                        pe.wait_ge(hidden_t_kept, i * 2 + (g + 1))
                        pe.wait_ge(out_kept, i * 2 + (g + 1))
                        for k in range(group):
                            mm = pe.matmul(ps[6 + g][:, FEAT * k:FEAT * k + FEAT], hidden_t[:, group * g + k, :], w2[:, bass.ds(expert[group * g + k] * FEAT, FEAT)], start=True, stop=True)
                        mm.then_inc(out_ready, 1)
                    for reg in registers:
                        pe.free_register(reg)

                def round_(i, place, step):
                    turn_rows(i, place)
                    turn_hidden(i - 1)
                    first_product(i, f"{step}_first")
                    second_product(i - 1, f"{step}_second")

                pe.wait_ge(experts_in, 32)
                pe.wait_ge(ones_ready, 1)
                turn_rows(0, 0)
                first_product(0, "start_first")
                with pe.Fori(0, rounds // 2 - 1) as m:
                    round_(m * 2 + 1, 1, "odd")
                    round_(m * 2 + 2, 0, "even")
                round_(rounds - 1, 1, "last")
                turn_hidden(rounds - 1)
                second_product(rounds - 1, "end_second")

            @block.vector
            def _(dve):
                dve.memset(rows_t[FEAT:FEAT + 1], 1.0).then_inc(ones_ready, 1)

                def keep_rows(i):
                    for g in range(2):
                        dve.wait_ge(rows_turned, i * 2 + (g + 1))
                        dve.tensor_copy(rows_t[0:FEAT, group * g:group * g + group, :], ps[g][0:FEAT, :].rearrange("p (k n) -> p k n", k=group)).then_inc(rows_kept, 1)

                def keep_hidden(i):
                    for g in range(2):
                        dve.wait_ge(hidden_turned, i * 2 + (g + 1))
                        dve.tensor_copy(hidden_t[:, group * g:group * g + group, :], ps[4 + g][:].rearrange("p (k n) -> p k n", k=group)).then_inc(hidden_t_kept, 1)

                keep_rows(0)
                with dve.Fori(1, rounds) as i:
                    keep_rows(i)
                    keep_hidden(i - 1)
                keep_hidden(rounds - 1)

            @block.scalar
            def _(act):

                def relu(i):
                    for g in range(2):
                        act.wait_ge(hidden_ready, i * 2 + (g + 1))
                        act.activation(hidden[:, group * g:group * g + group, :], ps[2 + g][:].rearrange("p (k n) -> p k n", k=group), ACT.Relu).then_inc(hidden_kept, 1)

                def keep_out(i):
                    for g in range(2):
                        act.wait_ge(out_ready, i * 2 + (g + 1))
                        act.wait_ge(stored[g], i * 16 + 16)
                        act.activation(out[:, group * g:group * g + group, :], ps[6 + g][:, 0:group * FEAT].rearrange("p (k n) -> p k n", k=group), ACT.Copy).then_inc(out_kept, 1)

                act.sem_inc(out_kept, 2)
                relu(0)
                with act.Fori(1, rounds) as i:
                    relu(i)
                    keep_out(i - 1)
                keep_out(rounds - 1)

            @block.sync
            def _(sp):
                for g in range(2):
                    sp.sem_inc(stored[g], 16)
                with sp.Fori(0, rounds) as i:
                    for g in range(2):
                        sp.wait_ge(out_kept, i * 2 + (g + 3))
                        sp.dma_start(table[:, bass.ds(ring * i + group * g, group), :], out[:, group * g:group * g + group, :]).then_inc(stored[g], 16)
                for g in range(2):
                    sp.wait_ge(stored[g], 16 * (rounds) + 16)


def expert_sum(nc, h, w, ps, r):
    cols = 2 * TILES
    with Stage(nc, "sum") as s:
        rows_in = s.sb("rows_in", [TILE, cols, 2, FEAT])
        total = s.sb("total", [TILE, cols, FEAT])
        gathered = [s.sem(f"gathered{c}") for c in range(CHUNKS)]
        scaled, total_ready, out_ready, h_ready = s.sem("scaled"), s.sem("total_ready"), s.sem("out_ready"), s.sem("h_ready")
        with nc.Block() as block:

            @block.gpsimd
            def _(pool):
                for a in range(cols):
                    for k in range(2):
                        n = 2 * a + k
                        pool.indirect_dma_start(out=rows_in[:, a, k, :], out_offset=None, in_=r["table"],
                                                in_offset=bass.IndirectOffsetOnAxis(ap=r["slot"][:, n:n + 1].bitcast(U32), axis=0)).then_inc(gathered[a // 8], 16)

            @block.vector
            def _(dve):
                for c in range(CHUNKS):
                    mine = slice(8 * c, 8 * c + 8)
                    dve.wait_ge(gathered[c], 256)
                    for k in range(2):
                        dve.tensor_tensor(rows_in[:, mine, k], rows_in[:, mine, k], r["gates"][:, k, mine].unsqueeze(2).to_broadcast([TILE, 8, FEAT]), ALU.mult).then_inc(scaled, 1)
                    dve.wait_ge(scaled, 2 * c + 2)
                    dve.tensor_tensor(total[:, mine], rows_in[:, mine, 0], rows_in[:, mine, 1], ALU.add).then_inc(total_ready, 1)
                    dve.wait_ge(out_ready, c + 1)
                    dve.tensor_tensor(h[:, chunk(c)], h[:, chunk(c)], ps[c][:, :CHUNK], ALU.add).then_inc(h_ready, 1)
                dve.wait_ge(h_ready, CHUNKS)

            @block.tensor
            def _(pe):
                for c in range(CHUNKS):
                    pe.matmul(ps[c][:, :CHUNK], w["moe_b2"], r["combine_t"][:, chunk(c)], start=True, stop=False, skip_group_check=True)
                for c in range(CHUNKS):
                    pe.wait_ge(total_ready, c + 1)
                    for k in range(4):
                        j = 4 * c + k
                        mm = pe.matmul(ps[c][:, tile(k)], total[:, 2 * j:2 * j + 2].rearrange("p a f -> p (a f)"), w["ident"][0:TILE, 0:TILE],
                                       start=False, stop=(k == 3), skip_group_check=True)
                    mm.then_inc(out_ready, 1)


def expert_ffn(nc, h, x, w, ps, d):
    cols = 2 * TILES
    with Stage(nc, "moe") as s:
        r = {
            "tokens": d["tokens"], "table": d["table"],
            "w1": s.sb("w1", [FEAT + 1, EXPERTS * 128]), "w2": s.sb("w2", [128, EXPERTS * FEAT]),
            "source": s.sb("source", [128, TABLE_TILES], U32), "expert": s.sb("expert", [1, TABLE_TILES], I32),
            "slot": s.sb("slot", [TILE, cols * 2], I32), "gates": s.sb("gates", [TILE, 2, cols]),
            "combine_t": s.sb("combine_t", [128, COLS]),
        }
        experts_in = s.sem("experts_in")
        with nc.Block() as block:

            @block.sync
            def _(sp):
                sp.dma_start(r["w1"][:], d["experts1"]).then_inc(experts_in, 16)
                sp.dma_start(r["w2"][:], d["experts2"]).then_inc(experts_in, 16)

        expert_routing(nc, x, w, ps, r)
        expert_tables(nc, w, ps, r, experts_in)
        expert_sum(nc, h, w, ps, r)


def retention(nc, h, x, w, ps):
    wide = POS + TILE
    with Stage(nc, "ret") as s:
        query = s.sb("query", [128, COLS])
        key = s.sb("key", [128, COLS])
        turned = s.sb("turned", [128, 2, COLS])
        value = s.sb("value", [TILE, TILES, 128])
        kept = s.sb("kept", [TILE, 4, wide])
        (q_ready, q_scaled, rotated, value_ready, value_kept, score_ready, score_kept, out_ready, h_ready) = (
            s.sem(n) for n in "q_ready q_scaled rotated value_ready value_kept score_ready score_kept out_ready h_ready".split())
        with nc.Block() as block:

            @block.tensor
            def _(pe):
                for i, n in enumerate("qk"):
                    for c in range(CHUNKS):
                        if i:
                            pe.wait_ge(q_scaled, 2 * c + 2)
                        pe.matmul(ps[c][:, :CHUNK], w["ret_" + n], x[:, chunk(c)], start=True, stop=True)
                        pe.matmul(ps[4 + c][:, :CHUNK], w["ret_" + n + "s"], x[:, chunk(c)], start=True, stop=True).then_inc(q_ready, 1)
                for b in range(4):
                    pe.wait_ge(q_scaled, 8 + 2 * b + 2)
                    for k in range(4):
                        mm = pe.matmul(ps[b][0:TILE, 128 * k:128 * k + 128], x[:, tile(4 * b + k)], w["ret_v"], start=True, stop=True)
                    mm.then_inc(value_ready, 1)
                pe.wait_ge(rotated, 8)
                pe.wait_ge(value_kept, 4)

                def scores(q):
                    p, a = q // 2, q % 2
                    if q >= 4:
                        pe.wait_ge(score_kept, q - 3)
                    half = slice(64 * a, 64 * a + 64)
                    at = POS * p
                    pe.matmul(ps[4 + q % 4][0:TILE, 0:POS], key[half, tile(2 * p)], query[half, at:at + POS], start=True, stop=True)
                    pe.matmul(ps[4 + q % 4][0:TILE, POS:wide], key[half, tile(2 * p + 1)], query[half, at + TILE:at + POS], start=True, stop=True).then_inc(score_ready, 1)

                def outputs(q):
                    p, a = q // 2, q % 2
                    pe.wait_ge(score_kept, q + 1)
                    dst = ps[p // 2][64 * a:64 * a + 64, POS * (p % 2):POS * (p % 2) + POS]
                    pe.matmul(dst, value[:, 2 * p, 64 * a:64 * a + 64], kept[:, q % 4, 0:POS], start=True, stop=False)
                    pe.matmul(dst[:, TILE:], value[:, 2 * p + 1, 64 * a:64 * a + 64], kept[:, q % 4, POS:wide], start=False, stop=True).then_inc(out_ready, 1)

                for q in range(SEQS):
                    scores(q)
                    if q >= 2:
                        outputs(q - 2)
                outputs(SEQS - 2)
                outputs(SEQS - 1)

            @block.scalar
            def _(act):
                for b in range(4):
                    act.wait_ge(value_ready, b + 1)
                    act.activation(value[:, 4 * b:4 * b + 4], ps[b][0:TILE, :].rearrange("p (k f) -> p k f", k=4), ACT.Copy).then_inc(value_kept, 1)

            @block.vector
            def _(dve):
                for i, dst in enumerate((query, key)):
                    for c in range(CHUNKS):
                        dve.wait_ge(q_ready, 4 * i + c + 1)
                        if i:
                            dve.wait_ge(rotated, c + 1)
                        for k, src in enumerate((ps[c], ps[4 + c])):
                            table = w["ret_table"][:, POS * (2 * i + k):POS * (2 * i + k) + POS].unsqueeze(1).to_broadcast([128, 2, POS])
                            out = (dst if k == 0 else turned[:, 0])[:, chunk(c)].rearrange("p (b n) -> p b n", b=2)
                            dve.tensor_tensor(out, src[:, :CHUNK].rearrange("p (b n) -> p b n", b=2), table, ALU.mult).then_inc(q_scaled, 1)
                for q in range(SEQS):
                    dve.wait_ge(score_ready, q + 1)
                    if q >= 4:
                        dve.wait_ge(out_ready, q - 3)
                    dve.tensor_tensor(kept[:, q % 4], ps[4 + q % 4][0:TILE, 0:wide], w["ret_decay"][0:TILE, :], ALU.mult).then_inc(score_kept, 1)
                for c in range(CHUNKS):
                    dve.wait_ge(out_ready, 4 * c + 4)
                    dve.tensor_tensor(h[:, chunk(c)], h[:, chunk(c)], ps[c][:, :CHUNK], ALU.add).then_inc(h_ready, 1)
                dve.wait_ge(h_ready, CHUNKS)

            @block.gpsimd
            def _(pool):
                for i, dst in enumerate((query, key)):
                    for c in range(CHUNKS):
                        pool.wait_ge(q_scaled, 2 * (4 * i + c) + 2)
                        pool.tensor_tensor(dst[:, chunk(c)], dst[:, chunk(c)], turned[:, 0, chunk(c)], ALU.add).then_inc(rotated, 1)


def soft_mixture(nc, h, x, w, ps):
    experts = 8
    with Stage(nc, "mixture") as s:
        feat = s.sb("feat", [128, POS])
        gate = s.sb("gate", [TILE, 2, experts])
        gate_tmp = s.sb("gate_tmp", [TILE, 2, experts])
        top = s.sb("top", [TILE, 2])
        total = s.sb("total", [TILE, 2])
        inverse = s.sb("inverse", [TILE, 2])
        gate_f = s.sb("gate_f", [128, experts, POS])
        gate_t = s.sb("gate_t", [experts, POS])
        bias = s.sb("bias", [128, POS])
        root = s.sb("root", [128, 2, experts])
        scale = s.sb("scale", [128, 2, experts])
        shift = s.sb("shift", [128, 2, experts])
        hidden = s.sb("hidden", [128, 2, 4, CHUNK])
        (feat_ready, logits_ready, gate_steps, exp_ready, gate_spread, gate_kept, gate_turned, gate_t_kept, bias_ready, bias_kept,
         root_ready, scale_steps, up_ready, up_kept, mid_ready, mid_kept, gated, out_ready, h_ready) = (s.sem(n) for n in (
             "feat_ready logits_ready gate_steps exp_ready gate_spread gate_kept gate_turned gate_t_kept bias_ready bias_kept "
             "root_ready scale_steps up_ready up_kept mid_ready mid_kept gated out_ready h_ready").split())
        steps = experts * CHUNKS

        def norm(name, layer):
            at = experts * (2 * "g b m v e".split().index(name) + layer)
            return w["bn"][:, at:at + experts]

        with nc.Block() as block:

            @block.tensor
            def _(pe):
                pe.wait_ge(feat_ready, 1)
                for t in range(2):
                    mm = pe.matmul(ps[0][0:TILE, 8 * t:8 * t + 8], feat[:, tile(t)], w["soft_r"], start=True, stop=True)
                mm.then_inc(logits_ready, 1)
                pe.wait_ge(gate_steps, 6)
                for b in range(4):
                    for k in range(4):
                        mm = pe.transpose(ps[4 + b][:, tile(k)], gate[:, k % 2, 2 * b + k // 2].unsqueeze(1).to_broadcast([TILE, 128]), w["ident"][0:TILE, 0:TILE])
                    mm.then_inc(gate_spread, 1)
                for t in range(2):
                    mm = pe.transpose(ps[1][0:experts, tile(t)], gate[:, t], w["ident"][0:TILE, 0:TILE])
                mm.then_inc(gate_turned, 1)
                pe.wait_ge(gate_t_kept, 1)
                pe.matmul(ps[2][:, 0:POS], w["soft_bo"][0:experts, :], gate_t[:], start=True, stop=True).then_inc(bias_ready, 1)
                pe.wait_ge(gate_kept, 4)
                pe.wait_ge(bias_kept, 1)

                def first(n):
                    if n >= 2:
                        pe.wait_ge(up_kept, n - 1)
                    pe.matmul(ps[4 + n % 2][:, :CHUNK], w["soft_1"][:, 128 * (n // 4):128 * (n // 4) + 128], x[:, chunk(n % 4)], start=True, stop=True).then_inc(up_ready, 1)

                def second(n):
                    pe.wait_ge(up_kept, n + 1)
                    if n >= 2:
                        pe.wait_ge(mid_kept, n - 1)
                    pe.matmul(ps[6 + n % 2][:, :CHUNK], w["soft_2"][:, 128 * (n // 4):128 * (n // 4) + 128], hidden[:, 0, n % 4], start=True, stop=True).then_inc(mid_ready, 1)

                def third(n):
                    pe.wait_ge(gated, n + 1)
                    pe.matmul(ps[n % 4][:, :CHUNK], w["soft_3"][:, 128 * (n // 4):128 * (n // 4) + 128], hidden[:, 1, n % 4],
                              start=(n < 4), stop=(n >= steps - 4)).then_inc(out_ready, 1)

                for n in range(steps + 3):
                    if n < steps:
                        first(n)
                    if 1 <= n <= steps:
                        second(n - 1)
                    if n >= 3:
                        third(n - 3)

            @block.scalar
            def _(act):
                for layer in range(2):
                    act.activation(root[:, layer], norm("v", layer), ACT.Sqrt, bias=w["bn_eps"]).then_inc(root_ready, 1)
                act.wait_ge(gate_steps, 3)
                act.activation(gate_tmp[:], gate_tmp[:], ACT.Exp).then_inc(exp_ready, 1)
                for b in range(4):
                    act.wait_ge(gate_spread, b + 1)
                    act.activation(gate_f[:, 2 * b:2 * b + 2].rearrange("p e n -> p (e n)"), ps[4 + b][:, :CHUNK], ACT.Copy).then_inc(gate_kept, 1)
                act.wait_ge(gate_turned, 1)
                act.activation(gate_t[:], ps[1][0:experts, 0:POS], ACT.Copy).then_inc(gate_t_kept, 1)
                act.wait_ge(bias_ready, 1)
                act.activation(bias[:], ps[2][:, 0:POS], ACT.Copy).then_inc(bias_kept, 1)
                act.wait_ge(scale_steps, 8)

                def first(n):
                    e = n // 4
                    act.wait_ge(up_ready, n + 1)
                    if n >= 4:
                        act.wait_ge(mid_ready, n - 3)
                    act.activation(hidden[:, 0, n % 4], ps[4 + n % 2][:, :CHUNK], ACT.Relu, bias=shift[:, 0, e:e + 1], scale=scale[:, 0, e:e + 1]).then_inc(up_kept, 1)

                def second(n):
                    e = n // 4
                    act.wait_ge(mid_ready, n + 1)
                    if n >= 4:
                        act.wait_ge(out_ready, n - 3)
                    act.activation(hidden[:, 1, n % 4], ps[6 + n % 2][:, :CHUNK], ACT.Relu, bias=shift[:, 1, e:e + 1], scale=scale[:, 1, e:e + 1]).then_inc(mid_kept, 1)

                for n in range(steps + 1):
                    if n < steps:
                        first(n)
                    if n >= 1:
                        second(n - 1)

            @block.vector
            def _(dve):
                dve.tensor_reduce(feat[:], x[:].rearrange("q (p n) -> q n p", n=POS), AX.X, ALU.add).then_inc(feat_ready, 1)
                dve.wait_ge(root_ready, 2)
                dve.reciprocal(scale[:], root[:]).then_inc(scale_steps, 1)
                dve.wait_ge(scale_steps, 1)
                for layer in range(2):
                    dve.tensor_tensor(root[:, layer], scale[:, layer], norm("g", layer), ALU.mult).then_inc(scale_steps, 1)
                    dve.tensor_tensor(shift[:, layer], norm("b", layer), norm("m", layer), ALU.subtract).then_inc(scale_steps, 1)
                dve.wait_ge(scale_steps, 5)
                dve.tensor_tensor(shift[:], shift[:], root[:], ALU.mult).then_inc(scale_steps, 1)
                dve.tensor_copy(scale[:], root[:]).then_inc(scale_steps, 1)
                dve.wait_ge(scale_steps, 7)
                dve.tensor_tensor(shift[:], shift[:], w["bn"][:, 8 * experts:10 * experts].rearrange("p (l e) -> p l e", l=2), ALU.add).then_inc(scale_steps, 1)
                dve.wait_ge(logits_ready, 1)
                dve.scalar_tensor_tensor(gate[:], ps[0][0:TILE, 0:16].rearrange("p (t e) -> p t e", t=2), 1.0 / SEQS,
                                         w["soft_br"][0:TILE, :].unsqueeze(1).to_broadcast([TILE, 2, experts]), ALU.mult, ALU.add).then_inc(gate_steps, 1)
                dve.wait_ge(gate_steps, 1)
                dve.tensor_reduce(top[:], gate[:], AX.X, ALU.max).then_inc(gate_steps, 1)
                dve.wait_ge(gate_steps, 2)
                dve.tensor_tensor(gate_tmp[:], gate[:], top[:].unsqueeze(2).to_broadcast([TILE, 2, experts]), ALU.subtract).then_inc(gate_steps, 1)
                dve.wait_ge(exp_ready, 1)
                dve.tensor_reduce(total[:], gate_tmp[:], AX.X, ALU.add).then_inc(gate_steps, 1)
                dve.wait_ge(gate_steps, 4)
                dve.reciprocal(inverse[:], total[:]).then_inc(gate_steps, 1)
                dve.wait_ge(gate_steps, 5)
                dve.tensor_tensor(gate[:], gate_tmp[:], inverse[:].unsqueeze(2).to_broadcast([TILE, 2, experts]), ALU.mult).then_inc(gate_steps, 1)
                dve.wait_ge(gate_kept, 4)
                for n in range(steps):
                    dve.wait_ge(mid_kept, n + 1)
                    hid = hidden[:, 1, n % 4].rearrange("p (b n) -> p b n", b=2)
                    dve.tensor_tensor(hid, hid, gate_f[:, n // 4].unsqueeze(1).to_broadcast([128, 2, POS]), ALU.mult).then_inc(gated, 1)
                dve.wait_ge(bias_kept, 1)
                for c in range(CHUNKS):
                    dve.wait_ge(out_ready, steps - 3 + c)
                    dve.tensor_tensor(h[:, chunk(c)], h[:, chunk(c)], ps[c][:, :CHUNK], ALU.add).then_inc(h_ready, 1)
                dve.wait_ge(h_ready, CHUNKS)
                dve.tensor_tensor(h[:].rearrange("p (b n) -> p b n", n=POS), h[:].rearrange("p (b n) -> p b n", n=POS),
                                  bias[:].unsqueeze(1).to_broadcast([128, PAIRS, POS]), ALU.add).then_inc(h_ready, 1)
                dve.wait_ge(h_ready, CHUNKS + 1)


def relative_attention(nc, h, x, w, ps):
    heads, hd, reach, near = 4, 16, 30, TILE + 29
    first_near = [0, POS - near]
    with Stage(nc, "rel") as s:
        xg = s.sb("xg", [128, COLS])
        query_u = s.sb("query_u", [128, 2, COLS])
        query_v = s.sb("query_v", [128, COLS])
        key = s.sb("key", [128, COLS])
        value = s.sb("value", [TILE, TILES, 2 * heads, 2 * hd])
        turn_a = s.sb("turn_a", [128, heads, COLS])
        turn_b = s.sb("turn_b", [128, 2, CHUNK])
        bias_u = s.sb("bias_u", [128, 2])
        bias_v = s.sb("bias_v", [128, 1])
        edge_w = s.sb("edge_w", [128, 3])
        edge_wide = s.sb("edge_wide", [128, 3, 8])
        edge = s.sb("edge", [TILE, TILES, 3, 8])
        shift = s.sb("shift", [TILE, TILES, 8])
        right = s.sb("right", [TILE, TILES, 8])
        near_b = [s.sb(f"near{t}", [TILE, 2, heads, POS]) for t in range(2)]
        scores = s.sb("scores", [TILE, 3, heads, POS])
        top = s.sb("top", [TILE, 3, heads])
        total = s.sb("total", [TILE, 3, heads])
        inverse = s.sb("inverse", [TILE, 3, heads])
        probs_t = s.sb("probs_t", [TILE, 2, 2, 4 * TILE])
        mixed = s.sb("mixed", [128, 2, COLS])
        (x_ready, biases, bias_turned, edge_w_ready, edge_steps, q_ready, q_kept, k_ready, k_kept, v_ready, v_kept, edge_ready,
         edge_kept, edge_done, turn_ready, turn_scaled, turned, zeroed, value_zeroed) = (s.sem(n) for n in (
             "x_ready biases bias_turned edge_w_ready edge_steps q_ready q_kept k_ready k_kept v_ready v_kept edge_ready "
             "edge_kept edge_done turn_ready turn_scaled turned zeroed value_zeroed").split())
        (dot_ready, near_ready, near_kept, far_added, score_kept, top_ready, exp_ready, prob_ready, prob_turned, prob_kept,
         mixed_ready, inverse_ready, mixed_kept, out_ready, h_ready) = (s.sem(n) for n in (
             "dot_ready near_ready near_kept far_added score_kept top_ready exp_ready prob_ready prob_turned prob_kept "
             "mixed_ready inverse_ready mixed_kept out_ready h_ready").split())
        with nc.Block() as block:

            @block.tensor
            def _(pe):
                pe.matmul(ps[7][:, 0:2], w["rel_pos_t"], w["rel_ends"], start=True, stop=True).then_inc(edge_w_ready, 1)
                pe.wait_ge(x_ready, CHUNKS)
                for c in range(CHUNKS):
                    pe.matmul(ps[c][:, :CHUNK], w["rel_q"], xg[:, chunk(c)], start=True, stop=True).then_inc(q_ready, 1)
                for c in range(CHUNKS):
                    if c == 3:
                        pe.wait_ge(edge_steps, 1)
                    pe.matmul(ps[4 + c][:, :CHUNK], w["rel_k"], xg[:, chunk(c)], start=True, stop=True).then_inc(k_ready, 1)
                for b in range(4):
                    pe.wait_ge(k_kept, b + 1)
                    for k in range(4):
                        mm = pe.matmul(ps[4 + b][0:TILE, 128 * k:128 * k + 128], xg[:, tile(4 * b + k)], w["rel_v"], start=True, stop=True)
                    mm.then_inc(v_ready, 1)
                pe.wait_ge(q_kept, 3 * CHUNKS)
                pe.wait_ge(edge_steps, 5)
                for j in range(TILES):
                    mm = pe.matmul(ps[0][0:TILE, 24 * j:24 * j + 24], query_v[:, tile(j)], edge_wide[:].rearrange("p i e -> p (i e)"), start=True, stop=True)
                mm.then_inc(edge_ready, 1)
                pe.wait_ge(v_kept, 4)
                for n in range(heads * CHUNKS):
                    hh, c = n // CHUNKS, n % CHUNKS
                    if n >= 3:
                        pe.wait_ge(turn_scaled, 2 * (n - 3) + 2)
                    pe.matmul(ps[1 + 2 * (n % 3)][:, :CHUNK], w["rel_pos"][:, 128 * hh:128 * hh + 128], query_v[:, chunk(c)], start=True, stop=True)
                    pe.matmul(ps[2 + 2 * (n % 3)][:, :CHUNK], w["rel_pos_s"][:, 128 * hh:128 * hh + 128], query_v[:, chunk(c)], start=True, stop=True).then_inc(turn_ready, 1)

            @block.scalar
            def _(act):
                for c in range(CHUNKS):
                    act.activation(xg[:, chunk(c)], x[:, chunk(c)], ACT.Identity, scale=w["rel_gamma"], bias=w["rel_beta"]).then_inc(x_ready, 1)
                act.wait_ge(biases, 3)
                for c in range(CHUNKS):
                    act.wait_ge(q_ready, c + 1)
                    for k in range(2):
                        act.activation(query_u[:, k, chunk(c)], ps[c][:, :CHUNK], ACT.Identity, scale=w["rel_parity"][:, k:k + 1], bias=bias_u[:, k:k + 1]).then_inc(q_kept, 1)
                    act.activation(query_v[:, chunk(c)], ps[c][:, :CHUNK], ACT.Identity, scale=float(hd) ** -0.5, bias=bias_v[:]).then_inc(q_kept, 1)

            @block.vector
            def _(dve):
                dve.tensor_scalar(bias_u[:], w["rel_parity"], w["rel_qu"][:, 0:1], None, ALU.mult).then_inc(biases, 1)
                dve.wait_ge(biases, 1)
                dve.scalar_tensor_tensor(bias_u[:], w["rel_parity"], w["rel_qu"][:, 1:2], bias_u[:], ALU.mult, ALU.add).then_inc(biases, 1)
                dve.tensor_scalar(bias_v[:], w["rel_qu"][:, 0:1], w["rel_qu"][:, 2:3], float(hd) ** -0.5, ALU.add, ALU.mult).then_inc(biases, 1)
                dve.wait_ge(edge_w_ready, 1)
                dve.tensor_tensor(edge_w[:, 0:2], ps[7][:, 0:2], w["rel_posb"].to_broadcast([128, 2]), ALU.add).then_inc(edge_steps, 1)
                dve.tensor_copy(edge_w[:, 2:3], w["rel_posb"]).then_inc(edge_steps, 1)
                dve.wait_ge(edge_steps, 2)
                for i in range(3):
                    dve.tensor_scalar(edge_wide[:, i], w["rel_head8"], edge_w[:, i:i + 1], None, ALU.mult).then_inc(edge_steps, 1)
                for c in range(CHUNKS):
                    dve.wait_ge(k_ready, c + 1)
                    dve.tensor_scalar(key[:, chunk(c)], ps[4 + c][:, :CHUNK], w["rel_kb"], None, ALU.add).then_inc(k_kept, 1)
                for b in range(4):
                    dve.wait_ge(v_ready, b + 1)
                    if b == 0:
                        dve.wait_ge(value_zeroed, 1)
                    dve.tensor_tensor(value[:, 4 * b:4 * b + 4, :, 0:hd], ps[4 + b][0:TILE, :].rearrange("p (k g e) -> p k g e", k=4, e=hd),
                                      w["rel_vb"][0:TILE, :].rearrange("p (g e) -> p g e", e=hd).unsqueeze(1).to_broadcast([TILE, 4, 2 * heads, hd]), ALU.add).then_inc(v_kept, 1)
                dve.wait_ge(edge_ready, 1)
                dve.tensor_copy(edge[:].rearrange("p j i e -> p (j i e)"), ps[0][0:TILE, 0:24 * TILES]).then_inc(edge_kept, 1)
                dve.wait_ge(edge_kept, 1)
                dve.tensor_tensor(right[:], edge[:, :, 1], edge[:, :, 0], ALU.subtract).then_inc(edge_done, 1)
                dve.tensor_tensor(shift[:], edge[:, :, 0], edge[:, :, 2], ALU.subtract).then_inc(edge_done, 1)
                for n in range(heads * CHUNKS):
                    hh, c = n // CHUNKS, n % CHUNKS
                    dve.wait_ge(turn_ready, n + 1)
                    if n >= 2:
                        dve.wait_ge(turned, n - 1)
                    for k in range(2):
                        table = w["rel_t"][:, POS * k:POS * k + POS].unsqueeze(1).to_broadcast([128, 2, POS])
                        out = turn_a[:, hh, chunk(c)] if k == 0 else turn_b[:, n % 2]
                        dve.tensor_tensor(out.rearrange("p (b n) -> p b n", b=2), ps[1 + k + 2 * (n % 3)][:, :CHUNK].rearrange("p (b n) -> p b n", b=2),
                                          table, ALU.mult).then_inc(turn_scaled, 1)
                dve.wait_ge(edge_done, 2)

            @block.gpsimd
            def _(pool):
                pool.memset(value[:], 0.0).then_inc(value_zeroed, 1)
                for t in range(2):
                    pool.memset(near_b[t][:], 0.0).then_inc(zeroed, 1)
                for n in range(heads * CHUNKS):
                    hh, c = n // CHUNKS, n % CHUNKS
                    pool.wait_ge(turn_scaled, 2 * n + 2)
                    pool.tensor_tensor(turn_a[:, hh, chunk(c)], turn_a[:, hh, chunk(c)], turn_b[:, n % 2], ALU.add).then_inc(turned, 1)
                pool.wait_ge(zeroed, 2)

        units = 2 * SEQS
        unit = [(u // 4, u % 2, (u // 2) % 2) for u in range(units)]
        with nc.Block() as block:

            @block.tensor
            def _(pe):

                def dots(u):
                    p, a, t = unit[u]
                    half = slice(64 * a, 64 * a + 64)
                    for hh in range(heads):
                        if u and hh % 2 == 0:
                            pe.wait_ge(near_kept, heads * (u - 1) + hh + 2)
                        pe.matmul(ps[2 + hh // 2][0:TILE, near * (hh % 2):near * (hh % 2) + near], turn_a[half, hh, tile(2 * p + t)],
                                  w["rel_s"][half, first_near[t]:first_near[t] + near], start=True, stop=True).then_inc(near_ready, 1)
                    for n, hh in enumerate((0, 2, 1, 3)):
                        if u and n < 2:
                            pe.wait_ge(far_added, heads * (u - 1) + 2 * n + 2)
                        rows_ = slice(64 * a + 32 * (hh // 2), 64 * a + 32 * (hh // 2) + 32)
                        pe.matmul(ps[hh // 2][0:TILE, POS * (hh % 2):POS * (hh % 2) + POS], query_u[rows_, hh % 2, tile(2 * p + t)],
                                  key[rows_, POS * p:POS * p + POS], start=True, stop=True, tile_position=(rows_.start, 0)).then_inc(dot_ready, 1)

                def turn_probs(u):
                    pe.wait_ge(prob_ready, u + 1)
                    for b in range(2):
                        if u:
                            pe.wait_ge(prob_kept, 2 * (u - 1) + b + 1)
                        for k in range(4):
                            mm = pe.transpose(ps[4 + b][0:TILE, tile(k)], scores[:, u % 3, 2 * b + k // 2, tile(k % 2)], w["ident"][0:TILE, 0:TILE])
                        mm.then_inc(prob_turned, 1)

                def mix(u):
                    p, a, t = unit[u]
                    if u >= 2:
                        pe.wait_ge(mixed_kept, u - 1)
                    pe.wait_ge(prob_kept, 2 * u + 2)
                    for k in range(2):
                        for hh in range(heads):
                            mm = pe.matmul(ps[6 + u % 2][32 * hh:32 * hh + 32, 0:TILE], value[:, 2 * p + k, 4 * a + hh], probs_t[:, u % 2, hh // 2, tile(2 * (hh % 2) + k)],
                                           start=(k == 0), stop=(k == 1), tile_position=(0, 32 * hh))
                    mm.then_inc(mixed_ready, 1)

                for n in range(units + 3):
                    if n < units:
                        dots(n)
                    if 2 <= n < units + 2:
                        turn_probs(n - 2)
                    if n >= 3:
                        mix(n - 3)
                pe.wait_ge(mixed_kept, units)
                for c in range(CHUNKS):
                    for a in range(2):
                        mm = pe.matmul(ps[c][64 * a:64 * a + 64, :CHUNK], w["rel_o"], mixed[:, a, chunk(c)], start=True, stop=True, tile_position=(0, 64 * a))
                    mm.then_inc(out_ready, 1)

            @block.scalar
            def _(act):

                def exps(u):
                    act.wait_ge(top_ready, u + 1)
                    if u >= 3:
                        act.wait_ge(inverse_ready, u - 2)
                    for hh in range(heads):
                        row = scores[:, u % 3, hh]
                        act.activation(row, row, ACT.Exp, bias=top[:, u % 3, hh:hh + 1], accum_out=total[:, u % 3, hh:hh + 1]).then_inc(exp_ready, 1)

                def keep_probs(u):
                    for b in range(2):
                        act.wait_ge(prob_turned, 2 * u + b + 1)
                        if u >= 2 and b == 0:
                            act.wait_ge(mixed_ready, u - 1)
                        act.activation(probs_t[:, u % 2, b], ps[4 + b][0:TILE, :CHUNK], ACT.Copy).then_inc(prob_kept, 1)

                def keep_mixed(u):
                    p, a, t = unit[u]
                    act.wait_ge(mixed_ready, u + 1)
                    act.activation(mixed[:, a, tile(2 * p + t)], ps[6 + u % 2][:, 0:TILE], ACT.Copy).then_inc(mixed_kept, 1)

                for n in range(units + 4):
                    if 2 <= n < units + 2:
                        keep_probs(n - 2)
                    if n >= 4:
                        keep_mixed(n - 4)
                    if n < units:
                        exps(n)

            @block.vector
            def _(dve):

                def keep_scores(u):
                    p, a, t = unit[u]
                    j, at = 2 * p + t, first_near[t]
                    if u >= 4:
                        dve.wait_ge(score_kept, u - 3)
                    for hh in range(heads):
                        if hh % 2 == 0:
                            dve.wait_ge(near_ready, heads * u + hh + 2)
                        dve.scalar_tensor_tensor(near_b[t][:, (u // 4) % 2, hh, at:at + near], ps[2 + hh // 2][0:TILE, near * (hh % 2):near * (hh % 2) + near],
                                                 shift[:, j, 4 * a + hh:4 * a + hh + 1], w["rel_near"][0:TILE, near * t:near * t + near],
                                                 ALU.subtract, ALU.mult).then_inc(near_kept, 1)
                    if u >= 3:
                        dve.wait_ge(prob_turned, 2 * (u - 2))
                    for hh in range(heads):
                        if hh % 2 == 0:
                            dve.wait_ge(dot_ready, heads * u + 3 + hh // 2)
                        dve.scalar_tensor_tensor(scores[:, u % 3, hh], w["rel_right"][0:TILE, POS * t:POS * t + POS], right[:, j, 4 * a + hh:4 * a + hh + 1],
                                                 ps[hh // 2][0:TILE, POS * (hh % 2):POS * (hh % 2) + POS], ALU.mult, ALU.add).then_inc(far_added, 1)

                def finish_scores(u):
                    t = unit[u][2]
                    dve.wait_ge(near_kept, heads * (u + 1))
                    dve.wait_ge(far_added, heads * (u + 1))
                    dve.tensor_tensor(scores[:, u % 3], scores[:, u % 3], near_b[t][:, (u // 4) % 2], ALU.add).then_inc(score_kept, 1)
                    dve.wait_ge(score_kept, u + 1)
                    if u >= 3:
                        dve.wait_ge(exp_ready, heads * (u - 2))
                    dve.tensor_reduce(top[:, u % 3], scores[:, u % 3], AX.X, ALU.max, negate=True).then_inc(top_ready, 1)

                def invert(u):
                    dve.wait_ge(exp_ready, heads * (u + 1))
                    if u >= 3:
                        dve.wait_ge(prob_ready, u - 2)
                    dve.reciprocal(inverse[:, u % 3], total[:, u % 3]).then_inc(inverse_ready, 1)

                for n in range(units + 1):
                    if n < units:
                        keep_scores(n)
                    if n >= 1:
                        invert(n - 1)
                    if n < units:
                        finish_scores(n)
                for c in range(CHUNKS):
                    dve.wait_ge(out_ready, c + 1)
                    dve.scalar_tensor_tensor(h[:, chunk(c)], ps[c][:, :CHUNK], w["rel_ob"], h[:, chunk(c)], ALU.add, ALU.add).then_inc(h_ready, 1)
                dve.wait_ge(h_ready, CHUNKS)

            @block.gpsimd
            def _(pool):
                for u in range(units):
                    pool.wait_ge(inverse_ready, u + 1)
                    pool.tensor_tensor(scores[:, u % 3], scores[:, u % 3], inverse[:, u % 3].unsqueeze(2).to_broadcast([TILE, heads, POS]), ALU.mult).then_inc(prob_ready, 1)


def best_expert_ffn(nc, h, x, w, ps, out_dram):
    experts, blocks = 8, 2
    cols = 2 * TILES
    with Stage(nc, "top1") as s:
        hidden = s.sb("hidden", [128, blocks, 2, COLS])
        prob = s.sb("prob", [TILE, cols, experts])
        part = s.sb("part", [TILE, cols, experts])
        best = s.sb("best", [TILE, cols])
        total = s.sb("total", [TILE, cols])
        inverse = s.sb("inverse", [TILE, cols])
        gate_t = s.sb("gate_t", [experts, cols, TILE])
        scaled = s.sb("scaled", [TILE, 4, experts, FEAT])
        summed = s.sb("summed", [TILE, 2, FEAT])
        final = s.sb("final", [TILE, cols, FEAT])
        (up_ready, up_kept, logits_ready, steps, exp_ready, gate_turned, gate_kept, y_ready, y_scaled, rest_ready, y_summed,
         final_ready, stored) = (s.sem(n) for n in (
             "up_ready up_kept logits_ready steps exp_ready gate_turned gate_kept y_ready y_scaled rest_ready y_summed final_ready stored").split())
        with nc.Block() as block:

            @block.tensor
            def _(pe):
                for n in range(16):
                    c, m, a = n // 4, (n // 2) % 2, n % 2
                    if n >= 8:
                        pe.wait_ge(up_kept, n - 7)
                    half = slice(64 * a, 64 * a + 64)
                    pe.matmul(ps[n % 8][:, :CHUNK], w["top_1"][half, 128 * m:128 * m + 128], x[half, chunk(c)], start=True, stop=True).then_inc(up_ready, 1)
                pe.wait_ge(up_kept, 16)
                for col in range(cols):
                    j, a = col // 2, col % 2
                    for m in range(blocks):
                        mm = pe.matmul(ps[0][0:TILE, 8 * col:8 * col + 8], hidden[:, m, a, tile(j)], w["top_g"][:, 8 * m:8 * m + 8], start=(m == 0), stop=(m == 1))
                mm.then_inc(logits_ready, 1)

                def experts_of(n):
                    if n >= 4:
                        pe.wait_ge(y_scaled, n - 3)
                    for m in range(blocks):
                        mm = pe.matmul(ps[4 + n % 4][0:TILE, :], hidden[:, m, n % 2, tile(n // 2)], w["top_d"][:, 512 * m:512 * m + 512], start=(m == 0), stop=(m == 1))
                    mm.then_inc(y_ready, 1)

                for n in range(4):
                    experts_of(n)
                pe.wait_ge(steps, 10)
                for b in range(8):
                    if b >= 4:
                        pe.wait_ge(gate_kept, b - 3)
                    for k in range(4):
                        mm = pe.transpose(ps[b % 4][0:experts, tile(k)], prob[:, 4 * b + k], w["ident"][0:TILE, 0:TILE])
                    mm.then_inc(gate_turned, 1)
                pe.wait_ge(gate_kept, 8)
                for n in range(cols):
                    if n >= 4:
                        experts_of(n)
                        pe.wait_ge(final_ready, n - 3)
                    pe.matmul(ps[n % 4][0:TILE, 0:FEAT], gate_t[:, n], w["top_bd"][0:experts, :], start=True, stop=False)
                    pe.matmul(ps[n % 4][0:TILE, 0:FEAT], h[:, tile(n // 2)], w["ident"][:, 64 * (n % 2):64 * (n % 2) + 64], start=False, stop=True).then_inc(rest_ready, 1)

            @block.scalar
            def _(act):
                for n in range(16):
                    c, m, a = n // 4, (n // 2) % 2, n % 2
                    act.wait_ge(up_ready, n + 1)
                    act.activation(hidden[:, m, a, chunk(c)], ps[n % 8][:, :CHUNK], ACT.Gelu, bias=w["top_b1"][:, m:m + 1]).then_inc(up_kept, 1)
                act.wait_ge(steps, 3)
                act.activation(prob[:], prob[:], ACT.Exp).then_inc(exp_ready, 1)
                for b in range(8):
                    act.wait_ge(gate_turned, b + 1)
                    act.activation(gate_t[:, 4 * b:4 * b + 4], ps[b % 4][0:experts, :CHUNK].rearrange("p (k n) -> p k n", k=4), ACT.Copy).then_inc(gate_kept, 1)

            @block.vector
            def _(dve):
                wide = [TILE, cols, experts]
                dve.wait_ge(logits_ready, 1)
                dve.tensor_tensor(prob[:], ps[0][0:TILE, 0:8 * cols].rearrange("p (a e) -> p a e", e=experts), w["top_bg"][0:TILE, :].unsqueeze(1).to_broadcast(wide), ALU.add).then_inc(steps, 1)
                dve.wait_ge(steps, 1)
                dve.tensor_reduce(best[:], prob[:], AX.X, ALU.max).then_inc(steps, 1)
                dve.wait_ge(steps, 2)
                dve.tensor_tensor(prob[:], prob[:], best[:].unsqueeze(2).to_broadcast(wide), ALU.subtract).then_inc(steps, 1)
                dve.wait_ge(exp_ready, 1)
                dve.tensor_reduce(total[:], prob[:], AX.X, ALU.add).then_inc(steps, 1)
                dve.wait_ge(steps, 4)
                dve.reciprocal(inverse[:], total[:]).then_inc(steps, 1)
                dve.wait_ge(steps, 5)
                dve.tensor_tensor(prob[:], prob[:], inverse[:].unsqueeze(2).to_broadcast(wide), ALU.mult).then_inc(steps, 1)
                dve.wait_ge(steps, 6)
                dve.tensor_reduce(best[:], prob[:], AX.X, ALU.max).then_inc(steps, 1)
                dve.wait_ge(steps, 7)
                dve.tensor_tensor(part[:], prob[:], best[:].unsqueeze(2).to_broadcast(wide), ALU.is_equal).then_inc(steps, 1)
                dve.wait_ge(steps, 8)
                dve.tensor_tensor(part[:], part[:], w["top_iota"][0:TILE, :].unsqueeze(1).to_broadcast(wide), ALU.mult).then_inc(steps, 1)
                dve.wait_ge(steps, 9)
                dve.tensor_reduce(best[:], part[:], AX.X, ALU.min).then_inc(exp_ready, 1)
                dve.wait_ge(exp_ready, 2)
                dve.tensor_tensor(part[:], w["top_iota"][0:TILE, :].unsqueeze(1).to_broadcast(wide), best[:].unsqueeze(2).to_broadcast(wide), ALU.is_equal).then_inc(exp_ready, 1)
                dve.wait_ge(exp_ready, 3)
                dve.tensor_tensor(prob[:], prob[:], part[:], ALU.mult).then_inc(steps, 1)
                dve.wait_ge(steps, 10)
                for n in range(cols):
                    dve.wait_ge(y_ready, n + 1)
                    if n >= 4:
                        dve.wait_ge(y_summed, n - 3)
                    dve.tensor_tensor(scaled[:, n % 4], ps[4 + n % 4][0:TILE, :].rearrange("p (e f) -> p e f", e=experts),
                                      prob[:, n].unsqueeze(2).to_broadcast([TILE, experts, FEAT]), ALU.mult).then_inc(y_scaled, 1)
                    dve.wait_ge(y_scaled, n + 1)
                    if n >= 2:
                        dve.wait_ge(final_ready, n - 1)
                    dve.tensor_reduce(summed[:, n % 2], scaled[:, n % 4].rearrange("p e f -> p f e"), AX.X, ALU.add).then_inc(y_summed, 1)
                    dve.wait_ge(y_summed, n + 1)
                    dve.wait_ge(rest_ready, n + 1)
                    dve.tensor_tensor(final[:, n], summed[:, n % 2], ps[n % 4][0:TILE, 0:FEAT], ALU.add).then_inc(final_ready, 1)

            @block.sync
            def _(sp):
                for p in range(PAIRS):
                    sp.wait_ge(final_ready, 4 * p + 4)
                    for t in range(2):
                        for a in range(2):
                            sp.dma_start(out_dram[8 * a + p, TILE * t:TILE * t + TILE, :], final[:, 4 * p + 2 * t + a, :]).then_inc(stored, 16)
                sp.wait_ge(stored, 16 * cols)



def both(a):
    return np.concatenate([a, a], 0)


def diagonal(a):
    k, n = a.shape
    out = np.zeros((2 * k, 2 * n), a.dtype)
    out[:k, :n] = a
    out[k:, n:] = a
    return out


def column(v):
    return both(v.reshape(-1, 1))


def rows(v, n=128):
    return np.broadcast_to(v.reshape(1, -1), (n, v.size))


def parts(i):
    f = np.float32
    out = []

    def add(group, name, a):
        out.append((group, name, np.ascontiguousarray(a, dtype=f)))

    half = np.arange(128) // 64
    add(0, "ident", np.eye(128, dtype=f))
    add(1, "win_q", diagonal(i["L0_tok_W_qry"]))
    add(1, "win_k", diagonal(i["L0_tok_W_key"]))
    add(1, "win_b", column(i["L0_tok_b"]))
    v = np.zeros((128, WINDOW, 18), f)
    for o in range(WINDOW):
        v[:64, o, o] = i["L0_tok_v"]
        v[64:, o, 9 + o] = i["L0_tok_v"]
    add(1, "win_v", v.reshape(128, -1))
    sel = np.zeros((18, WINDOW, 128), f)
    for o in range(WINDOW):
        sel[o, o, :64] = 1
        sel[9 + o, o, 64:] = 1
    add(1, "win_out", sel.reshape(18, -1))
    add(0, "mean", (half[:, None] == half[None, :]) / 64.0)
    var = np.zeros((128, TILES, 32), f)
    outm = np.zeros((32, TILES, 128), f)
    for j in range(TILES):
        for a in range(2):
            var[64 * a:64 * a + 64, j, 16 * a + j] = 1.0 / 64
            outm[16 * a + j, j, 64 * a:64 * a + 64] = 1
    add(0, "var_rows", var.reshape(128, -1))
    add(0, "rows_out", outm.reshape(32, -1))
    add(0, "ln_eps", np.full((128, 1), LN_EPS))
    add(2, "mix_qkv", np.concatenate([diagonal(i[f"L0_attn_W{n}"].T) for n in "qkv"], 1))
    add(2, "mix_qkvb", rows(np.concatenate([i[f"L0_attn_b{n}"] for n in "qkv"])))
    add(2, "cap_r", diagonal(i["L0_ffn_wr"]))
    add(2, "cap_br", rows(i["L0_ffn_br"]))
    add(2, "cap_1", both(i["L0_ffn_w1"]))
    add(2, "cap_b1", i["L0_ffn_b1"].reshape(2, 128).T)
    w2 = np.zeros((128, 2, 2, 2, 64), f)
    for a in range(2):
        w2[:, a, :, a, :] = i["L0_ffn_w2"].reshape(2, 128, 64).transpose(1, 0, 2)
    add(2, "cap_2", w2.reshape(128, -1))
    add(2, "cap_b2", column(i["L0_ffn_b2"]))
    n = np.arange(POS)
    add(2, "cap_earlier", np.concatenate([n[None, :] < (t * TILE + np.arange(TILE))[:, None] for t in range(2)], 1))
    add(3, "tay_qkv", np.concatenate([diagonal(i["L1_attn_Wqkv"][64 * n:64 * n + 64].T) for n in range(3)], 1))
    add(3, "tay_qkvb", rows(np.concatenate([np.concatenate([i["L1_attn_bqkv"][64 * n:64 * n + 64]] * 2) for n in range(3)])))
    add(3, "tay_temp", rows(i["L1_attn_temperature"]))
    coef = []
    for a in range(8):
        coef += [0.5] + [1.0] * (7 - a)
    coef += [8.0 ** 0.5] * 8 + [8.0]
    m = np.zeros((2, 45, 2, 9), f)
    for a in range(2):
        m[a, :, a, :] = np.array(coef)[:, None]
    add(3, "tay_coef", m.reshape(90, 18))
    add(3, "tay_o", diagonal(i["L1_attn_Wproj"].T))
    add(3, "tay_ob", column(i["L1_attn_bproj"]))
    add(4, "moe_r", diagonal(i["L1_ffn_Wr"]))
    add(4, "moe_br", rows(i["L1_ffn_br"]))
    add(4, "moe_b2", diagonal(i["L1_ffn_b2"]))
    n = np.arange(TILE)
    add(4, "moe_tri", n[:, None] < n[None, :])
    add(4, "moe_ones", np.ones((128, 128)))
    add(0, "iota", rows(np.arange(128)))
    add(0, "iota_p", np.arange(128).reshape(-1, 1))
    add(4, "moe_high", (n // 2).reshape(-1, 1))
    add(4, "moe_low", (n % 2)[:, None] * 32 + np.repeat(np.arange(32), 2)[None, :])
    swap = np.arange(64) ^ 1
    add(5, "ret_q", diagonal(i["L2_attn_W_Q"]))
    add(5, "ret_qs", diagonal(i["L2_attn_W_Q"][:, swap]))
    add(5, "ret_k", diagonal(i["L2_attn_W_K"]))
    add(5, "ret_ks", diagonal(i["L2_attn_W_K"][:, swap]))
    add(5, "ret_v", diagonal(i["L2_attn_W_V"]))
    pos = np.arange(POS, dtype=f)
    even = np.arange(0, 64, 2, dtype=f)
    ang = pos[None, :] * (f(1) / f(10000) ** (even / f(64)))[:, None]
    size = ((even + f(25.6)) / f(89.6))[:, None] ** (pos[None, :] / f(512))
    sign = np.tile(np.array([-1, 1], f), 32)[:, None]
    table = []
    for size_ in (size, f(1) / size):
        table += [both(np.repeat(np.cos(ang) * size_, 2, 0)), both(np.repeat(np.sin(ang) * size_, 2, 0) * sign)]
    add(5, "ret_table", np.concatenate(table, 1))
    diff = np.arange(POS)[None, :] - np.arange(TILE)[:, None]
    decay = np.where(diff >= 0, f(0.96875) ** np.maximum(diff, 0).astype(f), 0)
    add(5, "ret_decay", np.concatenate([decay, decay[:, :TILE]], 1))
    add(6, "soft_r", both(i["L2_ffn_Wr"]))
    add(6, "soft_br", rows(i["L2_ffn_br"]))
    add(6, "soft_bo", np.concatenate([i["L2_ffn_bo"]] * 2, 1))
    for n, name in ((1, "W1"), (2, "W2"), (3, "Wo")):
        add(6, f"soft_{n}", np.concatenate([diagonal(a) for a in i["L2_ffn_" + name]], 1))
    add(6, "bn", np.concatenate([both(i[f"L2_ffn_{n}{layer}"].T) for n in ("g", "b", "m", "v", "be") for layer in (1, 2)], 1))
    add(6, "bn_eps", np.full((128, 1), 1e-3))
    add(7, "rel_gamma", column(i["L3_attn_ln_gamma"]))
    add(7, "rel_beta", column(i["L3_attn_ln_beta"]))
    for n in "qkv":
        add(7, "rel_" + n, diagonal(i[f"L3_attn_W{n}"].T))
    wo = np.zeros((4, 32, 64), f)
    wo[:, :16] = i["L3_attn_Wo"].T.reshape(4, 16, 64)
    add(7, "rel_o", wo.reshape(128, 64))
    u, v = (np.ascontiguousarray(i[f"L3_attn_{n}_bias"]).reshape(64) for n in "uv")
    add(7, "rel_qu", np.concatenate([column(i["L3_attn_bq"]), column(u), column(v)], 1))
    add(7, "rel_kb", column(i["L3_attn_bk"]))
    add(7, "rel_vb", rows(np.concatenate([i["L3_attn_bv"]] * 2)))
    add(7, "rel_ob", column(i["L3_attn_bo"]))
    add(7, "rel_posb", column(i["L3_attn_bpos"]))
    wpos = i["L3_attn_Wpos"]
    add(7, "rel_pos_t", np.concatenate([wpos.T] * 2, 1))
    omega = np.exp(np.arange(0, 64, 2) * (-np.log(10000.0) / 64))
    ends = np.zeros((64, 2))
    for k, r in enumerate((0, 60)):
        ends[0::2, k], ends[1::2, k] = np.sin(r * omega), np.cos(r * omega)
    add(7, "rel_ends", ends)
    head = (np.arange(64) // 16)[:, None] == np.arange(4)[None, :]
    add(7, "rel_parity", both(head[:, 0:2] | head[:, 2:4]) * 0.25)
    h8 = np.zeros((128, 8))
    h8[:64, :4], h8[64:, 4:] = head, head
    add(7, "rel_head8", h8)
    cut = [np.where(head[:, g:g + 1], wpos, f(0)) for g in range(4)]
    add(7, "rel_pos", np.concatenate([diagonal(a) for a in cut], 1))
    add(7, "rel_pos_s", np.concatenate([diagonal(a[:, swap]) for a in cut], 1))
    n = np.arange(POS)
    th = (30 - n)[None, :] * np.repeat(omega, 2)[:, None]
    add(7, "rel_t", np.concatenate([both(np.cos(th)), both(np.sin(th) * np.tile([-1, 1], 32)[:, None])], 1))
    es = n[None, :] * np.repeat(omega, 2)[:, None]
    es[0::2], es[1::2] = np.sin(es[0::2]), np.cos(es[1::2])
    add(7, "rel_s", both(es))
    gap = [n[None, :] - (t * TILE + np.arange(TILE))[:, None] for t in range(2)]
    wide = TILE + 29
    add(7, "rel_near", np.concatenate([np.abs(gap[t])[:, (POS - wide) * t:(POS - wide) * t + wide] < 30 for t in range(2)], 1))
    add(7, "rel_right", np.concatenate([g >= 30 for g in gap], 1))
    add(8, "top_1", both(i["L3_ffn_W1"]))
    add(8, "top_b1", i["L3_ffn_b1"].reshape(2, 128).T)
    add(8, "top_g", i["L3_ffn_Wg"].reshape(2, 128, 8).transpose(1, 0, 2).reshape(128, 16))
    add(8, "top_bg", rows(i["L3_ffn_bg"]))
    add(8, "top_d", i["L3_ffn_Wd"].reshape(8, 2, 128, 64).transpose(2, 1, 0, 3).reshape(128, 1024))
    add(8, "top_bd", i["L3_ffn_bd"])
    add(8, "top_iota", rows(np.arange(8) - 8))
    return out


def pack(i):
    where, blocks, at, groups = {}, [], 0, {}
    for group, name, a in sorted(parts(i), key=lambda p: p[0]):
        where[name] = (group, a.shape[0], at, a.shape[1])
        block = np.zeros((128, a.shape[1]), np.float32)
        block[:a.shape[0]] = a
        blocks.append(block)
        lo, _ = groups.get(group, (at, at))
        at += a.shape[1]
        groups[group] = (lo, at)
    return np.concatenate(blocks, 1), where, [groups[g] for g in sorted(groups)]


def extra(i):
    w1 = np.concatenate([i["L1_ffn_W1"], i["L1_ffn_b1"][:, None, :]], 1)
    return {"experts1": np.ascontiguousarray(w1.transpose(1, 0, 2).reshape(FEAT + 1, -1)),
            "experts2": np.ascontiguousarray(i["L1_ffn_W2"].transpose(1, 0, 2).reshape(128, -1))}


def pairs_first(a):
    return np.ascontiguousarray(a.reshape(2, 8, a.shape[1], 64).transpose(0, 3, 1, 2).reshape(128, 8, a.shape[1]))


def program(nc, where, groups, d):
    with ExitStack() as ctx:
        h = ctx.enter_context(nc.sbuf_tensor("h", [128, COLS], F32))
        x = ctx.enter_context(nc.sbuf_tensor("x", [128, COLS], F32))
        ps = [ctx.enter_context(nc.psum_tensor(f"bank{b}", [128, 512], F32)) for b in range(8)]
        d["tokens"] = nc.dram_tensor("tokens", [SEQS * POS, FEAT], F32, kind="Internal").ap()
        d["table"] = nc.dram_tensor("table", [TABLE_TILES * 128, FEAT], F32, kind="Internal").ap()
        w = Weights(nc, ctx, d["weights"], where, groups)
        w.arrive(1)
        window_attention(nc, d["x"], h, w, ps)
        layer_norm(nc, "ln0", h, x, w, ps)
        w.arrive(2)
        batch_axis_attention(nc, h, x, w, ps)
        layer_norm(nc, "ln1", h, x, w, ps)
        top_half_ffn(nc, h, x, w, ps)
        layer_norm(nc, "ln2", h, x, w, ps)
        w.arrive(3)
        taylor_attention(nc, h, x, w, ps)
        layer_norm(nc, "ln3", h, x, w, ps)
        w.arrive(4)
        expert_ffn(nc, h, x, w, ps, d)
        layer_norm(nc, "ln4", h, x, w, ps)
        w.arrive(5)
        retention(nc, h, x, w, ps)
        layer_norm(nc, "ln5", h, x, w, ps)
        w.arrive(6)
        soft_mixture(nc, h, x, w, ps)
        layer_norm(nc, "ln6", h, x, w, ps)
        layer_norm(nc, "ln6b", x, x, w, ps)
        w.arrive(7)
        relative_attention(nc, h, x, w, ps)
        layer_norm(nc, "ln7", h, x, w, ps)
        w.arrive(8)
        best_expert_ffn(nc, h, x, w, ps, d["out"])


def kernel(**inputs):
    import numpy as _np
    import concourse.bacc as _bacc
    from concourse import mybir as _mybir
    from concourse.bass_utils import run_bass_kernel_spmd as _run

    given = {name: _np.asarray(a) for name, a in inputs.items()}
    weights, where, groups = pack(given)
    arrays = {"x": pairs_first(given["x"]), "weights": weights, **extra(given)}
    nc = _bacc.Bacc("TRN2", target_bir_lowering=False, num_devices=1)
    d = {name: nc.dram_tensor(f"in_{name}_dram", a.shape, _mybir.dt.float32, kind="ExternalInput").ap() for name, a in arrays.items()}
    d["out"] = nc.dram_tensor("out_0_dram", [SEQS, POS, FEAT], _mybir.dt.float32, kind="ExternalOutput").ap()
    program(nc, where, groups, d)
    r = _run(nc, [{f"in_{name}_dram": a for name, a in arrays.items()}], core_ids=[0])
    return r.results[0]["out_0_dram"]
```

```python
from contextlib import ExitStack

import numpy as np

import concourse.bass as bass
from concourse import mybir

F32 = mybir.dt.float32
I32 = mybir.dt.int32
U32 = mybir.dt.uint32
BF16 = mybir.dt.bfloat16
ALU = mybir.AluOpType
ACT = mybir.ActivationFunctionType
AX = mybir.AxisListType

SEQS, FRAMES, FEAT, WINDOW = 16, 250, 64, 9
POS = FRAMES - WINDOW + 1
PAIRS = SEQS // 2
COLS = PAIRS * POS
TILE = POS // 2
TILES = 2 * PAIRS
CHUNK = 4 * TILE
CHUNKS = COLS // CHUNK
LN_EPS = 1e-5
EXPERTS = 64
TABLE_TILES = 128


def chunk(c):
    return slice(c * CHUNK, (c + 1) * CHUNK)


def tile(j):
    return slice(j * TILE, (j + 1) * TILE)


class Stage:

    def __init__(self, nc, name):
        self.nc, self.name, self.ctx, self.sems = nc, name, ExitStack(), []

    def __enter__(self):
        self.ctx.__enter__()
        return self

    def __exit__(self, *e):
        if self.sems and e[0] is None:
            for sem in self.sems:
                self.nc.gpsimd.sem_clear(sem)
                self.nc.release_semaphore(sem)
        return self.ctx.__exit__(*e)

    def sb(self, name, shape, dt=F32):
        return self.ctx.enter_context(self.nc.sbuf_tensor(f"{self.name}_{name}", shape, dt))

    def sem(self, name):
        self.sems.append(self.nc.alloc_semaphore(f"{self.name}_{name}"))
        return self.sems[-1]

    def pool_dma_sem(self, name):
        return self.nc.alloc_semaphore(f"{self.name}_{name}")


class Weights:

    def __init__(self, nc, ctx, dram, where, groups):
        self.nc, self.dram, self.groups, self.views = nc, dram, groups, {}
        widest = max(b - a for a, b in groups[1:])
        widths = [groups[0][1], widest, widest]
        self.buffers = [ctx.enter_context(nc.sbuf_tensor(f"weights{n}", [128, k], F32)) for n, k in enumerate(widths)]
        self.loaded = [ctx.enter_context(nc.semaphore(f"loaded{g}")) for g in range(len(groups))]
        for name, (group, r, at, k) in where.items():
            at -= groups[group][0]
            self.views[name] = self.buffer(group)[:r, at:at + k]

    def buffer(self, group):
        return self.buffers[0 if group == 0 else 1 + group % 2]

    def __getitem__(self, name):
        return self.views[name]

    def load(self, eng, group):
        a, b = self.groups[group]
        eng.dma_start(self.buffer(group)[:, 0:b - a], self.dram[:, a:b]).then_inc(self.loaded[group], 16)

    def wait(self, eng, group):
        if group is not None:
            eng.wait_ge(self.loaded[group], 16)


def layer_norm(nc, name, h, x, w, ps, group=None):
    with Stage(nc, name) as s:
        centred = s.sb("centred", [128, COLS])
        squares = s.sb("squares", [128, COLS])
        std = s.sb("std", [32, TILE])
        rstd = s.sb("rstd", [128, TILE])
        warm = s.sb("warm", [128, 1])
        mean_ready, centred_ready, squares_ready = s.sem("mean_ready"), s.sem("centred_ready"), s.sem("squares_ready")
        var_ready, std_ready, rstd_ready = s.sem("var_ready"), s.sem("std_ready"), s.sem("rstd_ready")
        scale_ready, x_ready, warmed, zeroed = s.sem("scale_ready"), s.sem("x_ready"), s.sem("warmed"), s.sem("zeroed")
        with nc.Block() as block:

            @block.tensor
            def _(pe):
                for c in range(CHUNKS):
                    pe.matmul(ps[c][:, :CHUNK], w["mean"], h[:, chunk(c)], start=True, stop=True).then_inc(mean_ready, 1)
                for j in range(TILES):
                    if j % 4 == 0:
                        pe.wait_ge(squares_ready, j // 4 + 1)
                    last = pe.matmul(ps[4][0:32, 0:TILE], w["var_rows"][:, 32 * j:32 * j + 32], squares[:, tile(j)],
                                     start=(j == 0), stop=(j == TILES - 1))
                last.then_inc(var_ready, 1)
                pe.wait_ge(rstd_ready, 1)
                for j in range(TILES):
                    mm = pe.matmul(ps[j // 4][:, tile(j % 4)], w["rows_out"][:, 128 * j:128 * j + 128], rstd[:],
                                   start=True, stop=True)
                    if j % 4 == 3:
                        mm.then_inc(scale_ready, 1)
                w.wait(pe, group)

            @block.scalar
            def _(act):
                act.activation(warm[:], w["ln_eps"], ACT.Sqrt).then_inc(warmed, 1)
                for c in range(CHUNKS):
                    act.wait_ge(centred_ready, c + 1)
                    act.activation(squares[:, chunk(c)], centred[:, chunk(c)], ACT.Square).then_inc(squares_ready, 1)
                act.wait_ge(var_ready, 1)
                act.activation(std[:], ps[4][0:32, 0:TILE], ACT.Sqrt, bias=w["ln_eps"][0:32, :]).then_inc(std_ready, 1)
                w.wait(act, group)

            @block.vector
            def _(dve):
                for c in range(CHUNKS):
                    dve.wait_ge(mean_ready, c + 1)
                    dve.tensor_tensor(centred[:, chunk(c)], h[:, chunk(c)], ps[c][:, :CHUNK], ALU.subtract).then_inc(centred_ready, 1)
                dve.wait_ge(std_ready, 1)
                dve.wait_ge(zeroed, 1)
                dve.reciprocal(rstd[0:32, :], std[:]).then_inc(rstd_ready, 1)
                for c in range(CHUNKS):
                    dve.wait_ge(scale_ready, c + 1)
                    dve.tensor_tensor(x[:, chunk(c)], centred[:, chunk(c)], ps[c][:, :CHUNK], ALU.mult).then_inc(x_ready, 1)
                dve.wait_ge(x_ready, CHUNKS)
                w.wait(dve, group)

            @block.gpsimd
            def _(pool):
                pool.memset(rstd[:], 0.0).then_inc(zeroed, 1)

            @block.sync
            def _(sp):
                if group and group + 1 < len(w.groups):
                    w.load(sp, group + 1)


def window_attention(nc, x_dram, h, w, ps):
    with Stage(nc, "win") as s:
        frames = s.sb("frames", [128, PAIRS, FRAMES])
        query = s.sb("query", [128, PAIRS, POS])
        key = s.sb("key", [128, PAIRS, FRAMES])
        hidden = s.sb("hidden", [128, WINDOW, PAIRS, POS])
        scores = s.sb("scores", [2 * WINDOW, COLS])
        token = s.sb("token", [TILE, TILES * 2, WINDOW])
        top = s.sb("top", [TILE, TILES * 2])
        total = s.sb("total", [TILE, TILES * 2])
        weight_rows = s.sb("weight_rows", [128, COLS])
        product = s.sb("product", [128, 3, PAIRS, POS])
        frames_in = s.sem("frames_in")
        query_ready, query_kept, key_ready, key_kept = s.sem("query_ready"), s.sem("query_kept"), s.sem("key_ready"), s.sem("key_kept")
        sum_ready, hidden_ready, scores_ready, scores_kept = s.sem("sum_ready"), s.sem("hidden_ready"), s.sem("scores_ready"), s.sem("scores_kept")
        turned, top_ready, less_top, exp_ready = s.sem("turned"), s.sem("top_ready"), s.sem("less_top"), s.sem("exp_ready")
        total_ready, inverse_ready, weight_ready = s.sem("total_ready"), s.sem("inverse_ready"), s.sem("weight_ready")
        rows_turned, rows_kept = s.sem("rows_turned"), s.sem("rows_kept")
        spread_ready, product_ready, added, added_last, zeroed = (
            s.sem(n) for n in "spread_ready product_ready added added_last zeroed".split())
        with nc.Block() as block:

            @block.sync
            def _(sp):
                sp.dma_start(frames[:], x_dram).then_inc(frames_in, 16)
                sp.wait_ge(frames_in, 16)
                w.load(sp, 2)

            @block.tensor
            def _(pe):
                w.wait(pe, 1)
                pe.wait_ge(frames_in, 16)
                mid = WINDOW // 2
                for c in range(CHUNKS):
                    pe.matmul(ps[c][:, :CHUNK], w["win_q"], frames[:, 2 * c:2 * c + 2, mid:mid + POS], start=True, stop=True).then_inc(query_ready, 1)
                for c in range(CHUNKS):
                    pe.matmul(ps[4 + c][:, :2 * FRAMES], w["win_k"], frames[:, 2 * c:2 * c + 2, :], start=True, stop=True).then_inc(key_ready, 1)
                for o in range(WINDOW):
                    pe.wait_ge(hidden_ready, o + 1)
                    for c in range(CHUNKS):
                        if o == 0:
                            pe.wait_ge(query_kept, c + 1)
                        mm = pe.matmul(ps[c][32 * c:32 * c + 2 * WINDOW, :CHUNK], w["win_v"][:, 18 * o:18 * o + 18], hidden[:, o, 2 * c:2 * c + 2, :],
                                       start=(o == 0), stop=(o == WINDOW - 1), tile_position=(0, 32 * c))
                        if o == WINDOW - 1:
                            mm.then_inc(scores_ready, 1)
                w.wait(pe, 0)
                pe.wait_ge(key_kept, CHUNKS)
                for j in range(TILES):
                    pe.wait_ge(scores_kept, j // 4 + 1)
                    mm = pe.transpose(ps[4][0:TILE, 18 * j:18 * j + 18], scores[:, tile(j)], w["ident"][0:18, 0:18])
                mm.then_inc(turned, 1)
                pe.wait_ge(weight_ready, 1)
                for j in range(TILES):
                    mm = pe.transpose(ps[j // 4][0:18, tile(j % 4)], token[:, 2 * j:2 * j + 2, :], w["ident"][0:TILE, 0:TILE])
                    if j % 4 == 3:
                        mm.then_inc(rows_turned, 1)
                for o in range(WINDOW):
                    for c in range(CHUNKS):
                        n = o * CHUNKS + c
                        if o == 0:
                            pe.wait_ge(rows_kept, c + 1)
                        if n >= 8:
                            pe.wait_ge(product_ready, n - 7)
                        pe.matmul(ps[n % 8][:, :CHUNK], w["win_out"][:, 128 * o:128 * o + 128], weight_rows[:, chunk(c)],
                                  start=True, stop=True).then_inc(spread_ready, 1)

            @block.scalar
            def _(act):
                w.load(act, 1)
                w.load(act, 0)
                w.wait(act, 1)
                for c in range(CHUNKS):
                    act.wait_ge(query_ready, c + 1)
                    act.activation(query[:, 2 * c:2 * c + 2, :], ps[c][:, :CHUNK].rearrange("p (b n) -> p b n", b=2), ACT.Identity,
                                   bias=w["win_b"]).then_inc(query_kept, 1)
                for o in range(WINDOW):
                    act.wait_ge(sum_ready, o + 1)
                    act.activation(hidden[:, o], hidden[:, o], ACT.Tanh).then_inc(hidden_ready, 1)
                for c in range(CHUNKS):
                    act.wait_ge(scores_ready, c + 1)
                    act.activation(scores[:, chunk(c)], ps[c][32 * c:32 * c + 18, :CHUNK], ACT.Copy).then_inc(scores_kept, 1)
                act.wait_ge(less_top, 1)
                act.activation(token[:], token[:], ACT.Exp).then_inc(exp_ready, 1)
                act.wait_ge(zeroed, 1)
                for c in range(CHUNKS):
                    act.wait_ge(rows_turned, c + 1)
                    act.activation(weight_rows[0:18, chunk(c)], ps[c][0:18, :CHUNK], ACT.Copy).then_inc(rows_kept, 1)

            @block.vector
            def _(dve):
                for c in range(CHUNKS):
                    dve.wait_ge(key_ready, c + 1)
                    dve.tensor_copy(key[:, 2 * c:2 * c + 2, :], ps[4 + c][:, :2 * FRAMES].rearrange("p (b n) -> p b n", b=2)).then_inc(key_kept, 1)
                dve.wait_ge(key_kept, CHUNKS)
                dve.wait_ge(query_kept, CHUNKS)
                for o in range(WINDOW):
                    dve.tensor_tensor(hidden[:, o], query[:], key[:, :, o:o + POS], ALU.add).then_inc(sum_ready, 1)
                dve.wait_ge(turned, 1)
                got = ps[4][0:TILE, 0:18 * TILES].rearrange("p (a o) -> p a o", o=WINDOW)
                dve.tensor_reduce(top[:], got, AX.X, ALU.max).then_inc(top_ready, 1)
                dve.wait_ge(top_ready, 1)
                dve.tensor_tensor(token[:], got, top[:].unsqueeze(2).to_broadcast([TILE, 2 * TILES, WINDOW]), ALU.subtract).then_inc(less_top, 1)
                dve.wait_ge(exp_ready, 1)
                dve.tensor_reduce(total[:], token[:], AX.X, ALU.add).then_inc(total_ready, 1)
                dve.wait_ge(total_ready, 1)
                dve.reciprocal(top[:], total[:]).then_inc(inverse_ready, 1)
                dve.wait_ge(inverse_ready, 1)
                dve.tensor_tensor(token[:], token[:], top[:].unsqueeze(2).to_broadcast([TILE, 2 * TILES, WINDOW]), ALU.mult).then_inc(weight_ready, 1)
                for o in range(WINDOW):
                    for c in range(CHUNKS):
                        dve.wait_ge(spread_ready, o * CHUNKS + c + 1)
                        if o >= 4:
                            dve.wait_ge(added, (o - 3) * (CHUNKS - 1))
                        dst = h if o == 0 else product[:, o % 3]
                        dst = dst[:, chunk(c)].rearrange("p (b n) -> p b n", b=2) if o == 0 else dst[:, 2 * c:2 * c + 2, :]
                        dve.tensor_tensor(dst, frames[:, 2 * c:2 * c + 2, o:o + POS],
                                          ps[(o * CHUNKS + c) % 8][:, :CHUNK].rearrange("p (b n) -> p b n", b=2), ALU.mult).then_inc(product_ready, 1)
                    if o:
                        dve.wait_ge(product_ready, (o + 1) * CHUNKS)
                        if o > 1:
                            dve.wait_ge(added_last, o - 1)
                        dve.tensor_tensor(h[:, chunk(CHUNKS - 1)], h[:, chunk(CHUNKS - 1)], product[:, o % 3, 6:8, :].rearrange("p b n -> p (b n)"), ALU.add).then_inc(added_last, 1)
                dve.wait_ge(added_last, WINDOW - 1)

            @block.gpsimd
            def _(pool):
                pool.memset(weight_rows[:], 0.0).then_inc(zeroed, 1)
                for o in range(1, WINDOW):
                    for c in range(CHUNKS - 1):
                        pool.wait_ge(product_ready, o * CHUNKS + c + 1)
                        if o > 1:
                            pool.wait_ge(added, (o - 2) * (CHUNKS - 1) + c + 1)
                        pool.tensor_tensor(h[:, chunk(c)], h[:, chunk(c)], product[:, o % 3, 2 * c:2 * c + 2, :].rearrange("p b n -> p (b n)"), ALU.add).then_inc(added, 1)
                pool.wait_ge(added, (WINDOW - 1) * (CHUNKS - 1))


def batch_axis_attention(nc, h, x, w, ps):
    blocks, hd = 8, 8
    with Stage(nc, "mix") as s:
        pos_major = {n: s.sb(n + "_pos", [TILE, 2, blocks, SEQS, hd]) for n in ("query", "key", "value")}
        entry_major = {n: s.sb(n + "_entry", [128, COLS]) for n in ("query", "key", "value")}
        row_major = {n: s.sb(n + "_row", [TILE, TILES, 128]) for n in ("key", "value")}
        mixed = s.sb("mixed", [TILE, 2, SEQS, blocks, hd])
        top = s.sb("top", [TILE, 2 * blocks])
        total = s.sb("total", [TILE, 2 * blocks])
        inverse = s.sb("inverse", [TILE, 2 * blocks])
        key_top = s.sb("key_top", [128, blocks])
        key_total = s.sb("key_total", [128, blocks])
        key_inverse = s.sb("key_inverse", [128, blocks])
        context = s.sb("context", [128, blocks, 128])
        qkv_ready, qkv_kept = s.sem("qkv_ready"), s.sem("qkv_kept")
        q_top, q_less, q_exp, q_total, q_inverse, q_scaled = (
            s.sem(n) for n in ("q_top", "q_less", "q_exp", "q_total", "q_inverse", "q_scaled"))
        key_entry_ready, key_entry_kept, value_entry_ready, value_entry_kept = (
            s.sem(n) for n in ("key_entry_ready", "key_entry_kept", "value_entry_ready", "value_entry_kept"))
        key_top_ready, key_exp, key_inverse_ready, key_scaled = (
            s.sem(n) for n in ("key_top_ready", "key_exp", "key_inverse_ready", "key_scaled"))
        value_row_ready, value_row_kept, key_row_ready, key_row_kept = (
            s.sem(n) for n in ("value_row_ready", "value_row_kept", "key_row_ready", "key_row_kept"))
        q_entry_ready, q_entry_kept, context_ready, context_kept = (
            s.sem(n) for n in ("q_entry_ready", "q_entry_kept", "context_ready", "context_kept"))
        mixed_ready, mixed_kept, back_ready, h_ready = (s.sem(n) for n in ("mixed_ready", "mixed_kept", "back_ready", "h_ready"))

        def entries(n, b):
            t, g = b // 2, b % 2
            return entry_major[n][:].rearrange("p (c k) -> p k c", k=blocks)[:, 4 * g:4 * g + 4, TILE * t:TILE * t + TILE]

        with nc.Block() as block:

            @block.tensor
            def _(pe):
                for j in range(TILES):
                    if j >= 8:
                        pe.wait_ge(qkv_kept, 3 * (j - 7))
                    pe.matmul(ps[j % 8][0:TILE, 0:384], x[:, tile(j)], w["mix_qkv"], start=True, stop=True).then_inc(qkv_ready, 1)

                def turn(name, first, ready):
                    for b in range(4):
                        for k in range(4):
                            src = pos_major[name][:, b // 2, 4 * (b % 2) + k].rearrange("p r j -> p (r j)")
                            mm = pe.transpose(ps[first + b][:, tile(k)], src, w["ident"][0:TILE, 0:TILE])
                        mm.then_inc(ready, 1)

                def turn_rows(name, first, ready):
                    for b in range(4):
                        for k in range(4):
                            mm = pe.transpose(ps[first + b][0:TILE, 128 * k:128 * k + 128], entry_major[name][:, tile(4 * b + k)], w["ident"])
                        mm.then_inc(ready, 1)

                pe.wait_ge(qkv_kept, 3 * TILES)
                turn("key", 0, key_entry_ready)
                turn("value", 4, value_entry_ready)
                pe.wait_ge(value_entry_kept, 4)
                turn_rows("value", 4, value_row_ready)
                pe.wait_ge(key_scaled, blocks)
                turn_rows("key", 0, key_row_ready)
                pe.wait_ge(q_scaled, 1)
                pe.wait_ge(value_row_kept, 4)
                turn("query", 4, q_entry_ready)
                for n in range(2):
                    pe.wait_ge(key_row_kept, 4)
                    for k in range(4):
                        for t in range(2):
                            i = 2 * (4 * n + k) + t
                            mm = pe.matmul(ps[n][:, 128 * k:128 * k + 128], row_major["key"][:, i], row_major["value"][:, i],
                                           start=(t == 0), stop=(t == 1))
                    mm.then_inc(context_ready, 1)
                pe.wait_ge(q_entry_kept, 4)
                for t in range(2):
                    for n in range(2):
                        pe.wait_ge(context_kept, n + 1)
                        for k in range(4):
                            g = 4 * n + k
                            mm = pe.matmul(ps[4 + 2 * t + n][0:TILE, 128 * k:128 * k + 128], entry_major["query"][:, tile(2 * g + t)],
                                           context[:, g, :], start=True, stop=True)
                        mm.then_inc(mixed_ready, 1)
                pe.wait_ge(mixed_kept, 4)
                pe.wait_ge(context_kept, 2)
                for j in range(TILES):
                    src = mixed[:, j % 2, 2 * (j // 2):2 * (j // 2) + 2].rearrange("p r h j -> p (r h j)")
                    mm = pe.transpose(ps[j // 4][:, tile(j % 4)], src, w["ident"][0:TILE, 0:TILE])
                    if j % 4 == 3:
                        mm.then_inc(back_ready, 1)

            @block.scalar
            def _(act):
                for b in range(4):
                    act.wait_ge(key_entry_ready, b + 1)
                    act.activation(entries("key", b), ps[b][:, :CHUNK].rearrange("p (k c) -> p k c", k=4), ACT.Copy).then_inc(key_entry_kept, 1)
                act.wait_ge(q_less, 1)
                wide = pos_major["query"]
                act.activation(wide[:], wide[:], ACT.Exp).then_inc(q_exp, 1)
                act.wait_ge(key_top_ready, 1)
                for g in range(blocks):
                    rows_ = entry_major["key"][:, g * POS:(g + 1) * POS]
                    act.activation(rows_, rows_, ACT.Exp, bias=key_top[:, g:g + 1], accum_out=key_total[:, g:g + 1]).then_inc(key_exp, 1)
                for b in range(4):
                    act.wait_ge(key_row_ready, b + 1)
                    act.activation(row_major["key"][:, 4 * b:4 * b + 4, :], ps[b][0:TILE, :].rearrange("p (k e) -> p k e", k=4), ACT.Copy).then_inc(key_row_kept, 1)
                for b in range(4):
                    act.wait_ge(q_entry_ready, b + 1)
                    act.activation(entries("query", b), ps[4 + b][:, :CHUNK].rearrange("p (k c) -> p k c", k=4), ACT.Copy).then_inc(q_entry_kept, 1)
                for n in range(2):
                    act.wait_ge(context_ready, n + 1)
                    act.activation(context[:, 4 * n:4 * n + 4, :], ps[n][:].rearrange("p (a n) -> p a n", a=4), ACT.Copy).then_inc(context_kept, 1)

            @block.vector
            def _(dve):
                for j in range(TILES):
                    dve.wait_ge(qkv_ready, j + 1)
                    for i, n in enumerate(("query", "key", "value")):
                        got = ps[j % 8][0:TILE, 128 * i:128 * i + 128].rearrange("p (a h j) -> p h a j", a=2, h=blocks)
                        bias = w["mix_qkvb"][0:TILE, 64 * i:64 * i + 64].rearrange("p (h j) -> p h j", h=blocks).unsqueeze(2).to_broadcast([TILE, blocks, 2, hd])
                        dve.tensor_tensor(pos_major[n][:, j % 2, :, 2 * (j // 2):2 * (j // 2) + 2], got, bias, ALU.add).then_inc(qkv_kept, 1)
                dve.wait_ge(qkv_kept, 3 * TILES)
                wide = pos_major["query"][:].rearrange("p t h r j -> p (t h) (r j)")
                dve.tensor_reduce(top[:], wide, AX.X, ALU.max).then_inc(q_top, 1)
                dve.wait_ge(q_top, 1)
                dve.tensor_tensor(wide, wide, top[:].unsqueeze(2).to_broadcast([TILE, 2 * blocks, 128]), ALU.subtract).then_inc(q_less, 1)
                dve.wait_ge(key_entry_kept, 4)
                dve.tensor_reduce(key_top[:], entry_major["key"][:].rearrange("p (g n) -> p g n", n=POS), AX.X, ALU.max, negate=True).then_inc(key_top_ready, 1)
                for b in range(4):
                    dve.wait_ge(value_entry_ready, b + 1)
                    dve.tensor_copy(entries("value", b), ps[4 + b][:, :CHUNK].rearrange("p (k c) -> p k c", k=4)).then_inc(value_entry_kept, 1)
                dve.wait_ge(q_exp, 1)
                dve.tensor_reduce(total[:], wide, AX.X, ALU.add).then_inc(q_total, 1)
                dve.wait_ge(q_total, 1)
                dve.reciprocal(inverse[:], total[:]).then_inc(q_inverse, 1)
                dve.wait_ge(q_inverse, 1)
                dve.tensor_scalar(top[:], inverse[:], float(SEQS * hd) ** 0.5, None, ALU.mult).then_inc(q_inverse, 1)
                dve.wait_ge(key_exp, blocks)
                dve.reciprocal(key_inverse[:], key_total[:]).then_inc(key_inverse_ready, 1)
                dve.wait_ge(key_inverse_ready, 1)
                for g in range(blocks):
                    rows_ = entry_major["key"][:, g * POS:(g + 1) * POS]
                    dve.tensor_scalar(rows_, rows_, key_inverse[:, g:g + 1], None, ALU.mult).then_inc(key_scaled, 1)
                dve.wait_ge(q_inverse, 2)
                dve.tensor_tensor(wide, wide, top[:].unsqueeze(2).to_broadcast([TILE, 2 * blocks, 128]), ALU.mult).then_inc(q_scaled, 1)
                for b in range(4):
                    dve.wait_ge(value_row_ready, b + 1)
                    dve.tensor_copy(row_major["value"][:, 4 * b:4 * b + 4, :], ps[4 + b][0:TILE, :].rearrange("p (k e) -> p k e", k=4)).then_inc(value_row_kept, 1)
                for t in range(2):
                    for n in range(2):
                        dve.wait_ge(mixed_ready, 2 * t + n + 1)
                        dst = mixed[:, t, :, 4 * n:4 * n + 4].rearrange("p r h j -> p h r j")
                        dve.tensor_copy(dst, ps[4 + 2 * t + n][0:TILE, :].rearrange("p (h r j) -> p h r j", h=4, r=SEQS)).then_inc(mixed_kept, 1)
                for c in range(CHUNKS):
                    dve.wait_ge(back_ready, c + 1)
                    dve.tensor_tensor(h[:, chunk(c)], h[:, chunk(c)], ps[c][:, :CHUNK], ALU.add).then_inc(h_ready, 1)
                dve.wait_ge(h_ready, CHUNKS)


def top_half_ffn(nc, h, x, w, ps):
    kept_tokens = max(1, int(0.5 * POS)) - 1
    with Stage(nc, "cap") as s:
        score = s.sb("score", [TILE, TILES, 2])
        above = s.sb("above", [TILE, TILES, 2])
        equal = s.sb("equal", [TILE, TILES, 2])
        gate = s.sb("gate", [TILE, TILES, 2])
        gate_wide = s.sb("gate_wide", [TILE, TILES, 2, 64])
        gate_f = s.sb("gate_f", [128, COLS])
        scratch = s.sb("scratch", [TILE, 4, POS])
        hidden = s.sb("hidden", [128, 2, 2, COLS])
        out = s.sb("out", [128, COLS])
        score_ready, score_kept, score_spread = s.sem("score_ready"), s.sem("score_kept"), s.sem("score_spread")
        counted, rank_ready, gate_ready = s.sem("counted"), s.sem("rank_ready"), s.sem("gate_ready")
        gate_spread, gate_kept = s.sem("gate_spread"), s.sem("gate_kept")
        up_ready, up_kept, down_ready = s.sem("up_ready"), s.sem("up_kept"), s.sem("down_ready")
        gated, h_plus_x, h_ready = s.sem("gated"), s.sem("h_plus_x"), s.sem("h_ready")
        with nc.Block() as block:

            @block.tensor
            def _(pe):
                for j in range(TILES):
                    mm = pe.matmul(ps[0][0:TILE, 2 * j:2 * j + 2], x[:, tile(j)], w["cap_r"], start=True, stop=True)
                mm.then_inc(score_ready, 1)
                pe.wait_ge(score_kept, 1)

                def spread(b):
                    if b >= 4:
                        pe.wait_ge(counted, 8 * (b - 3))
                    for k in range(4):
                        j = 4 * (b % 4) + k
                        mm = pe.transpose(ps[b % 4][0:TILE, tile(k)], score[:, j, b // 4].unsqueeze(1).to_broadcast([TILE, TILE]), w["ident"][0:TILE, 0:TILE])
                    mm.then_inc(score_spread, 1)

                def up(n):
                    c, m, a = n // 4, (n // 2) % 2, n % 2
                    if n >= 4:
                        pe.wait_ge(up_kept, n - 3)
                    pe.matmul(ps[4 + n % 4][:, :CHUNK], w["cap_1"][:, 256 * a + 128 * m:256 * a + 128 * m + 128], x[:, chunk(c)], start=True, stop=True).then_inc(up_ready, 1)

                for b in range(4):
                    spread(b)
                for b in range(4):
                    for k in range(4):
                        up(4 * b + k)
                    spread(4 + b)
                pe.wait_ge(gate_ready, 2)
                for c in range(CHUNKS):
                    for k in range(4):
                        mm = pe.transpose(ps[c][:, tile(k)], gate_wide[:, 4 * c + k].rearrange("p a f -> p (a f)"), w["ident"][0:TILE, 0:TILE])
                    mm.then_inc(gate_spread, 1)
                pe.wait_ge(up_kept, 16)
                for c in range(CHUNKS):
                    for a in range(2):
                        for m in range(2):
                            mm = pe.matmul(ps[4 + c][:, :CHUNK], w["cap_2"][:, 128 * (2 * a + m):128 * (2 * a + m) + 128], hidden[:, m, a, chunk(c)],
                                           start=(a + m == 0), stop=(a + m == 2))
                    mm.then_inc(down_ready, 1)

            @block.scalar
            def _(act):
                for n in range(16):
                    c, m, a = n // 4, (n // 2) % 2, n % 2
                    act.wait_ge(up_ready, n + 1)
                    act.activation(hidden[:, m, a, chunk(c)], ps[4 + n % 4][:, :CHUNK], ACT.Gelu_apprx_tanh, bias=w["cap_b1"][:, m:m + 1]).then_inc(up_kept, 1)
                for c in range(CHUNKS):
                    act.wait_ge(gate_spread, c + 1)
                    act.activation(gate_f[:, chunk(c)], ps[c][:, :CHUNK], ACT.Copy).then_inc(gate_kept, 1)

            @block.vector
            def _(dve):
                dve.wait_ge(score_ready, 1)
                dve.tensor_scalar(score[:], ps[0][0:TILE, 0:2 * TILES].rearrange("p (j a) -> p j a", a=2), w["cap_br"][0:TILE, :], None, ALU.add).then_inc(score_kept, 1)
                dve.wait_ge(score_kept, 1)
                for b in range(8):
                    dve.wait_ge(score_spread, b + 1)
                    for k in range(4):
                        j, a, n = 4 * (b % 4) + k, b // 4, 8 * b + 2 * k
                        seq = ps[b % 4][0:TILE, (k // 2) * POS:(k // 2 + 1) * POS]
                        mine = score[:, j, a:a + 1]
                        if n >= 4:
                            dve.wait_ge(counted, n - 2)
                        dve.tensor_scalar(scratch[:, n % 4], seq, mine, None, ALU.is_gt, ALU.add, accum_out=above[:, j, a:a + 1]).then_inc(counted, 1)
                        dve.scalar_tensor_tensor(scratch[:, n % 4 + 1], seq, mine, w["cap_earlier"][0:TILE, POS * (j % 2):POS * (j % 2) + POS],
                                                 ALU.is_equal, ALU.mult, accum_out=equal[:, j, a:a + 1]).then_inc(counted, 1)
                dve.wait_ge(counted, 64)
                dve.tensor_tensor(above[:], above[:], equal[:], ALU.add).then_inc(rank_ready, 1)
                dve.wait_ge(rank_ready, 1)
                dve.scalar_tensor_tensor(gate[:].rearrange("p j a -> p (j a)"), above[:].rearrange("p j a -> p (j a)"), float(kept_tokens),
                                         score[:].rearrange("p j a -> p (j a)"), ALU.is_lt, ALU.mult).then_inc(gate_ready, 1)
                dve.wait_ge(gate_ready, 1)
                dve.tensor_copy(gate_wide[:], gate[:].unsqueeze(3).to_broadcast([TILE, TILES, 2, 64])).then_inc(gate_ready, 1)
                for c in range(CHUNKS):
                    dve.wait_ge(down_ready, c + 1)
                    dve.wait_ge(gate_kept, c + 1)
                    dve.scalar_tensor_tensor(out[:, chunk(c)], ps[4 + c][:, :CHUNK], w["cap_b2"], gate_f[:, chunk(c)], ALU.add, ALU.mult).then_inc(gated, 1)
                dve.wait_ge(h_plus_x, 1)
                for c in range(CHUNKS):
                    dve.wait_ge(gated, c + 1)
                    dve.tensor_tensor(h[:, chunk(c)], h[:, chunk(c)], out[:, chunk(c)], ALU.add).then_inc(h_ready, 1)
                dve.wait_ge(h_ready, CHUNKS)

            @block.gpsimd
            def _(pool):
                pool.tensor_tensor(h[:], h[:], x[:], ALU.add).then_inc(h_plus_x, 1)


def taylor_attention(nc, h, x, w, ps):
    heads, hd, feats, group = 8, 8, 45, 8
    eps = 1e-12
    scale = float(hd) ** 0.25
    seqs = 2 * TILES
    with Stage(nc, "tay") as s:
        qkv = s.sb("qkv", [TILE, 3, TILES, 2, FEAT])
        phi_k = s.sb("phi_k", [TILE, seqs, heads, feats])
        phi_q = s.sb("phi_q", [TILE, 2, group, heads, feats])
        value_wide = s.sb("value", [TILE, seqs * heads * (hd + 1) + 14])
        value = value_wide[:, 0:seqs * heads * (hd + 1)].rearrange("p (a h e) -> p a h e", a=seqs, h=heads)
        norm2 = s.sb("norm2", [TILE, 2, seqs, heads])
        norm = s.sb("norm", [TILE, 2, seqs, heads])
        factor = s.sb("factor", [TILE, 2, seqs, heads])
        kv_turned = s.sb("kv_turned", [128, SEQS, 90])
        kv = s.sb("kv", [90, SEQS, 128])
        phi_t = s.sb("phi_t", [90, 4, 4, TILE])
        inverse = s.sb("inverse", [128, 2, CHUNK])
        y = s.sb("y", [128, 2, CHUNK])
        y_scaled = s.sb("y_scaled", [128, 2, CHUNK])
        squares = phi_k[:].rearrange("p a h f -> p (a h f)")[:, 0:2 * seqs * FEAT].rearrange("p (i a f) -> p i a f", i=2, a=seqs)
        (qkv_ready, qkv_kept, squared, norm2_ready, norm_ready, norm_safe, norm_inverse, factor_ready, value_ready, ones_ready,
         key_unit, query_unit, key_products, query_products, kv_ready, kv_kept, kv_back, kv_masked, turned, turned_kept, y_ready,
         y_kept, sum_ready, y_inverse, y_done, out_ready, h_ready) = (s.sem(n) for n in (
             "qkv_ready qkv_kept squared norm2_ready norm_ready norm_safe norm_inverse factor_ready value_ready ones_ready "
             "key_unit query_unit key_products query_products kv_ready kv_kept kv_back kv_masked turned turned_kept y_ready "
             "y_kept sum_ready y_inverse y_done out_ready h_ready").split())

        def vectors(i, lo, n):
            return qkv[:, i].rearrange("p j a (h e) -> p (j a) h e", h=heads)[:, lo:lo + n]

        def products(eng, phi, n, done):
            flat = phi.rearrange("p a h f -> p (a h) f")
            at = 0
            for i in range(hd):
                k = hd - i
                last = eng.tensor_tensor(flat[:, :, at:at + k], flat[:, :, 36 + i:37 + i].to_broadcast([TILE, n * heads, k]),
                                         flat[:, :, 36 + i:44], ALU.mult)
                at += k
                last.then_inc(done, 1)

        with nc.Block() as block:

            @block.tensor
            def _(pe):
                for j in range(TILES):
                    if j >= 8:
                        pe.wait_ge(qkv_kept, j - 7)
                    pe.matmul(ps[j % 8][0:TILE, 0:384], x[:, tile(j)], w["tay_qkv"], start=True, stop=True).then_inc(qkv_ready, 1)
                pe.wait_ge(ones_ready, 5)
                pe.wait_ge(value_ready, 1)
                pe.wait_ge(qkv_kept, TILES)
                for n in range(4):
                    pe.wait_ge(key_products, hd * (n // 2 + 1))
                    for k in range(4):
                        p, a = 2 * n + k // 2, k % 2
                        for t in range(2):
                            col = 2 * (2 * p + t) + a
                            for g in range(4):
                                at = 72 * col + 18 * g
                                mm = pe.matmul(ps[n][32 * g:32 * g + 32, 90 * k:90 * k + 90], value_wide[:, at:at + 32],
                                               phi_k[:, col, 2 * g:2 * g + 2].rearrange("p h f -> p (h f)"), start=(t == 0), stop=(t == 1), tile_position=(0, 32 * g))
                    mm.then_inc(kv_ready, 1)
                for n in range(4):
                    pe.wait_ge(kv_kept, n + 1)
                    for k in range(4):
                        mm = pe.transpose(ps[4 + n][0:90, 128 * k:128 * k + 128], kv_turned[:, 4 * n + k], w["ident"])
                    mm.then_inc(kv_back, 1)

                def turn(col):
                    if col % group == 0:
                        pe.wait_ge(query_products, hd * (col // group + 1))
                    if col < 4:
                        pe.wait_ge(kv_masked, col + 1)
                    else:
                        pe.wait_ge(turned_kept, col - 3)
                    for g in range(4):
                        mm = pe.transpose(ps[4 + col % 4][0:90, tile(g)],
                                          phi_q[:, (col // group) % 2, col % group, 2 * g:2 * g + 2].rearrange("p h f -> p (h f)"),
                                          w["ident"][0:TILE, 0:TILE])
                    mm.then_inc(turned, 1)

                def outputs(col):
                    c, k, a = col // group, col % group // 2, col % 2
                    pe.wait_ge(turned_kept, col + 1)
                    if k == 0 and c >= 2:
                        pe.wait_ge(h_ready, c - 1)
                        pe.wait_ge(y_inverse, 2 * (c - 2) + a + 1)
                    for g in range(4):
                        mm = pe.matmul(ps[2 * (c % 2) + a][32 * g:32 * g + 32, tile(k)], kv[:, 2 * (col // 4) + a, 32 * g:32 * g + 32], phi_t[:, col % 4, g, :],
                                       start=True, stop=True, tile_position=(0, 32 * g))
                    mm.then_inc(y_ready, 1)

                def sums(u):
                    pe.wait_ge(y_kept, u + 1)
                    pe.matmul(ps[u % 4][:, :CHUNK], w["tay_sum"], y[:, u % 2], start=True, stop=True).then_inc(sum_ready, 1)

                def project(c):
                    pe.wait_ge(y_done, 2 * c + 2)
                    for a in range(2):
                        pe.matmul(ps[2 * (c % 2)][64 * a:64 * a + 64, :CHUNK], w["tay_o"], y_scaled[:, a], start=True, stop=True, tile_position=(0, 64 * a)).then_inc(out_ready, 1)

                for col in range(seqs + 2):
                    if col < seqs:
                        turn(col)
                    if col >= 2:
                        outputs(col - 2)
                    if col % group == 3 and col >= group:
                        sums(2 * (col // group) - 2)
                        sums(2 * (col // group) - 1)
                    if col % group == 1 and col >= 2 * group:
                        project(col // group - 2)
                sums(2 * CHUNKS - 2)
                sums(2 * CHUNKS - 1)
                project(CHUNKS - 1)

            @block.scalar
            def _(act):
                act.wait_ge(qkv_kept, TILES)
                act.activation(squares, qkv[:, 0:2].rearrange("p i j a f -> p i (j a) f"), ACT.Square).then_inc(squared, 1)
                act.wait_ge(norm2_ready, 1)
                act.activation(norm[:, 0], norm2[:, 0], ACT.Sqrt, scale=scale * scale).then_inc(norm_ready, 1)
                act.activation(norm[:, 1], norm2[:, 1], ACT.Sqrt).then_inc(norm_ready, 1)
                act.wait_ge(ones_ready, 2)
                act.activation(value[:, :, :, 1:], vectors(2, 0, seqs), ACT.Copy, scale=1.0 / POS).then_inc(value_ready, 1)
                for n in range(4):
                    act.wait_ge(kv_ready, n + 1)
                    act.activation(kv_turned[:, 4 * n:4 * n + 4], ps[n][:, 0:360].rearrange("p (s f) -> p s f", f=90), ACT.Copy).then_inc(kv_kept, 1)

                def keep_y(u):
                    act.wait_ge(y_ready, group * (u // 2) + group - 1 + u % 2)
                    if u >= 2:
                        act.wait_ge(y_done, u - 1)
                    act.activation(y[:, u % 2], ps[u % 4][:, :CHUNK], ACT.Copy).then_inc(y_kept, 1)

                for col in range(seqs):
                    if col % group == 2 and col >= group:
                        keep_y(2 * (col // group) - 2)
                        keep_y(2 * (col // group) - 1)
                    act.wait_ge(turned, col + 1)
                    if col >= 4:
                        act.wait_ge(y_ready, col - 3)
                    act.activation(phi_t[:, col % 4], ps[4 + col % 4][0:90, :CHUNK].rearrange("p (g n) -> p g n", g=4), ACT.Copy).then_inc(turned_kept, 1)
                keep_y(2 * CHUNKS - 2)
                keep_y(2 * CHUNKS - 1)

            @block.vector
            def _(dve):
                for j in range(TILES):
                    dve.wait_ge(qkv_ready, j + 1)
                    dve.tensor_tensor(qkv[:, :, j].rearrange("p i a f -> p i (a f)"), ps[j % 8][0:TILE, 0:384].rearrange("p (i f) -> p i f", i=3),
                                      w["tay_qkvb"][0:TILE, :].rearrange("p (i f) -> p i f", i=3), ALU.add).then_inc(qkv_kept, 1)
                dve.wait_ge(squared, 1)
                dve.tensor_reduce(norm2[:].rearrange("p i a h -> p (i a h)"), squares.rearrange("p i a (h e) -> p (i a h) e", e=hd), AX.X, ALU.add).then_inc(norm2_ready, 1)
                dve.wait_ge(norm_ready, 2)
                dve.tensor_scalar(norm[:], norm[:], eps, None, ALU.max).then_inc(norm_safe, 1)
                dve.wait_ge(norm_safe, 1)
                dve.reciprocal(norm2[:], norm[:]).then_inc(norm_inverse, 1)
                dve.wait_ge(norm_inverse, 1)
                dve.tensor_scalar(factor[:, 1], norm2[:, 1], scale, None, ALU.mult).then_inc(factor_ready, 1)
                dve.scalar_tensor_tensor(factor[:, 0], norm2[:, 0], scale * scale, w["tay_temp"][0:TILE, :].unsqueeze(1).to_broadcast([TILE, seqs, heads]),
                                         ALU.mult, ALU.mult).then_inc(factor_ready, 1)
                dve.wait_ge(factor_ready, 2)
                dve.wait_ge(ones_ready, 1)
                dve.tensor_tensor(phi_k[:, :, :, 36:44], vectors(1, 0, seqs), factor[:, 1].unsqueeze(3).to_broadcast([TILE, seqs, heads, hd]), ALU.mult).then_inc(key_unit, 1)
                dve.wait_ge(key_unit, 1)
                for n in range(2):
                    products(dve, phi_k[:, seqs // 2 * n:seqs // 2 * n + seqs // 2], seqs // 2, key_products)
                for n in range(4):
                    dve.wait_ge(kv_back, n + 1)
                    dve.tensor_tensor(kv[:, 4 * n:4 * n + 4], ps[4 + n][0:90, :].rearrange("p (s f) -> p s f", f=128),
                                      w["tay_coef"][0:90, :].unsqueeze(1).to_broadcast([90, 4, 128]), ALU.mult).then_inc(kv_masked, 1)

                def add_chunk(c):
                    dve.wait_ge(out_ready, 2 * c + 2)
                    dve.scalar_tensor_tensor(h[:, chunk(c)], ps[2 * (c % 2)][:, :CHUNK], w["tay_ob"], h[:, chunk(c)], ALU.add, ALU.add).then_inc(h_ready, 1)

                for u in range(2 * CHUNKS):
                    if u >= 2 and u % 2 == 0:
                        add_chunk(u // 2 - 1)
                    dve.wait_ge(sum_ready, u + 1)
                    dve.reciprocal(inverse[:, u % 2], ps[u % 4][:, :CHUNK]).then_inc(y_inverse, 1)
                    dve.wait_ge(y_inverse, u + 1)
                    if u >= 2:
                        dve.wait_ge(out_ready, u - u % 2)
                    dve.tensor_tensor(y_scaled[:, u % 2], y[:, u % 2], inverse[:, u % 2], ALU.mult).then_inc(y_done, 1)
                add_chunk(CHUNKS - 1)
                dve.wait_ge(h_ready, CHUNKS)

            @block.gpsimd
            def _(pool):
                pool.wait_ge(norm2_ready, 1)
                pool.memset(phi_k[:, :, :, 44:45], 1.0).then_inc(ones_ready, 1)
                pool.memset(value[:, :, :, 0:1], 1.0 / POS).then_inc(ones_ready, 1)
                pool.memset(value_wide[:, seqs * heads * (hd + 1):], 0.0).then_inc(ones_ready, 1)
                pool.memset(phi_q[:, 0, :, :, 44:45], 1.0).then_inc(ones_ready, 1)
                pool.memset(phi_q[:, 1, :, :, 44:45], 1.0).then_inc(ones_ready, 1)
                pool.wait_ge(factor_ready, 2)
                pool.wait_ge(ones_ready, 5)
                for n in range(seqs // group):
                    if n >= 2:
                        pool.wait_ge(turned, group * (n - 1))
                    lo = group * n
                    pool.tensor_tensor(phi_q[:, n % 2, :, :, 36:44], vectors(0, lo, group),
                                       factor[:, 0, lo:lo + group].unsqueeze(3).to_broadcast([TILE, group, heads, hd]), ALU.mult).then_inc(query_unit, 1)
                    pool.wait_ge(query_unit, n + 1)
                    products(pool, phi_q[:, n % 2], group, query_products)


def expert_routing(nc, x, w, ps, r):
    cols = 2 * TILES
    tokens = r["tokens"]
    with Stage(nc, "route") as s:
        token_major = s.sb("token_major", [TILE, cols, FEAT])
        logits = s.sb("logits", [TILE, cols, EXPERTS])
        best = s.sb("best", [TILE, cols, 8])
        best_at = s.sb("best_at", [TILE, cols, 8], U32)
        chosen = s.sb("chosen", [TILE, cols, 2])
        ratio = s.sb("ratio", [TILE, cols])
        denominator = s.sb("denominator", [TILE, cols])
        choice = [s.sb(f"choice{k}", [TILE, EXPERTS, cols], BF16) for k in range(2)]
        picked = s.sb("picked", [TILE, EXPERTS, cols], BF16)
        running = s.sb("running", [TILE, EXPERTS, cols], BF16)
        before = s.sb("before", [TILE, EXPERTS, cols], BF16)
        keep = s.sb("keep", [TILE, EXPERTS, cols], BF16)
        earlier = s.sb("earlier", [TILE, TILE], BF16)
        ones = s.sb("ones", [TILE, 128], BF16)
        rounded = s.sb("rounded", [128, EXPERTS], I32)
        shifted = s.sb("shifted", [128, EXPERTS], I32)
        tiles_of = s.sb("tiles_of", [128, EXPERTS])
        end_tile = s.sb("end_tile", [128, EXPERTS])
        first_slot = s.sb("first_slot", [128, EXPERTS])
        ended = s.sb("ended", [128, EXPERTS])
        expert_col = s.sb("expert_col", [128, 1])
        places = s.sb("places", [TILE, EXPERTS, cols])
        product = s.sb("product", [TILE, EXPERTS, cols])
        slot = s.sb("slot", [TILE, cols, 2])
        split_i = s.sb("split_i", [TILE, 2, cols * 2], I32)
        split = s.sb("split", [TILE, 2, cols * 2])
        lane_hot, tile_hot = (a[:].rearrange("p e a -> p (e a)").bitcast(BF16).rearrange("p (a l) -> p a l", a=cols) for a in (product, places))
        tile_high = s.sb("tile_high", [TILE, cols, 128], BF16)
        low_digit = s.sb("low_digit", [128, 128])
        combine = logits
        second = s.sb("second", [TILE, cols, EXPERTS])
        (logits_ready, logits_kept, token_ready, token_kept, best_ready, index_ready, chosen_ready, gap_ready, ratio_ready,
         gates_ready, hot_ready, picked_ready, consts_ready, running_ready, before_ready, counts_ready, count_steps, prefix_ready,
         places_ready, product_ready, slot_ready, split_ready, hot_tiles, source_ready, low_kept, expert_turned, expert_kept,
         combine_ready, combine_turned, combine_kept, stored) = (s.sem(n) for n in (
             "logits_ready logits_kept token_ready token_kept best_ready index_ready chosen_ready gap_ready ratio_ready "
             "gates_ready hot_ready picked_ready consts_ready running_ready before_ready counts_ready count_steps prefix_ready "
             "places_ready product_ready slot_ready split_ready hot_tiles source_ready low_kept expert_turned expert_kept "
             "combine_ready combine_turned combine_kept stored").split())
        with nc.Block() as block:

            @block.tensor
            def _(pe):
                for j in range(TILES):
                    mm = pe.matmul(ps[j // 4][0:TILE, 128 * (j % 4):128 * (j % 4) + 128], x[:, tile(j)], w["moe_r"], start=True, stop=True)
                    if j % 4 == 3:
                        mm.then_inc(logits_ready, 1)
                for j in range(TILES):
                    mm = pe.transpose(ps[4 + j // 4][0:TILE, 128 * (j % 4):128 * (j % 4) + 128], x[:, tile(j)], w["ident"])
                    if j % 4 == 3:
                        mm.then_inc(token_ready, 1)
                pe.wait_ge(consts_ready, 4)
                pe.wait_ge(running_ready, 1)
                pe.wait_ge(token_kept, 4)
                pe.matmul(ps[4][:, 0:EXPERTS], ones[:], running[:, :, cols - 1], start=True, stop=True).then_inc(counts_ready, 1)
                pe.wait_ge(before_ready, 1)
                for b in range(4):
                    pe.matmul(ps[b][0:TILE, :], earlier[:], picked[:, 16 * b:16 * b + 16, :].rearrange("p e a -> p (e a)"), start=True, stop=False)
                    pe.matmul(ps[b][0:TILE, :], ones[:, 0:TILE], before[:, 16 * b:16 * b + 16, :].rearrange("p e a -> p (e a)"), start=False, stop=True).then_inc(prefix_ready, 1)
                pe.wait_ge(count_steps, 8)
                pe.transpose(ps[4][0:1, 128:256], expert_col[:], w["ident"]).then_inc(expert_turned, 1)
                for half in range(2):
                    for d in range(2):
                        pe.wait_ge(hot_tiles, 4 * half + 3 + d)
                        for k in range(cols):
                            mm = pe.matmul(ps[5 + d][:, 0:128], lane_hot[:, k], (tile_high if d == 0 else tile_hot)[:, k],
                                           start=(half + k == 0), stop=(half == 1 and k == cols - 1))
                        mm.then_inc(source_ready, 1)
                pe.wait_ge(combine_ready, 3)
                pe.wait_ge(places_ready, 4)
                for j in range(TILES):
                    mm = pe.transpose(ps[j // 4][:, tile(j % 4)], combine[:, 2 * j:2 * j + 2].rearrange("p a e -> p (a e)"), w["ident"][0:TILE, 0:TILE])
                    if j % 4 == 3:
                        mm.then_inc(combine_turned, 1)

            @block.scalar
            def _(act):
                act.activation(earlier[:], w["moe_tri"][0:TILE, :], ACT.Copy).then_inc(consts_ready, 1)
                act.activation(ones[:], w["moe_ones"][0:TILE, :], ACT.Copy).then_inc(consts_ready, 1)
                for b in range(4):
                    act.wait_ge(token_ready, b + 1)
                    act.activation(token_major[:, 8 * b:8 * b + 8].rearrange("p a f -> p (a f)"), ps[4 + b][0:TILE, :], ACT.Copy).then_inc(token_kept, 1)
                act.wait_ge(gap_ready, 1)
                act.activation(ratio[:], ratio[:], ACT.Exp).then_inc(ratio_ready, 1)
                act.wait_ge(expert_turned, 1)
                act.activation(r["expert"][:], ps[4][0:1, 128:256], ACT.Copy).then_inc(expert_kept, 1)
                act.wait_ge(source_ready, 4)
                act.activation(low_digit[:], ps[6][:, 0:128], ACT.Copy).then_inc(low_kept, 1)
                for c in range(CHUNKS):
                    act.wait_ge(combine_turned, c + 1)
                    act.activation(r["combine_t"][:, chunk(c)], ps[c][:, :CHUNK], ACT.Copy).then_inc(combine_kept, 1)

            @block.vector
            def _(dve):
                for b in range(4):
                    dve.wait_ge(logits_ready, b + 1)
                    dve.tensor_tensor(logits[:, 8 * b:8 * b + 8], ps[b][0:TILE, :].rearrange("p (a e) -> p a e", e=EXPERTS),
                                      w["moe_br"][0:TILE, :].unsqueeze(1).to_broadcast([TILE, 8, EXPERTS]), ALU.add).then_inc(logits_kept, 1)
                dve.wait_ge(logits_kept, 4)
                for a in range(cols):
                    dve.max(best[:, a], logits[:, a]).then_inc(best_ready, 1)
                for a in range(cols):
                    dve.wait_ge(best_ready, a + 1)
                    dve.max_index(best_at[:, a], best[:, a], logits[:, a]).then_inc(index_ready, 1)
                dve.tensor_tensor(ratio[:].unsqueeze(2), best[:, :, 1:2], best[:, :, 0:1], ALU.subtract).then_inc(gap_ready, 1)
                dve.wait_ge(index_ready, cols)
                dve.tensor_copy(chosen[:], best_at[:, :, 0:2]).then_inc(chosen_ready, 1)
                dve.wait_ge(chosen_ready, 1)
                for k in range(2):
                    dve.tensor_tensor(choice[k][:], w["iota"][0:TILE, 0:EXPERTS].unsqueeze(2).to_broadcast([TILE, EXPERTS, cols]),
                                      chosen[:, :, k].unsqueeze(1).to_broadcast([TILE, EXPERTS, cols]), ALU.is_equal).then_inc(hot_ready, 1)
                dve.wait_ge(ratio_ready, 1)
                dve.tensor_scalar(denominator[:], ratio[:], 1.0, None, ALU.add).then_inc(gates_ready, 1)
                dve.wait_ge(gates_ready, 1)
                dve.reciprocal(r["gates"][:, 0], denominator[:]).then_inc(gates_ready, 1)
                dve.wait_ge(gates_ready, 2)
                dve.tensor_tensor(r["gates"][:, 1], r["gates"][:, 0], ratio[:], ALU.mult).then_inc(gates_ready, 1)
                dve.wait_ge(hot_ready, 2)
                dve.tensor_tensor(picked[:], choice[0][:], choice[1][:], ALU.add).then_inc(picked_ready, 1)
                dve.wait_ge(picked_ready, 1)
                dve.wait_ge(consts_ready, 4)
                dve.tensor_tensor_scan(running[:].rearrange("p e a -> p (e a)"), keep[:].rearrange("p e a -> p (e a)"),
                                       picked[:].rearrange("p e a -> p (e a)"), 0.0, ALU.mult, ALU.add).then_inc(running_ready, 1)
                dve.wait_ge(running_ready, 1)
                dve.tensor_tensor(before[:], running[:], picked[:], ALU.subtract).then_inc(before_ready, 1)
                dve.wait_ge(counts_ready, 1)
                dve.tensor_scalar(rounded[:], ps[4][:, 0:EXPERTS], 127.0, None, ALU.add).then_inc(count_steps, 1)
                dve.wait_ge(count_steps, 1)
                dve.tensor_scalar(shifted[:], rounded[:], 7, None, ALU.arith_shift_right).then_inc(count_steps, 1)
                dve.wait_ge(count_steps, 2)
                dve.tensor_copy(tiles_of[:], shifted[:]).then_inc(count_steps, 1)
                dve.wait_ge(count_steps, 3)
                dve.tensor_tensor_scan(end_tile[:], w["moe_ones"][:, 0:EXPERTS], tiles_of[:], 0.0, ALU.mult, ALU.add).then_inc(count_steps, 1)
                dve.wait_ge(count_steps, 4)
                dve.tensor_tensor(first_slot[:], end_tile[:], tiles_of[:], ALU.subtract).then_inc(count_steps, 1)
                dve.tensor_scalar(ended[:], end_tile[:], w["iota_p"], None, ALU.is_le, ALU.add, accum_out=expert_col[:]).then_inc(count_steps, 1)
                dve.wait_ge(count_steps, 6)
                dve.tensor_scalar(first_slot[:], first_slot[:], 128.0, None, ALU.mult).then_inc(count_steps, 1)
                dve.tensor_scalar(expert_col[:], expert_col[:], EXPERTS - 1.0, None, ALU.min).then_inc(count_steps, 1)
                dve.wait_ge(count_steps, 8)
                for b in range(4):
                    dve.wait_ge(prefix_ready, b + 1)
                    dve.tensor_tensor(places[:, 16 * b:16 * b + 16], ps[b][0:TILE, :].rearrange("p (e a) -> p e a", a=cols),
                                      first_slot[0:TILE, 16 * b:16 * b + 16].unsqueeze(2).to_broadcast([TILE, 16, cols]), ALU.add).then_inc(places_ready, 1)
                dve.wait_ge(places_ready, 4)
                for k in range(2):
                    if k:
                        dve.wait_ge(slot_ready, k)
                    dve.tensor_tensor(product[:], choice[k][:], places[:], ALU.mult).then_inc(product_ready, 1)
                    dve.wait_ge(product_ready, k + 1)
                    dve.tensor_reduce(slot[:, :, k], product[:].rearrange("p e a -> p a e"), AX.X, ALU.add).then_inc(slot_ready, 1)
                dve.wait_ge(slot_ready, 2)
                dve.tensor_copy(r["slot"][:], slot[:].rearrange("p a k -> p (a k)")).then_inc(slot_ready, 1)
                dve.wait_ge(slot_ready, 3)
                dve.tensor_scalar(split_i[:, 0], r["slot"][:], 127, None, ALU.bitwise_and).then_inc(split_ready, 1)
                dve.tensor_scalar(split_i[:, 1], r["slot"][:], 7, None, ALU.arith_shift_right).then_inc(split_ready, 1)
                dve.wait_ge(split_ready, 2)
                dve.tensor_copy(split[:], split_i[:]).then_inc(split_ready, 1)
                dve.wait_ge(split_ready, 3)
                iota = w["iota"][0:TILE, :].unsqueeze(1).to_broadcast([TILE, cols, 128])
                for half in range(2):
                    mine = slice(cols * half, cols * half + cols)
                    if half:
                        dve.wait_ge(source_ready, 2)
                    dve.tensor_tensor(lane_hot, iota, split[:, 0, mine].unsqueeze(2).to_broadcast([TILE, cols, 128]), ALU.is_equal).then_inc(hot_tiles, 1)
                    dve.tensor_tensor(tile_hot, iota, split[:, 1, mine].unsqueeze(2).to_broadcast([TILE, cols, 128]), ALU.is_equal).then_inc(hot_tiles, 1)
                    dve.wait_ge(hot_tiles, 4 * half + 2)
                    dve.tensor_scalar(tile_high[:], tile_hot, w["moe_high"][0:TILE, :], None, ALU.mult).then_inc(hot_tiles, 1)
                    dve.wait_ge(hot_tiles, 4 * half + 3)
                    dve.tensor_tensor(tile_hot, tile_hot, w["moe_low"][0:TILE, mine].unsqueeze(2).to_broadcast([TILE, cols, 128]), ALU.mult).then_inc(hot_tiles, 1)
                dve.wait_ge(low_kept, 1)
                dve.scalar_tensor_tensor(r["source"][:], ps[5][:, 0:128], 64.0, low_digit[:], ALU.mult, ALU.add).then_inc(source_ready, 1)
                dve.wait_ge(source_ready, 5)

            @block.gpsimd
            def _(pool):
                pool.memset(keep[:, :, 1:], 1.0).then_inc(consts_ready, 1)
                pool.memset(keep[:, :, 0:1], 0.0).then_inc(consts_ready, 1)
                pool.wait_ge(gates_ready, 3)
                pool.wait_ge(index_ready, cols)
                for k, dst in enumerate((combine, second)):
                    pool.tensor_tensor(dst[:], choice[k][:].rearrange("p e a -> p a e"),
                                       r["gates"][:, k].unsqueeze(2).to_broadcast([TILE, cols, EXPERTS]), ALU.mult).then_inc(combine_ready, 1)
                pool.wait_ge(combine_ready, 2)
                pool.tensor_tensor(combine[:], combine[:], second[:], ALU.add).then_inc(combine_ready, 1)

            @block.sync
            def _(sp):
                sp.wait_ge(token_kept, 4)
                sp.dma_start(tokens.rearrange("(n a) f -> n (a f)", a=cols), token_major[:].rearrange("p a f -> p (a f)")).then_inc(stored, 16)
                sp.wait_ge(stored, 16)

def expert_tables(nc, w, ps, r, experts_in):
    ring, group = 8, 4
    rounds = TABLE_TILES // ring
    with Stage(nc, "table") as s:
        rows_in = s.sb("rows_in", [128, 2, ring, FEAT])
        rows_t = s.sb("rows_t", [FEAT + 1, ring, 128])
        hidden = s.sb("hidden", [128, ring, 128])
        hidden_t = s.sb("hidden_t", [128, ring, 128])
        out = s.sb("out", [128, ring, FEAT])
        gathered = [s.pool_dma_sem(f"gathered{g}") for g in range(4)]
        rows_here = s.sem("rows_here")
        rows_turned, rows_kept, hidden_ready, hidden_kept, hidden_turned, hidden_t_kept, out_ready, out_kept, ones_ready = (
            s.sem(n) for n in "rows_turned rows_kept hidden_ready hidden_kept hidden_turned hidden_t_kept out_ready out_kept ones_ready".split())
        stored = [s.sem(f"stored{g}") for g in range(2)]
        w1, w2 = r["w1"], r["w2"]
        table = r["table"].rearrange("(t l) f -> l t f", l=128)
        with nc.Block() as block:

            @block.gpsimd
            def _(pool):
                for n in range(TABLE_TILES):
                    if n >= 2 * ring:
                        pool.wait_ge(rows_turned, (n - 2 * ring) // group + 1)
                    pool.indirect_dma_start(out=rows_in[:, n // ring % 2, n % ring, :], out_offset=None, in_=r["tokens"],
                                            in_offset=bass.IndirectOffsetOnAxis(ap=r["source"][:, n:n + 1], axis=0)).then_inc(gathered[n // group % 4], 16)

            @block.tensor
            def _(pe):

                def turn_rows(i, place):
                    for g in range(2):
                        pe.wait_ge(gathered[2 * place + g], (i - place) * (16 * group // 2) + 16 * group)
                        pe.sem_inc(rows_here, 1)
                        for k in range(group):
                            mm = pe.transpose(ps[g][0:FEAT, 128 * k:128 * k + 128], rows_in[:, place, group * g + k, :], w["ident"])
                        mm.then_inc(rows_turned, 1)

                def experts_of(i, step):
                    registers = [pe.alloc_register(f"{step}_expert{k}") for k in range(ring)]
                    pe.load(registers, r["expert"][0:1, bass.ds(i * ring, ring)])
                    return registers, [bass.RuntimeValue.of_register_unchecked(reg, min_val=0, max_val=EXPERTS - 1) for reg in registers]

                def first_product(i, step):
                    registers, expert = experts_of(i, step)
                    for g in range(2):
                        pe.wait_ge(rows_kept, i * 2 + (g + 1))
                        for k in range(group):
                            mm = pe.matmul(ps[2 + g][:, 128 * k:128 * k + 128], rows_t[:, group * g + k, :], w1[:, bass.ds(expert[group * g + k] * 128, 128)], start=True, stop=True)
                        mm.then_inc(hidden_ready, 1)
                    for reg in registers:
                        pe.free_register(reg)

                def turn_hidden(i):
                    for g in range(2):
                        pe.wait_ge(hidden_kept, i * 2 + (g + 1))
                        for k in range(group):
                            mm = pe.transpose(ps[4 + g][:, 128 * k:128 * k + 128], hidden[:, group * g + k, :], w["ident"])
                        mm.then_inc(hidden_turned, 1)

                def second_product(i, step):
                    registers, expert = experts_of(i, step)
                    for g in range(2):
                        pe.wait_ge(hidden_t_kept, i * 2 + (g + 1))
                        pe.wait_ge(out_kept, i * 2 + (g + 1))
                        for k in range(group):
                            mm = pe.matmul(ps[6 + g][:, FEAT * k:FEAT * k + FEAT], hidden_t[:, group * g + k, :], w2[:, bass.ds(expert[group * g + k] * FEAT, FEAT)], start=True, stop=True)
                        mm.then_inc(out_ready, 1)
                    for reg in registers:
                        pe.free_register(reg)

                def round_(i, place, step):
                    turn_rows(i, place)
                    turn_hidden(i - 1)
                    first_product(i, f"{step}_first")
                    second_product(i - 1, f"{step}_second")

                pe.wait_ge(experts_in, 32)
                pe.wait_ge(ones_ready, 1)
                turn_rows(0, 0)
                first_product(0, "start_first")
                with pe.Fori(0, rounds // 2 - 1) as m:
                    round_(m * 2 + 1, 1, "odd")
                    round_(m * 2 + 2, 0, "even")
                round_(rounds - 1, 1, "last")
                turn_hidden(rounds - 1)
                second_product(rounds - 1, "end_second")

            @block.vector
            def _(dve):
                dve.memset(rows_t[FEAT:FEAT + 1], 1.0).then_inc(ones_ready, 1)

                def keep_rows(i):
                    for g in range(2):
                        dve.wait_ge(rows_turned, i * 2 + (g + 1))
                        dve.tensor_copy(rows_t[0:FEAT, group * g:group * g + group, :], ps[g][0:FEAT, :].rearrange("p (k n) -> p k n", k=group)).then_inc(rows_kept, 1)

                def keep_hidden(i):
                    for g in range(2):
                        dve.wait_ge(hidden_turned, i * 2 + (g + 1))
                        dve.tensor_copy(hidden_t[:, group * g:group * g + group, :], ps[4 + g][:].rearrange("p (k n) -> p k n", k=group)).then_inc(hidden_t_kept, 1)

                keep_rows(0)
                with dve.Fori(1, rounds) as i:
                    keep_rows(i)
                    keep_hidden(i - 1)
                keep_hidden(rounds - 1)

            @block.scalar
            def _(act):

                def relu(i):
                    for g in range(2):
                        act.wait_ge(hidden_ready, i * 2 + (g + 1))
                        act.activation(hidden[:, group * g:group * g + group, :], ps[2 + g][:].rearrange("p (k n) -> p k n", k=group), ACT.Relu).then_inc(hidden_kept, 1)

                def keep_out(i):
                    for g in range(2):
                        act.wait_ge(out_ready, i * 2 + (g + 1))
                        act.wait_ge(stored[g], i * 16 + 16)
                        act.activation(out[:, group * g:group * g + group, :], ps[6 + g][:, 0:group * FEAT].rearrange("p (k n) -> p k n", k=group), ACT.Copy).then_inc(out_kept, 1)

                act.sem_inc(out_kept, 2)
                relu(0)
                with act.Fori(1, rounds) as i:
                    relu(i)
                    keep_out(i - 1)
                keep_out(rounds - 1)

            @block.sync
            def _(sp):
                for g in range(2):
                    sp.sem_inc(stored[g], 16)
                with sp.Fori(0, rounds) as i:
                    for g in range(2):
                        sp.wait_ge(out_kept, i * 2 + (g + 3))
                        sp.dma_start(table[:, bass.ds(ring * i + group * g, group), :], out[:, group * g:group * g + group, :]).then_inc(stored[g], 16)
                for g in range(2):
                    sp.wait_ge(stored[g], 16 * (rounds) + 16)


def expert_sum(nc, h, w, ps, r):
    cols = 2 * TILES
    with Stage(nc, "sum") as s:
        rows_in = s.sb("rows_in", [TILE, cols, 2, FEAT])
        total = s.sb("total", [TILE, cols, FEAT])
        gathered = [s.pool_dma_sem(f"gathered{c}") for c in range(CHUNKS)]
        scaled, total_ready, out_ready, h_ready = s.sem("scaled"), s.sem("total_ready"), s.sem("out_ready"), s.sem("h_ready")
        with nc.Block() as block:

            @block.gpsimd
            def _(pool):
                for a in range(cols):
                    for k in range(2):
                        n = 2 * a + k
                        pool.indirect_dma_start(out=rows_in[:, a, k, :], out_offset=None, in_=r["table"],
                                                in_offset=bass.IndirectOffsetOnAxis(ap=r["slot"][:, n:n + 1].bitcast(U32), axis=0)).then_inc(gathered[a // 8], 16)

            @block.vector
            def _(dve):
                for c in range(CHUNKS):
                    mine = slice(8 * c, 8 * c + 8)
                    dve.wait_ge(gathered[c], 256)
                    for k in range(2):
                        dve.tensor_tensor(rows_in[:, mine, k], rows_in[:, mine, k], r["gates"][:, k, mine].unsqueeze(2).to_broadcast([TILE, 8, FEAT]), ALU.mult).then_inc(scaled, 1)
                    dve.wait_ge(scaled, 2 * c + 2)
                    dve.tensor_tensor(total[:, mine], rows_in[:, mine, 0], rows_in[:, mine, 1], ALU.add).then_inc(total_ready, 1)
                    dve.wait_ge(out_ready, c + 1)
                    dve.tensor_tensor(h[:, chunk(c)], h[:, chunk(c)], ps[c][:, :CHUNK], ALU.add).then_inc(h_ready, 1)
                dve.wait_ge(h_ready, CHUNKS)

            @block.tensor
            def _(pe):
                for c in range(CHUNKS):
                    pe.matmul(ps[c][:, :CHUNK], w["moe_b2"], r["combine_t"][:, chunk(c)], start=True, stop=False, skip_group_check=True)
                for c in range(CHUNKS):
                    pe.wait_ge(total_ready, c + 1)
                    for k in range(4):
                        j = 4 * c + k
                        mm = pe.matmul(ps[c][:, tile(k)], total[:, 2 * j:2 * j + 2].rearrange("p a f -> p (a f)"), w["ident"][0:TILE, 0:TILE],
                                       start=False, stop=(k == 3), skip_group_check=True)
                    mm.then_inc(out_ready, 1)


def expert_ffn(nc, h, x, w, ps, d):
    cols = 2 * TILES
    with Stage(nc, "moe") as s:
        r = {
            "tokens": d["tokens"], "table": d["table"],
            "w1": s.sb("w1", [FEAT + 1, EXPERTS * 128]), "w2": s.sb("w2", [128, EXPERTS * FEAT]),
            "source": s.sb("source", [128, TABLE_TILES], U32), "expert": s.sb("expert", [1, TABLE_TILES], I32),
            "slot": s.sb("slot", [TILE, cols * 2], I32), "gates": s.sb("gates", [TILE, 2, cols]),
            "combine_t": s.sb("combine_t", [128, COLS]),
        }
        experts_in = s.sem("experts_in")
        with nc.Block() as block:

            @block.sync
            def _(sp):
                sp.dma_start(r["w1"][:], d["experts1"]).then_inc(experts_in, 16)
                sp.dma_start(r["w2"][:], d["experts2"]).then_inc(experts_in, 16)

        expert_routing(nc, x, w, ps, r)
        expert_tables(nc, w, ps, r, experts_in)
        expert_sum(nc, h, w, ps, r)


def retention(nc, h, x, w, ps):
    wide = POS + TILE
    with Stage(nc, "ret") as s:
        query = s.sb("query", [128, COLS])
        key = s.sb("key", [128, COLS])
        turned = s.sb("turned", [128, 2, COLS])
        value = s.sb("value", [TILE, TILES, 128])
        kept = s.sb("kept", [TILE, 4, wide])
        (q_ready, q_scaled, rotated, value_ready, value_kept, score_ready, score_kept, out_ready, h_ready) = (
            s.sem(n) for n in "q_ready q_scaled rotated value_ready value_kept score_ready score_kept out_ready h_ready".split())
        with nc.Block() as block:

            @block.tensor
            def _(pe):
                for i, n in enumerate("qk"):
                    for c in range(CHUNKS):
                        if i:
                            pe.wait_ge(q_scaled, 2 * c + 2)
                        pe.matmul(ps[c][:, :CHUNK], w["ret_" + n], x[:, chunk(c)], start=True, stop=True)
                        pe.matmul(ps[4 + c][:, :CHUNK], w["ret_" + n + "s"], x[:, chunk(c)], start=True, stop=True).then_inc(q_ready, 1)
                for b in range(4):
                    pe.wait_ge(q_scaled, 8 + 2 * b + 2)
                    for k in range(4):
                        mm = pe.matmul(ps[b][0:TILE, 128 * k:128 * k + 128], x[:, tile(4 * b + k)], w["ret_v"], start=True, stop=True)
                    mm.then_inc(value_ready, 1)
                pe.wait_ge(rotated, 8)
                pe.wait_ge(value_kept, 4)

                def scores(q):
                    p, a = q // 2, q % 2
                    if q >= 4:
                        pe.wait_ge(score_kept, q - 3)
                    half = slice(64 * a, 64 * a + 64)
                    at = POS * p
                    pe.matmul(ps[4 + q % 4][0:TILE, 0:POS], key[half, tile(2 * p)], query[half, at:at + POS], start=True, stop=True)
                    pe.matmul(ps[4 + q % 4][0:TILE, POS:wide], key[half, tile(2 * p + 1)], query[half, at + TILE:at + POS], start=True, stop=True).then_inc(score_ready, 1)

                def outputs(q):
                    p, a = q // 2, q % 2
                    pe.wait_ge(score_kept, q + 1)
                    dst = ps[p // 2][64 * a:64 * a + 64, POS * (p % 2):POS * (p % 2) + POS]
                    pe.matmul(dst, value[:, 2 * p, 64 * a:64 * a + 64], kept[:, q % 4, 0:POS], start=True, stop=False)
                    pe.matmul(dst[:, TILE:], value[:, 2 * p + 1, 64 * a:64 * a + 64], kept[:, q % 4, POS:wide], start=False, stop=True).then_inc(out_ready, 1)

                for q in range(SEQS):
                    scores(q)
                    if q >= 2:
                        outputs(q - 2)
                outputs(SEQS - 2)
                outputs(SEQS - 1)

            @block.scalar
            def _(act):
                for b in range(4):
                    act.wait_ge(value_ready, b + 1)
                    act.activation(value[:, 4 * b:4 * b + 4], ps[b][0:TILE, :].rearrange("p (k f) -> p k f", k=4), ACT.Copy).then_inc(value_kept, 1)

            @block.vector
            def _(dve):
                for i, dst in enumerate((query, key)):
                    for c in range(CHUNKS):
                        dve.wait_ge(q_ready, 4 * i + c + 1)
                        if i:
                            dve.wait_ge(rotated, c + 1)
                        for k, src in enumerate((ps[c], ps[4 + c])):
                            table = w["ret_table"][:, POS * (2 * i + k):POS * (2 * i + k) + POS].unsqueeze(1).to_broadcast([128, 2, POS])
                            out = (dst if k == 0 else turned[:, 0])[:, chunk(c)].rearrange("p (b n) -> p b n", b=2)
                            dve.tensor_tensor(out, src[:, :CHUNK].rearrange("p (b n) -> p b n", b=2), table, ALU.mult).then_inc(q_scaled, 1)
                for q in range(SEQS):
                    dve.wait_ge(score_ready, q + 1)
                    if q >= 4:
                        dve.wait_ge(out_ready, q - 3)
                    dve.tensor_tensor(kept[:, q % 4], ps[4 + q % 4][0:TILE, 0:wide], w["ret_decay"][0:TILE, :], ALU.mult).then_inc(score_kept, 1)
                for c in range(CHUNKS):
                    dve.wait_ge(out_ready, 4 * c + 4)
                    dve.tensor_tensor(h[:, chunk(c)], h[:, chunk(c)], ps[c][:, :CHUNK], ALU.add).then_inc(h_ready, 1)
                dve.wait_ge(h_ready, CHUNKS)

            @block.gpsimd
            def _(pool):
                for i, dst in enumerate((query, key)):
                    for c in range(CHUNKS):
                        pool.wait_ge(q_scaled, 2 * (4 * i + c) + 2)
                        pool.tensor_tensor(dst[:, chunk(c)], dst[:, chunk(c)], turned[:, 0, chunk(c)], ALU.add).then_inc(rotated, 1)


def soft_mixture(nc, h, x, w, ps):
    experts = 8
    with Stage(nc, "mixture") as s:
        feat = s.sb("feat", [128, POS])
        gate = s.sb("gate", [TILE, 2, experts])
        gate_tmp = s.sb("gate_tmp", [TILE, 2, experts])
        top = s.sb("top", [TILE, 2])
        total = s.sb("total", [TILE, 2])
        inverse = s.sb("inverse", [TILE, 2])
        gate_f = s.sb("gate_f", [128, experts, POS])
        gate_t = s.sb("gate_t", [experts, POS])
        bias = s.sb("bias", [128, POS])
        root = s.sb("root", [128, 2, experts])
        scale = s.sb("scale", [128, 2, experts])
        shift = s.sb("shift", [128, 2, experts])
        hidden = s.sb("hidden", [128, 2, 4, CHUNK])
        (feat_ready, logits_ready, gate_steps, exp_ready, gate_spread, gate_kept, gate_turned, gate_t_kept, bias_ready, bias_kept,
         root_ready, scale_steps, up_ready, up_kept, mid_ready, mid_kept, gated, out_ready, h_ready) = (s.sem(n) for n in (
             "feat_ready logits_ready gate_steps exp_ready gate_spread gate_kept gate_turned gate_t_kept bias_ready bias_kept "
             "root_ready scale_steps up_ready up_kept mid_ready mid_kept gated out_ready h_ready").split())
        steps = experts * CHUNKS

        def norm(name, layer):
            at = experts * (2 * "g b m v e".split().index(name) + layer)
            return w["bn"][:, at:at + experts]

        with nc.Block() as block:

            @block.tensor
            def _(pe):
                pe.wait_ge(feat_ready, 1)
                for t in range(2):
                    mm = pe.matmul(ps[0][0:TILE, 8 * t:8 * t + 8], feat[:, tile(t)], w["soft_r"], start=True, stop=True)
                mm.then_inc(logits_ready, 1)
                pe.wait_ge(gate_steps, 6)
                for b in range(4):
                    for k in range(4):
                        mm = pe.transpose(ps[4 + b][:, tile(k)], gate[:, k % 2, 2 * b + k // 2].unsqueeze(1).to_broadcast([TILE, 128]), w["ident"][0:TILE, 0:TILE])
                    mm.then_inc(gate_spread, 1)
                for t in range(2):
                    mm = pe.transpose(ps[1][0:experts, tile(t)], gate[:, t], w["ident"][0:TILE, 0:TILE])
                mm.then_inc(gate_turned, 1)
                pe.wait_ge(gate_t_kept, 1)
                pe.matmul(ps[2][:, 0:POS], w["soft_bo"][0:experts, :], gate_t[:], start=True, stop=True).then_inc(bias_ready, 1)
                pe.wait_ge(gate_kept, 4)
                pe.wait_ge(bias_kept, 1)

                def first(n):
                    if n >= 2:
                        pe.wait_ge(up_kept, n - 1)
                    pe.matmul(ps[4 + n % 2][:, :CHUNK], w["soft_1"][:, 128 * (n // 4):128 * (n // 4) + 128], x[:, chunk(n % 4)], start=True, stop=True).then_inc(up_ready, 1)

                def second(n):
                    pe.wait_ge(up_kept, n + 1)
                    if n >= 2:
                        pe.wait_ge(mid_kept, n - 1)
                    pe.matmul(ps[6 + n % 2][:, :CHUNK], w["soft_2"][:, 128 * (n // 4):128 * (n // 4) + 128], hidden[:, 0, n % 4], start=True, stop=True).then_inc(mid_ready, 1)

                def third(n):
                    pe.wait_ge(gated, n + 1)
                    pe.matmul(ps[n % 4][:, :CHUNK], w["soft_3"][:, 128 * (n // 4):128 * (n // 4) + 128], hidden[:, 1, n % 4],
                              start=(n < 4), stop=(n >= steps - 4)).then_inc(out_ready, 1)

                for n in range(steps + 3):
                    if n < steps:
                        first(n)
                    if 1 <= n <= steps:
                        second(n - 1)
                    if n >= 3:
                        third(n - 3)

            @block.scalar
            def _(act):
                for layer in range(2):
                    act.activation(root[:, layer], norm("v", layer), ACT.Sqrt, bias=w["bn_eps"]).then_inc(root_ready, 1)
                act.wait_ge(gate_steps, 3)
                act.activation(gate_tmp[:], gate_tmp[:], ACT.Exp).then_inc(exp_ready, 1)
                for b in range(4):
                    act.wait_ge(gate_spread, b + 1)
                    act.activation(gate_f[:, 2 * b:2 * b + 2].rearrange("p e n -> p (e n)"), ps[4 + b][:, :CHUNK], ACT.Copy).then_inc(gate_kept, 1)
                act.wait_ge(gate_turned, 1)
                act.activation(gate_t[:], ps[1][0:experts, 0:POS], ACT.Copy).then_inc(gate_t_kept, 1)
                act.wait_ge(bias_ready, 1)
                act.activation(bias[:], ps[2][:, 0:POS], ACT.Copy).then_inc(bias_kept, 1)
                act.wait_ge(scale_steps, 8)

                def first(n):
                    e = n // 4
                    act.wait_ge(up_ready, n + 1)
                    if n >= 4:
                        act.wait_ge(mid_ready, n - 3)
                    act.activation(hidden[:, 0, n % 4], ps[4 + n % 2][:, :CHUNK], ACT.Relu, bias=shift[:, 0, e:e + 1], scale=scale[:, 0, e:e + 1]).then_inc(up_kept, 1)

                def second(n):
                    e = n // 4
                    act.wait_ge(mid_ready, n + 1)
                    if n >= 4:
                        act.wait_ge(out_ready, n - 3)
                    act.activation(hidden[:, 1, n % 4], ps[6 + n % 2][:, :CHUNK], ACT.Relu, bias=shift[:, 1, e:e + 1], scale=scale[:, 1, e:e + 1]).then_inc(mid_kept, 1)

                for n in range(steps + 1):
                    if n < steps:
                        first(n)
                    if n >= 1:
                        second(n - 1)

            @block.vector
            def _(dve):
                dve.tensor_reduce(feat[:], x[:].rearrange("q (p n) -> q n p", n=POS), AX.X, ALU.add).then_inc(feat_ready, 1)
                dve.wait_ge(root_ready, 2)
                dve.reciprocal(scale[:], root[:]).then_inc(scale_steps, 1)
                dve.wait_ge(scale_steps, 1)
                for layer in range(2):
                    dve.tensor_tensor(root[:, layer], scale[:, layer], norm("g", layer), ALU.mult).then_inc(scale_steps, 1)
                    dve.tensor_tensor(shift[:, layer], norm("b", layer), norm("m", layer), ALU.subtract).then_inc(scale_steps, 1)
                dve.wait_ge(scale_steps, 5)
                dve.tensor_tensor(shift[:], shift[:], root[:], ALU.mult).then_inc(scale_steps, 1)
                dve.tensor_copy(scale[:], root[:]).then_inc(scale_steps, 1)
                dve.wait_ge(scale_steps, 7)
                dve.tensor_tensor(shift[:], shift[:], w["bn"][:, 8 * experts:10 * experts].rearrange("p (l e) -> p l e", l=2), ALU.add).then_inc(scale_steps, 1)
                dve.wait_ge(logits_ready, 1)
                dve.scalar_tensor_tensor(gate[:], ps[0][0:TILE, 0:16].rearrange("p (t e) -> p t e", t=2), 1.0 / SEQS,
                                         w["soft_br"][0:TILE, :].unsqueeze(1).to_broadcast([TILE, 2, experts]), ALU.mult, ALU.add).then_inc(gate_steps, 1)
                dve.wait_ge(gate_steps, 1)
                dve.tensor_reduce(top[:], gate[:], AX.X, ALU.max).then_inc(gate_steps, 1)
                dve.wait_ge(gate_steps, 2)
                dve.tensor_tensor(gate_tmp[:], gate[:], top[:].unsqueeze(2).to_broadcast([TILE, 2, experts]), ALU.subtract).then_inc(gate_steps, 1)
                dve.wait_ge(exp_ready, 1)
                dve.tensor_reduce(total[:], gate_tmp[:], AX.X, ALU.add).then_inc(gate_steps, 1)
                dve.wait_ge(gate_steps, 4)
                dve.reciprocal(inverse[:], total[:]).then_inc(gate_steps, 1)
                dve.wait_ge(gate_steps, 5)
                dve.tensor_tensor(gate[:], gate_tmp[:], inverse[:].unsqueeze(2).to_broadcast([TILE, 2, experts]), ALU.mult).then_inc(gate_steps, 1)
                dve.wait_ge(gate_kept, 4)
                for n in range(steps):
                    dve.wait_ge(mid_kept, n + 1)
                    hid = hidden[:, 1, n % 4].rearrange("p (b n) -> p b n", b=2)
                    dve.tensor_tensor(hid, hid, gate_f[:, n // 4].unsqueeze(1).to_broadcast([128, 2, POS]), ALU.mult).then_inc(gated, 1)
                dve.wait_ge(bias_kept, 1)
                for c in range(CHUNKS):
                    dve.wait_ge(out_ready, steps - 3 + c)
                    dve.tensor_tensor(h[:, chunk(c)], h[:, chunk(c)], ps[c][:, :CHUNK], ALU.add).then_inc(h_ready, 1)
                dve.wait_ge(h_ready, CHUNKS)
                dve.tensor_tensor(h[:].rearrange("p (b n) -> p b n", n=POS), h[:].rearrange("p (b n) -> p b n", n=POS),
                                  bias[:].unsqueeze(1).to_broadcast([128, PAIRS, POS]), ALU.add).then_inc(h_ready, 1)
                dve.wait_ge(h_ready, CHUNKS + 1)


def relative_attention(nc, h, x, w, ps):
    heads, hd, reach, near = 4, 16, 30, TILE + 29
    first_near = [0, POS - near]
    with Stage(nc, "rel") as s:
        mixed = s.sb("mixed", [128, 2, COLS])
        xg, query_v = mixed[:, 0], mixed[:, 1]
        query_u = s.sb("query_u", [128, heads, COLS])
        key = s.sb("key", [128, 2, COLS])
        value = s.sb("value", [TILE, TILES, 2 * heads, 2 * hd])
        turn_a = s.sb("turn_a", [128, heads, COLS])
        turn_b = s.sb("turn_b", [128, 2, CHUNK])
        bias_u = s.sb("bias_u", [128, heads])
        bias_v = s.sb("bias_v", [128, 1])
        edge_w = s.sb("edge_w", [128, 3])
        edge_wide = s.sb("edge_wide", [128, 3, 8])
        edge = s.sb("edge", [TILE, TILES, 3, 8])
        shift = s.sb("shift", [TILE, TILES, 8])
        right = s.sb("right", [TILE, TILES, 8])
        near_b = [s.sb(f"near{t}", [TILE, 2, heads, POS]) for t in range(2)]
        near_raw = s.sb("near_raw", [TILE, 2, heads, near])
        scores = s.sb("scores", [TILE, 3, heads, POS])
        top = s.sb("top", [TILE, 3, heads])
        total = s.sb("total", [TILE, 3, heads])
        inverse = s.sb("inverse", [TILE, 3, heads])
        probs_t = s.sb("probs_t", [TILE, 2, 2, 4 * TILE])
        (x_ready, biases, bias_turned, edge_w_ready, edge_steps, q_ready, q_kept, k_ready, k_kept, v_ready, v_kept, edge_ready,
         edge_kept, edge_done, turn_ready, turn_scaled, turned, zeroed, value_zeroed, keys_zeroed) = (s.sem(n) for n in (
             "x_ready biases bias_turned edge_w_ready edge_steps q_ready q_kept k_ready k_kept v_ready v_kept edge_ready "
             "edge_kept edge_done turn_ready turn_scaled turned zeroed value_zeroed keys_zeroed").split())
        (dot_ready, near_ready, near_out, near_kept, far_added, score_kept, top_ready, exp_ready, prob_ready, prob_turned, prob_kept,
         mixed_ready, inverse_ready, mixed_kept, out_ready, h_ready) = (s.sem(n) for n in (
             "dot_ready near_ready near_out near_kept far_added score_kept top_ready exp_ready prob_ready prob_turned prob_kept "
             "mixed_ready inverse_ready mixed_kept out_ready h_ready").split())
        with nc.Block() as block:

            @block.tensor
            def _(pe):
                pe.matmul(ps[7][:, 0:2], w["rel_pos_t"], w["rel_ends"], start=True, stop=True).then_inc(edge_w_ready, 1)
                pe.wait_ge(x_ready, CHUNKS)
                for c in range(CHUNKS):
                    pe.matmul(ps[c][:, :CHUNK], w["rel_q"], xg[:, chunk(c)], start=True, stop=True).then_inc(q_ready, 1)
                for c in range(CHUNKS):
                    if c == 3:
                        pe.wait_ge(edge_steps, 1)
                    pe.matmul(ps[4 + c][:, :CHUNK], w["rel_k"], xg[:, chunk(c)], start=True, stop=True).then_inc(k_ready, 1)
                for b in range(4):
                    pe.wait_ge(k_kept, 2 * b + 2)
                    for k in range(4):
                        mm = pe.matmul(ps[4 + b][0:TILE, 128 * k:128 * k + 128], xg[:, tile(4 * b + k)], w["rel_v"], start=True, stop=True)
                    mm.then_inc(v_ready, 1)
                pe.wait_ge(q_kept, 5 * CHUNKS)
                pe.wait_ge(edge_steps, 5)
                for j in range(TILES):
                    mm = pe.matmul(ps[0][0:TILE, 24 * j:24 * j + 24], query_v[:, tile(j)], edge_wide[:].rearrange("p i e -> p (i e)"), start=True, stop=True)
                mm.then_inc(edge_ready, 1)
                pe.wait_ge(v_kept, 4)
                for n in range(heads * CHUNKS):
                    hh, c = n // CHUNKS, n % CHUNKS
                    if n >= 3:
                        pe.wait_ge(turn_scaled, 2 * (n - 3) + 2)
                    pe.matmul(ps[1 + 2 * (n % 3)][:, :CHUNK], w["rel_pos"][:, 128 * hh:128 * hh + 128], query_v[:, chunk(c)], start=True, stop=True)
                    pe.matmul(ps[2 + 2 * (n % 3)][:, :CHUNK], w["rel_pos_s"][:, 128 * hh:128 * hh + 128], query_v[:, chunk(c)], start=True, stop=True).then_inc(turn_ready, 1)

            @block.scalar
            def _(act):
                for c in range(CHUNKS):
                    act.activation(xg[:, chunk(c)], x[:, chunk(c)], ACT.Identity, scale=w["rel_gamma"], bias=w["rel_beta"]).then_inc(x_ready, 1)
                act.wait_ge(biases, 3)
                for c in range(CHUNKS):
                    act.wait_ge(q_ready, c + 1)
                    for hh in range(heads):
                        act.activation(query_u[:, hh, chunk(c)], ps[c][:, :CHUNK], ACT.Identity, scale=w["rel_head"][:, hh:hh + 1], bias=bias_u[:, hh:hh + 1]).then_inc(q_kept, 1)
                    act.activation(query_v[:, chunk(c)], ps[c][:, :CHUNK], ACT.Identity, scale=float(hd) ** -0.5, bias=bias_v[:]).then_inc(q_kept, 1)

            @block.vector
            def _(dve):
                dve.tensor_scalar(bias_u[:], w["rel_head"], w["rel_qu"][:, 0:1], None, ALU.mult).then_inc(biases, 1)
                dve.wait_ge(biases, 1)
                dve.scalar_tensor_tensor(bias_u[:], w["rel_head"], w["rel_qu"][:, 1:2], bias_u[:], ALU.mult, ALU.add).then_inc(biases, 1)
                dve.tensor_scalar(bias_v[:], w["rel_qu"][:, 0:1], w["rel_qu"][:, 2:3], float(hd) ** -0.5, ALU.add, ALU.mult).then_inc(biases, 1)
                dve.wait_ge(edge_w_ready, 1)
                dve.tensor_tensor(edge_w[:, 0:2], ps[7][:, 0:2], w["rel_posb"].to_broadcast([128, 2]), ALU.add).then_inc(edge_steps, 1)
                dve.tensor_copy(edge_w[:, 2:3], w["rel_posb"]).then_inc(edge_steps, 1)
                dve.wait_ge(edge_steps, 2)
                for i in range(3):
                    dve.tensor_scalar(edge_wide[:, i], w["rel_head8"], edge_w[:, i:i + 1], None, ALU.mult).then_inc(edge_steps, 1)
                for c in range(CHUNKS):
                    dve.wait_ge(k_ready, c + 1)
                    if c == 0:
                        dve.wait_ge(keys_zeroed, 1)
                    for a in range(2):
                        half = slice(64 * a, 64 * a + 64)
                        dve.tensor_scalar(key[half, a, chunk(c)], ps[4 + c][half, :CHUNK], w["rel_kb"][half, :], None, ALU.add).then_inc(k_kept, 1)
                for b in range(4):
                    dve.wait_ge(v_ready, b + 1)
                    if b == 0:
                        dve.wait_ge(value_zeroed, 1)
                    dve.tensor_tensor(value[:, 4 * b:4 * b + 4, :, 0:hd], ps[4 + b][0:TILE, :].rearrange("p (k g e) -> p k g e", k=4, e=hd),
                                      w["rel_vb"][0:TILE, :].rearrange("p (g e) -> p g e", e=hd).unsqueeze(1).to_broadcast([TILE, 4, 2 * heads, hd]), ALU.add).then_inc(v_kept, 1)
                dve.wait_ge(edge_ready, 1)
                dve.tensor_copy(edge[:].rearrange("p j i e -> p (j i e)"), ps[0][0:TILE, 0:24 * TILES]).then_inc(edge_kept, 1)
                dve.wait_ge(edge_kept, 1)
                dve.tensor_tensor(right[:], edge[:, :, 1], edge[:, :, 0], ALU.subtract).then_inc(edge_done, 1)
                dve.tensor_tensor(shift[:], edge[:, :, 2], edge[:, :, 0], ALU.subtract).then_inc(edge_done, 1)
                for n in range(heads * CHUNKS):
                    hh, c = n // CHUNKS, n % CHUNKS
                    dve.wait_ge(turn_ready, n + 1)
                    if n >= 2:
                        dve.wait_ge(turned, n - 1)
                    for k in range(2):
                        table = w["rel_t"][:, POS * k:POS * k + POS].unsqueeze(1).to_broadcast([128, 2, POS])
                        out = turn_a[:, hh, chunk(c)] if k == 0 else turn_b[:, n % 2]
                        dve.tensor_tensor(out.rearrange("p (b n) -> p b n", b=2), ps[1 + k + 2 * (n % 3)][:, :CHUNK].rearrange("p (b n) -> p b n", b=2),
                                          table, ALU.mult).then_inc(turn_scaled, 1)
                dve.wait_ge(edge_done, 2)

            @block.gpsimd
            def _(pool):
                pool.memset(key[:], 0.0).then_inc(keys_zeroed, 1)
                pool.memset(value[:], 0.0).then_inc(value_zeroed, 1)
                for t in range(2):
                    pool.memset(near_b[t][:], 0.0).then_inc(zeroed, 1)
                for n in range(heads * CHUNKS):
                    hh, c = n // CHUNKS, n % CHUNKS
                    pool.wait_ge(turn_scaled, 2 * n + 2)
                    pool.tensor_tensor(turn_a[:, hh, chunk(c)], turn_a[:, hh, chunk(c)], turn_b[:, n % 2], ALU.add).then_inc(turned, 1)
                pool.wait_ge(zeroed, 2)

        units = 2 * SEQS
        unit = [(u // 4, u % 2, (u // 2) % 2) for u in range(units)]
        with nc.Block() as block:

            @block.tensor
            def _(pe):

                def dots(u):
                    p, a, t = unit[u]
                    for hh in range(heads):
                        if u and hh % 2 == 0:
                            pe.wait_ge(near_out, heads * (u - 1) + hh + 2)
                        pe.matmul(ps[2 + hh // 2][0:TILE, near * (hh % 2):near * (hh % 2) + near], turn_a[:, hh, tile(2 * p + t)],
                                  w["rel_s"][:, POS * a + first_near[t]:POS * a + first_near[t] + near], start=True, stop=True).then_inc(near_ready, 1)
                    for hh in range(heads):
                        if u and hh % 2 == 0:
                            pe.wait_ge(far_added, heads * (u - 1) + hh + 2)
                        pe.matmul(ps[hh // 2][0:TILE, POS * (hh % 2):POS * (hh % 2) + POS], query_u[:, hh, tile(2 * p + t)],
                                  key[:, a, POS * p:POS * p + POS], start=True, stop=True).then_inc(dot_ready, 1)

                def turn_probs(u):
                    pe.wait_ge(prob_ready, u + 1)
                    for b in range(2):
                        if u:
                            pe.wait_ge(prob_kept, 2 * (u - 1) + b + 1)
                        for k in range(4):
                            mm = pe.transpose(ps[4 + b][0:TILE, tile(k)], scores[:, u % 3, 2 * b + k // 2, tile(k % 2)], w["ident"][0:TILE, 0:TILE])
                        mm.then_inc(prob_turned, 1)

                def mix(u):
                    p, a, t = unit[u]
                    if u >= 2:
                        pe.wait_ge(mixed_kept, u - 1)
                    pe.wait_ge(prob_kept, 2 * u + 2)
                    for k in range(2):
                        for hh in range(heads):
                            mm = pe.matmul(ps[6 + u % 2][32 * hh:32 * hh + 32, 0:TILE], value[:, 2 * p + k, 4 * a + hh], probs_t[:, u % 2, hh // 2, tile(2 * (hh % 2) + k)],
                                           start=(k == 0), stop=(k == 1), tile_position=(0, 32 * hh))
                    mm.then_inc(mixed_ready, 1)

                for n in range(units + 3):
                    if n < units:
                        dots(n)
                    if 2 <= n < units + 2:
                        turn_probs(n - 2)
                    if n >= 3:
                        mix(n - 3)
                pe.wait_ge(mixed_kept, units)
                for c in range(CHUNKS):
                    for a in range(2):
                        mm = pe.matmul(ps[c][64 * a:64 * a + 64, :CHUNK], w["rel_o"], mixed[:, a, chunk(c)], start=True, stop=True, tile_position=(0, 64 * a))
                    mm.then_inc(out_ready, 1)

            @block.scalar
            def _(act):

                def exps(u):
                    act.wait_ge(top_ready, u + 1)
                    if u >= 3:
                        act.wait_ge(inverse_ready, u - 2)
                    for hh in range(heads):
                        row = scores[:, u % 3, hh]
                        act.activation(row, row, ACT.Exp, bias=top[:, u % 3, hh:hh + 1], accum_out=total[:, u % 3, hh:hh + 1]).then_inc(exp_ready, 1)

                def keep_probs(u):
                    for b in range(2):
                        act.wait_ge(prob_turned, 2 * u + b + 1)
                        if u >= 2 and b == 0:
                            act.wait_ge(mixed_ready, u - 1)
                        act.activation(probs_t[:, u % 2, b], ps[4 + b][0:TILE, :CHUNK], ACT.Copy).then_inc(prob_kept, 1)

                def keep_mixed(u):
                    p, a, t = unit[u]
                    act.wait_ge(mixed_ready, u + 1)
                    act.activation(mixed[:, a, tile(2 * p + t)], ps[6 + u % 2][:, 0:TILE], ACT.Copy).then_inc(mixed_kept, 1)

                def keep_near(u):
                    p, a, t = unit[u]
                    if u >= 2:
                        act.wait_ge(near_kept, u - 1)
                    for hh in range(heads):
                        if hh % 2 == 0:
                            act.wait_ge(near_ready, heads * u + hh + 2)
                        act.activation(near_raw[:, u % 2, hh], ps[2 + hh // 2][0:TILE, near * (hh % 2):near * (hh % 2) + near], ACT.Identity,
                                       bias=shift[:, 2 * p + t, 4 * a + hh:4 * a + hh + 1]).then_inc(near_out, 1)

                keep_near(0)
                for n in range(units + 4):
                    if 2 <= n < units + 2:
                        keep_probs(n - 2)
                    if n >= 4:
                        keep_mixed(n - 4)
                    if n + 1 < units:
                        keep_near(n + 1)
                    if n < units:
                        exps(n)

            @block.vector
            def _(dve):

                def keep_scores(u):
                    p, a, t = unit[u]
                    j = 2 * p + t
                    if u >= 3:
                        dve.wait_ge(prob_turned, 2 * (u - 2))
                    for hh in range(heads):
                        if hh % 2 == 0:
                            dve.wait_ge(dot_ready, heads * u + hh + 2)
                        dve.scalar_tensor_tensor(scores[:, u % 3, hh], w["rel_right"][0:TILE, POS * t:POS * t + POS], right[:, j, 4 * a + hh:4 * a + hh + 1],
                                                 ps[hh // 2][0:TILE, POS * (hh % 2):POS * (hh % 2) + POS], ALU.mult, ALU.add).then_inc(far_added, 1)

                def finish_scores(u):
                    t = unit[u][2]
                    dve.wait_ge(near_kept, u + 1)
                    dve.wait_ge(far_added, heads * (u + 1))
                    dve.tensor_tensor(scores[:, u % 3], scores[:, u % 3], near_b[t][:, u % 2], ALU.add).then_inc(score_kept, 1)
                    dve.wait_ge(score_kept, u + 1)
                    if u >= 3:
                        dve.wait_ge(exp_ready, heads * (u - 2))
                    dve.tensor_reduce(top[:, u % 3], scores[:, u % 3], AX.X, ALU.max, negate=True).then_inc(top_ready, 1)

                def invert(u):
                    dve.wait_ge(exp_ready, heads * (u + 1))
                    if u >= 3:
                        dve.wait_ge(prob_ready, u - 2)
                    dve.reciprocal(inverse[:, u % 3], total[:, u % 3]).then_inc(inverse_ready, 1)

                for n in range(units + 1):
                    if n < units:
                        keep_scores(n)
                    if n >= 1:
                        invert(n - 1)
                    if n < units:
                        finish_scores(n)
                for c in range(CHUNKS):
                    dve.wait_ge(out_ready, c + 1)
                    dve.scalar_tensor_tensor(h[:, chunk(c)], ps[c][:, :CHUNK], w["rel_ob"], h[:, chunk(c)], ALU.add, ALU.add).then_inc(h_ready, 1)
                dve.wait_ge(h_ready, CHUNKS)

            @block.gpsimd
            def _(pool):

                def mask_near(u):
                    t = unit[u][2]
                    at = first_near[t]
                    pool.wait_ge(near_out, heads * (u + 1))
                    if u >= 4:
                        pool.wait_ge(score_kept, u - 3)
                    pool.tensor_tensor(near_b[t][:, u % 2, :, at:at + near], near_raw[:, u % 2],
                                       w["rel_near"][0:TILE, near * t:near * t + near].unsqueeze(1).to_broadcast([TILE, heads, near]), ALU.mult).then_inc(near_kept, 1)

                def scale_probs(u):
                    pool.wait_ge(inverse_ready, u + 1)
                    pool.tensor_tensor(scores[:, u % 3], scores[:, u % 3], inverse[:, u % 3].unsqueeze(2).to_broadcast([TILE, heads, POS]), ALU.mult).then_inc(prob_ready, 1)

                for n in range(units + 1):
                    if n < units:
                        mask_near(n)
                    if n >= 1:
                        scale_probs(n - 1)


def best_expert_ffn(nc, h, x, w, ps, out_dram):
    experts, blocks = 8, 2
    cols = 2 * TILES
    with Stage(nc, "top1") as s:
        hidden = s.sb("hidden", [128, blocks, 2, COLS])
        prob = s.sb("prob", [TILE, cols, experts])
        part = s.sb("part", [TILE, cols, experts])
        best = s.sb("best", [TILE, cols])
        total = s.sb("total", [TILE, cols])
        inverse = s.sb("inverse", [TILE, cols])
        gate_t = s.sb("gate_t", [2 * experts, TILES, TILE])
        scaled = s.sb("scaled", [TILE, 4, experts, FEAT])
        summed = s.sb("summed", [TILE, 2, FEAT])
        final = s.sb("final", [TILE, cols, FEAT])
        (up_ready, up_kept, logits_ready, steps, exp_ready, gate_turned, gate_kept, y_ready, y_scaled, rest_ready, y_summed,
         final_ready, stored) = (s.sem(n) for n in (
             "up_ready up_kept logits_ready steps exp_ready gate_turned gate_kept y_ready y_scaled rest_ready y_summed final_ready stored").split())
        with nc.Block() as block:

            @block.tensor
            def _(pe):
                for n in range(16):
                    c, m, a = n // 4, (n // 2) % 2, n % 2
                    if n >= 8:
                        pe.wait_ge(up_kept, n - 7)
                    pe.matmul(ps[n % 8][:, :CHUNK], w["top_1"][:, 256 * a + 128 * m:256 * a + 128 * m + 128], x[:, chunk(c)], start=True, stop=True).then_inc(up_ready, 1)
                pe.wait_ge(up_kept, 16)
                for col in range(cols):
                    j, a = col // 2, col % 2
                    for m in range(blocks):
                        mm = pe.matmul(ps[0][0:TILE, 8 * col:8 * col + 8], hidden[:, m, a, tile(j)], w["top_g"][:, 8 * m:8 * m + 8], start=(m == 0), stop=(m == 1))
                mm.then_inc(logits_ready, 1)

                def experts_of(n):
                    if n >= 4:
                        pe.wait_ge(y_scaled, n - 3)
                    for m in range(blocks):
                        mm = pe.matmul(ps[4 + n % 4][0:TILE, :], hidden[:, m, n % 2, tile(n // 2)], w["top_d"][:, 512 * m:512 * m + 512], start=(m == 0), stop=(m == 1))
                    mm.then_inc(y_ready, 1)

                for n in range(4):
                    experts_of(n)
                pe.wait_ge(steps, 10)
                for b in range(4):
                    for k in range(4):
                        j = 4 * b + k
                        mm = pe.transpose(ps[b][0:2 * experts, tile(k)], prob[:, 2 * j:2 * j + 2].rearrange("p a e -> p (a e)"), w["ident"][0:TILE, 0:TILE])
                    mm.then_inc(gate_turned, 1)
                pe.wait_ge(gate_kept, 4)
                for j in range(TILES):
                    if j >= 4:
                        pe.wait_ge(final_ready, 2 * (j - 4) + 2)
                    pe.matmul(ps[j % 4][0:TILE, 0:2 * FEAT], gate_t[:, j], w["top_bd"], start=True, stop=False)
                    pe.matmul(ps[j % 4][0:TILE, 0:2 * FEAT], h[:, tile(j)], w["ident"], start=False, stop=True).then_inc(rest_ready, 1)
                    for n in (2 * j + 4, 2 * j + 5):
                        if n < cols:
                            experts_of(n)

            @block.scalar
            def _(act):
                for n in range(16):
                    c, m, a = n // 4, (n // 2) % 2, n % 2
                    act.wait_ge(up_ready, n + 1)
                    act.activation(hidden[:, m, a, chunk(c)], ps[n % 8][:, :CHUNK], ACT.Gelu, bias=w["top_b1"][:, m:m + 1]).then_inc(up_kept, 1)
                act.wait_ge(steps, 3)
                act.activation(prob[:], prob[:], ACT.Exp).then_inc(exp_ready, 1)
                for b in range(4):
                    act.wait_ge(gate_turned, b + 1)
                    act.activation(gate_t[:, 4 * b:4 * b + 4], ps[b][0:2 * experts, :CHUNK].rearrange("p (k n) -> p k n", k=4), ACT.Copy).then_inc(gate_kept, 1)

            @block.vector
            def _(dve):
                wide = [TILE, cols, experts]
                dve.wait_ge(logits_ready, 1)
                dve.tensor_tensor(prob[:], ps[0][0:TILE, 0:8 * cols].rearrange("p (a e) -> p a e", e=experts), w["top_bg"][0:TILE, :].unsqueeze(1).to_broadcast(wide), ALU.add).then_inc(steps, 1)
                dve.wait_ge(steps, 1)
                dve.tensor_reduce(best[:], prob[:], AX.X, ALU.max).then_inc(steps, 1)
                dve.wait_ge(steps, 2)
                dve.tensor_tensor(prob[:], prob[:], best[:].unsqueeze(2).to_broadcast(wide), ALU.subtract).then_inc(steps, 1)
                dve.wait_ge(exp_ready, 1)
                dve.tensor_reduce(total[:], prob[:], AX.X, ALU.add).then_inc(steps, 1)
                dve.wait_ge(steps, 4)
                dve.reciprocal(inverse[:], total[:]).then_inc(steps, 1)
                dve.wait_ge(steps, 5)
                dve.tensor_tensor(prob[:], prob[:], inverse[:].unsqueeze(2).to_broadcast(wide), ALU.mult).then_inc(steps, 1)
                dve.wait_ge(steps, 6)
                dve.tensor_reduce(best[:], prob[:], AX.X, ALU.max).then_inc(steps, 1)
                dve.wait_ge(steps, 7)
                dve.tensor_tensor(part[:], prob[:], best[:].unsqueeze(2).to_broadcast(wide), ALU.is_equal).then_inc(steps, 1)
                dve.wait_ge(steps, 8)
                dve.tensor_tensor(part[:], part[:], w["top_iota"][0:TILE, :].unsqueeze(1).to_broadcast(wide), ALU.mult).then_inc(steps, 1)
                dve.wait_ge(steps, 9)
                dve.tensor_reduce(best[:], part[:], AX.X, ALU.min).then_inc(exp_ready, 1)
                dve.wait_ge(exp_ready, 2)
                dve.tensor_tensor(part[:], w["top_iota"][0:TILE, :].unsqueeze(1).to_broadcast(wide), best[:].unsqueeze(2).to_broadcast(wide), ALU.is_equal).then_inc(exp_ready, 1)
                dve.wait_ge(exp_ready, 3)
                dve.tensor_tensor(prob[:], prob[:], part[:], ALU.mult).then_inc(steps, 1)
                dve.wait_ge(steps, 10)
                for n in range(cols):
                    dve.wait_ge(y_ready, n + 1)
                    if n >= 4:
                        dve.wait_ge(y_summed, n - 3)
                    dve.tensor_tensor(scaled[:, n % 4], ps[4 + n % 4][0:TILE, :].rearrange("p (e f) -> p e f", e=experts),
                                      prob[:, n].unsqueeze(2).to_broadcast([TILE, experts, FEAT]), ALU.mult).then_inc(y_scaled, 1)
                    dve.wait_ge(y_scaled, n + 1)
                    if n >= 2:
                        dve.wait_ge(final_ready, n - 1)
                    dve.tensor_reduce(summed[:, n % 2], scaled[:, n % 4].rearrange("p e f -> p f e"), AX.X, ALU.add).then_inc(y_summed, 1)
                    dve.wait_ge(y_summed, n + 1)
                    dve.wait_ge(rest_ready, n // 2 + 1)
                    dve.tensor_tensor(final[:, n], summed[:, n % 2], ps[n // 2 % 4][0:TILE, 64 * (n % 2):64 * (n % 2) + 64], ALU.add).then_inc(final_ready, 1)

            @block.sync
            def _(sp):
                for p in range(PAIRS):
                    sp.wait_ge(final_ready, 4 * p + 4)
                    for t in range(2):
                        for a in range(2):
                            sp.dma_start(out_dram[8 * a + p, TILE * t:TILE * t + TILE, :], final[:, 4 * p + 2 * t + a, :]).then_inc(stored, 16)
                sp.wait_ge(stored, 16 * cols)



def both(a):
    return np.concatenate([a, a], 0)


def diagonal(a):
    k, n = a.shape
    out = np.zeros((2 * k, 2 * n), a.dtype)
    out[:k, :n] = a
    out[k:, n:] = a
    return out


def column(v):
    return both(v.reshape(-1, 1))


def rows(v, n=128):
    return np.broadcast_to(v.reshape(1, -1), (n, v.size))


def parts(i):
    f = np.float32
    out = []

    def add(group, name, a):
        out.append((group, name, np.ascontiguousarray(a, dtype=f)))

    half = np.arange(128) // 64
    add(0, "ident", np.eye(128, dtype=f))
    add(1, "win_q", diagonal(i["L0_tok_W_qry"]))
    add(1, "win_k", diagonal(i["L0_tok_W_key"]))
    add(1, "win_b", column(i["L0_tok_b"]))
    v = np.zeros((128, WINDOW, 18), f)
    for o in range(WINDOW):
        v[:64, o, o] = i["L0_tok_v"]
        v[64:, o, 9 + o] = i["L0_tok_v"]
    add(1, "win_v", v.reshape(128, -1))
    sel = np.zeros((128, WINDOW, 128), f)
    for o in range(WINDOW):
        sel[o, o, :64] = 1
        sel[9 + o, o, 64:] = 1
    add(1, "win_out", sel.reshape(128, -1))
    add(0, "mean", (half[:, None] == half[None, :]) / 64.0)
    var = np.zeros((128, TILES, 32), f)
    outm = np.zeros((128, TILES, 128), f)
    for j in range(TILES):
        for a in range(2):
            var[64 * a:64 * a + 64, j, 16 * a + j] = 1.0 / 64
            outm[16 * a + j, j, 64 * a:64 * a + 64] = 1
    add(0, "var_rows", var.reshape(128, -1))
    add(0, "rows_out", outm.reshape(128, -1))
    add(0, "ln_eps", np.full((128, 1), LN_EPS))
    add(2, "mix_qkv", np.concatenate([diagonal(i[f"L0_attn_W{n}"].T) for n in "qkv"], 1))
    add(2, "mix_qkvb", rows(np.concatenate([i[f"L0_attn_b{n}"] for n in "qkv"])))
    add(2, "cap_r", diagonal(i["L0_ffn_wr"]))
    add(2, "cap_br", rows(i["L0_ffn_br"]))
    add(2, "cap_1", diagonal(i["L0_ffn_w1"]))
    add(2, "cap_b1", i["L0_ffn_b1"].reshape(2, 128).T)
    w2 = np.zeros((128, 2, 2, 2, 64), f)
    for a in range(2):
        w2[:, a, :, a, :] = i["L0_ffn_w2"].reshape(2, 128, 64).transpose(1, 0, 2)
    add(2, "cap_2", w2.reshape(128, -1))
    add(2, "cap_b2", column(i["L0_ffn_b2"]))
    n = np.arange(POS)
    add(2, "cap_earlier", np.concatenate([n[None, :] < (t * TILE + np.arange(TILE))[:, None] for t in range(2)], 1))
    add(3, "tay_qkv", np.concatenate([diagonal(i["L1_attn_Wqkv"][64 * n:64 * n + 64].T) for n in range(3)], 1))
    add(3, "tay_qkvb", rows(np.concatenate([np.concatenate([i["L1_attn_bqkv"][64 * n:64 * n + 64]] * 2) for n in range(3)])))
    add(3, "tay_temp", rows(i["L1_attn_temperature"]))
    coef = []
    for a in range(8):
        coef += [0.5] + [1.0] * (7 - a)
    coef += [8.0 ** 0.5] * 8 + [8.0]
    m = np.zeros((2, 45, 4, 32), f)
    for a in range(2):
        m[a, :, :, 9 * a:9 * a + 9] = np.array(coef)[:, None, None]
    add(3, "tay_coef", m.reshape(90, 128))
    wo = np.zeros((4, 32, 64), f)
    wo[:, 1:9], wo[:, 10:18] = (i["L1_attn_Wproj"].T.reshape(4, 2, 8, 64)[:, n] for n in range(2))
    add(3, "tay_o", wo.reshape(128, 64))
    total = np.zeros((128, 4, 32), f)
    for g in range(4):
        total[32 * g, g, :], total[32 * g, g, 9:18], total[32 * g + 9, g, 9:18] = 1, 0, 1
    add(3, "tay_sum", total.reshape(128, 128))
    add(3, "tay_ob", column(i["L1_attn_bproj"]))
    add(4, "moe_r", diagonal(i["L1_ffn_Wr"]))
    add(4, "moe_br", rows(i["L1_ffn_br"]))
    add(4, "moe_b2", diagonal(i["L1_ffn_b2"]))
    n = np.arange(TILE)
    add(4, "moe_tri", n[:, None] < n[None, :])
    add(4, "moe_ones", np.ones((128, 128)))
    add(0, "iota", rows(np.arange(128)))
    add(0, "iota_p", np.arange(128).reshape(-1, 1))
    add(4, "moe_high", (n // 2).reshape(-1, 1))
    add(4, "moe_low", (n % 2)[:, None] * 32 + np.repeat(np.arange(32), 2)[None, :])
    swap = np.arange(64) ^ 1
    add(5, "ret_q", diagonal(i["L2_attn_W_Q"]))
    add(5, "ret_qs", diagonal(i["L2_attn_W_Q"][:, swap]))
    add(5, "ret_k", diagonal(i["L2_attn_W_K"]))
    add(5, "ret_ks", diagonal(i["L2_attn_W_K"][:, swap]))
    add(5, "ret_v", diagonal(i["L2_attn_W_V"]))
    pos = np.arange(POS, dtype=f)
    even = np.arange(0, 64, 2, dtype=f)
    ang = pos[None, :] * (f(1) / f(10000) ** (even / f(64)))[:, None]
    size = ((even + f(25.6)) / f(89.6))[:, None] ** (pos[None, :] / f(512))
    sign = np.tile(np.array([-1, 1], f), 32)[:, None]
    table = []
    for size_ in (size, f(1) / size):
        table += [both(np.repeat(np.cos(ang) * size_, 2, 0)), both(np.repeat(np.sin(ang) * size_, 2, 0) * sign)]
    add(5, "ret_table", np.concatenate(table, 1))
    diff = np.arange(POS)[None, :] - np.arange(TILE)[:, None]
    decay = np.where(diff >= 0, f(0.96875) ** np.maximum(diff, 0).astype(f), 0)
    add(5, "ret_decay", np.concatenate([decay, decay[:, :TILE]], 1))
    add(6, "soft_r", both(i["L2_ffn_Wr"]))
    add(6, "soft_br", rows(i["L2_ffn_br"]))
    add(6, "soft_bo", np.concatenate([i["L2_ffn_bo"]] * 2, 1))
    for n, name in ((1, "W1"), (2, "W2"), (3, "Wo")):
        add(6, f"soft_{n}", np.concatenate([diagonal(a) for a in i["L2_ffn_" + name]], 1))
    add(6, "bn", np.concatenate([both(i[f"L2_ffn_{n}{layer}"].T) for n in ("g", "b", "m", "v", "be") for layer in (1, 2)], 1))
    add(6, "bn_eps", np.full((128, 1), 1e-3))
    add(7, "rel_gamma", column(i["L3_attn_ln_gamma"]))
    add(7, "rel_beta", column(i["L3_attn_ln_beta"]))
    for n in "qkv":
        add(7, "rel_" + n, diagonal(i[f"L3_attn_W{n}"].T))
    wo = np.zeros((4, 32, 64), f)
    wo[:, :16] = i["L3_attn_Wo"].T.reshape(4, 16, 64)
    add(7, "rel_o", wo.reshape(128, 64))
    u, v = (np.ascontiguousarray(i[f"L3_attn_{n}_bias"]).reshape(64) for n in "uv")
    add(7, "rel_qu", np.concatenate([column(i["L3_attn_bq"]), column(u), column(v)], 1))
    add(7, "rel_kb", column(i["L3_attn_bk"]))
    add(7, "rel_vb", rows(np.concatenate([i["L3_attn_bv"]] * 2)))
    add(7, "rel_ob", column(i["L3_attn_bo"]))
    add(7, "rel_posb", column(i["L3_attn_bpos"]))
    wpos = i["L3_attn_Wpos"]
    add(7, "rel_pos_t", np.concatenate([wpos.T] * 2, 1))
    omega = np.exp(np.arange(0, 64, 2) * (-np.log(10000.0) / 64))
    ends = np.zeros((64, 2))
    for k, r in enumerate((0, 60)):
        ends[0::2, k], ends[1::2, k] = np.sin(r * omega), np.cos(r * omega)
    add(7, "rel_ends", ends)
    head = (np.arange(64) // 16)[:, None] == np.arange(4)[None, :]
    add(7, "rel_head", both(head) * 0.25)
    h8 = np.zeros((128, 8))
    h8[:64, :4], h8[64:, 4:] = head, head
    add(7, "rel_head8", h8)
    cut = [np.where(head[:, g:g + 1], wpos, f(0)) for g in range(4)]
    add(7, "rel_pos", np.concatenate([diagonal(a) for a in cut], 1))
    add(7, "rel_pos_s", np.concatenate([diagonal(a[:, swap]) for a in cut], 1))
    n = np.arange(POS)
    th = (30 - n)[None, :] * np.repeat(omega, 2)[:, None]
    add(7, "rel_t", np.concatenate([both(np.cos(th)), both(np.sin(th) * np.tile([-1, 1], 32)[:, None])], 1))
    es = n[None, :] * np.repeat(omega, 2)[:, None]
    es[0::2], es[1::2] = np.sin(es[0::2]), np.cos(es[1::2])
    add(7, "rel_s", diagonal(es))
    gap = [n[None, :] - (t * TILE + np.arange(TILE))[:, None] for t in range(2)]
    wide = TILE + 29
    add(7, "rel_near", np.concatenate([np.abs(gap[t])[:, (POS - wide) * t:(POS - wide) * t + wide] < 30 for t in range(2)], 1))
    add(7, "rel_right", np.concatenate([g >= 30 for g in gap], 1))
    add(8, "top_1", diagonal(i["L3_ffn_W1"]))
    add(8, "top_b1", i["L3_ffn_b1"].reshape(2, 128).T)
    add(8, "top_g", i["L3_ffn_Wg"].reshape(2, 128, 8).transpose(1, 0, 2).reshape(128, 16))
    add(8, "top_bg", rows(i["L3_ffn_bg"]))
    add(8, "top_d", i["L3_ffn_Wd"].reshape(8, 2, 128, 64).transpose(2, 1, 0, 3).reshape(128, 1024))
    add(8, "top_bd", diagonal(i["L3_ffn_bd"]))
    add(8, "top_iota", rows(np.arange(8) - 8))
    return out


def pack(i):
    where, blocks, at, groups = {}, [], 0, {}
    for group, name, a in sorted(parts(i), key=lambda p: p[0]):
        where[name] = (group, a.shape[0], at, a.shape[1])
        block = np.zeros((128, a.shape[1]), np.float32)
        block[:a.shape[0]] = a
        blocks.append(block)
        lo, _ = groups.get(group, (at, at))
        at += a.shape[1]
        groups[group] = (lo, at)
    return np.concatenate(blocks, 1), where, [groups[g] for g in sorted(groups)]


def extra(i):
    w1 = np.concatenate([i["L1_ffn_W1"], i["L1_ffn_b1"][:, None, :]], 1)
    return {"experts1": np.ascontiguousarray(w1.transpose(1, 0, 2).reshape(FEAT + 1, -1)),
            "experts2": np.ascontiguousarray(i["L1_ffn_W2"].transpose(1, 0, 2).reshape(128, -1))}


def pairs_first(a):
    return np.ascontiguousarray(a.reshape(2, 8, a.shape[1], 64).transpose(0, 3, 1, 2).reshape(128, 8, a.shape[1]))


def program(nc, where, groups, d):
    with ExitStack() as ctx:
        h = ctx.enter_context(nc.sbuf_tensor("h", [128, COLS], F32))
        x = ctx.enter_context(nc.sbuf_tensor("x", [128, COLS], F32))
        ps = [ctx.enter_context(nc.psum_tensor(f"bank{b}", [128, 512], F32)) for b in range(8)]
        d["tokens"] = nc.dram_tensor("tokens", [SEQS * POS, FEAT], F32, kind="Internal").ap()
        d["table"] = nc.dram_tensor("table", [TABLE_TILES * 128, FEAT], F32, kind="Internal").ap()
        w = Weights(nc, ctx, d["weights"], where, groups)
        window_attention(nc, d["x"], h, w, ps)
        layer_norm(nc, "ln0", h, x, w, ps, group=2)
        batch_axis_attention(nc, h, x, w, ps)
        layer_norm(nc, "ln1", h, x, w, ps)
        top_half_ffn(nc, h, x, w, ps)
        layer_norm(nc, "ln2", h, x, w, ps, group=3)
        taylor_attention(nc, h, x, w, ps)
        layer_norm(nc, "ln3", h, x, w, ps, group=4)
        expert_ffn(nc, h, x, w, ps, d)
        layer_norm(nc, "ln4", h, x, w, ps, group=5)
        retention(nc, h, x, w, ps)
        layer_norm(nc, "ln5", h, x, w, ps, group=6)
        soft_mixture(nc, h, x, w, ps)
        layer_norm(nc, "ln6", h, x, w, ps)
        layer_norm(nc, "ln6b", x, x, w, ps, group=7)
        relative_attention(nc, h, x, w, ps)
        layer_norm(nc, "ln7", h, x, w, ps, group=8)
        best_expert_ffn(nc, h, x, w, ps, d["out"])


def kernel(**inputs):
    import numpy as _np
    import concourse.bacc as _bacc
    from concourse import mybir as _mybir
    from concourse.bass_utils import run_bass_kernel_spmd as _run

    given = {name: _np.asarray(a) for name, a in inputs.items()}
    weights, where, groups = pack(given)
    arrays = {"x": pairs_first(given["x"]), "weights": weights, **extra(given)}
    nc = _bacc.Bacc("TRN2", target_bir_lowering=False, num_devices=1)
    d = {name: nc.dram_tensor(f"in_{name}_dram", a.shape, _mybir.dt.float32, kind="ExternalInput").ap() for name, a in arrays.items()}
    d["out"] = nc.dram_tensor("out_0_dram", [SEQS, POS, FEAT], _mybir.dt.float32, kind="ExternalOutput").ap()
    program(nc, where, groups, d)
    r = _run(nc, [{f"in_{name}_dram": a for name, a in arrays.items()}], core_ids=[0])
    return r.results[0]["out_0_dram"]
```

```python
from contextlib import ExitStack

import numpy as np

import concourse.bass as bass
from concourse import mybir

F32 = mybir.dt.float32
I32 = mybir.dt.int32
U32 = mybir.dt.uint32
BF16 = mybir.dt.bfloat16
ALU = mybir.AluOpType
ACT = mybir.ActivationFunctionType
AX = mybir.AxisListType

SEQS, FRAMES, FEAT, WINDOW = 16, 250, 64, 9
POS = FRAMES - WINDOW + 1
PAIRS = SEQS // 2
COLS = PAIRS * POS
TILE = POS // 2
TILES = 2 * PAIRS
CHUNK = 4 * TILE
CHUNKS = COLS // CHUNK
LN_EPS = 1e-5
EXPERTS = 64
TABLE_TILES = 128
FILLED_TILES = (2 * SEQS * POS - EXPERTS) // 128 + EXPERTS


def chunk(c):
    return slice(c * CHUNK, (c + 1) * CHUNK)


def tile(j):
    return slice(j * TILE, (j + 1) * TILE)


class Stage:

    def __init__(self, nc, name):
        self.nc, self.name, self.ctx, self.sems = nc, name, ExitStack(), []

    def __enter__(self):
        self.ctx.__enter__()
        return self

    def __exit__(self, *e):
        if self.sems and e[0] is None:
            for sem in self.sems:
                self.nc.gpsimd.sem_clear(sem)
                self.nc.release_semaphore(sem)
        return self.ctx.__exit__(*e)

    def sb(self, name, shape, dt=F32):
        return self.ctx.enter_context(self.nc.sbuf_tensor(f"{self.name}_{name}", shape, dt))

    def sem(self, name):
        self.sems.append(self.nc.alloc_semaphore(f"{self.name}_{name}"))
        return self.sems[-1]

    def pool_dma_sem(self, name):
        return self.nc.alloc_semaphore(f"{self.name}_{name}")


class Weights:

    def __init__(self, nc, ctx, dram, where, groups):
        self.nc, self.dram, self.groups, self.views = nc, dram, groups, {}
        widest = max(b - a for a, b in groups[1:])
        widths = [groups[0][1], widest, widest]
        self.buffers = [ctx.enter_context(nc.sbuf_tensor(f"weights{n}", [128, k], F32)) for n, k in enumerate(widths)]
        self.loaded = [ctx.enter_context(nc.semaphore(f"loaded{g}")) for g in range(len(groups))]
        for name, (group, r, at, k) in where.items():
            at -= groups[group][0]
            self.views[name] = self.buffer(group)[:r, at:at + k]

    def buffer(self, group):
        return self.buffers[0 if group == 0 else 1 + group % 2]

    def __getitem__(self, name):
        return self.views[name]

    def load(self, eng, group):
        a, b = self.groups[group]
        eng.dma_start(self.buffer(group)[:, 0:b - a], self.dram[:, a:b]).then_inc(self.loaded[group], 16)

    def wait(self, eng, group):
        if group is not None:
            eng.wait_ge(self.loaded[group], 16)


class LayerNorm:

    def __init__(self, s, h, x, w, ps, h_final, group=None, name="ln", squares=None):
        self.h, self.x, self.w, self.ps, self.h_final, self.group = h, x, w, ps, h_final, group
        self.squares = s.sb(name + "_squares", [128, COLS]) if squares is None else squares
        self.std = s.sb(name + "_std", [32, TILE])
        self.rstd = s.sb(name + "_rstd", [128, TILE])
        self.warm = s.sb(name + "_warm", [128, 1])
        (self.mean_ready, self.centred_ready, self.squares_ready, self.var_ready, self.std_ready, self.rstd_ready,
         self.scale_ready, self.x_ready, self.warmed, self.zeroed) = (s.sem(f"{name}_{n}") for n in (
             "mean_ready centred_ready squares_ready var_ready std_ready rstd_ready scale_ready x_ready warmed zeroed").split())

    def mean(self, pe, c):
        self.h_final(pe, c)
        pe.matmul(self.ps[c][:, :CHUNK], self.w["mean"], self.h[:, chunk(c)], start=True, stop=True).then_inc(self.mean_ready, 1)

    def centre(self, dve, c):
        dve.wait_ge(self.mean_ready, c + 1)
        dve.tensor_tensor(self.x[:, chunk(c)], self.h[:, chunk(c)], self.ps[c][:, :CHUNK], ALU.subtract).then_inc(self.centred_ready, 1)

    def tensor(self, pe, done=0):
        ps, w = self.ps, self.w
        for c in range(done, CHUNKS):
            self.mean(pe, c)
        for j in range(TILES):
            if j % 4 == 0:
                pe.wait_ge(self.squares_ready, j // 4 + 1)
            last = pe.matmul(ps[4][0:32, 0:TILE], w["var_rows"][:, 32 * j:32 * j + 32], self.squares[:, tile(j)],
                             start=(j == 0), stop=(j == TILES - 1))
        last.then_inc(self.var_ready, 1)
        pe.wait_ge(self.rstd_ready, 1)
        for j in range(TILES):
            mm = pe.matmul(ps[j // 4][:, tile(j % 4)], w["rows_out"][:, 128 * j:128 * j + 128], self.rstd[:],
                           start=True, stop=True)
            if j % 4 == 3:
                mm.then_inc(self.scale_ready, 1)
        w.wait(pe, self.group)

    def scalar(self, act):
        act.activation(self.warm[:], self.w["ln_eps"], ACT.Sqrt).then_inc(self.warmed, 1)
        for c in range(CHUNKS):
            act.wait_ge(self.centred_ready, c + 1)
            act.activation(self.squares[:, chunk(c)], self.x[:, chunk(c)], ACT.Square).then_inc(self.squares_ready, 1)
        act.wait_ge(self.var_ready, 1)
        act.activation(self.std[:], self.ps[4][0:32, 0:TILE], ACT.Sqrt, bias=self.w["ln_eps"][0:32, :]).then_inc(self.std_ready, 1)
        self.w.wait(act, self.group)

    def vector(self, dve, done=0):
        x = self.x
        for c in range(done, CHUNKS):
            self.centre(dve, c)
        dve.wait_ge(self.std_ready, 1)
        dve.wait_ge(self.zeroed, 1)
        dve.reciprocal(self.rstd[0:32, :], self.std[:]).then_inc(self.rstd_ready, 1)
        for c in range(CHUNKS):
            dve.wait_ge(self.scale_ready, c + 1)
            dve.tensor_tensor(x[:, chunk(c)], x[:, chunk(c)], self.ps[c][:, :CHUNK], ALU.mult).then_inc(self.x_ready, 1)
        dve.wait_ge(self.x_ready, CHUNKS)
        self.w.wait(dve, self.group)

    def gpsimd(self, pool):
        pool.memset(self.rstd[:], 0.0).then_inc(self.zeroed, 1)

    def sync(self, sp):
        if self.group and self.group + 1 < len(self.w.groups):
            sp.wait_ge(self.mean_ready, CHUNKS)
            self.w.load(sp, self.group + 1)


def window_attention(nc, x_dram, h, x, w, ps):
    with Stage(nc, "win") as s:
        frames = s.sb("frames", [128, PAIRS, FRAMES])
        query = s.sb("query", [128, PAIRS, POS])
        key = s.sb("key", [128, PAIRS, FRAMES])
        hidden = s.sb("hidden", [128, WINDOW, PAIRS, POS])
        scores = s.sb("scores", [2 * WINDOW, COLS])
        token = s.sb("token", [TILE, TILES * 2, WINDOW])
        top = s.sb("top", [TILE, TILES * 2])
        total = s.sb("total", [TILE, TILES * 2])
        weight_rows = s.sb("weight_rows", [128, COLS])
        product = s.sb("product", [128, 3, PAIRS, POS])
        frames_in = s.sem("frames_in")
        query_ready, query_kept, key_ready, key_kept = s.sem("query_ready"), s.sem("query_kept"), s.sem("key_ready"), s.sem("key_kept")
        sum_ready, hidden_ready, scores_ready, scores_kept = s.sem("sum_ready"), s.sem("hidden_ready"), s.sem("scores_ready"), s.sem("scores_kept")
        turned, top_ready, less_top, exp_ready = s.sem("turned"), s.sem("top_ready"), s.sem("less_top"), s.sem("exp_ready")
        total_ready, inverse_ready, weight_ready = s.sem("total_ready"), s.sem("inverse_ready"), s.sem("weight_ready")
        rows_turned, rows_kept = s.sem("rows_turned"), s.sem("rows_kept")
        spread_ready, product_ready, added, added_last, zeroed = (
            s.sem(n) for n in "spread_ready product_ready added added_last zeroed".split())
        ln = LayerNorm(s, h, x, w, ps, lambda eng, c: eng.wait_ge(*((added, (WINDOW - 2) * (CHUNKS - 1) + c + 1) if c < CHUNKS - 1 else (added_last, WINDOW - 1))), group=2)
        with nc.Block() as block:

            @block.sync
            def _(sp):
                sp.dma_start(frames[:], x_dram).then_inc(frames_in, 16)
                sp.wait_ge(frames_in, 16)
                w.load(sp, 2)
                ln.sync(sp)

            @block.tensor
            def _(pe):
                w.wait(pe, 1)
                pe.wait_ge(frames_in, 16)
                mid = WINDOW // 2
                for c in range(CHUNKS):
                    pe.matmul(ps[c][:, :CHUNK], w["win_q"], frames[:, 2 * c:2 * c + 2, mid:mid + POS], start=True, stop=True).then_inc(query_ready, 1)
                    pe.matmul(ps[4 + c][:, :2 * FRAMES], w["win_k"], frames[:, 2 * c:2 * c + 2, :], start=True, stop=True).then_inc(key_ready, 1)
                for o in range(WINDOW):
                    pe.wait_ge(hidden_ready, o + 2)
                    for c in range(CHUNKS):
                        if o == 0:
                            pe.wait_ge(query_kept, c + 1)
                        mm = pe.matmul(ps[c][32 * c:32 * c + 2 * WINDOW, :CHUNK], w["win_v"][:, 18 * o:18 * o + 18], hidden[:, o, 2 * c:2 * c + 2, :],
                                       start=(o == 0), stop=(o == WINDOW - 1), tile_position=(0, 32 * c))
                        if o == WINDOW - 1:
                            mm.then_inc(scores_ready, 1)
                w.wait(pe, 0)
                pe.wait_ge(key_kept, CHUNKS)
                for j in range(TILES):
                    pe.wait_ge(scores_kept, j // 4 + 1)
                    mm = pe.transpose(ps[4][0:TILE, 18 * j:18 * j + 18], scores[:, tile(j)], w["ident"][0:18, 0:18])
                mm.then_inc(turned, 1)
                pe.wait_ge(weight_ready, 1)
                for j in range(TILES):
                    mm = pe.transpose(ps[j // 4][0:18, tile(j % 4)], token[:, 2 * j:2 * j + 2, :], w["ident"][0:TILE, 0:TILE])
                    if j % 4 == 3:
                        mm.then_inc(rows_turned, 1)
                for o in range(WINDOW):
                    for c in range(CHUNKS):
                        n = o * CHUNKS + c
                        if o == 0:
                            pe.wait_ge(rows_kept, c + 1)
                        if n >= 8:
                            pe.wait_ge(product_ready, n - 7)
                        pe.matmul(ps[n % 8][:, :CHUNK], w["win_out"][:, 128 * o:128 * o + 128], weight_rows[:, chunk(c)],
                                  start=True, stop=True).then_inc(spread_ready, 1)
                ln.tensor(pe)

            @block.scalar
            def _(act):
                w.load(act, 1)
                w.load(act, 0)
                w.wait(act, 1)
                for c in range(CHUNKS):
                    act.wait_ge(query_ready, c + 1)
                    act.activation(query[:, 2 * c:2 * c + 2, :], ps[c][:, :CHUNK].rearrange("p (b n) -> p b n", b=2), ACT.Identity,
                                   bias=w["win_b"]).then_inc(query_kept, 1)
                    act.wait_ge(key_ready, c + 1)
                    act.activation(key[:, 2 * c:2 * c + 2, :], ps[4 + c][:, :2 * FRAMES].rearrange("p (b n) -> p b n", b=2), ACT.Copy).then_inc(key_kept, 1)
                for part in range(2):
                    act.wait_ge(sum_ready, part + 1)
                    mine = hidden[:, 0, 4 * part:4 * part + 4]
                    act.activation(mine, mine, ACT.Tanh).then_inc(hidden_ready, 1)
                for o in range(1, WINDOW):
                    act.wait_ge(sum_ready, o + 2)
                    act.activation(hidden[:, o], hidden[:, o], ACT.Tanh).then_inc(hidden_ready, 1)
                for c in range(CHUNKS):
                    act.wait_ge(scores_ready, c + 1)
                    act.activation(scores[:, chunk(c)], ps[c][32 * c:32 * c + 18, :CHUNK], ACT.Copy).then_inc(scores_kept, 1)
                act.wait_ge(less_top, 1)
                act.activation(token[:], token[:], ACT.Exp).then_inc(exp_ready, 1)
                act.wait_ge(zeroed, 1)
                for c in range(CHUNKS):
                    act.wait_ge(rows_turned, c + 1)
                    act.activation(weight_rows[0:18, chunk(c)], ps[c][0:18, :CHUNK], ACT.Copy).then_inc(rows_kept, 1)
                ln.scalar(act)

            @block.vector
            def _(dve):
                for part in range(2):
                    mine = slice(4 * part, 4 * part + 4)
                    dve.wait_ge(key_kept, 2 * part + 2)
                    dve.wait_ge(query_kept, 2 * part + 2)
                    dve.tensor_tensor(hidden[:, 0, mine], query[:, mine], key[:, mine, 0:POS], ALU.add).then_inc(sum_ready, 1)
                for o in range(1, WINDOW):
                    dve.tensor_tensor(hidden[:, o], query[:], key[:, :, o:o + POS], ALU.add).then_inc(sum_ready, 1)
                dve.wait_ge(turned, 1)
                got = ps[4][0:TILE, 0:18 * TILES].rearrange("p (a o) -> p a o", o=WINDOW)
                dve.tensor_reduce(top[:], got, AX.X, ALU.max).then_inc(top_ready, 1)
                dve.wait_ge(top_ready, 1)
                dve.tensor_tensor(token[:], got, top[:].unsqueeze(2).to_broadcast([TILE, 2 * TILES, WINDOW]), ALU.subtract).then_inc(less_top, 1)
                dve.wait_ge(exp_ready, 1)
                dve.tensor_reduce(total[:], token[:], AX.X, ALU.add).then_inc(total_ready, 1)
                dve.wait_ge(total_ready, 1)
                dve.reciprocal(top[:], total[:]).then_inc(inverse_ready, 1)
                dve.wait_ge(inverse_ready, 1)
                dve.tensor_tensor(token[:], token[:], top[:].unsqueeze(2).to_broadcast([TILE, 2 * TILES, WINDOW]), ALU.mult).then_inc(weight_ready, 1)
                for o in range(WINDOW):
                    for c in range(CHUNKS):
                        dve.wait_ge(spread_ready, o * CHUNKS + c + 1)
                        if o >= 4:
                            dve.wait_ge(added, (o - 3) * (CHUNKS - 1))
                        dst = h if o == 0 else product[:, o % 3]
                        dst = dst[:, chunk(c)].rearrange("p (b n) -> p b n", b=2) if o == 0 else dst[:, 2 * c:2 * c + 2, :]
                        dve.tensor_tensor(dst, frames[:, 2 * c:2 * c + 2, o:o + POS],
                                          ps[(o * CHUNKS + c) % 8][:, :CHUNK].rearrange("p (b n) -> p b n", b=2), ALU.mult).then_inc(product_ready, 1)
                    if o:
                        dve.wait_ge(product_ready, (o + 1) * CHUNKS)
                        if o > 1:
                            dve.wait_ge(added_last, o - 1)
                        dve.tensor_tensor(h[:, chunk(CHUNKS - 1)], h[:, chunk(CHUNKS - 1)], product[:, o % 3, 6:8, :].rearrange("p b n -> p (b n)"), ALU.add).then_inc(added_last, 1)
                dve.wait_ge(added_last, WINDOW - 1)
                ln.vector(dve)

            @block.gpsimd
            def _(pool):
                pool.memset(weight_rows[:], 0.0).then_inc(zeroed, 1)
                for o in range(1, WINDOW):
                    for c in range(CHUNKS - 1):
                        pool.wait_ge(product_ready, o * CHUNKS + c + 1)
                        if o > 1:
                            pool.wait_ge(added, (o - 2) * (CHUNKS - 1) + c + 1)
                        pool.tensor_tensor(h[:, chunk(c)], h[:, chunk(c)], product[:, o % 3, 2 * c:2 * c + 2, :].rearrange("p b n -> p (b n)"), ALU.add).then_inc(added, 1)
                pool.wait_ge(added, (WINDOW - 1) * (CHUNKS - 1))
                ln.gpsimd(pool)

def batch_axis_attention(nc, h, x, w, ps):
    blocks, hd = 8, 8
    with Stage(nc, "mix") as s:
        pos_major = {n: s.sb(n + "_pos", [TILE, 2, blocks, SEQS, hd]) for n in ("query", "key", "value")}
        entry_major = {n: s.sb(n + "_entry", [128, COLS]) for n in ("query", "key", "value")}
        row_major = {n: s.sb(n + "_row", [TILE, TILES, 128]) for n in ("key", "value")}
        mixed = s.sb("mixed", [TILE, 2, SEQS, blocks, hd])
        top = s.sb("top", [TILE, 2 * blocks])
        total = s.sb("total", [TILE, 2 * blocks])
        inverse = s.sb("inverse", [TILE, 2 * blocks])
        factor = s.sb("factor", [TILE, 2 * blocks])
        key_top = s.sb("key_top", [128, blocks])
        key_total = s.sb("key_total", [128, blocks])
        key_inverse = s.sb("key_inverse", [128, blocks])
        context = s.sb("context", [128, blocks, 128])
        qkv_ready, qkv_kept = s.sem("qkv_ready"), s.sem("qkv_kept")
        q_top, q_less, q_exp, q_total, q_inverse, q_scaled = (
            s.sem(n) for n in ("q_top", "q_less", "q_exp", "q_total", "q_inverse", "q_scaled"))
        key_entry_ready, key_entry_kept, value_entry_ready, value_entry_kept = (
            s.sem(n) for n in ("key_entry_ready", "key_entry_kept", "value_entry_ready", "value_entry_kept"))
        key_top_ready, key_exp, key_inverse_ready, key_scaled = (
            s.sem(n) for n in ("key_top_ready", "key_exp", "key_inverse_ready", "key_scaled"))
        value_row_ready, value_row_kept, key_row_ready, key_row_kept = (
            s.sem(n) for n in ("value_row_ready", "value_row_kept", "key_row_ready", "key_row_kept"))
        q_entry_ready, q_entry_kept, context_ready, context_kept = (
            s.sem(n) for n in ("q_entry_ready", "q_entry_kept", "context_ready", "context_kept"))
        mixed_ready, mixed_kept, back_ready, h_ready = (s.sem(n) for n in ("mixed_ready", "mixed_kept", "back_ready", "h_ready"))

        def entries(n, b):
            t, g = b // 2, b % 2
            return entry_major[n][:].rearrange("p (c k) -> p k c", k=blocks)[:, 4 * g:4 * g + 4, TILE * t:TILE * t + TILE]

        ln = LayerNorm(s, h, x, w, ps, lambda eng, c: eng.wait_ge(h_ready, c + 1))
        with nc.Block() as block:

            @block.tensor
            def _(pe):
                for j in range(TILES):
                    if j >= 8:
                        pe.wait_ge(qkv_kept, 3 * (j - 7))
                    pe.matmul(ps[j % 8][0:TILE, 0:384], x[:, tile(j)], w["mix_qkv"], start=True, stop=True).then_inc(qkv_ready, 1)

                def turn(name, first, ready):
                    for b in range(4):
                        for k in range(4):
                            src = pos_major[name][:, b // 2, 4 * (b % 2) + k].rearrange("p r j -> p (r j)")
                            mm = pe.transpose(ps[first + b][:, tile(k)], src, w["ident"][0:TILE, 0:TILE])
                        mm.then_inc(ready, 1)

                def turn_rows(name, first, ready):
                    for b in range(4):
                        for k in range(4):
                            mm = pe.transpose(ps[first + b][0:TILE, 128 * k:128 * k + 128], entry_major[name][:, tile(4 * b + k)], w["ident"])
                        mm.then_inc(ready, 1)

                pe.wait_ge(qkv_kept, 3 * TILES)
                turn("key", 0, key_entry_ready)
                turn("value", 4, value_entry_ready)
                pe.wait_ge(value_entry_kept, 4)
                turn_rows("value", 4, value_row_ready)
                pe.wait_ge(key_scaled, blocks)
                turn_rows("key", 0, key_row_ready)
                pe.wait_ge(q_scaled, 1)
                pe.wait_ge(value_row_kept, 4)
                turn("query", 4, q_entry_ready)
                for n in range(2):
                    pe.wait_ge(key_row_kept, 4)
                    for k in range(4):
                        for t in range(2):
                            i = 2 * (4 * n + k) + t
                            mm = pe.matmul(ps[n][:, 128 * k:128 * k + 128], row_major["key"][:, i], row_major["value"][:, i],
                                           start=(t == 0), stop=(t == 1))
                    mm.then_inc(context_ready, 1)
                pe.wait_ge(q_entry_kept, 4)
                for t in range(2):
                    for n in range(2):
                        pe.wait_ge(context_kept, n + 1)
                        for k in range(4):
                            g = 4 * n + k
                            mm = pe.matmul(ps[4 + 2 * t + n][0:TILE, 128 * k:128 * k + 128], entry_major["query"][:, tile(2 * g + t)],
                                           context[:, g, :], start=True, stop=True)
                        mm.then_inc(mixed_ready, 1)
                pe.wait_ge(mixed_kept, 4)
                pe.wait_ge(context_kept, 2)
                for j in range(TILES):
                    src = mixed[:, j % 2, 2 * (j // 2):2 * (j // 2) + 2].rearrange("p r h j -> p (r h j)")
                    mm = pe.transpose(ps[j // 4][:, tile(j % 4)], src, w["ident"][0:TILE, 0:TILE])
                    if j % 4 == 3:
                        mm.then_inc(back_ready, 1)
                ln.tensor(pe)

            @block.scalar
            def _(act):
                for b in range(4):
                    act.wait_ge(key_entry_ready, b + 1)
                    act.activation(entries("key", b), ps[b][:, :CHUNK].rearrange("p (k c) -> p k c", k=4), ACT.Copy).then_inc(key_entry_kept, 1)
                act.wait_ge(q_less, 1)
                wide = pos_major["query"]
                act.activation(wide[:], wide[:], ACT.Exp).then_inc(q_exp, 1)
                act.wait_ge(key_top_ready, 1)
                for g in range(blocks):
                    rows_ = entry_major["key"][:, g * POS:(g + 1) * POS]
                    act.activation(rows_, rows_, ACT.Exp, bias=key_top[:, g:g + 1], accum_out=key_total[:, g:g + 1]).then_inc(key_exp, 1)
                for b in range(4):
                    act.wait_ge(key_row_ready, b + 1)
                    act.activation(row_major["key"][:, 4 * b:4 * b + 4, :], ps[b][0:TILE, :].rearrange("p (k e) -> p k e", k=4), ACT.Copy).then_inc(key_row_kept, 1)
                for b in range(4):
                    act.wait_ge(q_entry_ready, b + 1)
                    act.activation(entries("query", b), ps[4 + b][:, :CHUNK].rearrange("p (k c) -> p k c", k=4), ACT.Copy).then_inc(q_entry_kept, 1)
                for n in range(2):
                    act.wait_ge(context_ready, n + 1)
                    act.activation(context[:, 4 * n:4 * n + 4, :], ps[n][:].rearrange("p (a n) -> p a n", a=4), ACT.Copy).then_inc(context_kept, 1)
                ln.scalar(act)

            @block.vector
            def _(dve):
                for j in range(TILES):
                    dve.wait_ge(qkv_ready, j + 1)
                    for i, n in enumerate(("query", "key", "value")):
                        got = ps[j % 8][0:TILE, 128 * i:128 * i + 128].rearrange("p (a h j) -> p h a j", a=2, h=blocks)
                        bias = w["mix_qkvb"][0:TILE, 64 * i:64 * i + 64].rearrange("p (h j) -> p h j", h=blocks).unsqueeze(2).to_broadcast([TILE, blocks, 2, hd])
                        dve.tensor_tensor(pos_major[n][:, j % 2, :, 2 * (j // 2):2 * (j // 2) + 2], got, bias, ALU.add).then_inc(qkv_kept, 1)
                dve.wait_ge(qkv_kept, 3 * TILES)
                wide = pos_major["query"][:].rearrange("p t h r j -> p (t h) (r j)")
                dve.tensor_reduce(top[:], wide, AX.X, ALU.max).then_inc(q_top, 1)
                dve.wait_ge(key_entry_kept, 4)
                dve.tensor_reduce(key_top[:], entry_major["key"][:].rearrange("p (g n) -> p g n", n=POS), AX.X, ALU.max, negate=True).then_inc(key_top_ready, 1)
                for b in range(4):
                    dve.wait_ge(value_entry_ready, b + 1)
                    dve.tensor_copy(entries("value", b), ps[4 + b][:, :CHUNK].rearrange("p (k c) -> p k c", k=4)).then_inc(value_entry_kept, 1)
                dve.wait_ge(q_exp, 1)
                dve.tensor_reduce(total[:], wide, AX.X, ALU.add).then_inc(q_total, 1)
                dve.wait_ge(q_total, 1)
                dve.reciprocal(inverse[:], total[:]).then_inc(q_inverse, 1)
                dve.wait_ge(q_inverse, 1)
                dve.tensor_scalar(factor[:], inverse[:], float(SEQS * hd) ** 0.5, None, ALU.mult).then_inc(q_inverse, 1)
                dve.wait_ge(key_exp, blocks)
                dve.reciprocal(key_inverse[:], key_total[:]).then_inc(key_inverse_ready, 1)
                dve.wait_ge(key_inverse_ready, 1)
                for g in range(blocks):
                    rows_ = entry_major["key"][:, g * POS:(g + 1) * POS]
                    dve.tensor_scalar(rows_, rows_, key_inverse[:, g:g + 1], None, ALU.mult).then_inc(key_scaled, 1)
                for b in range(4):
                    dve.wait_ge(value_row_ready, b + 1)
                    dve.tensor_copy(row_major["value"][:, 4 * b:4 * b + 4, :], ps[4 + b][0:TILE, :].rearrange("p (k e) -> p k e", k=4)).then_inc(value_row_kept, 1)
                for t in range(2):
                    for n in range(2):
                        dve.wait_ge(mixed_ready, 2 * t + n + 1)
                        dst = mixed[:, t, :, 4 * n:4 * n + 4].rearrange("p r h j -> p h r j")
                        dve.tensor_copy(dst, ps[4 + 2 * t + n][0:TILE, :].rearrange("p (h r j) -> p h r j", h=4, r=SEQS)).then_inc(mixed_kept, 1)
                for c in range(CHUNKS):
                    dve.wait_ge(back_ready, c + 1)
                    dve.tensor_tensor(h[:, chunk(c)], h[:, chunk(c)], ps[c][:, :CHUNK], ALU.add).then_inc(h_ready, 1)
                dve.wait_ge(h_ready, CHUNKS)
                ln.vector(dve)

            @block.gpsimd
            def _(pool):
                wide = pos_major["query"][:].rearrange("p t h r j -> p (t h) (r j)")
                pool.wait_ge(q_top, 1)
                pool.tensor_tensor(wide, wide, top[:].unsqueeze(2).to_broadcast([TILE, 2 * blocks, 128]), ALU.subtract).then_inc(q_less, 1)
                pool.wait_ge(q_inverse, 2)
                pool.tensor_tensor(wide, wide, factor[:].unsqueeze(2).to_broadcast([TILE, 2 * blocks, 128]), ALU.mult).then_inc(q_scaled, 1)
                ln.gpsimd(pool)

            @block.sync
            def _(sp):
                ln.sync(sp)

def top_half_ffn(nc, h, x, w, ps):
    kept_tokens = max(1, int(0.5 * POS)) - 1
    with Stage(nc, "cap") as s:
        score = s.sb("score", [TILE, TILES, 2])
        above = s.sb("above", [TILE, TILES, 2])
        equal = s.sb("equal", [TILE, TILES, 2])
        gate = s.sb("gate", [TILE, TILES, 2])
        gate_wide = s.sb("gate_wide", [TILE, TILES, 2, 64])
        gate_f = s.sb("gate_f", [128, COLS])
        scratch = s.sb("scratch", [TILE, 4, POS])
        hidden = s.sb("hidden", [128, 2, 2, COLS])
        out = s.sb("out", [128, COLS])
        score_ready, score_kept, score_spread = s.sem("score_ready"), s.sem("score_kept"), s.sem("score_spread")
        counted, rank_ready, gate_ready = s.sem("counted"), s.sem("rank_ready"), s.sem("gate_ready")
        gate_spread, gate_kept = s.sem("gate_spread"), s.sem("gate_kept")
        up_ready, up_kept, down_ready = s.sem("up_ready"), s.sem("up_kept"), s.sem("down_ready")
        gated, h_plus_x, h_ready = s.sem("gated"), s.sem("h_plus_x"), s.sem("h_ready")
        ln = LayerNorm(s, h, x, w, ps, lambda eng, c: eng.wait_ge(h_ready, c + 1), group=3)
        with nc.Block() as block:

            @block.tensor
            def _(pe):
                for j in range(TILES):
                    mm = pe.matmul(ps[0][0:TILE, 2 * j:2 * j + 2], x[:, tile(j)], w["cap_r"], start=True, stop=True)
                mm.then_inc(score_ready, 1)
                pe.wait_ge(score_kept, 1)

                def spread(b):
                    if b >= 4:
                        pe.wait_ge(counted, 8 * (b - 3))
                    for k in range(4):
                        j = 4 * (b % 4) + k
                        mm = pe.transpose(ps[b % 4][0:TILE, tile(k)], score[:, j, b // 4].unsqueeze(1).to_broadcast([TILE, TILE]), w["ident"][0:TILE, 0:TILE])
                    mm.then_inc(score_spread, 1)

                def up(n):
                    c, m, a = n // 4, (n // 2) % 2, n % 2
                    if n >= 4:
                        pe.wait_ge(up_kept, n - 3)
                    pe.matmul(ps[4 + n % 4][:, :CHUNK], w["cap_1"][:, 256 * a + 128 * m:256 * a + 128 * m + 128], x[:, chunk(c)], start=True, stop=True).then_inc(up_ready, 1)

                for b in range(4):
                    spread(b)
                for b in range(4):
                    for k in range(4):
                        up(4 * b + k)
                    spread(4 + b)
                pe.wait_ge(up_kept, 16)
                for c in range(CHUNKS):
                    for a in range(2):
                        for m in range(2):
                            mm = pe.matmul(ps[4 + c][:, :CHUNK], w["cap_2"][:, 128 * (2 * a + m):128 * (2 * a + m) + 128], hidden[:, m, a, chunk(c)],
                                           start=(a + m == 0), stop=(a + m == 2))
                    mm.then_inc(down_ready, 1)
                pe.wait_ge(gate_ready, 2)
                for c in range(CHUNKS):
                    for k in range(4):
                        mm = pe.transpose(ps[c][:, tile(k)], gate_wide[:, 4 * c + k].rearrange("p a f -> p (a f)"), w["ident"][0:TILE, 0:TILE])
                    mm.then_inc(gate_spread, 1)
                ln.tensor(pe)

            @block.scalar
            def _(act):
                for n in range(16):
                    c, m, a = n // 4, (n // 2) % 2, n % 2
                    act.wait_ge(up_ready, n + 1)
                    act.activation(hidden[:, m, a, chunk(c)], ps[4 + n % 4][:, :CHUNK], ACT.Gelu_apprx_tanh, bias=w["cap_b1"][:, m:m + 1]).then_inc(up_kept, 1)
                for c in range(CHUNKS):
                    act.wait_ge(gate_spread, c + 1)
                    act.activation(gate_f[:, chunk(c)], ps[c][:, :CHUNK], ACT.Copy).then_inc(gate_kept, 1)
                ln.scalar(act)

            @block.vector
            def _(dve):
                dve.wait_ge(score_ready, 1)
                dve.tensor_scalar(score[:], ps[0][0:TILE, 0:2 * TILES].rearrange("p (j a) -> p j a", a=2), w["cap_br"][0:TILE, :], None, ALU.add).then_inc(score_kept, 1)
                dve.wait_ge(score_kept, 1)
                for b in range(8):
                    dve.wait_ge(score_spread, b + 1)
                    for k in range(4):
                        j, a, n = 4 * (b % 4) + k, b // 4, 8 * b + 2 * k
                        seq = ps[b % 4][0:TILE, (k // 2) * POS:(k // 2 + 1) * POS]
                        mine = score[:, j, a:a + 1]
                        if n >= 4:
                            dve.wait_ge(counted, n - 2)
                        dve.tensor_scalar(scratch[:, n % 4], seq, mine, None, ALU.is_gt, ALU.add, accum_out=above[:, j, a:a + 1]).then_inc(counted, 1)
                        dve.scalar_tensor_tensor(scratch[:, n % 4 + 1], seq, mine, w["cap_earlier"][0:TILE, POS * (j % 2):POS * (j % 2) + POS],
                                                 ALU.is_equal, ALU.mult, accum_out=equal[:, j, a:a + 1]).then_inc(counted, 1)
                dve.wait_ge(counted, 64)
                dve.tensor_tensor(above[:], above[:], equal[:], ALU.add).then_inc(rank_ready, 1)
                dve.wait_ge(rank_ready, 1)
                dve.scalar_tensor_tensor(gate[:].rearrange("p j a -> p (j a)"), above[:].rearrange("p j a -> p (j a)"), float(kept_tokens),
                                         score[:].rearrange("p j a -> p (j a)"), ALU.is_lt, ALU.mult).then_inc(gate_ready, 1)
                dve.wait_ge(gate_ready, 1)
                dve.tensor_copy(gate_wide[:], gate[:].unsqueeze(3).to_broadcast([TILE, TILES, 2, 64])).then_inc(gate_ready, 1)
                for c in range(CHUNKS):
                    dve.wait_ge(down_ready, c + 1)
                    dve.wait_ge(gate_kept, c + 1)
                    dve.scalar_tensor_tensor(out[:, chunk(c)], ps[4 + c][:, :CHUNK], w["cap_b2"], gate_f[:, chunk(c)], ALU.add, ALU.mult).then_inc(gated, 1)
                dve.wait_ge(h_plus_x, 1)
                for c in range(CHUNKS):
                    dve.wait_ge(gated, c + 1)
                    dve.tensor_tensor(h[:, chunk(c)], h[:, chunk(c)], out[:, chunk(c)], ALU.add).then_inc(h_ready, 1)
                dve.wait_ge(h_ready, CHUNKS)
                ln.vector(dve)

            @block.gpsimd
            def _(pool):
                pool.tensor_tensor(h[:], h[:], x[:], ALU.add).then_inc(h_plus_x, 1)
                ln.gpsimd(pool)

            @block.sync
            def _(sp):
                ln.sync(sp)

def taylor_attention(nc, h, x, w, ps):
    heads, hd, feats, group = 8, 8, 45, 8
    eps = 1e-12
    scale = float(hd) ** 0.25
    seqs = 2 * TILES
    with Stage(nc, "tay") as s:
        qkv = s.sb("qkv", [TILE, 3, TILES, 2, FEAT])
        phi_k = s.sb("phi_k", [TILE, seqs, heads, feats])
        phi_q = s.sb("phi_q", [TILE, 2, group, heads, feats])
        value_wide = s.sb("value", [TILE, seqs * heads * (hd + 1) + 14])
        value = value_wide[:, 0:seqs * heads * (hd + 1)].rearrange("p (a h e) -> p a h e", a=seqs, h=heads)
        norm2 = s.sb("norm2", [TILE, 2, seqs, heads])
        norm = s.sb("norm", [TILE, 2, seqs, heads])
        factor = s.sb("factor", [TILE, 2, seqs, heads])
        kv_turned = s.sb("kv_turned", [128, SEQS, 90])
        kv = s.sb("kv", [90, SEQS, 128])
        phi_t = s.sb("phi_t", [90, 4, 4, TILE])
        inverse = s.sb("inverse", [128, 2, CHUNK])
        y = s.sb("y", [128, 2, CHUNK])
        y_scaled = s.sb("y_scaled", [128, 2, CHUNK])
        squares = phi_q[:].rearrange("p n a h f -> p (n a h f)")[:, 0:2 * seqs * FEAT].rearrange("p (i a f) -> p i a f", i=2, a=seqs)
        (qkv_ready, qkv_kept, squared, norm2_ready, norm_ready, norm_safe, norm_inverse, factor_ready, value_ready, ones_ready,
         key_unit, query_unit, key_products, query_products, kv_ready, kv_kept, kv_back, kv_masked, turned, turned_kept, y_ready,
         y_kept, sum_ready, y_inverse, y_done, out_ready, h_ready) = (s.sem(n) for n in (
             "qkv_ready qkv_kept squared norm2_ready norm_ready norm_safe norm_inverse factor_ready value_ready ones_ready "
             "key_unit query_unit key_products query_products kv_ready kv_kept kv_back kv_masked turned turned_kept y_ready "
             "y_kept sum_ready y_inverse y_done out_ready h_ready").split())

        def vectors(i, lo, n):
            return qkv[:, i].rearrange("p j a (h e) -> p (j a) h e", h=heads)[:, lo:lo + n]

        def products(eng, phi, n, done):
            flat = phi.rearrange("p a h f -> p (a h) f")
            at = 0
            for i in range(hd):
                k = hd - i
                last = eng.tensor_tensor(flat[:, :, at:at + k], flat[:, :, 36 + i:37 + i].to_broadcast([TILE, n * heads, k]),
                                         flat[:, :, 36 + i:44], ALU.mult)
                at += k
                last.then_inc(done, 1)

        ln = LayerNorm(s, h, x, w, ps, lambda eng, c: eng.wait_ge(h_ready, 2 if c < 2 else CHUNKS), group=4)
        with nc.Block() as block:

            @block.tensor
            def _(pe):
                for j in range(TILES):
                    if j >= 8:
                        pe.wait_ge(qkv_kept, j - 7)
                    pe.matmul(ps[j % 8][0:TILE, 0:384], x[:, tile(j)], w["tay_qkv"], start=True, stop=True).then_inc(qkv_ready, 1)
                pe.wait_ge(ones_ready, 3)
                pe.wait_ge(value_ready, 1)
                pe.wait_ge(qkv_kept, TILES)
                for n in range(4):
                    pe.wait_ge(key_products, hd * (n // 2 + 1))
                    for k in range(4):
                        p, a = 2 * n + k // 2, k % 2
                        for t in range(2):
                            col = 2 * (2 * p + t) + a
                            for g in range(4):
                                at = 72 * col + 18 * g
                                mm = pe.matmul(ps[n][32 * g:32 * g + 32, 90 * k:90 * k + 90], value_wide[:, at:at + 32],
                                               phi_k[:, col, 2 * g:2 * g + 2].rearrange("p h f -> p (h f)"), start=(t == 0), stop=(t == 1), tile_position=(0, 32 * g))
                    mm.then_inc(kv_ready, 1)
                for n in range(4):
                    pe.wait_ge(kv_kept, n + 1)
                    for k in range(4):
                        mm = pe.transpose(ps[4 + n][0:90, 128 * k:128 * k + 128], kv_turned[:, 4 * n + k], w["ident"])
                    mm.then_inc(kv_back, 1)

                def turn(col):
                    if col % group == 0:
                        pe.wait_ge(query_products, hd * (col // group + 1))
                    if col < 4:
                        pe.wait_ge(kv_masked, col + 1)
                    else:
                        pe.wait_ge(turned_kept, col - 3)
                    for g in range(4):
                        mm = pe.transpose(ps[4 + col % 4][0:90, tile(g)],
                                          phi_q[:, (col // group) % 2, col % group, 2 * g:2 * g + 2].rearrange("p h f -> p (h f)"),
                                          w["ident"][0:TILE, 0:TILE])
                    mm.then_inc(turned, 1)

                def outputs(col):
                    c, k, a = col // group, col % group // 2, col % 2
                    pe.wait_ge(turned_kept, col + 1)
                    if k == 0 and c >= 2:
                        pe.wait_ge(h_ready, c - 1)
                        pe.wait_ge(y_inverse, 2 * (c - 2) + a + 1)
                    for g in range(4):
                        mm = pe.matmul(ps[2 * (c % 2) + a][32 * g:32 * g + 32, tile(k)], kv[:, 2 * (col // 4) + a, 32 * g:32 * g + 32], phi_t[:, col % 4, g, :],
                                       start=True, stop=True, tile_position=(0, 32 * g))
                    mm.then_inc(y_ready, 1)

                def sums(u):
                    pe.wait_ge(y_kept, u + 1)
                    pe.matmul(ps[u % 4][:, :CHUNK], w["tay_sum"], y[:, u % 2], start=True, stop=True).then_inc(sum_ready, 1)

                def project(c):
                    pe.wait_ge(y_done, 2 * c + 2)
                    for a in range(2):
                        pe.matmul(ps[2 * (c % 2)][64 * a:64 * a + 64, :CHUNK], w["tay_o"], y_scaled[:, a], start=True, stop=True, tile_position=(0, 64 * a)).then_inc(out_ready, 1)

                for col in range(seqs + 2):
                    if col < seqs:
                        turn(col)
                    if col >= 2:
                        outputs(col - 2)
                    if col % group == 3 and col >= group:
                        sums(2 * (col // group) - 2)
                        sums(2 * (col // group) - 1)
                    if col % group == 1 and col >= 2 * group:
                        project(col // group - 2)
                sums(2 * CHUNKS - 2)
                sums(2 * CHUNKS - 1)
                project(CHUNKS - 1)
                ln.tensor(pe)

            @block.scalar
            def _(act):
                act.wait_ge(qkv_kept, TILES)
                for i in (1, 0):
                    act.activation(squares[:, i], qkv[:, i].rearrange("p j a f -> p (j a) f"), ACT.Square).then_inc(squared, 1)
                act.wait_ge(norm2_ready, 1)
                act.activation(norm[:, 1], norm2[:, 1], ACT.Sqrt).then_inc(norm_ready, 1)
                act.wait_ge(ones_ready, 2)
                act.activation(value[:, :, :, 1:], vectors(2, 0, seqs), ACT.Copy, scale=1.0 / POS).then_inc(value_ready, 1)
                act.wait_ge(norm2_ready, 2)
                act.activation(norm[:, 0], norm2[:, 0], ACT.Sqrt, scale=scale * scale).then_inc(norm_ready, 1)
                for n in range(4):
                    act.wait_ge(kv_ready, n + 1)
                    act.activation(kv_turned[:, 4 * n:4 * n + 4], ps[n][:, 0:360].rearrange("p (s f) -> p s f", f=90), ACT.Copy).then_inc(kv_kept, 1)

                def keep_y(u):
                    act.wait_ge(y_ready, group * (u // 2) + group - 1 + u % 2)
                    if u >= 2:
                        act.wait_ge(y_done, u - 1)
                    act.activation(y[:, u % 2], ps[u % 4][:, :CHUNK], ACT.Copy).then_inc(y_kept, 1)

                for col in range(seqs):
                    if col % group == 2 and col >= group:
                        keep_y(2 * (col // group) - 2)
                        keep_y(2 * (col // group) - 1)
                    act.wait_ge(turned, col + 1)
                    if col >= 4:
                        act.wait_ge(y_ready, col - 3)
                    act.activation(phi_t[:, col % 4], ps[4 + col % 4][0:90, :CHUNK].rearrange("p (g n) -> p g n", g=4), ACT.Copy).then_inc(turned_kept, 1)
                keep_y(2 * CHUNKS - 2)
                keep_y(2 * CHUNKS - 1)
                ln.scalar(act)

            @block.vector
            def _(dve):
                for j in range(TILES):
                    dve.wait_ge(qkv_ready, j + 1)
                    dve.tensor_tensor(qkv[:, :, j].rearrange("p i a f -> p i (a f)"), ps[j % 8][0:TILE, 0:384].rearrange("p (i f) -> p i f", i=3),
                                      w["tay_qkvb"][0:TILE, :].rearrange("p (i f) -> p i f", i=3), ALU.add).then_inc(qkv_kept, 1)

                def sum_squares(i):
                    dve.tensor_reduce(norm2[:, i].rearrange("p a h -> p (a h)"), squares[:, i].rearrange("p a (h e) -> p (a h) e", e=hd), AX.X, ALU.add).then_inc(norm2_ready, 1)

                def invert_norm(i, n):
                    dve.wait_ge(norm_ready, n + 1)
                    dve.tensor_scalar(norm[:, i], norm[:, i], eps, None, ALU.max).then_inc(norm_safe, 1)
                    dve.wait_ge(norm_safe, n + 1)
                    dve.reciprocal(norm2[:, i], norm[:, i]).then_inc(norm_inverse, 1)
                    dve.wait_ge(norm_inverse, n + 1)

                dve.wait_ge(squared, 1)
                sum_squares(1)
                invert_norm(1, 0)
                dve.tensor_scalar(factor[:, 1], norm2[:, 1], scale, None, ALU.mult).then_inc(factor_ready, 1)
                dve.wait_ge(factor_ready, 1)
                dve.wait_ge(ones_ready, 1)
                dve.tensor_tensor(phi_k[:, :, :, 36:44], vectors(1, 0, seqs), factor[:, 1].unsqueeze(3).to_broadcast([TILE, seqs, heads, hd]), ALU.mult).then_inc(key_unit, 1)
                dve.wait_ge(squared, 2)
                sum_squares(0)
                dve.wait_ge(key_unit, 1)
                products(dve, phi_k[:, 0:seqs // 2], seqs // 2, key_products)
                invert_norm(0, 1)
                dve.scalar_tensor_tensor(factor[:, 0], norm2[:, 0], scale * scale, w["tay_temp"][0:TILE, :].unsqueeze(1).to_broadcast([TILE, seqs, heads]),
                                         ALU.mult, ALU.mult).then_inc(factor_ready, 1)
                products(dve, phi_k[:, seqs // 2:], seqs // 2, key_products)
                for n in range(4):
                    dve.wait_ge(kv_back, n + 1)
                    dve.tensor_tensor(kv[:, 4 * n:4 * n + 4], ps[4 + n][0:90, :].rearrange("p (s f) -> p s f", f=128),
                                      w["tay_coef"][0:90, :].unsqueeze(1).to_broadcast([90, 4, 128]), ALU.mult).then_inc(kv_masked, 1)

                def add_chunk(c):
                    dve.wait_ge(out_ready, 2 * c + 2)
                    dve.scalar_tensor_tensor(h[:, chunk(c)], ps[2 * (c % 2)][:, :CHUNK], w["tay_ob"], h[:, chunk(c)], ALU.add, ALU.add).then_inc(h_ready, 1)

                for u in range(2 * CHUNKS):
                    if u >= 2 and u % 2 == 0:
                        add_chunk(u // 2 - 1)
                    dve.wait_ge(sum_ready, u + 1)
                    dve.reciprocal(inverse[:, u % 2], ps[u % 4][:, :CHUNK]).then_inc(y_inverse, 1)
                    dve.wait_ge(y_inverse, u + 1)
                    if u >= 2:
                        dve.wait_ge(out_ready, u - u % 2)
                    dve.tensor_tensor(y_scaled[:, u % 2], y[:, u % 2], inverse[:, u % 2], ALU.mult).then_inc(y_done, 1)
                add_chunk(CHUNKS - 1)
                dve.wait_ge(h_ready, CHUNKS)
                ln.vector(dve)

            @block.gpsimd
            def _(pool):
                pool.memset(phi_k[:, :, :, 44:45], 1.0).then_inc(ones_ready, 1)
                pool.memset(value[:, :, :, 0:1], 1.0 / POS).then_inc(ones_ready, 1)
                pool.memset(value_wide[:, seqs * heads * (hd + 1):], 0.0).then_inc(ones_ready, 1)
                pool.wait_ge(norm2_ready, 2)
                pool.memset(phi_q[:, 0, :, :, 44:45], 1.0).then_inc(ones_ready, 1)
                pool.memset(phi_q[:, 1, :, :, 44:45], 1.0).then_inc(ones_ready, 1)
                pool.wait_ge(factor_ready, 2)
                pool.wait_ge(ones_ready, 5)
                for n in range(seqs // group):
                    if n >= 2:
                        pool.wait_ge(turned, group * (n - 1))
                    lo = group * n
                    pool.tensor_tensor(phi_q[:, n % 2, :, :, 36:44], vectors(0, lo, group),
                                       factor[:, 0, lo:lo + group].unsqueeze(3).to_broadcast([TILE, group, heads, hd]), ALU.mult).then_inc(query_unit, 1)
                    pool.wait_ge(query_unit, n + 1)
                    products(pool, phi_q[:, n % 2], group, query_products)
                ln.gpsimd(pool)

            @block.sync
            def _(sp):
                ln.sync(sp)

def expert_routing(nc, x, w, ps, r, d, experts_in):
    cols = 2 * TILES
    tokens = r["tokens"]
    with Stage(nc, "route") as s:
        token_major = s.sb("token_major", [TILE, cols, FEAT])
        logits = s.sb("logits", [TILE, cols, EXPERTS])
        best = s.sb("best", [TILE, cols, 8])
        best_at = s.sb("best_at", [TILE, cols, 8], U32)
        chosen = s.sb("chosen", [TILE, 2, cols], BF16)
        low_of = s.sb("low_of", [TILE, 2 * cols], BF16)
        ratio = s.sb("ratio", [TILE, cols])
        denominator = s.sb("denominator", [TILE, cols])
        choice = [s.sb(f"choice{k}", [TILE, EXPERTS, cols], BF16) for k in range(2)]
        picked = s.sb("picked", [TILE, EXPERTS, cols], BF16)
        running = s.sb("running", [TILE, EXPERTS, cols], BF16)
        before = s.sb("before", [TILE, EXPERTS, cols], BF16)
        keep = s.sb("keep", [TILE, EXPERTS, cols], BF16)
        earlier = s.sb("earlier", [TILE, TILE], BF16)
        ones = s.sb("ones", [TILE, 128], BF16)
        rounded = s.sb("rounded", [128, EXPERTS], I32)
        shifted = s.sb("shifted", [128, EXPERTS], I32)
        tiles_of = s.sb("tiles_of", [128, EXPERTS])
        end_tile = s.sb("end_tile", [128, EXPERTS])
        first_slot = s.sb("first_slot", [128, EXPERTS])
        ended = s.sb("ended", [128, EXPERTS])
        expert_col = s.sb("expert_col", [128, 1])
        places = s.sb("places", [TILE, EXPERTS, cols])
        product = s.sb("product", [TILE, EXPERTS, cols])
        slot = s.sb("slot", [TILE, cols, 2])
        split_i = s.sb("split_i", [TILE, 2, cols * 2], I32)
        split = s.sb("split", [TILE, 2, cols * 2], BF16)
        lane_hot, tile_hot = (a[:].rearrange("p e a -> p (e a)").bitcast(BF16).rearrange("p (l a) -> p l a", a=cols) for a in (product, places))
        tile_high = s.sb("tile_high", [TILE, 128, cols], BF16)
        low_digit = s.sb("low_digit", [128, 128])
        combine = logits
        second = s.sb("second", [TILE, cols, EXPERTS])
        numbers_wide = s.sb("numbers_wide", [TILE, 128, cols], BF16)
        (logits_ready, logits_kept, token_ready, token_kept, best_ready, index_ready, chosen_ready, gap_ready, ratio_ready,
         gates_ready, numbers_ready, hot_ready, picked_ready, consts_ready, running_ready, before_ready, counts_ready, count_steps, prefix_ready,
         places_ready, product_ready, slot_ready, split_ready, hot_tiles, source_ready, low_kept, expert_turned, expert_kept,
         combine_ready, combine_turned, combine_kept, stored) = (s.sem(n) for n in (
             "logits_ready logits_kept token_ready token_kept best_ready index_ready chosen_ready gap_ready ratio_ready "
             "gates_ready numbers_ready hot_ready picked_ready consts_ready running_ready before_ready counts_ready count_steps prefix_ready "
             "places_ready product_ready slot_ready split_ready hot_tiles source_ready low_kept expert_turned expert_kept "
             "combine_ready combine_turned combine_kept stored").split())
        with nc.Block() as block:

            @block.tensor
            def _(pe):
                for j in range(TILES):
                    mm = pe.matmul(ps[j // 4][0:TILE, 128 * (j % 4):128 * (j % 4) + 128], x[:, tile(j)], w["moe_r"], start=True, stop=True)
                    if j % 4 == 3:
                        mm.then_inc(logits_ready, 1)
                for j in range(TILES):
                    mm = pe.transpose(ps[4 + j // 4][0:TILE, 128 * (j % 4):128 * (j % 4) + 128], x[:, tile(j)], w["ident"])
                    if j % 4 == 3:
                        mm.then_inc(token_ready, 1)
                pe.wait_ge(consts_ready, 4)
                pe.wait_ge(running_ready, 1)
                pe.wait_ge(token_kept, 4)
                pe.matmul(ps[4][:, 0:EXPERTS], ones[:], running[:, :, cols - 1], start=True, stop=True).then_inc(counts_ready, 1)
                pe.wait_ge(before_ready, 1)
                for b in range(4):
                    pe.matmul(ps[b][0:TILE, :], earlier[:], picked[:, 16 * b:16 * b + 16, :].rearrange("p e a -> p (e a)"), start=True, stop=False)
                    pe.matmul(ps[b][0:TILE, :], ones[:, 0:TILE], before[:, 16 * b:16 * b + 16, :].rearrange("p e a -> p (e a)"), start=False, stop=True).then_inc(prefix_ready, 1)
                pe.wait_ge(count_steps, 8)
                pe.transpose(ps[4][0:1, 128:256], expert_col[:], w["ident"]).then_inc(expert_turned, 1)
                for half in range(2):
                    for d in range(2):
                        pe.wait_ge(hot_tiles, 4 * half + 3 + d)
                        for k in range(cols):
                            mm = pe.matmul(ps[5 + d][:, 0:128], lane_hot[:, :, k], (tile_high if d == 0 else tile_hot)[:, :, k],
                                           start=(half + k == 0), stop=(half == 1 and k == cols - 1))
                        mm.then_inc(source_ready, 1)
                pe.wait_ge(combine_ready, 3)
                pe.wait_ge(places_ready, 4)
                for j in range(TILES):
                    mm = pe.transpose(ps[j // 4][:, tile(j % 4)], combine[:, 2 * j:2 * j + 2].rearrange("p a e -> p (a e)"), w["ident"][0:TILE, 0:TILE])
                    if j % 4 == 3:
                        mm.then_inc(combine_turned, 1)

            @block.scalar
            def _(act):
                act.activation(earlier[:], w["moe_tri"][0:TILE, :], ACT.Copy).then_inc(consts_ready, 1)
                act.activation(ones[:], w["moe_ones"][0:TILE, :], ACT.Copy).then_inc(consts_ready, 1)
                act.activation(numbers_wide[:], w["iota"][0:TILE, :].unsqueeze(2).to_broadcast([TILE, 128, cols]), ACT.Copy).then_inc(numbers_ready, 1)
                act.activation(low_of[:], w["moe_low"][0:TILE, :], ACT.Copy).then_inc(numbers_ready, 1)
                for b in range(4):
                    act.wait_ge(token_ready, b + 1)
                    act.activation(token_major[:, 8 * b:8 * b + 8].rearrange("p a f -> p (a f)"), ps[4 + b][0:TILE, :], ACT.Copy).then_inc(token_kept, 1)
                act.wait_ge(gap_ready, 1)
                act.activation(ratio[:], ratio[:], ACT.Exp).then_inc(ratio_ready, 1)
                act.wait_ge(expert_turned, 1)
                act.activation(r["expert"][:], ps[4][0:1, 128:256], ACT.Copy).then_inc(expert_kept, 1)
                act.wait_ge(source_ready, 4)
                act.activation(low_digit[:], ps[6][:, 0:128], ACT.Copy).then_inc(low_kept, 1)
                for c in range(CHUNKS):
                    act.wait_ge(combine_turned, c + 1)
                    act.activation(r["combine_t"][:, chunk(c)], ps[c][:, :CHUNK], ACT.Copy).then_inc(combine_kept, 1)

            @block.vector
            def _(dve):
                for b in range(4):
                    dve.wait_ge(logits_ready, b + 1)
                    dve.tensor_tensor(logits[:, 8 * b:8 * b + 8], ps[b][0:TILE, :].rearrange("p (a e) -> p a e", e=EXPERTS),
                                      w["moe_br"][0:TILE, :].unsqueeze(1).to_broadcast([TILE, 8, EXPERTS]), ALU.add).then_inc(logits_kept, 1)
                dve.wait_ge(logits_kept, 4)
                for a in range(cols):
                    dve.max(best[:, a], logits[:, a]).then_inc(best_ready, 1)
                for a in range(cols):
                    dve.wait_ge(best_ready, a + 1)
                    dve.max_index(best_at[:, a], best[:, a], logits[:, a]).then_inc(index_ready, 1)
                dve.tensor_tensor(ratio[:].unsqueeze(2), best[:, :, 1:2], best[:, :, 0:1], ALU.subtract).then_inc(gap_ready, 1)
                dve.wait_ge(index_ready, cols)
                dve.tensor_copy(chosen[:].rearrange("p k a -> p a k"), best_at[:, :, 0:2]).then_inc(chosen_ready, 1)
                dve.wait_ge(chosen_ready, 1)
                dve.wait_ge(numbers_ready, 2)
                for k in range(2):
                    dve.tensor_tensor(choice[k][:], numbers_wide[:, 0:EXPERTS],
                                      chosen[:, k].unsqueeze(1).to_broadcast([TILE, EXPERTS, cols]), ALU.is_equal).then_inc(hot_ready, 1)
                dve.wait_ge(ratio_ready, 1)
                dve.tensor_scalar(denominator[:], ratio[:], 1.0, None, ALU.add).then_inc(gates_ready, 1)
                dve.wait_ge(gates_ready, 1)
                dve.reciprocal(r["gates"][:, 0], denominator[:]).then_inc(gates_ready, 1)
                dve.wait_ge(gates_ready, 2)
                dve.tensor_tensor(r["gates"][:, 1], r["gates"][:, 0], ratio[:], ALU.mult).then_inc(gates_ready, 1)
                dve.wait_ge(hot_ready, 2)
                dve.tensor_tensor(picked[:], choice[0][:], choice[1][:], ALU.add).then_inc(picked_ready, 1)
                dve.wait_ge(picked_ready, 1)
                dve.wait_ge(consts_ready, 4)
                dve.tensor_tensor_scan(running[:].rearrange("p e a -> p (e a)"), keep[:].rearrange("p e a -> p (e a)"),
                                       picked[:].rearrange("p e a -> p (e a)"), 0.0, ALU.mult, ALU.add).then_inc(running_ready, 1)
                dve.wait_ge(running_ready, 1)
                dve.tensor_tensor(before[:], running[:], picked[:], ALU.subtract).then_inc(before_ready, 1)
                dve.wait_ge(counts_ready, 1)
                dve.tensor_scalar(rounded[:], ps[4][:, 0:EXPERTS], 127.0, None, ALU.add).then_inc(count_steps, 1)
                dve.wait_ge(count_steps, 1)
                dve.tensor_scalar(shifted[:], rounded[:], 7, None, ALU.arith_shift_right).then_inc(count_steps, 1)
                dve.wait_ge(count_steps, 2)
                dve.tensor_copy(tiles_of[:], shifted[:]).then_inc(count_steps, 1)
                dve.wait_ge(count_steps, 3)
                dve.tensor_tensor_scan(end_tile[:], w["moe_ones"][:, 0:EXPERTS], tiles_of[:], 0.0, ALU.mult, ALU.add).then_inc(count_steps, 1)
                dve.wait_ge(count_steps, 4)
                dve.tensor_tensor(first_slot[:], end_tile[:], tiles_of[:], ALU.subtract).then_inc(count_steps, 1)
                dve.tensor_scalar(ended[:], end_tile[:], w["iota_p"], None, ALU.is_le, ALU.add, accum_out=expert_col[:]).then_inc(count_steps, 1)
                dve.wait_ge(count_steps, 6)
                dve.tensor_scalar(first_slot[:], first_slot[:], 128.0, None, ALU.mult).then_inc(count_steps, 1)
                dve.tensor_scalar(expert_col[:], expert_col[:], EXPERTS - 1.0, None, ALU.min).then_inc(count_steps, 1)
                dve.wait_ge(count_steps, 8)
                for b in range(4):
                    dve.wait_ge(prefix_ready, b + 1)
                    dve.tensor_tensor(places[:, 16 * b:16 * b + 16], ps[b][0:TILE, :].rearrange("p (e a) -> p e a", a=cols),
                                      first_slot[0:TILE, 16 * b:16 * b + 16].unsqueeze(2).to_broadcast([TILE, 16, cols]), ALU.add).then_inc(places_ready, 1)
                dve.wait_ge(places_ready, 4)
                for k in range(2):
                    if k:
                        dve.wait_ge(slot_ready, k)
                    dve.tensor_tensor(product[:], choice[k][:], places[:], ALU.mult).then_inc(product_ready, 1)
                    dve.wait_ge(product_ready, k + 1)
                    dve.tensor_reduce(slot[:, :, k], product[:].rearrange("p e a -> p a e"), AX.X, ALU.add).then_inc(slot_ready, 1)
                dve.wait_ge(slot_ready, 2)
                dve.tensor_copy(r["slot"][:], slot[:].rearrange("p a k -> p (a k)")).then_inc(slot_ready, 1)
                dve.wait_ge(slot_ready, 3)
                dve.tensor_scalar(split_i[:, 0], r["slot"][:], 127, None, ALU.bitwise_and).then_inc(split_ready, 1)
                dve.tensor_scalar(split_i[:, 1], r["slot"][:], 7, None, ALU.arith_shift_right).then_inc(split_ready, 1)
                dve.wait_ge(split_ready, 2)
                dve.tensor_copy(split[:], split_i[:]).then_inc(split_ready, 1)
                dve.wait_ge(split_ready, 3)
                wide = [TILE, 128, cols]
                for half in range(2):
                    mine = slice(cols * half, cols * half + cols)
                    if half:
                        dve.wait_ge(source_ready, 2)
                    dve.tensor_tensor(lane_hot, numbers_wide[:], split[:, 0, mine].unsqueeze(1).to_broadcast(wide), ALU.is_equal).then_inc(hot_tiles, 1)
                    dve.tensor_tensor(tile_hot, numbers_wide[:], split[:, 1, mine].unsqueeze(1).to_broadcast(wide), ALU.is_equal).then_inc(hot_tiles, 1)
                    dve.wait_ge(hot_tiles, 4 * half + 2)
                    dve.tensor_scalar(tile_high[:], tile_hot, w["moe_high"][0:TILE, :], None, ALU.mult).then_inc(hot_tiles, 1)
                    dve.wait_ge(hot_tiles, 4 * half + 3)
                    dve.tensor_tensor(tile_hot, tile_hot, low_of[:, mine].unsqueeze(1).to_broadcast(wide), ALU.mult).then_inc(hot_tiles, 1)
                dve.wait_ge(low_kept, 1)
                dve.scalar_tensor_tensor(r["source"][:], ps[5][:, 0:128], 64.0, low_digit[:], ALU.mult, ALU.add).then_inc(source_ready, 1)
                dve.wait_ge(source_ready, 5)

            @block.gpsimd
            def _(pool):
                pool.memset(keep[:, :, 1:], 1.0).then_inc(consts_ready, 1)
                pool.memset(keep[:, :, 0:1], 0.0).then_inc(consts_ready, 1)
                pool.wait_ge(gates_ready, 3)
                pool.wait_ge(index_ready, cols)
                for k, dst in enumerate((combine, second)):
                    pool.tensor_tensor(dst[:], choice[k][:].rearrange("p e a -> p a e"),
                                       r["gates"][:, k].unsqueeze(2).to_broadcast([TILE, cols, EXPERTS]), ALU.mult).then_inc(combine_ready, 1)
                pool.wait_ge(combine_ready, 2)
                pool.tensor_tensor(combine[:], combine[:], second[:], ALU.add).then_inc(combine_ready, 1)

            @block.sync
            def _(sp):
                sp.dma_start(r["w1"][:], d["experts1"]).then_inc(experts_in, 16)
                sp.dma_start(r["w2"][:], d["experts2"]).then_inc(experts_in, 16)
                sp.wait_ge(token_kept, 4)
                sp.dma_start(tokens.rearrange("(n a) f -> n (a f)", a=cols), token_major[:].rearrange("p a f -> p (a f)")).then_inc(stored, 16)
                sp.wait_ge(stored, 16)

def expert_tables(nc, w, ps, r, experts_in):
    ring, group = 8, 4
    rounds = TABLE_TILES // ring
    gathers = -(-FILLED_TILES // group) * group
    with Stage(nc, "table") as s:
        rows_in = s.sb("rows_in", [128, 2, ring, FEAT])
        rows_t = s.sb("rows_t", [FEAT + 1, ring, 128])
        hidden = s.sb("hidden", [128, ring, 128])
        hidden_t = s.sb("hidden_t", [128, ring, 128])
        out = s.sb("out", [128, ring, FEAT])
        gathered = [s.pool_dma_sem(f"gathered{g}") for g in range(4)]
        rows_here = s.sem("rows_here")
        rows_turned, rows_kept, hidden_ready, hidden_kept, hidden_turned, hidden_t_kept, out_ready, out_kept, ones_ready = (
            s.sem(n) for n in "rows_turned rows_kept hidden_ready hidden_kept hidden_turned hidden_t_kept out_ready out_kept ones_ready".split())
        stored = [s.sem(f"stored{g}") for g in range(2)]
        w1, w2 = r["w1"], r["w2"]
        table = r["table"].rearrange("(t l) f -> l t f", l=128)
        with nc.Block() as block:

            @block.gpsimd
            def _(pool):
                for n in range(gathers):
                    if n >= 2 * ring:
                        pool.wait_ge(rows_turned, (n - 2 * ring) // group + 1)
                    pool.indirect_dma_start(out=rows_in[:, n // ring % 2, n % ring, :], out_offset=None, in_=r["tokens"],
                                            in_offset=bass.IndirectOffsetOnAxis(ap=r["source"][:, n:n + 1], axis=0)).then_inc(gathered[n // group % 4], 16)

            @block.tensor
            def _(pe):

                def turn_rows(i, place, gathered_groups=2):
                    for g in range(2):
                        if g < gathered_groups:
                            pe.wait_ge(gathered[2 * place + g], (i - place) * (16 * group // 2) + 16 * group)
                            pe.sem_inc(rows_here, 1)
                        for k in range(group):
                            mm = pe.transpose(ps[g][0:FEAT, 128 * k:128 * k + 128], rows_in[:, place, group * g + k, :], w["ident"])
                        mm.then_inc(rows_turned, 1)

                def experts_of(i, step):
                    registers = [pe.alloc_register(f"{step}_expert{k}") for k in range(ring)]
                    pe.load(registers, r["expert"][0:1, bass.ds(i * ring, ring)])
                    return registers, [bass.RuntimeValue.of_register_unchecked(reg, min_val=0, max_val=EXPERTS - 1) for reg in registers]

                def first_product(i, step):
                    registers, expert = experts_of(i, step)
                    for g in range(2):
                        pe.wait_ge(rows_kept, i * 2 + (g + 1))
                        for k in range(group):
                            mm = pe.matmul(ps[2 + g][:, 128 * k:128 * k + 128], rows_t[:, group * g + k, :], w1[:, bass.ds(expert[group * g + k] * 128, 128)], start=True, stop=True)
                        mm.then_inc(hidden_ready, 1)
                    for reg in registers:
                        pe.free_register(reg)

                def turn_hidden(i):
                    for g in range(2):
                        pe.wait_ge(hidden_kept, i * 2 + (g + 1))
                        for k in range(group):
                            mm = pe.transpose(ps[4 + g][:, 128 * k:128 * k + 128], hidden[:, group * g + k, :], w["ident"])
                        mm.then_inc(hidden_turned, 1)

                def second_product(i, step):
                    registers, expert = experts_of(i, step)
                    for g in range(2):
                        pe.wait_ge(hidden_t_kept, i * 2 + (g + 1))
                        pe.wait_ge(out_kept, i * 2 + (g + 1))
                        for k in range(group):
                            mm = pe.matmul(ps[6 + g][:, FEAT * k:FEAT * k + FEAT], hidden_t[:, group * g + k, :], w2[:, bass.ds(expert[group * g + k] * FEAT, FEAT)], start=True, stop=True)
                        mm.then_inc(out_ready, 1)
                    for reg in registers:
                        pe.free_register(reg)

                def round_(i, place, step, gathered_groups=2):
                    turn_rows(i, place, gathered_groups)
                    turn_hidden(i - 1)
                    first_product(i, f"{step}_first")
                    second_product(i - 1, f"{step}_second")

                pe.wait_ge(experts_in, 32)
                pe.wait_ge(ones_ready, 1)
                turn_rows(0, 0)
                first_product(0, "start_first")
                with pe.Fori(0, rounds // 2 - 1) as m:
                    round_(m * 2 + 1, 1, "odd")
                    round_(m * 2 + 2, 0, "even")
                round_(rounds - 1, 1, "last", (gathers - (rounds - 1) * ring) // group)
                turn_hidden(rounds - 1)
                second_product(rounds - 1, "end_second")

            @block.vector
            def _(dve):
                dve.memset(rows_t[FEAT:FEAT + 1], 1.0).then_inc(ones_ready, 1)

                def keep_rows(i):
                    for g in range(2):
                        dve.wait_ge(rows_turned, i * 2 + (g + 1))
                        dve.tensor_copy(rows_t[0:FEAT, group * g:group * g + group, :], ps[g][0:FEAT, :].rearrange("p (k n) -> p k n", k=group)).then_inc(rows_kept, 1)

                def keep_hidden(i):
                    for g in range(2):
                        dve.wait_ge(hidden_turned, i * 2 + (g + 1))
                        dve.tensor_copy(hidden_t[:, group * g:group * g + group, :], ps[4 + g][:].rearrange("p (k n) -> p k n", k=group)).then_inc(hidden_t_kept, 1)

                keep_rows(0)
                with dve.Fori(1, rounds) as i:
                    keep_rows(i)
                    keep_hidden(i - 1)
                keep_hidden(rounds - 1)

            @block.scalar
            def _(act):

                def relu(i):
                    for g in range(2):
                        act.wait_ge(hidden_ready, i * 2 + (g + 1))
                        act.activation(hidden[:, group * g:group * g + group, :], ps[2 + g][:].rearrange("p (k n) -> p k n", k=group), ACT.Relu).then_inc(hidden_kept, 1)

                def keep_out(i):
                    for g in range(2):
                        act.wait_ge(out_ready, i * 2 + (g + 1))
                        act.wait_ge(stored[g], i * 16 + 16)
                        act.activation(out[:, group * g:group * g + group, :], ps[6 + g][:, 0:group * FEAT].rearrange("p (k n) -> p k n", k=group), ACT.Copy).then_inc(out_kept, 1)

                act.sem_inc(out_kept, 2)
                relu(0)
                with act.Fori(1, rounds) as i:
                    relu(i)
                    keep_out(i - 1)
                keep_out(rounds - 1)

            @block.sync
            def _(sp):
                for g in range(2):
                    sp.sem_inc(stored[g], 16)
                with sp.Fori(0, rounds) as i:
                    for g in range(2):
                        sp.wait_ge(out_kept, i * 2 + (g + 3))
                        sp.dma_start(table[:, bass.ds(ring * i + group * g, group), :], out[:, group * g:group * g + group, :]).then_inc(stored[g], 16)
                for g in range(2):
                    sp.wait_ge(stored[g], 16 * (rounds) + 16)


def expert_sum(nc, h, x, w, ps, r):
    cols = 2 * TILES
    with Stage(nc, "sum") as s:
        rows_in = s.sb("rows_in", [TILE, cols, 2, FEAT])
        total = s.sb("total", [TILE, cols, FEAT])
        gathered = [s.pool_dma_sem(f"gathered{c}") for c in range(CHUNKS)]
        scaled, total_ready, out_ready, h_ready = s.sem("scaled"), s.sem("total_ready"), s.sem("out_ready"), s.sem("h_ready")
        ln = LayerNorm(s, h, x, w, ps, lambda eng, c: eng.wait_ge(h_ready, c + 1), group=5)
        with nc.Block() as block:

            @block.gpsimd
            def _(pool):
                for a in range(cols):
                    for k in range(2):
                        n = 2 * a + k
                        pool.indirect_dma_start(out=rows_in[:, a, k, :], out_offset=None, in_=r["table"],
                                                in_offset=bass.IndirectOffsetOnAxis(ap=r["slot"][:, n:n + 1].bitcast(U32), axis=0)).then_inc(gathered[a // 8], 16)
                ln.gpsimd(pool)

            @block.vector
            def _(dve):
                for c in range(CHUNKS):
                    mine = slice(8 * c, 8 * c + 8)
                    dve.wait_ge(gathered[c], 256)
                    for k in range(2):
                        dve.tensor_tensor(rows_in[:, mine, k], rows_in[:, mine, k], r["gates"][:, k, mine].unsqueeze(2).to_broadcast([TILE, 8, FEAT]), ALU.mult).then_inc(scaled, 1)
                    dve.wait_ge(scaled, 2 * c + 2)
                    dve.tensor_tensor(total[:, mine], rows_in[:, mine, 0], rows_in[:, mine, 1], ALU.add).then_inc(total_ready, 1)
                    dve.wait_ge(out_ready, c + 1)
                    dve.tensor_tensor(h[:, chunk(c)], h[:, chunk(c)], ps[c][:, :CHUNK], ALU.add).then_inc(h_ready, 1)
                    if c < CHUNKS - 1:
                        ln.centre(dve, c)
                dve.wait_ge(h_ready, CHUNKS)
                ln.vector(dve, CHUNKS - 1)

            @block.tensor
            def _(pe):
                for c in range(CHUNKS):
                    pe.matmul(ps[c][:, :CHUNK], w["moe_b2"], r["combine_t"][:, chunk(c)], start=True, stop=False, skip_group_check=True)
                for c in range(CHUNKS):
                    pe.wait_ge(total_ready, c + 1)
                    for k in range(4):
                        j = 4 * c + k
                        mm = pe.matmul(ps[c][:, tile(k)], total[:, 2 * j:2 * j + 2].rearrange("p a f -> p (a f)"), w["ident"][0:TILE, 0:TILE],
                                       start=False, stop=(k == 3), skip_group_check=True)
                    mm.then_inc(out_ready, 1)
                    if c < CHUNKS - 1:
                        ln.mean(pe, c)
                ln.tensor(pe, CHUNKS - 1)

            @block.scalar
            def _(act):
                ln.scalar(act)

            @block.sync
            def _(sp):
                ln.sync(sp)

def expert_ffn(nc, h, x, w, ps, d):
    cols = 2 * TILES
    with Stage(nc, "moe") as s:
        r = {
            "tokens": d["tokens"], "table": d["table"],
            "w1": s.sb("w1", [FEAT + 1, EXPERTS * 128]), "w2": s.sb("w2", [128, EXPERTS * FEAT]),
            "source": s.sb("source", [128, TABLE_TILES], U32), "expert": s.sb("expert", [1, TABLE_TILES], I32),
            "slot": s.sb("slot", [TILE, cols * 2], I32), "gates": s.sb("gates", [TILE, 2, cols]),
            "combine_t": s.sb("combine_t", [128, COLS]),
        }
        experts_in = s.sem("experts_in")
        expert_routing(nc, x, w, ps, r, d, experts_in)
        expert_tables(nc, w, ps, r, experts_in)
        expert_sum(nc, h, x, w, ps, r)


def retention(nc, h, x, w, ps):
    wide = POS + TILE
    with Stage(nc, "ret") as s:
        query = s.sb("query", [128, COLS])
        key = s.sb("key", [128, COLS])
        turned = s.sb("turned", [128, 2, COLS])
        value = s.sb("value", [TILE, TILES, 128])
        kept = s.sb("kept", [TILE, 4, wide])
        (q_ready, q_scaled, rotated, value_ready, value_kept, score_ready, score_kept, out_ready, h_ready) = (
            s.sem(n) for n in "q_ready q_scaled rotated value_ready value_kept score_ready score_kept out_ready h_ready".split())
        ln = LayerNorm(s, h, x, w, ps, lambda eng, c: eng.wait_ge(h_ready, c + 1), group=6)
        with nc.Block() as block:

            @block.tensor
            def _(pe):
                for i, n in enumerate("qk"):
                    for c in range(CHUNKS):
                        if i:
                            pe.wait_ge(q_scaled, 2 * c + 2)
                        pe.matmul(ps[c][:, :CHUNK], w["ret_" + n], x[:, chunk(c)], start=True, stop=True)
                        pe.matmul(ps[4 + c][:, :CHUNK], w["ret_" + n + "s"], x[:, chunk(c)], start=True, stop=True).then_inc(q_ready, 1)
                for b in range(4):
                    pe.wait_ge(q_scaled, 8 + 2 * b + 2)
                    for k in range(4):
                        mm = pe.matmul(ps[b][0:TILE, 128 * k:128 * k + 128], x[:, tile(4 * b + k)], w["ret_v"], start=True, stop=True)
                    mm.then_inc(value_ready, 1)
                pe.wait_ge(rotated, 8)
                pe.wait_ge(value_kept, 4)

                def scores(q):
                    p, a = q // 2, q % 2
                    if q >= 4:
                        pe.wait_ge(score_kept, q - 3)
                    half = slice(64 * a, 64 * a + 64)
                    at = POS * p
                    pe.matmul(ps[4 + q % 4][0:TILE, 0:POS], key[half, tile(2 * p)], query[half, at:at + POS], start=True, stop=True)
                    pe.matmul(ps[4 + q % 4][0:TILE, POS:wide], key[half, tile(2 * p + 1)], query[half, at + TILE:at + POS], start=True, stop=True).then_inc(score_ready, 1)

                def outputs(q):
                    p, a = q // 2, q % 2
                    pe.wait_ge(score_kept, q + 1)
                    dst = ps[p // 2][64 * a:64 * a + 64, POS * (p % 2):POS * (p % 2) + POS]
                    pe.matmul(dst, value[:, 2 * p, 64 * a:64 * a + 64], kept[:, q % 4, 0:POS], start=True, stop=False)
                    pe.matmul(dst[:, TILE:], value[:, 2 * p + 1, 64 * a:64 * a + 64], kept[:, q % 4, POS:wide], start=False, stop=True).then_inc(out_ready, 1)

                for q in range(SEQS):
                    scores(q)
                    if q >= 2:
                        outputs(q - 2)
                outputs(SEQS - 2)
                outputs(SEQS - 1)
                ln.tensor(pe)

            @block.scalar
            def _(act):
                for b in range(4):
                    act.wait_ge(value_ready, b + 1)
                    act.activation(value[:, 4 * b:4 * b + 4], ps[b][0:TILE, :].rearrange("p (k f) -> p k f", k=4), ACT.Copy).then_inc(value_kept, 1)
                ln.scalar(act)

            @block.vector
            def _(dve):
                for i, dst in enumerate((query, key)):
                    for c in range(CHUNKS):
                        dve.wait_ge(q_ready, 4 * i + c + 1)
                        if i:
                            dve.wait_ge(rotated, c + 1)
                        for k, src in enumerate((ps[c], ps[4 + c])):
                            table = w["ret_table"][:, POS * (2 * i + k):POS * (2 * i + k) + POS].unsqueeze(1).to_broadcast([128, 2, POS])
                            out = (dst if k == 0 else turned[:, 0])[:, chunk(c)].rearrange("p (b n) -> p b n", b=2)
                            dve.tensor_tensor(out, src[:, :CHUNK].rearrange("p (b n) -> p b n", b=2), table, ALU.mult).then_inc(q_scaled, 1)
                for q in range(SEQS):
                    dve.wait_ge(score_ready, q + 1)
                    if q >= 4:
                        dve.wait_ge(out_ready, q - 3)
                    dve.tensor_tensor(kept[:, q % 4], ps[4 + q % 4][0:TILE, 0:wide], w["ret_decay"][0:TILE, :], ALU.mult).then_inc(score_kept, 1)
                for c in range(CHUNKS):
                    dve.wait_ge(out_ready, 4 * c + 4)
                    dve.tensor_tensor(h[:, chunk(c)], h[:, chunk(c)], ps[c][:, :CHUNK], ALU.add).then_inc(h_ready, 1)
                dve.wait_ge(h_ready, CHUNKS)
                ln.vector(dve)

            @block.gpsimd
            def _(pool):
                for i, dst in enumerate((query, key)):
                    for c in range(CHUNKS):
                        pool.wait_ge(q_scaled, 2 * (4 * i + c) + 2)
                        pool.tensor_tensor(dst[:, chunk(c)], dst[:, chunk(c)], turned[:, 0, chunk(c)], ALU.add).then_inc(rotated, 1)
                ln.gpsimd(pool)

            @block.sync
            def _(sp):
                ln.sync(sp)

def soft_mixture(nc, h, x, w, ps):
    experts = 8
    pairs = experts // 2
    with Stage(nc, "mixture") as s:
        feat = s.sb("feat", [128, POS])
        gate = s.sb("gate", [TILE, 2, experts])
        gate_tmp = s.sb("gate_tmp", [TILE, 2, experts])
        top = s.sb("top", [TILE, 2])
        total = s.sb("total", [TILE, 2])
        inverse = s.sb("inverse", [TILE, 2])
        gate_wide = s.sb("gate_wide", [TILE, 2, experts, 64])
        gate_f = s.sb("gate_f", [128, pairs, POS])
        gate_t = s.sb("gate_t", [experts, POS])
        bias = s.sb("bias", [128, POS])
        root = s.sb("root", [128, 2, pairs])
        scale = s.sb("scale", [128, 2, pairs])
        shift = s.sb("shift", [128, 2, pairs])
        hidden = s.sb("hidden", [128, 2, 4, CHUNK])
        (feat_ready, logits_ready, gate_steps, exp_ready, gate_spread, gate_kept, gate_turned, gate_t_kept, bias_ready, bias_kept,
         root_ready, scale_steps, up_ready, up_kept, mid_ready, mid_kept, gated, out_ready, h_ready, biased) = (s.sem(n) for n in (
             "feat_ready logits_ready gate_steps exp_ready gate_spread gate_kept gate_turned gate_t_kept bias_ready bias_kept "
             "root_ready scale_steps up_ready up_kept mid_ready mid_kept gated out_ready h_ready biased").split())
        steps = experts * CHUNKS

        def norm(name, layer):
            at = pairs * (2 * "g b m v e".split().index(name) + layer)
            return w["bn"][:, at:at + pairs]

        ln = LayerNorm(s, h, x, w, ps, lambda eng, c: eng.wait_ge(biased, c + 1))
        again = LayerNorm(s, x, x, w, ps, lambda eng, c: eng.wait_ge(ln.x_ready, c + 1), group=7, name="ln_again")
        with nc.Block() as block:

            @block.tensor
            def _(pe):
                pe.wait_ge(feat_ready, 1)
                for t in range(2):
                    mm = pe.matmul(ps[0][0:TILE, 8 * t:8 * t + 8], feat[:, tile(t)], w["soft_r"], start=True, stop=True)
                mm.then_inc(logits_ready, 1)
                pe.wait_ge(gate_steps, 7)
                for b in range(2):
                    for k in range(4):
                        q = 2 * b + k // 2
                        mm = pe.transpose(ps[4 + b][:, tile(k)], gate_wide[:, k % 2, 2 * q:2 * q + 2].rearrange("p e f -> p (e f)"), w["ident"][0:TILE, 0:TILE])
                    mm.then_inc(gate_spread, 1)
                for t in range(2):
                    mm = pe.transpose(ps[1][0:experts, tile(t)], gate[:, t], w["ident"][0:TILE, 0:TILE])
                mm.then_inc(gate_turned, 1)
                pe.wait_ge(gate_t_kept, 1)
                pe.matmul(ps[2][:, 0:POS], w["soft_bo"][0:experts, :], gate_t[:], start=True, stop=True).then_inc(bias_ready, 1)
                pe.wait_ge(gate_kept, 2)
                pe.wait_ge(bias_kept, 1)

                def first(n):
                    if n >= 2:
                        pe.wait_ge(up_kept, n - 1)
                    pe.matmul(ps[4 + n % 2][:, :CHUNK], w["soft_1"][:, 256 * (n // 8) + 128 * (n % 2):256 * (n // 8) + 128 * (n % 2) + 128], x[:, chunk(n // 2 % 4)], start=True, stop=True).then_inc(up_ready, 1)

                def second(n):
                    pe.wait_ge(up_kept, n + 1)
                    if n >= 2:
                        pe.wait_ge(mid_kept, n - 1)
                    pe.matmul(ps[6 + n % 2][:, :CHUNK], w["soft_2"][:, 128 * (n // 8):128 * (n // 8) + 128], hidden[:, 0, n % 4], start=True, stop=True).then_inc(mid_ready, 1)

                def third(n):
                    a, q = n % 2, n // 8
                    pe.wait_ge(gated, n + 1)
                    pe.matmul(ps[n // 2 % 4][64 * a:64 * a + 64, :CHUNK], w["soft_3"][:, 64 * q:64 * q + 64], hidden[:, 1, n % 4],
                              start=(q == 0), stop=(q == pairs - 1), tile_position=(0, 64 * a)).then_inc(out_ready, 1)

                for n in range(steps + 3):
                    if n < steps:
                        first(n)
                    if 1 <= n <= steps:
                        second(n - 1)
                    if n >= 4 and n % 2 == 0:
                        third(n - 4)
                        third(n - 3)
                ln.tensor(pe)
                again.tensor(pe)

            @block.scalar
            def _(act):
                for layer in range(2):
                    act.activation(root[:, layer], norm("v", layer), ACT.Sqrt, bias=w["bn_eps"]).then_inc(root_ready, 1)
                act.wait_ge(gate_steps, 3)
                act.activation(gate_tmp[:], gate_tmp[:], ACT.Exp).then_inc(exp_ready, 1)
                for b in range(2):
                    act.wait_ge(gate_spread, b + 1)
                    act.activation(gate_f[:, 2 * b:2 * b + 2].rearrange("p e n -> p (e n)"), ps[4 + b][:, :CHUNK], ACT.Copy).then_inc(gate_kept, 1)
                act.wait_ge(gate_turned, 1)
                act.activation(gate_t[:], ps[1][0:experts, 0:POS], ACT.Copy).then_inc(gate_t_kept, 1)
                act.wait_ge(bias_ready, 1)
                act.activation(bias[:], ps[2][:, 0:POS], ACT.Copy).then_inc(bias_kept, 1)
                act.wait_ge(scale_steps, 8)

                def first(n):
                    q = n // 8
                    act.wait_ge(up_ready, n + 1)
                    if n >= 4:
                        act.wait_ge(mid_ready, n - 3)
                    act.activation(hidden[:, 0, n % 4], ps[4 + n % 2][:, :CHUNK], ACT.Relu, bias=shift[:, 0, q:q + 1], scale=scale[:, 0, q:q + 1]).then_inc(up_kept, 1)

                def second(n):
                    q = n // 8
                    act.wait_ge(mid_ready, n + 1)
                    if n >= 4:
                        act.wait_ge(out_ready, n - 3)
                    act.activation(hidden[:, 1, n % 4], ps[6 + n % 2][:, :CHUNK], ACT.Relu, bias=shift[:, 1, q:q + 1], scale=scale[:, 1, q:q + 1]).then_inc(mid_kept, 1)

                for n in range(steps + 1):
                    if n < steps:
                        first(n)
                    if n >= 1:
                        second(n - 1)
                ln.scalar(act)
                again.scalar(act)

            @block.vector
            def _(dve):
                dve.tensor_reduce(feat[:], x[:].rearrange("q (p n) -> q n p", n=POS), AX.X, ALU.add).then_inc(feat_ready, 1)
                dve.wait_ge(root_ready, 2)
                dve.reciprocal(scale[:], root[:]).then_inc(scale_steps, 1)
                dve.wait_ge(scale_steps, 1)
                for layer in range(2):
                    dve.tensor_tensor(root[:, layer], scale[:, layer], norm("g", layer), ALU.mult).then_inc(scale_steps, 1)
                    dve.tensor_tensor(shift[:, layer], norm("b", layer), norm("m", layer), ALU.subtract).then_inc(scale_steps, 1)
                dve.wait_ge(scale_steps, 5)
                dve.tensor_tensor(shift[:], shift[:], root[:], ALU.mult).then_inc(scale_steps, 1)
                dve.tensor_copy(scale[:], root[:]).then_inc(scale_steps, 1)
                dve.wait_ge(scale_steps, 7)
                dve.tensor_tensor(shift[:], shift[:], w["bn"][:, 8 * pairs:10 * pairs].rearrange("p (l q) -> p l q", l=2), ALU.add).then_inc(scale_steps, 1)
                dve.wait_ge(logits_ready, 1)
                dve.scalar_tensor_tensor(gate[:], ps[0][0:TILE, 0:16].rearrange("p (t e) -> p t e", t=2), 1.0 / SEQS,
                                         w["soft_br"][0:TILE, :].unsqueeze(1).to_broadcast([TILE, 2, experts]), ALU.mult, ALU.add).then_inc(gate_steps, 1)
                dve.wait_ge(gate_steps, 1)
                dve.tensor_reduce(top[:], gate[:], AX.X, ALU.max).then_inc(gate_steps, 1)
                dve.wait_ge(gate_steps, 2)
                dve.tensor_tensor(gate_tmp[:], gate[:], top[:].unsqueeze(2).to_broadcast([TILE, 2, experts]), ALU.subtract).then_inc(gate_steps, 1)
                dve.wait_ge(exp_ready, 1)
                dve.tensor_reduce(total[:], gate_tmp[:], AX.X, ALU.add).then_inc(gate_steps, 1)
                dve.wait_ge(gate_steps, 4)
                dve.reciprocal(inverse[:], total[:]).then_inc(gate_steps, 1)
                dve.wait_ge(gate_steps, 5)
                dve.tensor_tensor(gate[:], gate_tmp[:], inverse[:].unsqueeze(2).to_broadcast([TILE, 2, experts]), ALU.mult).then_inc(gate_steps, 1)
                dve.wait_ge(gate_steps, 6)
                dve.tensor_copy(gate_wide[:], gate[:].unsqueeze(3).to_broadcast([TILE, 2, experts, 64])).then_inc(gate_steps, 1)
                dve.wait_ge(gate_kept, 2)
                for n in range(steps):
                    dve.wait_ge(mid_kept, n + 1)
                    hid = hidden[:, 1, n % 4].rearrange("p (b n) -> p b n", b=2)
                    dve.tensor_tensor(hid, hid, gate_f[:, n // 8].unsqueeze(1).to_broadcast([128, 2, POS]), ALU.mult).then_inc(gated, 1)
                dve.wait_ge(bias_kept, 1)
                for c in range(CHUNKS):
                    dve.wait_ge(out_ready, steps - 6 + 2 * c)
                    dve.tensor_tensor(h[:, chunk(c)], h[:, chunk(c)], ps[c][:, :CHUNK], ALU.add).then_inc(h_ready, 1)
                dve.wait_ge(h_ready, CHUNKS)
                for c in range(CHUNKS):
                    two = h[:, chunk(c)].rearrange("p (b n) -> p b n", n=POS)
                    dve.tensor_tensor(two, two, bias[:].unsqueeze(1).to_broadcast([128, 2, POS]), ALU.add).then_inc(biased, 1)
                ln.vector(dve)
                again.vector(dve)

            @block.gpsimd
            def _(pool):
                ln.gpsimd(pool)
                again.gpsimd(pool)

            @block.sync
            def _(sp):
                ln.sync(sp)
                again.sync(sp)

def relative_attention(nc, h, x, w, ps):
    heads, hd, reach, near = 4, 16, 30, TILE + 29
    first_near = [0, POS - near]
    with Stage(nc, "rel") as s:
        mixed = s.sb("mixed", [128, 2, COLS])
        xg, query_v = mixed[:, 0], mixed[:, 1]
        query_u = s.sb("query_u", [128, heads, COLS])
        key = s.sb("key", [128, 2, COLS])
        value = s.sb("value", [TILE, TILES, 2 * heads, 2 * hd])
        turn_a = s.sb("turn_a", [128, heads, COLS])
        turn_b = s.sb("turn_b", [128, 2, CHUNK])
        bias_u = s.sb("bias_u", [128, heads])
        bias_v = s.sb("bias_v", [128, 1])
        edge_w = s.sb("edge_w", [128, 3])
        edge_wide = s.sb("edge_wide", [128, 3, 8])
        edge = s.sb("edge", [TILE, TILES, 3, 8])
        shift = s.sb("shift", [TILE, TILES, 8])
        right = s.sb("right", [TILE, TILES, 8])
        near_b = [s.sb(f"near{t}", [TILE, 2, heads, POS]) for t in range(2)]
        near_raw = s.sb("near_raw", [TILE, 2, heads, near])
        scores = s.sb("scores", [TILE, 3, heads, POS])
        top = s.sb("top", [TILE, 3, heads])
        total = s.sb("total", [TILE, 3, heads])
        inverse = s.sb("inverse", [TILE, 3, heads])
        probs_t = s.sb("probs_t", [TILE, 2, 2, 4 * TILE])
        (x_ready, biases, edge_w_ready, edge_steps, q_ready, q_kept, k_ready, k_kept, v_ready, v_kept, edge_ready,
         edge_kept, edge_done, turn_ready, turn_scaled, turned, zeroed, value_zeroed, keys_zeroed) = (s.sem(n) for n in (
             "x_ready biases edge_w_ready edge_steps q_ready q_kept k_ready k_kept v_ready v_kept edge_ready "
             "edge_kept edge_done turn_ready turn_scaled turned zeroed value_zeroed keys_zeroed").split())
        (dot_ready, near_ready, near_out, near_kept, far_added, score_kept, top_ready, exp_ready, prob_ready, prob_turned, prob_kept,
         mixed_ready, inverse_ready, mixed_kept, out_ready, h_ready) = (s.sem(n) for n in (
             "dot_ready near_ready near_out near_kept far_added score_kept top_ready exp_ready prob_ready prob_turned prob_kept "
             "mixed_ready inverse_ready mixed_kept out_ready h_ready").split())
        with nc.Block() as block:

            @block.tensor
            def _(pe):
                pe.matmul(ps[7][:, 0:2], w["rel_pos_t"], w["rel_ends"], start=True, stop=True).then_inc(edge_w_ready, 1)
                pe.wait_ge(x_ready, CHUNKS)
                for c in range(CHUNKS):
                    pe.matmul(ps[c][:, :CHUNK], w["rel_q"], xg[:, chunk(c)], start=True, stop=True).then_inc(q_ready, 1)
                for c in range(CHUNKS):
                    if c == 3:
                        pe.wait_ge(edge_steps, 1)
                    pe.matmul(ps[4 + c][:, :CHUNK], w["rel_k"], xg[:, chunk(c)], start=True, stop=True).then_inc(k_ready, 1)
                for b in range(4):
                    pe.wait_ge(k_kept, 2 * b + 2)
                    for k in range(4):
                        mm = pe.matmul(ps[4 + b][0:TILE, 128 * k:128 * k + 128], xg[:, tile(4 * b + k)], w["rel_v"], start=True, stop=True)
                    mm.then_inc(v_ready, 1)
                pe.wait_ge(q_kept, 5 * CHUNKS)
                pe.wait_ge(v_kept, 4)
                for n in range(heads * CHUNKS):
                    hh, c = n // CHUNKS, n % CHUNKS
                    if n >= 3:
                        pe.wait_ge(turn_scaled, 2 * (n - 3) + 2)
                    pe.matmul(ps[1 + 2 * (n % 3)][:, :CHUNK], w["rel_pos"][:, 128 * hh:128 * hh + 128], query_v[:, chunk(c)], start=True, stop=True)
                    pe.matmul(ps[2 + 2 * (n % 3)][:, :CHUNK], w["rel_pos_s"][:, 128 * hh:128 * hh + 128], query_v[:, chunk(c)], start=True, stop=True).then_inc(turn_ready, 1)
                pe.wait_ge(edge_steps, 5)
                for j in range(TILES):
                    mm = pe.matmul(ps[0][0:TILE, 24 * j:24 * j + 24], query_v[:, tile(j)], edge_wide[:].rearrange("p i e -> p (i e)"), start=True, stop=True)
                mm.then_inc(edge_ready, 1)

            @block.scalar
            def _(act):
                for c in range(CHUNKS):
                    act.activation(xg[:, chunk(c)], x[:, chunk(c)], ACT.Identity, scale=w["rel_gamma"], bias=w["rel_beta"]).then_inc(x_ready, 1)
                act.wait_ge(biases, 3)
                for c in range(CHUNKS):
                    act.wait_ge(q_ready, c + 1)
                    for hh in range(heads):
                        act.activation(query_u[:, hh, chunk(c)], ps[c][:, :CHUNK], ACT.Identity, scale=w["rel_head"][:, hh:hh + 1], bias=bias_u[:, hh:hh + 1]).then_inc(q_kept, 1)
                    act.activation(query_v[:, chunk(c)], ps[c][:, :CHUNK], ACT.Identity, scale=float(hd) ** -0.5, bias=bias_v[:]).then_inc(q_kept, 1)

            @block.vector
            def _(dve):
                dve.tensor_scalar(bias_u[:], w["rel_head"], w["rel_qu"][:, 0:1], None, ALU.mult).then_inc(biases, 1)
                dve.wait_ge(biases, 1)
                dve.scalar_tensor_tensor(bias_u[:], w["rel_head"], w["rel_qu"][:, 1:2], bias_u[:], ALU.mult, ALU.add).then_inc(biases, 1)
                dve.tensor_scalar(bias_v[:], w["rel_qu"][:, 0:1], w["rel_qu"][:, 2:3], float(hd) ** -0.5, ALU.add, ALU.mult).then_inc(biases, 1)
                dve.wait_ge(edge_w_ready, 1)
                dve.tensor_tensor(edge_w[:, 0:2], ps[7][:, 0:2], w["rel_posb"].to_broadcast([128, 2]), ALU.add).then_inc(edge_steps, 1)
                dve.tensor_copy(edge_w[:, 2:3], w["rel_posb"]).then_inc(edge_steps, 1)
                dve.wait_ge(edge_steps, 2)
                for i in range(3):
                    dve.tensor_scalar(edge_wide[:, i], w["rel_head8"], edge_w[:, i:i + 1], None, ALU.mult).then_inc(edge_steps, 1)
                for c in range(CHUNKS):
                    dve.wait_ge(k_ready, c + 1)
                    if c == 0:
                        dve.wait_ge(keys_zeroed, 1)
                    for a in range(2):
                        half = slice(64 * a, 64 * a + 64)
                        dve.tensor_scalar(key[half, a, chunk(c)], ps[4 + c][half, :CHUNK], w["rel_kb"][half, :], None, ALU.add).then_inc(k_kept, 1)
                for b in range(4):
                    dve.wait_ge(v_ready, b + 1)
                    if b == 0:
                        dve.wait_ge(value_zeroed, 1)
                    dve.tensor_tensor(value[:, 4 * b:4 * b + 4, :, 0:hd], ps[4 + b][0:TILE, :].rearrange("p (k g e) -> p k g e", k=4, e=hd),
                                      w["rel_vb"][0:TILE, :].rearrange("p (g e) -> p g e", e=hd).unsqueeze(1).to_broadcast([TILE, 4, 2 * heads, hd]), ALU.add).then_inc(v_kept, 1)
                for n in range(heads * CHUNKS):
                    hh, c = n // CHUNKS, n % CHUNKS
                    dve.wait_ge(turn_ready, n + 1)
                    if n >= 2:
                        dve.wait_ge(turned, n - 1)
                    for k in range(2):
                        table = w["rel_t"][:, POS * k:POS * k + POS].unsqueeze(1).to_broadcast([128, 2, POS])
                        out = turn_a[:, hh, chunk(c)] if k == 0 else turn_b[:, n % 2]
                        dve.tensor_tensor(out.rearrange("p (b n) -> p b n", b=2), ps[1 + k + 2 * (n % 3)][:, :CHUNK].rearrange("p (b n) -> p b n", b=2),
                                          table, ALU.mult).then_inc(turn_scaled, 1)
                dve.wait_ge(edge_ready, 1)
                dve.tensor_copy(edge[:].rearrange("p j i e -> p (j i e)"), ps[0][0:TILE, 0:24 * TILES]).then_inc(edge_kept, 1)
                dve.wait_ge(edge_kept, 1)
                dve.tensor_tensor(right[:], edge[:, :, 1], edge[:, :, 0], ALU.subtract).then_inc(edge_done, 1)
                dve.tensor_tensor(shift[:], edge[:, :, 2], edge[:, :, 0], ALU.subtract).then_inc(edge_done, 1)
                dve.wait_ge(edge_done, 2)

            @block.gpsimd
            def _(pool):
                pool.memset(key[:], 0.0).then_inc(keys_zeroed, 1)
                pool.memset(value[:], 0.0).then_inc(value_zeroed, 1)
                for t in range(2):
                    pool.memset(near_b[t][:], 0.0).then_inc(zeroed, 1)
                for n in range(heads * CHUNKS):
                    hh, c = n // CHUNKS, n % CHUNKS
                    pool.wait_ge(turn_scaled, 2 * n + 2)
                    pool.tensor_tensor(turn_a[:, hh, chunk(c)], turn_a[:, hh, chunk(c)], turn_b[:, n % 2], ALU.add).then_inc(turned, 1)
                pool.wait_ge(zeroed, 2)

        units = 2 * SEQS
        unit = [(u // 4, u % 2, (u // 2) % 2) for u in range(units)]
        ln = LayerNorm(s, h, x, w, ps, lambda eng, c: eng.wait_ge(h_ready, c + 1), group=8, squares=mixed[:, 0])
        with nc.Block() as block:

            @block.tensor
            def _(pe):

                def dots(u):
                    p, a, t = unit[u]
                    for hh in range(heads):
                        if u and hh % 2 == 0:
                            pe.wait_ge(near_out, heads * (u - 1) + hh + 2)
                        pe.matmul(ps[2 + hh // 2][0:TILE, near * (hh % 2):near * (hh % 2) + near], turn_a[:, hh, tile(2 * p + t)],
                                  w["rel_s"][:, POS * a + first_near[t]:POS * a + first_near[t] + near], start=True, stop=True).then_inc(near_ready, 1)
                    for hh in range(heads):
                        if u and hh % 2 == 0:
                            pe.wait_ge(far_added, heads * (u - 1) + hh + 2)
                        pe.matmul(ps[hh // 2][0:TILE, POS * (hh % 2):POS * (hh % 2) + POS], query_u[:, hh, tile(2 * p + t)],
                                  key[:, a, POS * p:POS * p + POS], start=True, stop=True).then_inc(dot_ready, 1)

                def turn_probs(u):
                    pe.wait_ge(prob_ready, u + 1)
                    for b in range(2):
                        if u:
                            pe.wait_ge(prob_kept, 2 * (u - 1) + b + 1)
                        for k in range(4):
                            mm = pe.transpose(ps[4 + b][0:TILE, tile(k)], scores[:, u % 3, 2 * b + k // 2, tile(k % 2)], w["ident"][0:TILE, 0:TILE])
                        mm.then_inc(prob_turned, 1)

                def mix(u):
                    p, a, t = unit[u]
                    if u >= 2:
                        pe.wait_ge(mixed_kept, u - 1)
                    pe.wait_ge(prob_kept, 2 * u + 2)
                    for k in range(2):
                        for hh in range(heads):
                            mm = pe.matmul(ps[6 + u % 2][32 * hh:32 * hh + 32, 0:TILE], value[:, 2 * p + k, 4 * a + hh], probs_t[:, u % 2, hh // 2, tile(2 * (hh % 2) + k)],
                                           start=(k == 0), stop=(k == 1), tile_position=(0, 32 * hh))
                    mm.then_inc(mixed_ready, 1)

                for n in range(units + 3):
                    if n < units:
                        dots(n)
                    if 2 <= n < units + 2:
                        turn_probs(n - 2)
                    if n >= 3:
                        mix(n - 3)
                pe.wait_ge(mixed_kept, units)
                for c in range(CHUNKS):
                    for a in range(2):
                        mm = pe.matmul(ps[c][64 * a:64 * a + 64, :CHUNK], w["rel_o"], mixed[:, a, chunk(c)], start=True, stop=True, tile_position=(0, 64 * a))
                    mm.then_inc(out_ready, 1)
                ln.tensor(pe)

            @block.scalar
            def _(act):

                def exps(u):
                    act.wait_ge(top_ready, u + 1)
                    if u >= 3:
                        act.wait_ge(inverse_ready, u - 2)
                    for hh in range(heads):
                        row = scores[:, u % 3, hh]
                        act.activation(row, row, ACT.Exp, bias=top[:, u % 3, hh:hh + 1], accum_out=total[:, u % 3, hh:hh + 1]).then_inc(exp_ready, 1)

                def keep_probs(u):
                    for b in range(2):
                        act.wait_ge(prob_turned, 2 * u + b + 1)
                        if u >= 2 and b == 0:
                            act.wait_ge(mixed_ready, u - 1)
                        act.activation(probs_t[:, u % 2, b], ps[4 + b][0:TILE, :CHUNK], ACT.Copy).then_inc(prob_kept, 1)

                def keep_mixed(u):
                    p, a, t = unit[u]
                    act.wait_ge(mixed_ready, u + 1)
                    act.activation(mixed[:, a, tile(2 * p + t)], ps[6 + u % 2][:, 0:TILE], ACT.Copy).then_inc(mixed_kept, 1)

                def keep_near(u):
                    p, a, t = unit[u]
                    if u >= 2:
                        act.wait_ge(near_kept, u - 1)
                    for hh in range(heads):
                        if hh % 2 == 0:
                            act.wait_ge(near_ready, heads * u + hh + 2)
                        act.activation(near_raw[:, u % 2, hh], ps[2 + hh // 2][0:TILE, near * (hh % 2):near * (hh % 2) + near], ACT.Identity,
                                       bias=shift[:, 2 * p + t, 4 * a + hh:4 * a + hh + 1]).then_inc(near_out, 1)

                keep_near(0)
                for n in range(units + 4):
                    if 2 <= n < units + 2:
                        keep_probs(n - 2)
                    if n >= 4:
                        keep_mixed(n - 4)
                    if n + 1 < units:
                        keep_near(n + 1)
                    if n < units:
                        exps(n)
                ln.scalar(act)

            @block.vector
            def _(dve):

                def keep_scores(u):
                    p, a, t = unit[u]
                    j = 2 * p + t
                    if u >= 3:
                        dve.wait_ge(prob_turned, 2 * (u - 2))
                    for hh in range(heads):
                        if hh % 2 == 0:
                            dve.wait_ge(dot_ready, heads * u + hh + 2)
                        dve.scalar_tensor_tensor(scores[:, u % 3, hh], w["rel_right"][0:TILE, POS * t:POS * t + POS], right[:, j, 4 * a + hh:4 * a + hh + 1],
                                                 ps[hh // 2][0:TILE, POS * (hh % 2):POS * (hh % 2) + POS], ALU.mult, ALU.add).then_inc(far_added, 1)

                def finish_scores(u):
                    t = unit[u][2]
                    dve.wait_ge(near_kept, u + 1)
                    dve.wait_ge(far_added, heads * (u + 1))
                    dve.tensor_tensor(scores[:, u % 3], scores[:, u % 3], near_b[t][:, u % 2], ALU.add).then_inc(score_kept, 1)
                    dve.wait_ge(score_kept, u + 1)
                    if u >= 3:
                        dve.wait_ge(exp_ready, heads * (u - 2))
                    dve.tensor_reduce(top[:, u % 3], scores[:, u % 3], AX.X, ALU.max, negate=True).then_inc(top_ready, 1)

                def invert(u):
                    dve.wait_ge(exp_ready, heads * (u + 1))
                    if u >= 3:
                        dve.wait_ge(prob_ready, u - 2)
                    dve.reciprocal(inverse[:, u % 3], total[:, u % 3]).then_inc(inverse_ready, 1)

                for n in range(units + 1):
                    if n < units:
                        keep_scores(n)
                    if n >= 1:
                        invert(n - 1)
                    if n < units:
                        finish_scores(n)
                for c in range(CHUNKS):
                    dve.wait_ge(out_ready, c + 1)
                    dve.scalar_tensor_tensor(h[:, chunk(c)], ps[c][:, :CHUNK], w["rel_ob"], h[:, chunk(c)], ALU.add, ALU.add).then_inc(h_ready, 1)
                dve.wait_ge(h_ready, CHUNKS)
                ln.vector(dve)

            @block.gpsimd
            def _(pool):

                def mask_near(u):
                    t = unit[u][2]
                    at = first_near[t]
                    pool.wait_ge(near_out, heads * (u + 1))
                    if u >= 4:
                        pool.wait_ge(score_kept, u - 3)
                    pool.tensor_tensor(near_b[t][:, u % 2, :, at:at + near], near_raw[:, u % 2],
                                       w["rel_near"][0:TILE, near * t:near * t + near].unsqueeze(1).to_broadcast([TILE, heads, near]), ALU.mult).then_inc(near_kept, 1)

                def scale_probs(u):
                    pool.wait_ge(inverse_ready, u + 1)
                    pool.tensor_tensor(scores[:, u % 3], scores[:, u % 3], inverse[:, u % 3].unsqueeze(2).to_broadcast([TILE, heads, POS]), ALU.mult).then_inc(prob_ready, 1)

                for n in range(units + 1):
                    if n < units:
                        mask_near(n)
                    if n >= 1:
                        scale_probs(n - 1)
                ln.gpsimd(pool)

            @block.sync
            def _(sp):
                ln.sync(sp)

def best_expert_ffn(nc, h, x, w, ps, out_dram):
    experts, blocks = 8, 2
    cols = 2 * TILES
    with Stage(nc, "top1") as s:
        hidden = s.sb("hidden", [128, blocks, 2, COLS])
        logits = s.sb("logits", [128, CHUNK])
        prob = s.sb("prob", [TILE, cols, experts])
        part = s.sb("part", [TILE, cols, experts])
        best = s.sb("best", [TILE, cols])
        total = s.sb("total", [TILE, cols])
        inverse = s.sb("inverse", [TILE, cols])
        gate_t = s.sb("gate_t", [2 * experts, TILES, TILE])
        scaled = s.sb("scaled", [TILE, 4, experts, FEAT])
        summed = s.sb("summed", [TILE, 2, FEAT])
        final = s.sb("final", [TILE, cols, FEAT])
        (up_ready, up_kept, logits_ready, logits_kept, logits_turned, bias_added, steps, exp_ready, gate_turned, gate_kept, y_ready, y_scaled, rest_ready, y_summed,
         final_ready, stored) = (s.sem(n) for n in (
             "up_ready up_kept logits_ready logits_kept logits_turned bias_added steps exp_ready gate_turned gate_kept y_ready y_scaled rest_ready y_summed final_ready stored").split())
        with nc.Block() as block:

            @block.tensor
            def _(pe):
                for n in range(16):
                    c, m, a = n // 4, (n // 2) % 2, n % 2
                    if n >= 8:
                        pe.wait_ge(up_kept, n - 7)
                    pe.matmul(ps[n % 8][:, :CHUNK], w["top_1"][:, 256 * a + 128 * m:256 * a + 128 * m + 128], x[:, chunk(c)], start=True, stop=True).then_inc(up_ready, 1)
                pe.wait_ge(up_kept, 16)
                for n in range(4):
                    m, a = n // 2, n % 2
                    for c in range(CHUNKS):
                        pe.matmul(ps[0][32 * c:32 * c + 32, :CHUNK], w["top_g"][:, 32 * n:32 * n + 32], hidden[:, m, a, chunk(c)],
                                  start=(n == 0), stop=(n == 3), tile_position=(0, 32 * c)).then_inc(logits_ready, 1)
                pe.wait_ge(logits_kept, 1)
                for k in range(4):
                    mm = pe.transpose(ps[1][0:TILE, 128 * k:128 * k + 128], logits[:, tile(k)], w["ident"])
                mm.then_inc(logits_turned, 1)

                def experts_of(n):
                    if n >= 4:
                        pe.wait_ge(y_scaled, n - 3)
                    for m in range(blocks):
                        mm = pe.matmul(ps[4 + n % 4][0:TILE, :], hidden[:, m, n % 2, tile(n // 2)], w["top_d"][:, 512 * m:512 * m + 512], start=(m == 0), stop=(m == 1))
                    mm.then_inc(y_ready, 1)

                for n in range(4):
                    experts_of(n)
                pe.wait_ge(steps, 10)
                for b in range(4):
                    for k in range(4):
                        j = 4 * b + k
                        mm = pe.transpose(ps[b][0:2 * experts, tile(k)], prob[:, 2 * j:2 * j + 2].rearrange("p a e -> p (a e)"), w["ident"][0:TILE, 0:TILE])
                    mm.then_inc(gate_turned, 1)
                pe.wait_ge(gate_kept, 4)
                for j in range(TILES):
                    if j >= 4:
                        pe.wait_ge(final_ready, 2 * (j - 4) + 2)
                    pe.matmul(ps[j % 4][0:TILE, 0:2 * FEAT], gate_t[:, j], w["top_bd"], start=True, stop=False)
                    pe.matmul(ps[j % 4][0:TILE, 0:2 * FEAT], h[:, tile(j)], w["ident"], start=False, stop=True).then_inc(rest_ready, 1)
                    for n in (2 * j + 4, 2 * j + 5):
                        if n < cols:
                            experts_of(n)

            @block.scalar
            def _(act):
                for n in range(16):
                    c, m, a = n // 4, (n // 2) % 2, n % 2
                    act.wait_ge(up_ready, n + 1)
                    act.activation(hidden[:, m, a, chunk(c)], ps[n % 8][:, :CHUNK], ACT.Gelu, bias=w["top_b1"][:, m:m + 1]).then_inc(up_kept, 1)
                act.wait_ge(logits_ready, 16)
                act.activation(logits[:], ps[0][:, :CHUNK], ACT.Copy).then_inc(logits_kept, 1)
                act.wait_ge(steps, 3)
                act.activation(prob[:], prob[:], ACT.Exp).then_inc(exp_ready, 1)
                for b in range(4):
                    act.wait_ge(gate_turned, b + 1)
                    act.activation(gate_t[:, 4 * b:4 * b + 4], ps[b][0:2 * experts, :CHUNK].rearrange("p (k n) -> p k n", k=4), ACT.Copy).then_inc(gate_kept, 1)

            @block.vector
            def _(dve):
                wide = [TILE, cols, experts]
                dve.wait_ge(logits_turned, 1)
                for k in range(4):
                    dve.tensor_tensor(prob[:].rearrange("p (c k a) e -> p k c (a e)", c=CHUNKS, k=4)[:, k], ps[1][0:TILE, 128 * k:128 * k + 128].rearrange("p (c r) -> p c r", c=CHUNKS)[:, :, 0:16],
                                      w["top_bg"][0:TILE, :].unsqueeze(1).to_broadcast([TILE, CHUNKS, 16]), ALU.add).then_inc(bias_added, 1)
                dve.wait_ge(bias_added, 4)
                dve.tensor_reduce(best[:], prob[:], AX.X, ALU.max).then_inc(steps, 2)
                dve.wait_ge(steps, 2)
                dve.tensor_tensor(prob[:], prob[:], best[:].unsqueeze(2).to_broadcast(wide), ALU.subtract).then_inc(steps, 1)
                dve.wait_ge(exp_ready, 1)
                dve.tensor_reduce(total[:], prob[:], AX.X, ALU.add).then_inc(steps, 1)
                dve.wait_ge(steps, 4)
                dve.reciprocal(inverse[:], total[:]).then_inc(steps, 1)
                dve.wait_ge(steps, 5)
                dve.tensor_tensor(prob[:], prob[:], inverse[:].unsqueeze(2).to_broadcast(wide), ALU.mult).then_inc(steps, 1)
                dve.wait_ge(steps, 6)
                dve.tensor_reduce(best[:], prob[:], AX.X, ALU.max).then_inc(steps, 1)
                dve.wait_ge(steps, 7)
                dve.tensor_tensor(part[:], prob[:], best[:].unsqueeze(2).to_broadcast(wide), ALU.is_equal).then_inc(steps, 1)
                dve.wait_ge(steps, 8)
                dve.tensor_tensor(part[:], part[:], w["top_iota"][0:TILE, :].unsqueeze(1).to_broadcast(wide), ALU.mult).then_inc(steps, 1)
                dve.wait_ge(steps, 9)
                dve.tensor_reduce(best[:], part[:], AX.X, ALU.min).then_inc(exp_ready, 1)
                dve.wait_ge(exp_ready, 2)
                dve.tensor_tensor(part[:], w["top_iota"][0:TILE, :].unsqueeze(1).to_broadcast(wide), best[:].unsqueeze(2).to_broadcast(wide), ALU.is_equal).then_inc(exp_ready, 1)
                dve.wait_ge(exp_ready, 3)
                dve.tensor_tensor(prob[:], prob[:], part[:], ALU.mult).then_inc(steps, 1)
                dve.wait_ge(steps, 10)
                for n in range(cols):
                    dve.wait_ge(y_ready, n + 1)
                    if n >= 4:
                        dve.wait_ge(y_summed, n - 3)
                    dve.tensor_tensor(scaled[:, n % 4], ps[4 + n % 4][0:TILE, :].rearrange("p (e f) -> p e f", e=experts),
                                      prob[:, n].unsqueeze(2).to_broadcast([TILE, experts, FEAT]), ALU.mult).then_inc(y_scaled, 1)
                    dve.wait_ge(y_scaled, n + 1)
                    if n >= 2:
                        dve.wait_ge(final_ready, n - 1)
                    dve.tensor_reduce(summed[:, n % 2], scaled[:, n % 4].rearrange("p e f -> p f e"), AX.X, ALU.add).then_inc(y_summed, 1)
                    dve.wait_ge(y_summed, n + 1)
                    dve.wait_ge(rest_ready, n // 2 + 1)
                    dve.tensor_tensor(final[:, n], summed[:, n % 2], ps[n // 2 % 4][0:TILE, 64 * (n % 2):64 * (n % 2) + 64], ALU.add).then_inc(final_ready, 1)

            @block.sync
            def _(sp):
                for p in range(PAIRS):
                    sp.wait_ge(final_ready, 4 * p + 4)
                    for t in range(2):
                        for a in range(2):
                            sp.dma_start(out_dram[8 * a + p, TILE * t:TILE * t + TILE, :], final[:, 4 * p + 2 * t + a, :]).then_inc(stored, 16)
                sp.wait_ge(stored, 16 * cols)



def both(a):
    return np.concatenate([a, a], 0)


def diagonal(a):
    k, n = a.shape
    out = np.zeros((2 * k, 2 * n), a.dtype)
    out[:k, :n] = a
    out[k:, n:] = a
    return out


def column(v):
    return both(v.reshape(-1, 1))


def rows(v, n=128):
    return np.broadcast_to(v.reshape(1, -1), (n, v.size))


def parts(i):
    f = np.float32
    out = []

    def add(group, name, a):
        out.append((group, name, np.ascontiguousarray(a, dtype=f)))

    half = np.arange(128) // 64
    add(0, "ident", np.eye(128, dtype=f))
    add(1, "win_q", diagonal(i["L0_tok_W_qry"]))
    add(1, "win_k", diagonal(i["L0_tok_W_key"]))
    add(1, "win_b", column(i["L0_tok_b"]))
    v = np.zeros((128, WINDOW, 18), f)
    for o in range(WINDOW):
        v[:64, o, o] = i["L0_tok_v"]
        v[64:, o, 9 + o] = i["L0_tok_v"]
    add(1, "win_v", v.reshape(128, -1))
    sel = np.zeros((128, WINDOW, 128), f)
    for o in range(WINDOW):
        sel[o, o, :64] = 1
        sel[9 + o, o, 64:] = 1
    add(1, "win_out", sel.reshape(128, -1))
    add(0, "mean", (half[:, None] == half[None, :]) / 64.0)
    var = np.zeros((128, TILES, 32), f)
    outm = np.zeros((128, TILES, 128), f)
    for j in range(TILES):
        for a in range(2):
            var[64 * a:64 * a + 64, j, 16 * a + j] = 1.0 / 64
            outm[16 * a + j, j, 64 * a:64 * a + 64] = 1
    add(0, "var_rows", var.reshape(128, -1))
    add(0, "rows_out", outm.reshape(128, -1))
    add(0, "ln_eps", np.full((128, 1), LN_EPS))
    add(2, "mix_qkv", np.concatenate([diagonal(i[f"L0_attn_W{n}"].T) for n in "qkv"], 1))
    add(2, "mix_qkvb", rows(np.concatenate([i[f"L0_attn_b{n}"] for n in "qkv"])))
    add(2, "cap_r", diagonal(i["L0_ffn_wr"]))
    add(2, "cap_br", rows(i["L0_ffn_br"]))
    add(2, "cap_1", diagonal(i["L0_ffn_w1"]))
    add(2, "cap_b1", i["L0_ffn_b1"].reshape(2, 128).T)
    w2 = np.zeros((128, 2, 2, 2, 64), f)
    for a in range(2):
        w2[:, a, :, a, :] = i["L0_ffn_w2"].reshape(2, 128, 64).transpose(1, 0, 2)
    add(2, "cap_2", w2.reshape(128, -1))
    add(2, "cap_b2", column(i["L0_ffn_b2"]))
    n = np.arange(POS)
    add(2, "cap_earlier", np.concatenate([n[None, :] < (t * TILE + np.arange(TILE))[:, None] for t in range(2)], 1))
    add(3, "tay_qkv", np.concatenate([diagonal(i["L1_attn_Wqkv"][64 * n:64 * n + 64].T) for n in range(3)], 1))
    add(3, "tay_qkvb", rows(np.concatenate([np.concatenate([i["L1_attn_bqkv"][64 * n:64 * n + 64]] * 2) for n in range(3)])))
    add(3, "tay_temp", rows(i["L1_attn_temperature"]))
    coef = []
    for a in range(8):
        coef += [0.5] + [1.0] * (7 - a)
    coef += [8.0 ** 0.5] * 8 + [8.0]
    m = np.zeros((2, 45, 4, 32), f)
    for a in range(2):
        m[a, :, :, 9 * a:9 * a + 9] = np.array(coef)[:, None, None]
    add(3, "tay_coef", m.reshape(90, 128))
    wo = np.zeros((4, 32, 64), f)
    wo[:, 1:9], wo[:, 10:18] = (i["L1_attn_Wproj"].T.reshape(4, 2, 8, 64)[:, n] for n in range(2))
    add(3, "tay_o", wo.reshape(128, 64))
    total = np.zeros((128, 4, 32), f)
    for g in range(4):
        total[32 * g, g, :], total[32 * g, g, 9:18], total[32 * g + 9, g, 9:18] = 1, 0, 1
    add(3, "tay_sum", total.reshape(128, 128))
    add(3, "tay_ob", column(i["L1_attn_bproj"]))
    add(4, "moe_r", diagonal(i["L1_ffn_Wr"]))
    add(4, "moe_br", rows(i["L1_ffn_br"]))
    add(4, "moe_b2", diagonal(i["L1_ffn_b2"]))
    n = np.arange(TILE)
    add(4, "moe_tri", n[:, None] < n[None, :])
    add(4, "moe_ones", np.ones((128, 128)))
    add(0, "iota", rows(np.arange(128)))
    add(0, "iota_p", np.arange(128).reshape(-1, 1))
    add(4, "moe_high", (n // 2).reshape(-1, 1))
    add(4, "moe_low", (n % 2)[:, None] * 32 + np.repeat(np.arange(32), 2)[None, :])
    swap = np.arange(64) ^ 1
    add(5, "ret_q", diagonal(i["L2_attn_W_Q"]))
    add(5, "ret_qs", diagonal(i["L2_attn_W_Q"][:, swap]))
    add(5, "ret_k", diagonal(i["L2_attn_W_K"]))
    add(5, "ret_ks", diagonal(i["L2_attn_W_K"][:, swap]))
    add(5, "ret_v", diagonal(i["L2_attn_W_V"]))
    pos = np.arange(POS, dtype=f)
    even = np.arange(0, 64, 2, dtype=f)
    ang = pos[None, :] * (f(1) / f(10000) ** (even / f(64)))[:, None]
    size = ((even + f(25.6)) / f(89.6))[:, None] ** (pos[None, :] / f(512))
    sign = np.tile(np.array([-1, 1], f), 32)[:, None]
    table = []
    for size_ in (size, f(1) / size):
        table += [both(np.repeat(np.cos(ang) * size_, 2, 0)), both(np.repeat(np.sin(ang) * size_, 2, 0) * sign)]
    add(5, "ret_table", np.concatenate(table, 1))
    diff = np.arange(POS)[None, :] - np.arange(TILE)[:, None]
    decay = np.where(diff >= 0, f(0.96875) ** np.maximum(diff, 0).astype(f), 0)
    add(5, "ret_decay", np.concatenate([decay, decay[:, :TILE]], 1))
    add(6, "soft_r", both(i["L2_ffn_Wr"]))
    add(6, "soft_br", rows(i["L2_ffn_br"]))
    add(6, "soft_bo", np.concatenate([i["L2_ffn_bo"]] * 2, 1))
    w1, w2, w3 = (i["L2_ffn_" + n] for n in ("W1", "W2", "Wo"))
    add(6, "soft_1", np.concatenate([diagonal(np.concatenate([w1[e], w1[e + 1]], 1)) for e in range(0, 8, 2)], 1))
    pair = np.zeros((4, 128, 128), f)
    pair[:, :64, :64], pair[:, 64:, 64:] = w2[0::2], w2[1::2]
    add(6, "soft_2", np.concatenate(list(pair), 1))
    add(6, "soft_3", np.concatenate([np.concatenate([w3[e], w3[e + 1]], 0) for e in range(0, 8, 2)], 1))
    add(6, "bn", np.concatenate([np.concatenate([v[0::2].T, v[1::2].T], 0) for v in (i[f"L2_ffn_{n}{layer}"] for n in ("g", "b", "m", "v", "be") for layer in (1, 2))], 1))
    add(6, "bn_eps", np.full((128, 1), 1e-3))
    add(7, "rel_gamma", column(i["L3_attn_ln_gamma"]))
    add(7, "rel_beta", column(i["L3_attn_ln_beta"]))
    for n in "qkv":
        add(7, "rel_" + n, diagonal(i[f"L3_attn_W{n}"].T))
    wo = np.zeros((4, 32, 64), f)
    wo[:, :16] = i["L3_attn_Wo"].T.reshape(4, 16, 64)
    add(7, "rel_o", wo.reshape(128, 64))
    u, v = (np.ascontiguousarray(i[f"L3_attn_{n}_bias"]).reshape(64) for n in "uv")
    add(7, "rel_qu", np.concatenate([column(i["L3_attn_bq"]), column(u), column(v)], 1))
    add(7, "rel_kb", column(i["L3_attn_bk"]))
    add(7, "rel_vb", rows(np.concatenate([i["L3_attn_bv"]] * 2)))
    add(7, "rel_ob", column(i["L3_attn_bo"]))
    add(7, "rel_posb", column(i["L3_attn_bpos"]))
    wpos = i["L3_attn_Wpos"]
    add(7, "rel_pos_t", np.concatenate([wpos.T] * 2, 1))
    omega = np.exp(np.arange(0, 64, 2) * (-np.log(10000.0) / 64))
    ends = np.zeros((64, 2))
    for k, r in enumerate((0, 60)):
        ends[0::2, k], ends[1::2, k] = np.sin(r * omega), np.cos(r * omega)
    add(7, "rel_ends", ends)
    head = (np.arange(64) // 16)[:, None] == np.arange(4)[None, :]
    add(7, "rel_head", both(head) * 0.25)
    h8 = np.zeros((128, 8))
    h8[:64, :4], h8[64:, 4:] = head, head
    add(7, "rel_head8", h8)
    cut = [np.where(head[:, g:g + 1], wpos, f(0)) for g in range(4)]
    add(7, "rel_pos", np.concatenate([diagonal(a) for a in cut], 1))
    add(7, "rel_pos_s", np.concatenate([diagonal(a[:, swap]) for a in cut], 1))
    n = np.arange(POS)
    th = (30 - n)[None, :] * np.repeat(omega, 2)[:, None]
    add(7, "rel_t", np.concatenate([both(np.cos(th)), both(np.sin(th) * np.tile([-1, 1], 32)[:, None])], 1))
    es = n[None, :] * np.repeat(omega, 2)[:, None]
    es[0::2], es[1::2] = np.sin(es[0::2]), np.cos(es[1::2])
    add(7, "rel_s", diagonal(es))
    gap = [n[None, :] - (t * TILE + np.arange(TILE))[:, None] for t in range(2)]
    wide = TILE + 29
    add(7, "rel_near", np.concatenate([np.abs(gap[t])[:, (POS - wide) * t:(POS - wide) * t + wide] < 30 for t in range(2)], 1))
    add(7, "rel_right", np.concatenate([g >= 30 for g in gap], 1))
    add(8, "top_1", diagonal(i["L3_ffn_W1"]))
    add(8, "top_b1", i["L3_ffn_b1"].reshape(2, 128).T)
    gate = np.zeros((128, 2, 2, 32), f)
    for a in range(2):
        gate[:, :, a, 8 * a:8 * a + 8] = i["L3_ffn_Wg"].reshape(2, 128, 8).transpose(1, 0, 2)
    add(8, "top_g", gate.reshape(128, 128))
    add(8, "top_bg", rows(np.concatenate([i["L3_ffn_bg"]] * 2)))
    add(8, "top_d", i["L3_ffn_Wd"].reshape(8, 2, 128, 64).transpose(2, 1, 0, 3).reshape(128, 1024))
    add(8, "top_bd", diagonal(i["L3_ffn_bd"]))
    add(8, "top_iota", rows(np.arange(8) - 8))
    return out


def pack(i):
    where, blocks, at, groups = {}, [], 0, {}
    for group, name, a in sorted(parts(i), key=lambda p: p[0]):
        where[name] = (group, a.shape[0], at, a.shape[1])
        block = np.zeros((128, a.shape[1]), np.float32)
        block[:a.shape[0]] = a
        blocks.append(block)
        lo, _ = groups.get(group, (at, at))
        at += a.shape[1]
        groups[group] = (lo, at)
    return np.concatenate(blocks, 1), where, [groups[g] for g in sorted(groups)]


def extra(i):
    w1 = np.concatenate([i["L1_ffn_W1"], i["L1_ffn_b1"][:, None, :]], 1)
    return {"experts1": np.ascontiguousarray(w1.transpose(1, 0, 2).reshape(FEAT + 1, -1)),
            "experts2": np.ascontiguousarray(i["L1_ffn_W2"].transpose(1, 0, 2).reshape(128, -1))}


def pairs_first(a):
    return np.ascontiguousarray(a.reshape(2, 8, a.shape[1], 64).transpose(0, 3, 1, 2).reshape(128, 8, a.shape[1]))


def program(nc, where, groups, d):
    with ExitStack() as ctx:
        h = ctx.enter_context(nc.sbuf_tensor("h", [128, COLS], F32))
        x = ctx.enter_context(nc.sbuf_tensor("x", [128, COLS], F32))
        ps = [ctx.enter_context(nc.psum_tensor(f"bank{b}", [128, 512], F32)) for b in range(8)]
        d["tokens"] = nc.dram_tensor("tokens", [SEQS * POS, FEAT], F32, kind="Internal").ap()
        d["table"] = nc.dram_tensor("table", [TABLE_TILES * 128, FEAT], F32, kind="Internal").ap()
        w = Weights(nc, ctx, d["weights"], where, groups)
        window_attention(nc, d["x"], h, x, w, ps)
        batch_axis_attention(nc, h, x, w, ps)
        top_half_ffn(nc, h, x, w, ps)
        taylor_attention(nc, h, x, w, ps)
        expert_ffn(nc, h, x, w, ps, d)
        retention(nc, h, x, w, ps)
        soft_mixture(nc, h, x, w, ps)
        relative_attention(nc, h, x, w, ps)
        best_expert_ffn(nc, h, x, w, ps, d["out"])


def kernel(**inputs):
    import numpy as _np
    import concourse.bacc as _bacc
    from concourse import mybir as _mybir
    from concourse.bass_utils import run_bass_kernel_spmd as _run

    given = {name: _np.asarray(a) for name, a in inputs.items()}
    weights, where, groups = pack(given)
    arrays = {"x": pairs_first(given["x"]), "weights": weights, **extra(given)}
    nc = _bacc.Bacc("TRN2", target_bir_lowering=False, num_devices=1)
    d = {name: nc.dram_tensor(f"in_{name}_dram", a.shape, _mybir.dt.float32, kind="ExternalInput").ap() for name, a in arrays.items()}
    d["out"] = nc.dram_tensor("out_0_dram", [SEQS, POS, FEAT], _mybir.dt.float32, kind="ExternalOutput").ap()
    program(nc, where, groups, d)
    r = _run(nc, [{f"in_{name}_dram": a for name, a in arrays.items()}], core_ids=[0])
    return r.results[0]["out_0_dram"]
```
